# Optimizing a Trainium2 kernel written in Bass

```python
import numpy as np
import jax
import jax.numpy as jnp

def _softmax(x, axis=-1):
    return jax.nn.softmax(x, axis=axis)

def _gelu(x):
    return jax.nn.gelu(x, approximate=True)

def _silu(x):
    return jax.nn.silu(x)

def _sigmoid(x):
    return jax.nn.sigmoid(x)

def _layernorm(x, axis=-1, eps=1e-05):
    m = jnp.mean(x, axis=axis, keepdims=True)
    v = jnp.var(x, axis=axis, keepdims=True)
    return (x - m) / jnp.sqrt(v + eps)

def _scatter_add(tgt, idx, src, axis=0):
    return tgt.at[idx].add(src)

def _segment_sum(src, seg, n):
    return jax.ops.segment_sum(src, seg, n)
kernel_name = 'mk_early_fusion_embed_d1_tok_img256_r4_e0c425'

def setup_inputs(seed: int=0):
    np.random.seed(seed)
    _w = jnp.asarray

    def _rec_inputs():
        import jax
        import jax.numpy as jnp
        _rk = jax.random.key(seed)
        x = -4.65018e-05 + 0.999886 * jax.random.normal(jax.random.fold_in(_rk, 1), (64, 3, 128, 128), jnp.float32)
        x_txt = jax.random.randint(jax.random.fold_in(_rk, 51), (64, 128), 0, 64, jnp.int32)
        return (x, x_txt)
    x, x_txt = _rec_inputs()

    def _L0_tok_setup():
        import jax, jax.numpy as jnp
        import numpy as np
        B = 64
        IMG = 128
        P = 32
        DIM = 64
        DEPTH = 4
        HEADS = 4
        DH = 64
        MLP = 128
        PD = 3 * P * P
        GRID = IMG // P
        NPATCH = GRID * GRID

        def _ln(x, g, b):
            m = jnp.mean(x, -1, keepdims=True)
            v = jnp.mean((x - m) ** 2, -1, keepdims=True)
            return (x - m) * jax.lax.rsqrt(v + 1e-05) * g + b
        key = jax.random.key(seed)
        ks = jax.random.split(key, 10)

        def n(k, shape, s=0.02):
            return jax.random.normal(k, shape, jnp.float32) * s
        return {'img': jax.random.normal(ks[0], (B, 3, IMG, IMG), jnp.float32), 'ln_p1_g': jnp.ones((PD,), jnp.float32), 'ln_p1_b': jnp.zeros((PD,), jnp.float32), 'W_patch': n(ks[1], (PD, DIM)), 'b_patch': jnp.zeros((DIM,), jnp.float32), 'ln_p2_g': jnp.ones((DIM,), jnp.float32), 'ln_p2_b': jnp.zeros((DIM,), jnp.float32), 'cls': n(ks[2], (1, 1, DIM), 1.0), 'pos': n(ks[3], (1, NPATCH + 1, DIM), 1.0), 'attn_ln_g': jnp.ones((DEPTH, DIM), jnp.float32), 'attn_ln_b': jnp.zeros((DEPTH, DIM), jnp.float32), 'Wqkv': n(ks[4], (DEPTH, DIM, 3 * HEADS * DH)), 'Wo': n(ks[5], (DEPTH, HEADS * DH, DIM)), 'bo': jnp.zeros((DEPTH, DIM), jnp.float32), 'ff_ln_g': jnp.ones((DEPTH, DIM), jnp.float32), 'ff_ln_b': jnp.zeros((DEPTH, DIM), jnp.float32), 'W1': n(ks[6], (DEPTH, DIM, MLP)), 'b1': jnp.zeros((DEPTH, MLP), jnp.float32), 'W2': n(ks[7], (DEPTH, MLP, DIM)), 'b2': jnp.zeros((DEPTH, DIM), jnp.float32), 'ln_f_g': jnp.ones((DIM,), jnp.float32), 'ln_f_b': jnp.zeros((DIM,), jnp.float32)}
    _L0_tok_all = _L0_tok_setup()
    _L0_tok_in = {k: v for k, v in _L0_tok_all.items() if k in ('ln_p1_g', 'ln_p1_b', 'W_patch', 'b_patch', 'ln_p2_g', 'ln_p2_b', 'cls', 'pos', 'attn_ln_g', 'attn_ln_b', 'Wqkv', 'Wo', 'bo', 'ff_ln_g', 'ff_ln_b', 'W1', 'b1', 'W2', 'b2', 'ln_f_g', 'ln_f_b')}
    del _L0_tok_all

    def _L0_txt_setup():
        import jax, jax.numpy as jnp
        import numpy as np
        V, C, D, N_ROUNDS, WIN = (64, 8, 128, 3, 4)
        B, T = (16, 2048)
        EPS = 1e-05

        def _ln(x, g, b):
            mu = jnp.mean(x, axis=-1, keepdims=True)
            var = jnp.mean((x - mu) ** 2, axis=-1, keepdims=True)
            return (x - mu) * jax.lax.rsqrt(var + EPS) * g + b

        def _mlp2(x, w1, b1, w2, b2):
            return jax.nn.gelu(x @ w1 + b1, approximate=False) @ w2 + b2
        key = jax.random.key(seed)
        ks = iter(jax.random.split(key, 32))
        nrm = lambda shp, s: jax.random.normal(next(ks), shp, jnp.float32) * s
        inp = {'x': jax.random.randint(next(ks), (B, T), 0, V, dtype=jnp.int32), 'emb': nrm((V, D), 0.02), 'pos': nrm((C, D), 0.02), 'lw1': nrm((D, 2 * D), 0.05), 'lb1': jnp.zeros((2 * D,)), 'lw2': nrm((2 * D, D), 0.05), 'lb2': jnp.zeros((D,)), 'lln_g': jnp.ones((D,)), 'lln_b': jnp.zeros((D,)), 'pool_w': nrm((D, D), 0.05), 'pool_b': jnp.zeros((D,)), 'msg_w1': nrm((2 * D, D), 0.05), 'msg_b1': jnp.zeros((D,)), 'msg_w2': nrm((D, D), 0.05), 'msg_b2': jnp.zeros((D,)), 'upd_w1': nrm((2 * D, D), 0.05), 'upd_b1': jnp.zeros((D,)), 'upd_w2': nrm((D, D), 0.05), 'upd_b2': jnp.zeros((D,)), 'mln_g': jnp.ones((D,)), 'mln_b': jnp.zeros((D,)), 'bc_w': nrm((D, D), 0.05), 'bc_b': jnp.zeros((D,)), 'fln_g': jnp.ones((D,)), 'fln_b': jnp.zeros((D,)), 'head_w': nrm((D, V), 0.05)}
        return inp
    _L0_txt_all = _L0_txt_setup()
    _L0_txt_in = {k: v for k, v in _L0_txt_all.items() if k in ('emb', 'pos', 'lw1', 'lb1', 'lw2', 'lb2', 'lln_g', 'lln_b', 'pool_w', 'pool_b', 'msg_w1', 'msg_b1', 'msg_w2', 'msg_b2', 'upd_w1', 'upd_b1', 'upd_w2', 'upd_b2', 'mln_g', 'mln_b', 'bc_w', 'bc_b', 'fln_g', 'fln_b', 'head_w')}
    del _L0_txt_all

    def _L0_attn_setup():
        import jax, jax.numpy as jnp
        import numpy as np
        B, S, C = (8, 256, 64)
        H, KD = (8, 64)
        HEAD_DIM = KD // H
        key = jax.random.key(seed)
        ks = jax.random.split(key, 5)
        sc = 0.02
        return {'x': jax.random.normal(ks[0], (B, S, C), dtype=jnp.float32), 'Wq': jax.random.normal(ks[1], (H * KD, C), dtype=jnp.float32) * sc, 'Wk': jax.random.normal(ks[2], (KD, C), dtype=jnp.float32) * sc, 'Wv': jax.random.normal(ks[3], (KD, C), dtype=jnp.float32) * sc, 'Wo': jax.random.normal(ks[4], (C, H * KD), dtype=jnp.float32) * sc}
    _L0_attn_all = _L0_attn_setup()
    _L0_attn_in = {k: v for k, v in _L0_attn_all.items() if k in ('Wq', 'Wk', 'Wv', 'Wo')}
    del _L0_attn_all

    def _L0_ffn_setup():
        import jax, jax.numpy as jnp
        import numpy as np
        B, T, C = (64, 96, 64)
        NH, NKV = (4, 2)
        HD = C // NH
        NREP = NH // NKV
        NE, TOPK = (8, 2)
        HID = int(8 / 3 * C)
        EPS_RMS = 1e-06

        def _rope_tables(t_len):
            inv_freq = 1.0 / 10000.0 ** (np.arange(0, HD, 2, dtype=np.float32) / HD)
            t = np.arange(t_len, dtype=np.float32)
            freqs = np.outer(t, inv_freq)
            emb = np.concatenate([freqs, freqs], axis=-1)
            return (jnp.asarray(np.cos(emb)), jnp.asarray(np.sin(emb)))

        def _rotate_half(x):
            h = x.shape[-1] // 2
            return jnp.concatenate([-x[..., h:], x[..., :h]], axis=-1)

        def _rmsnorm(v, w):
            return v * jax.lax.rsqrt(jnp.mean(v * v, axis=-1, keepdims=True) + EPS_RMS) * w
        key = jax.random.key(seed)
        ks = jax.random.split(key, 10)
        s = lambda k, shape: jax.random.normal(k, shape, jnp.float32) * 0.02
        return {'x': jax.random.normal(ks[0], (B, T, C), jnp.float32), 'ln1_w': jnp.ones((C,), jnp.float32), 'ln2_w': jnp.ones((C,), jnp.float32), 'wq': s(ks[1], (NH * HD, C)), 'wk': s(ks[2], (NKV * HD, C)), 'wv': s(ks[3], (NKV * HD, C)), 'wo': s(ks[4], (C, C)), 'router_w': s(ks[5], (NE, C)), 'w1': s(ks[6], (NE, HID, C)), 'w2': s(ks[7], (NE, C, HID)), 'w3': s(ks[8], (NE, HID, C))}
    _L0_ffn_all = _L0_ffn_setup()
    _L0_ffn_in = {k: v for k, v in _L0_ffn_all.items() if k in ('ln1_w', 'ln2_w', 'wq', 'wk', 'wv', 'wo', 'router_w', 'w1', 'w2', 'w3')}
    del _L0_ffn_all
    return {'x': x, 'x_txt': x_txt, 'L0_tok_ln_p1_g': _L0_tok_in['ln_p1_g'], 'L0_tok_ln_p1_b': _L0_tok_in['ln_p1_b'], 'L0_tok_W_patch': _L0_tok_in['W_patch'], 'L0_tok_b_patch': _L0_tok_in['b_patch'], 'L0_tok_ln_p2_g': _L0_tok_in['ln_p2_g'], 'L0_tok_ln_p2_b': _L0_tok_in['ln_p2_b'], 'L0_tok_cls': _L0_tok_in['cls'], 'L0_tok_pos': _L0_tok_in['pos'], 'L0_tok_attn_ln_g': _L0_tok_in['attn_ln_g'], 'L0_tok_attn_ln_b': _L0_tok_in['attn_ln_b'], 'L0_tok_Wqkv': _L0_tok_in['Wqkv'], 'L0_tok_Wo': _L0_tok_in['Wo'], 'L0_tok_bo': _L0_tok_in['bo'], 'L0_tok_ff_ln_g': _L0_tok_in['ff_ln_g'], 'L0_tok_ff_ln_b': _L0_tok_in['ff_ln_b'], 'L0_tok_W1': _L0_tok_in['W1'], 'L0_tok_b1': _L0_tok_in['b1'], 'L0_tok_W2': _L0_tok_in['W2'], 'L0_tok_b2': _L0_tok_in['b2'], 'L0_tok_ln_f_g': _L0_tok_in['ln_f_g'], 'L0_tok_ln_f_b': _L0_tok_in['ln_f_b'], 'L0_txt_emb': _L0_txt_in['emb'], 'L0_txt_pos': _L0_txt_in['pos'], 'L0_txt_lw1': _L0_txt_in['lw1'], 'L0_txt_lb1': _L0_txt_in['lb1'], 'L0_txt_lw2': _L0_txt_in['lw2'], 'L0_txt_lb2': _L0_txt_in['lb2'], 'L0_txt_lln_g': _L0_txt_in['lln_g'], 'L0_txt_lln_b': _L0_txt_in['lln_b'], 'L0_txt_pool_w': _L0_txt_in['pool_w'], 'L0_txt_pool_b': _L0_txt_in['pool_b'], 'L0_txt_msg_w1': _L0_txt_in['msg_w1'], 'L0_txt_msg_b1': _L0_txt_in['msg_b1'], 'L0_txt_msg_w2': _L0_txt_in['msg_w2'], 'L0_txt_msg_b2': _L0_txt_in['msg_b2'], 'L0_txt_upd_w1': _L0_txt_in['upd_w1'], 'L0_txt_upd_b1': _L0_txt_in['upd_b1'], 'L0_txt_upd_w2': _L0_txt_in['upd_w2'], 'L0_txt_upd_b2': _L0_txt_in['upd_b2'], 'L0_txt_mln_g': _L0_txt_in['mln_g'], 'L0_txt_mln_b': _L0_txt_in['mln_b'], 'L0_txt_bc_w': _L0_txt_in['bc_w'], 'L0_txt_bc_b': _L0_txt_in['bc_b'], 'L0_txt_fln_g': _L0_txt_in['fln_g'], 'L0_txt_fln_b': _L0_txt_in['fln_b'], 'L0_txt_head_w': _L0_txt_in['head_w'], 'L0_attn_Wq': _L0_attn_in['Wq'], 'L0_attn_Wk': _L0_attn_in['Wk'], 'L0_attn_Wv': _L0_attn_in['Wv'], 'L0_attn_Wo': _L0_attn_in['Wo'], 'L0_ffn_ln1_w': _L0_ffn_in['ln1_w'], 'L0_ffn_ln2_w': _L0_ffn_in['ln2_w'], 'L0_ffn_wq': _L0_ffn_in['wq'], 'L0_ffn_wk': _L0_ffn_in['wk'], 'L0_ffn_wv': _L0_ffn_in['wv'], 'L0_ffn_wo': _L0_ffn_in['wo'], 'L0_ffn_router_w': _L0_ffn_in['router_w'], 'L0_ffn_w1': _L0_ffn_in['w1'], 'L0_ffn_w2': _L0_ffn_in['w2'], 'L0_ffn_w3': _L0_ffn_in['w3']}

def reference(x, x_txt, L0_tok_ln_p1_g, L0_tok_ln_p1_b, L0_tok_W_patch, L0_tok_b_patch, L0_tok_ln_p2_g, L0_tok_ln_p2_b, L0_tok_cls, L0_tok_pos, L0_tok_attn_ln_g, L0_tok_attn_ln_b, L0_tok_Wqkv, L0_tok_Wo, L0_tok_bo, L0_tok_ff_ln_g, L0_tok_ff_ln_b, L0_tok_W1, L0_tok_b1, L0_tok_W2, L0_tok_b2, L0_tok_ln_f_g, L0_tok_ln_f_b, L0_txt_emb, L0_txt_pos, L0_txt_lw1, L0_txt_lb1, L0_txt_lw2, L0_txt_lb2, L0_txt_lln_g, L0_txt_lln_b, L0_txt_pool_w, L0_txt_pool_b, L0_txt_msg_w1, L0_txt_msg_b1, L0_txt_msg_w2, L0_txt_msg_b2, L0_txt_upd_w1, L0_txt_upd_b1, L0_txt_upd_w2, L0_txt_upd_b2, L0_txt_mln_g, L0_txt_mln_b, L0_txt_bc_w, L0_txt_bc_b, L0_txt_fln_g, L0_txt_fln_b, L0_txt_head_w, L0_attn_Wq, L0_attn_Wk, L0_attn_Wv, L0_attn_Wo, L0_ffn_ln1_w, L0_ffn_ln2_w, L0_ffn_wq, L0_ffn_wk, L0_ffn_wv, L0_ffn_wo, L0_ffn_router_w, L0_ffn_w1, L0_ffn_w2, L0_ffn_w3):
    import jax
    import jax.numpy as jnp

    def _L0_tok_ref(img, ln_p1_g, ln_p1_b, W_patch, b_patch, ln_p2_g, ln_p2_b, cls, pos, attn_ln_g, attn_ln_b, Wqkv, Wo, bo, ff_ln_g, ff_ln_b, W1, b1, W2, b2, ln_f_g, ln_f_b):
        import jax, jax.numpy as jnp
        import numpy as np
        B = 64
        IMG = 128
        P = 32
        DIM = 64
        DEPTH = 4
        HEADS = 4
        DH = 64
        MLP = 128
        PD = 3 * P * P
        GRID = IMG // P
        NPATCH = GRID * GRID

        def _ln(x, g, b):
            m = jnp.mean(x, -1, keepdims=True)
            v = jnp.mean((x - m) ** 2, -1, keepdims=True)
            return (x - m) * jax.lax.rsqrt(v + 1e-05) * g + b
        Bsz = img.shape[0]
        x = img.reshape(Bsz, 3, GRID, P, GRID, P)
        x = x.transpose(0, 2, 4, 1, 3, 5).reshape(Bsz, NPATCH, PD)
        x = _ln(x, ln_p1_g, ln_p1_b) @ W_patch + b_patch
        x = _ln(x, ln_p2_g, ln_p2_b)
        x = jnp.concatenate([jnp.broadcast_to(cls, (Bsz, 1, DIM)), x], axis=1) + pos
        scale = DH ** (-0.5)
        for i in range(DEPTH):
            h = _ln(x, attn_ln_g[i], attn_ln_b[i])
            qkv = h @ Wqkv[i]
            q, k, v = jnp.split(qkv, 3, axis=-1)

            def to_heads(t):
                return t.reshape(Bsz, -1, HEADS, DH).transpose(0, 2, 1, 3)
            q, k, v = (to_heads(q), to_heads(k), to_heads(v))
            a = jax.nn.softmax(jnp.einsum('bhqd,bhkd->bhqk', q, k) * scale, axis=-1)
            o = jnp.einsum('bhqk,bhkd->bhqd', a, v)
            o = o.transpose(0, 2, 1, 3).reshape(Bsz, -1, HEADS * DH)
            x = x + o @ Wo[i] + bo[i]
            h = _ln(x, ff_ln_g[i], ff_ln_b[i])
            x = x + jax.nn.gelu(h @ W1[i] + b1[i], approximate=False) @ W2[i] + b2[i]
        return _ln(x, ln_f_g, ln_f_b)

    def _L0_txt_ref(x, emb, pos, lw1, lb1, lw2, lb2, lln_g, lln_b, pool_w, pool_b, msg_w1, msg_b1, msg_w2, msg_b2, upd_w1, upd_b1, upd_w2, upd_b2, mln_g, mln_b, bc_w, bc_b, fln_g, fln_b, head_w):
        import jax, jax.numpy as jnp
        import numpy as np
        V, C, D, N_ROUNDS, WIN = (64, 8, 128, 3, 4)
        B, T = (16, 2048)
        EPS = 1e-05

        def _ln(x, g, b):
            mu = jnp.mean(x, axis=-1, keepdims=True)
            var = jnp.mean((x - mu) ** 2, axis=-1, keepdims=True)
            return (x - mu) * jax.lax.rsqrt(var + EPS) * g + b

        def _mlp2(x, w1, b1, w2, b2):
            return jax.nn.gelu(x @ w1 + b1, approximate=False) @ w2 + b2
        Bv, Tv = x.shape
        pad = -Tv % C
        padded_T = Tv + pad
        n_chunks = padded_T // C
        x_pad = jnp.pad(x, ((0, 0), (0, pad)))
        chunks = x_pad.reshape(Bv, n_chunks, C)
        h = emb[chunks] + pos[None, None, :, :]
        local = h + _mlp2(_ln(h, lln_g, lln_b), lw1, lb1, lw2, lb2)
        summ = local.mean(axis=2) @ pool_w + pool_b
        i = jnp.arange(n_chunks)[:, None]
        d = jnp.arange(WIN + 1)[None, :]
        idx = jnp.clip(i - d, 0, None)
        valid = (i - d >= 0).astype(summ.dtype)
        count = valid.sum(axis=1)
        hmsg = summ
        for _ in range(N_ROUNDS):
            nbr = hmsg[:, idx]
            self_e = jnp.broadcast_to(hmsg[:, :, None, :], nbr.shape)
            msgs = _mlp2(jnp.concatenate([self_e, nbr], -1), msg_w1, msg_b1, msg_w2, msg_b2)
            agg = (msgs * valid[None, :, :, None]).sum(axis=2) / count[None, :, None]
            upd = _mlp2(jnp.concatenate([hmsg, agg], -1), upd_w1, upd_b1, upd_w2, upd_b2)
            hmsg = _ln(hmsg + upd, mln_g, mln_b)
        bc = hmsg @ bc_w + bc_b
        combined = (local + bc[:, :, None, :]).reshape(Bv, padded_T, D)[:, :Tv, :]
        logits = _ln(combined, fln_g, fln_b) @ head_w
        return logits

    def _L0_attn_ref(x, Wq, Wk, Wv, Wo):
        import jax, jax.numpy as jnp
        import numpy as np
        B, S, C = (8, 256, 64)
        H, KD = (8, 64)
        HEAD_DIM = KD // H
        b, s, c = x.shape
        q = jnp.einsum('bsc,oc->bso', x, Wq).reshape(b, s, H, KD).transpose(0, 2, 1, 3)
        k = jnp.einsum('bsc,oc->bos', x, Wk)
        v_conv = jnp.einsum('bsc,oc->bos', x, Wv)
        v = v_conv.reshape(b, s, KD)
        scale = 1.0 / np.sqrt(HEAD_DIM).astype(np.float32)
        scores = jnp.einsum('bhsd,bdt->bhst', q, k) * scale
        attn = jax.nn.softmax(scores, axis=-1)
        ctx = jnp.einsum('bhst,btd->bhsd', attn, v)
        ctx = ctx.transpose(0, 2, 1, 3).reshape(b, H * KD, s)
        out = jnp.einsum('bcp,oc->bop', ctx, Wo)
        return out.transpose(0, 2, 1)

    def _L0_ffn_ref(x, ln1_w, ln2_w, wq, wk, wv, wo, router_w, w1, w2, w3):
        import jax, jax.numpy as jnp
        import numpy as np
        B, T, C = (64, 96, 64)
        NH, NKV = (4, 2)
        HD = C // NH
        NREP = NH // NKV
        NE, TOPK = (8, 2)
        HID = int(8 / 3 * C)
        EPS_RMS = 1e-06

        def _rope_tables(t_len):
            inv_freq = 1.0 / 10000.0 ** (np.arange(0, HD, 2, dtype=np.float32) / HD)
            t = np.arange(t_len, dtype=np.float32)
            freqs = np.outer(t, inv_freq)
            emb = np.concatenate([freqs, freqs], axis=-1)
            return (jnp.asarray(np.cos(emb)), jnp.asarray(np.sin(emb)))

        def _rotate_half(x):
            h = x.shape[-1] // 2
            return jnp.concatenate([-x[..., h:], x[..., :h]], axis=-1)

        def _rmsnorm(v, w):
            return v * jax.lax.rsqrt(jnp.mean(v * v, axis=-1, keepdims=True) + EPS_RMS) * w
        Bx, Tx, Cx = x.shape
        h = _rmsnorm(x, ln1_w)
        q = (h @ wq.T).reshape(Bx, Tx, NH, HD).transpose(0, 2, 1, 3)
        k = (h @ wk.T).reshape(Bx, Tx, NKV, HD).transpose(0, 2, 1, 3)
        v = (h @ wv.T).reshape(Bx, Tx, NKV, HD).transpose(0, 2, 1, 3)
        cos, sin = _rope_tables(Tx)
        cos, sin = (cos[None, None], sin[None, None])
        q = q * cos + _rotate_half(q) * sin
        k = k * cos + _rotate_half(k) * sin
        k = jnp.repeat(k, NREP, axis=1)
        v = jnp.repeat(v, NREP, axis=1)
        scores = jnp.einsum('bhtd,bhsd->bhts', q, k) / jnp.sqrt(jnp.float32(HD))
        causal = jnp.tril(jnp.ones((Tx, Tx), dtype=bool))
        scores = jnp.where(causal[None, None], scores, jnp.float32(-1e+30))
        att = jax.nn.softmax(scores, axis=-1)
        y = jnp.einsum('bhts,bhsd->bhtd', att, v).transpose(0, 2, 1, 3).reshape(Bx, Tx, Cx)
        x = x + y @ wo.T
        flat = _rmsnorm(x, ln2_w).reshape(-1, Cx)
        probs = jax.nn.softmax(flat @ router_w.T, axis=-1)
        tp, ti = jax.lax.top_k(probs, TOPK)
        tp = tp / (jnp.sum(tp, axis=-1, keepdims=True) + 1e-09)
        weights = jnp.sum(tp[..., None] * jax.nn.one_hot(ti, NE, dtype=flat.dtype), axis=1)
        out = jnp.zeros_like(flat)
        for e in range(NE):
            hh = jax.nn.silu(flat @ w1[e].T) * (flat @ w3[e].T)
            out = out + weights[:, e:e + 1] * (hh @ w2[e].T)
        return x + out.reshape(Bx, Tx, Cx)
    h = _L0_tok_ref(x, L0_tok_ln_p1_g, L0_tok_ln_p1_b, L0_tok_W_patch, L0_tok_b_patch, L0_tok_ln_p2_g, L0_tok_ln_p2_b, L0_tok_cls, L0_tok_pos, L0_tok_attn_ln_g, L0_tok_attn_ln_b, L0_tok_Wqkv, L0_tok_Wo, L0_tok_bo, L0_tok_ff_ln_g, L0_tok_ff_ln_b, L0_tok_W1, L0_tok_b1, L0_tok_W2, L0_tok_b2, L0_tok_ln_f_g, L0_tok_ln_f_b)
    h = jnp.concatenate([h, _L0_txt_ref(x_txt, L0_txt_emb, L0_txt_pos, L0_txt_lw1, L0_txt_lb1, L0_txt_lw2, L0_txt_lb2, L0_txt_lln_g, L0_txt_lln_b, L0_txt_pool_w, L0_txt_pool_b, L0_txt_msg_w1, L0_txt_msg_b1, L0_txt_msg_w2, L0_txt_msg_b2, L0_txt_upd_w1, L0_txt_upd_b1, L0_txt_upd_w2, L0_txt_upd_b2, L0_txt_mln_g, L0_txt_mln_b, L0_txt_bc_w, L0_txt_bc_b, L0_txt_fln_g, L0_txt_fln_b, L0_txt_head_w)], axis=1)
    h = h + _L0_attn_ref(_layernorm(h, axis=-1), L0_attn_Wq, L0_attn_Wk, L0_attn_Wv, L0_attn_Wo)
    h = h + _L0_ffn_ref(_layernorm(h, axis=-1), L0_ffn_ln1_w, L0_ffn_ln2_w, L0_ffn_wq, L0_ffn_wk, L0_ffn_wv, L0_ffn_wo, L0_ffn_router_w, L0_ffn_w1, L0_ffn_w2, L0_ffn_w3)
    return h

_drawn_inputs = setup_inputs


def setup_inputs(seed=0):
    import zlib

    import numpy as np

    out = dict(_drawn_inputs(seed))
    spreads = {'L0_tok_ln_p1_g': (1.0, 0.2),
     'L0_tok_ln_p1_b': (0.0, 0.375),
     'L0_tok_b_patch': (0.0, 0.333),
     'L0_tok_ln_p2_g': (1.0, 0.2),
     'L0_tok_ln_p2_b': (0.0, 0.271),
     'L0_tok_attn_ln_g': (1.0, 0.6),
     'L0_tok_attn_ln_b': (0.0, 0.8),
     'L0_tok_bo': (0.0, 0.1),
     'L0_tok_ff_ln_g': (1.0, 0.6),
     'L0_tok_ff_ln_b': (0.0, 0.8),
     'L0_tok_b1': (0.0, 0.8),
     'L0_tok_b2': (0.0, 0.1),
     'L0_tok_ln_f_g': (1.0, 0.2),
     'L0_tok_ln_f_b': (0.0, 0.1),
     'L0_txt_lb1': (0.0, 0.1),
     'L0_txt_lb2': (0.0, 0.1),
     'L0_txt_lln_g': (1.0, 0.2),
     'L0_txt_lln_b': (0.0, 0.1),
     'L0_txt_pool_b': (0.0, 0.1),
     'L0_txt_msg_b1': (0.0, 0.465),
     'L0_txt_msg_b2': (0.0, 0.1),
     'L0_txt_upd_b1': (0.0, 0.1),
     'L0_txt_upd_b2': (0.0, 0.1),
     'L0_txt_mln_g': (1.0, 0.2),
     'L0_txt_mln_b': (0.0, 0.1),
     'L0_txt_bc_b': (0.0, 0.1),
     'L0_txt_fln_g': (1.0, 0.2),
     'L0_txt_fln_b': (0.0, 0.1),
     'L0_ffn_ln1_w': (1.0, 0.6),
     'L0_ffn_ln2_w': (1.0, 0.6)}
    factors = {'L0_tok_Wqkv': 5.947,
     'L0_tok_Wo': 6.699,
     'L0_tok_W1': 5.189,
     'L0_tok_W2': 4.47,
     'L0_attn_Wq': 8.0,
     'L0_attn_Wk': 8.0,
     'L0_attn_Wv': 8.0,
     'L0_attn_Wo': 7.357,
     'L0_ffn_wq': 8.0,
     'L0_ffn_wk': 8.0,
     'L0_ffn_wv': 5.757,
     'L0_ffn_wo': 6.897,
     'L0_ffn_router_w': 8.0,
     'L0_ffn_w1': 8.0,
     'L0_ffn_w2': 8.0,
     'L0_ffn_w3': 8.0}
    for name, (base, spread) in spreads.items():
        noise = np.random.default_rng([zlib.crc32(name.encode()), seed]).standard_normal(out[name].shape)
        drawn = base * np.exp(spread * noise) if base else spread * noise
        out[name] = jnp.asarray(drawn.astype(out[name].dtype))
    for name, factor in factors.items():
        out[name] = (out[name] * factor).astype(out[name].dtype)
    return out
```

```python
from contextlib import ExitStack

import concourse.bass as bass
from concourse import mybir

F32 = mybir.dt.float32
BF16 = mybir.dt.bfloat16
I32 = mybir.dt.int32
ALU = mybir.AluOpType
ACT = mybir.ActivationFunctionType
X = mybir.AxisListType.X

NB = 64
C = 64
NTOK = 17
T = 145
TOKENS = NB * T
TM = 116
GB = 4
GT = GB * T
GJ = GT // TM
NG = NB // GB
EPS = 1e-5
MASKED = -1e30
BANK = 512


class Steps:

    def __init__(self, nc, stack, name, steps):
        self.sem = stack.enter_context(nc.semaphore(name))
        self.steps = steps
        self.n = len(steps)
        self.next = 0

    def start(self, eng):
        eng.sem_inc(self.sem, self.n)

    def mark(self, step):
        assert self.steps[self.next % self.n] == step, (step, self.steps[self.next % self.n])
        self.next += 1
        return self.sem

    def at(self, step, i=0):
        return i * self.n + (self.n + self.steps.index(step) + 1)

    def before(self, step, i=0):
        return i * self.n + (self.steps.index(step) + 1)


class Landed:

    def __init__(self, nc, stack, name, k):
        self.sem = stack.enter_context(nc.semaphore(name))
        self.k = 16 * k

    def start(self, eng):
        eng.sem_inc(self.sem, self.k)

    def at(self, i=0):
        return i * self.k + 2 * self.k

    def before(self, i=0):
        return i * self.k + self.k


class Shared:

    def __init__(self, dram):
        self.dram = dram


def cols(ap, n):
    return ap.broadcast_to(list(ap.shape[:-1]) + [n])


def phase_end(m, eng, phase):
    eng.drain().then_inc(m.phase_done, 1)
    eng.wait_ge(m.phase_done, 5 * (phase + 1))
    eng.sem_inc(m.gate, 1)


def patch_phase(nc, m, st, ph):
    IMG, P, GRID, DIM = 128, 32, 4, 64
    CH = 3
    K = CH * P
    B8 = 8
    NI = NB // B8
    NP = B8 * GRID * GRID
    PD = CH * P * P
    sb = lambda n, s, d=F32: st.enter_context(nc.sbuf_tensor(n, s, d))
    img = [sb(f"img{s}", [K, B8, GRID, IMG]) for s in range(2)]
    sq = [sb(f"img_sq{s}", [K, NP // 4, 4 * P]) for s in range(2)]
    sqsum = [sb(f"sqsum{s}", [K, NP]) for s in range(2)]
    proj = [sb(f"proj{s}", [DIM + 1, NP]) for s in range(2)]
    w = sb("w_patch", [K, P, DIM])
    wg = sb("w_patch_gained", [K, P, DIM + 1])
    wb = sb("w_patch_biased", [K, P, DIM])
    gain, shift = sb("patch_gain", [K, P]), sb("patch_shift", [K, P])
    wsum, wbsum = sb("w_gained_sum", [K, DIM]), sb("w_biased_sum", [K, DIM])
    ones = sb("ones_patch", [K, 128])
    colsum, bias = sb("colsum", [128, DIM]), sb("bias_p", [128, DIM])
    bp = sb("b_patch_rows", [128, DIM])
    g2, b2 = sb("ln_p2_g_rows", [128, DIM]), sb("ln_p2_b_rows", [128, DIM])
    pos = sb("pos_rows", [128, DIM])
    cls = sb("cls_rows", [128, DIM])
    raw = sb("raw_tokens", [128, NI, DIM + 2])
    y, t = sb("patch_y", [128, NI, DIM]), sb("patch_t", [128, NI, DIM])
    mean, var, tmp = sb("p_mean", [128, NI]), sb("p_var", [128, NI]), sb("p_tmp", [128, NI])
    eps = sb("p_eps", [128, 1])
    ps = m.psum
    sem = lambda n: m.whole.enter_context(nc.semaphore(n))
    consts = sem("patch_consts_landed")
    placed = sem("patch_tokens_placed")
    imgs = [Landed(nc, m.whole, f"img_landed{s}", CH * GRID) for s in range(2)]
    pe_s = Steps(nc, m.whole, "patch_pe", [f"{k}{s}" for s in range(2) for k in ("projected", "squares", "turned")])
    act_s = Steps(nc, m.whole, "patch_act", [f"{k}{s}" for s in range(2) for k in ("squared", "proj_copied")])
    dve_s = Steps(nc, m.whole, "patch_dve", [f"{k}{s}" for s in range(2) for k in ("sq_reduced", "raw_copied", "sumsq_copied")])
    pe_w = Steps(nc, m.whole, "patch_pe_w", ["sums"])
    dve_w = Steps(nc, m.whole, "patch_dve_w", ["ones", "gained", "ones_col", "biased", "wsum", "wbsum", "colsum", "bias", "eps", "x_clear"])
    fin = ["mean", "msq", "ex2", "var", "recip", "mu_w", "minus", "scaled", "biased", "sum", "mean2", "cent",
           "sq2", "ss2", "recip2", "norm2", "gain2", "shift2", "pos_added"]
    dve_f = Steps(nc, m.whole, "patch_dve_f", fin)
    act_f = Steps(nc, m.whole, "patch_act_f", ["std", "std2"])

    def sync(sp):
        sp.dma_start(w[:], m.dram["tok_W_patch"].rearrange("(p x) o -> p x o", x=P)).then_inc(consts, 16)
        sp.dma_start(gain[:], m.dram["tok_ln_p1_g"].rearrange("(p x) -> p x", x=P)).then_inc(consts, 16)
        sp.dma_start(shift[:], m.dram["tok_ln_p1_b"].rearrange("(p x) -> p x", x=P)).then_inc(consts, 16)
        sp.dma_start(bp[:], m.dram["tok_b_patch"].partition_broadcast(128)).then_inc(consts, 16)
        sp.dma_start(g2[:], m.dram["tok_ln_p2_g"].partition_broadcast(128)).then_inc(consts, 16)
        sp.dma_start(b2[:], m.dram["tok_ln_p2_b"].partition_broadcast(128)).then_inc(consts, 16)
        for s in range(2):
            imgs[s].start(sp)
        with sp.Fori(0, NI // 2) as i:
            for s in range(2):
                sp.wait_ge(pe_s.sem, pe_s.before(f"projected{s}", i))
                sp.sem_inc(m.gate, 1)
                sp.wait_ge(act_s.sem, act_s.before(f"squared{s}", i))
                sp.sem_inc(m.gate, 1)
                for c in range(CH):
                    for g in range(GRID):
                        sp.dma_start(img[s][c * P:(c + 1) * P, :, g, :],
                                     m.dram["x"][bass.ds(i * 2 * B8 + s * B8, B8), c, g * P:(g + 1) * P].rearrange("b r w -> r b w")
                                     ).then_inc(imgs[s].sem, 16)
        sp.wait_ge(dve_w.sem, dve_w.at("x_clear"))
        for j in range(4):
            sp.dma_start(m.pos_tile[32 * j:32 * j + NTOK], m.dram["tok_pos"][0]).then_inc(consts, 16)
            sp.dma_start(m.vit_x[32 * j:32 * j + 1], m.dram["tok_cls"][0, 0:1].unsqueeze(1).broadcast_to([1, 16, DIM])).then_inc(placed, 16)
        sp.wait_ge(dve_f.sem, dve_f.at("shift2"))
        for j in range(4):
            for half in range(2):
                p0 = (4 * half + j) * 16
                sp.dma_start(m.vit_x[32 * j + 1:32 * j + NTOK, half::2, :], y[p0:p0 + 16]).then_inc(placed, 16)
        sp.wait_ge(placed, 16 * 12)
        phase_end(m, sp, ph)

    def tensor(pe):
        pe_w.start(pe)
        pe_s.start(pe)
        pe.wait_ge(dve_w.sem, dve_w.at("wbsum"))
        pe.matmul(ps[:, 0, 0:DIM], ones[:], wsum[:], start=True, stop=True)
        pe.matmul(ps[:, 1, 0:DIM], ones[:], wbsum[:], start=True, stop=True).then_inc(pe_w.mark("sums"), 1)
        with pe.Fori(0, NI // 2) as i:
            for s in range(2):
                pe.wait_ge(imgs[s].sem, imgs[s].at(i))
                pe.wait_ge(act_s.sem, act_s.before(f"proj_copied{s}", i))
                pe.sem_inc(m.gate, 1)
                for px in range(P):
                    mm = pe.matmul(ps[0:DIM + 1, 2 + s, 0:NP], wg[:, px, :],
                                   img[s][:].rearrange("k b g (h x) -> k (b g h) x", x=P)[:, :, px],
                                   start=px == 0, stop=px == P - 1)
                mm.then_inc(pe_s.mark(f"projected{s}"), 1)
                pe.wait_ge(dve_s.sem, dve_s.at(f"sq_reduced{s}", i))
                pe.wait_ge(dve_s.sem, dve_s.before(f"sumsq_copied{s}", i))
                pe.sem_inc(m.gate, 1)
                pe.matmul(ps[:, 4 + s, 0:1], sqsum[s][:], ones[:, 0:1], start=True, stop=True).then_inc(pe_s.mark(f"squares{s}"), 1)
                pe.wait_ge(act_s.sem, act_s.at(f"proj_copied{s}", i))
                pe.sem_inc(m.gate, 1)
                pe.transpose(ps[:, 6 + s, 0:DIM + 1], proj[s][:], m.ident[0:DIM + 1, 0:DIM + 1]).then_inc(pe_s.mark(f"turned{s}"), 1)
        phase_end(m, pe, ph)

    def scalar(act):
        act_s.start(act)
        act_f.start(act)
        with act.Fori(0, NI // 2) as i:
            for s in range(2):
                act.wait_ge(imgs[s].sem, imgs[s].at(i))
                act.wait_ge(dve_s.sem, dve_s.before(f"sq_reduced{s}", i))
                act.activation(sq[s][:].rearrange("k n (g p) -> k (n g p)", g=4), img[s][:].rearrange("k b g w -> k (b g w)"),
                               ACT.Square).then_inc(act_s.mark(f"squared{s}"), 1)
                act.wait_ge(pe_s.sem, pe_s.at(f"projected{s}", i))
                act.wait_ge(pe_s.sem, pe_s.before(f"turned{s}", i))
                act.activation(proj[s][:], ps[0:DIM + 1, 2 + s, 0:NP], ACT.Copy).then_inc(act_s.mark(f"proj_copied{s}"), 1)
        act.wait_ge(dve_w.sem, dve_w.at("eps"))
        act.wait_ge(dve_f.sem, dve_f.at("var"))
        act.activation(tmp[:], var[:], ACT.Sqrt, bias=eps[:]).then_inc(act_f.mark("std"), 1)
        act.wait_ge(dve_f.sem, dve_f.at("ss2"))
        act.activation(tmp[:], var[:], ACT.Sqrt, bias=eps[:], scale=1.0 / DIM).then_inc(act_f.mark("std2"), 1)
        phase_end(m, act, ph)

    def vector(dve):
        dve_w.start(dve)
        dve_s.start(dve)
        dve_f.start(dve)
        dve.memset(ones[:], 1.0).then_inc(dve_w.mark("ones"), 1)
        dve.wait_ge(consts, 16 * 6)
        dve.tensor_tensor(wg[:, :, 0:DIM], w[:], cols(gain[:].unsqueeze(2), DIM), ALU.mult).then_inc(dve_w.mark("gained"), 1)
        dve.memset(wg[:, :, DIM:DIM + 1], 1.0).then_inc(dve_w.mark("ones_col"), 1)
        dve.tensor_tensor(wb[:], w[:], cols(shift[:].unsqueeze(2), DIM), ALU.mult).then_inc(dve_w.mark("biased"), 1)
        dve.wait_ge(dve_w.sem, dve_w.at("biased"))
        dve.tensor_reduce(wsum[:], wg[:, :, 0:DIM].rearrange("k x o -> k o x"), X, ALU.add).then_inc(dve_w.mark("wsum"), 1)
        dve.tensor_reduce(wbsum[:], wb[:].rearrange("k x o -> k o x"), X, ALU.add).then_inc(dve_w.mark("wbsum"), 1)
        dve.wait_ge(pe_w.sem, pe_w.at("sums"))
        dve.tensor_copy(colsum[:], ps[:, 0, 0:DIM]).then_inc(dve_w.mark("colsum"), 1)
        dve.tensor_tensor(bias[:], ps[:, 1, 0:DIM], bp[:], ALU.add).then_inc(dve_w.mark("bias"), 1)
        dve.memset(eps[:], EPS).then_inc(dve_w.mark("eps"), 1)
        dve.memset(m.pos_tile[:], 0.0)
        dve.memset(m.vit_x[:], 0.0).then_inc(dve_w.mark("x_clear"), 1)
        with dve.Fori(0, NI // 2) as i:
            for s in range(2):
                dve.wait_ge(act_s.sem, act_s.at(f"squared{s}", i))
                dve.wait_ge(pe_s.sem, pe_s.before(f"squares{s}", i))
                dve.tensor_reduce(sqsum[s][:], sq[s][:].rearrange("k n (g p) -> k (n g) p", g=4), X, ALU.add
                                  ).then_inc(dve_s.mark(f"sq_reduced{s}"), 1)
                dve.wait_ge(pe_s.sem, pe_s.at(f"turned{s}", i))
                dve.tensor_scalar(raw[:, bass.ds(2 * i + s, 1), 0:DIM + 1], ps[:, 6 + s, 0:DIM + 1].unsqueeze(1), 1.0, None, ALU.mult
                                  ).then_inc(dve_s.mark(f"raw_copied{s}"), 1)
                dve.tensor_scalar(raw[:, bass.ds(2 * i + s, 1), DIM + 1:DIM + 2], ps[:, 4 + s, 0:1].unsqueeze(1), 1.0, None, ALU.mult
                                  ).then_inc(dve_s.mark(f"sumsq_copied{s}"), 1)
        dve.wait_ge(dve_s.sem, dve_s.at("sumsq_copied1", NI // 2 - 1))
        F = dve_f
        dve.tensor_scalar(mean[:], raw[:, :, DIM], 1.0 / PD, None, ALU.mult).then_inc(F.mark("mean"), 1)
        dve.wait_ge(F.sem, F.at("mean"))
        dve.tensor_tensor(tmp[:], mean[:], mean[:], ALU.mult).then_inc(F.mark("msq"), 1)
        dve.tensor_scalar(var[:], raw[:, :, DIM + 1], 1.0 / PD, None, ALU.mult).then_inc(F.mark("ex2"), 1)
        dve.wait_ge(F.sem, F.at("ex2"))
        dve.tensor_tensor(var[:], var[:], tmp[:], ALU.subtract).then_inc(F.mark("var"), 1)
        dve.wait_ge(act_f.sem, act_f.at("std"))
        dve.reciprocal(var[:], tmp[:]).then_inc(F.mark("recip"), 1)
        dve.tensor_tensor(t[:], colsum[:].unsqueeze(1).broadcast_to([128, NI, DIM]), cols(mean[:].unsqueeze(2), DIM), ALU.mult).then_inc(F.mark("mu_w"), 1)
        dve.wait_ge(F.sem, F.at("mu_w"))
        dve.tensor_tensor(y[:], raw[:, :, 0:DIM], t[:], ALU.subtract).then_inc(F.mark("minus"), 1)
        dve.wait_ge(F.sem, F.at("minus"))
        dve.tensor_tensor(y[:], y[:], cols(var[:].unsqueeze(2), DIM), ALU.mult).then_inc(F.mark("scaled"), 1)
        dve.wait_ge(F.sem, F.at("scaled"))
        dve.tensor_tensor(y[:], y[:], bias[:].unsqueeze(1).broadcast_to([128, NI, DIM]), ALU.add).then_inc(F.mark("biased"), 1)
        dve.wait_ge(F.sem, F.at("biased"))
        dve.tensor_reduce(mean[:], y[:], X, ALU.add).then_inc(F.mark("sum"), 1)
        dve.wait_ge(F.sem, F.at("sum"))
        dve.tensor_scalar(mean[:], mean[:], 1.0 / DIM, None, ALU.mult).then_inc(F.mark("mean2"), 1)
        dve.wait_ge(F.sem, F.at("mean2"))
        dve.tensor_tensor(y[:], y[:], cols(mean[:].unsqueeze(2), DIM), ALU.subtract).then_inc(F.mark("cent"), 1)
        dve.wait_ge(F.sem, F.at("cent"))
        dve.tensor_tensor(t[:], y[:], y[:], ALU.mult).then_inc(F.mark("sq2"), 1)
        dve.wait_ge(F.sem, F.at("sq2"))
        dve.tensor_reduce(var[:], t[:], X, ALU.add).then_inc(F.mark("ss2"), 1)
        dve.wait_ge(act_f.sem, act_f.at("std2"))
        dve.reciprocal(mean[:], tmp[:]).then_inc(F.mark("recip2"), 1)
        dve.wait_ge(F.sem, F.at("recip2"))
        dve.tensor_tensor(y[:], y[:], cols(mean[:].unsqueeze(2), DIM), ALU.mult).then_inc(F.mark("norm2"), 1)
        dve.wait_ge(F.sem, F.at("norm2"))
        dve.tensor_tensor(y[:], y[:], g2[:].unsqueeze(1).broadcast_to([128, NI, DIM]), ALU.mult).then_inc(F.mark("gain2"), 1)
        dve.wait_ge(F.sem, F.at("gain2"))
        dve.tensor_tensor(y[:], y[:], b2[:].unsqueeze(1).broadcast_to([128, NI, DIM]), ALU.add).then_inc(F.mark("shift2"), 1)
        dve.wait_ge(placed, 16 * 12)
        dve.wait_ge(consts, 16 * 10)
        dve.tensor_tensor(m.vit_x[:], m.vit_x[:], m.pos_tile[:].unsqueeze(1).broadcast_to([128, 16, DIM]), ALU.add).then_inc(F.mark("pos_added"), 1)
        phase_end(m, dve, ph)

    def gpsimd(pool):
        phase_end(m, pool, ph)

    return dict(sync=sync, tensor=tensor, scalar=scalar, vector=vector, gpsimd=gpsimd)


def vit_phase(nc, m, st, ph):
    G, R, H, DH, MLP, DEPTH = 16, 32, 4, 64, 128, 4
    sb = lambda n, s, d=F32: st.enter_context(nc.sbuf_tensor(n, s, d))
    wqkv, wo, w1, w2 = sb("wqkv", [C, 3 * H * DH]), sb("wo_h", [DH, H, C]), sb("w1_v", [C, MLP]), sb("w2_v", [MLP, C])
    ag, ab, fg, fb = (sb(n, [C, 1]) for n in ("attn_g", "attn_b", "ff_g", "ff_b"))
    b1 = sb("b1_col", [MLP, 1])
    bo, b2 = sb("bo_rows", [128, C]), sb("b2_rows", [128, C])
    lfg, lfb = sb("ln_f_g_rows", [128, C]), sb("ln_f_b_rows", [128, C])
    wT = sb("wqkv_t", [DH, 3 * H, C])
    wqk = sb("wq_wk", [C, H, C])
    wvo = sb("wv_wo", [C, H * C])
    cent, sq, xh = sb("v_cent", [128, G, C]), sb("v_sq", [128, G, C]), sb("v_xh", [128, G, C])
    mean, ss, rstd = sb("v_mean", [128, G]), sb("v_ss", [128, G]), sb("v_rstd", [128, G])
    eps = sb("v_eps", [128, 1])
    hT = sb("v_ht", [C, G * 4, R])
    tT = sb("v_tt", [C, H, G * 4, R])
    vv = sb("v_vv", [128, G, H * C])
    sc, ex = sb("v_scores", [128, G * H, NTOK]), sb("v_exp", [128, G * H, NTOK])
    mx, rs = sb("v_max", [128, G * H]), sb("v_rs", [128, G * H])
    pr = sb("v_probs", [128, G * H, R])
    prT = sb("v_probs_t", [128, G * H, R])
    pd = sb("v_probs_diag", [128, G * H, 4 * R])
    gl = sb("v_gelu", [MLP, G * 4, R])
    ps = m.psum
    X4 = m.vit_x
    fin_landed = m.whole.enter_context(nc.semaphore("vit_final_landed"))
    stored = m.whole.enter_context(nc.semaphore("vit_stored"))
    NW = 11
    wts = Landed(nc, m.whole, "vit_weights_landed", NW)
    pe_s = Steps(nc, m.whole, "vit_pe", ["w_turned", "combined", "h_turned"] + [f"t_proj{q}" for q in range(4)]
                 + ["v_proj0", "v_proj1"] + [f"scores{q}" for q in range(4)] + ["attended", "f_turned", "mlp1", "mlp2"])
    act_s = Steps(nc, m.whole, "vit_act", ["w_copied", "wqk_copied", "wvo_copied", "std_a"] + [f"ha{q}" for q in range(4)]
                  + ["t0", "t2", "v0", "v1"] + [f"sc{q}{j}" for q in range(4) for j in range(2)] + ["exp", "std_f"]
                  + [f"hf{q}" for q in range(4)] + ["gelu"])
    ln = lambda k: [f"{k}_{n}" for n in ("sum", "mean", "cent", "sq", "ss", "recip", "xh")]
    dve_s = Steps(nc, m.whole, "vit_dve", ln("a") + ["t1", "t3"] + [f"sc{q}{j}" for q in range(4) for j in (2, 3)]
                  + ["max", "minus", "rsum", "rrecip", "probs", "probs_t", "diag0", "diag1", "x_attn", "x_bo"] + ln("f") + ["x_mlp", "x_b2"])
    pool_s = Steps(nc, m.whole, "vit_pool", ["diag2", "diag3"])
    dve_c = Steps(nc, m.whole, "vit_dve_c", ["clear"])
    dve_f = Steps(nc, m.whole, "vit_dve_f", ln("z") + ["gain", "shift"])
    act_f = Steps(nc, m.whole, "vit_act_f", ["std_z"])

    def sync(sp):
        sp.dma_start(lfg[:], m.dram["tok_ln_f_g"].partition_broadcast(128)).then_inc(fin_landed, 16)
        sp.dma_start(lfb[:], m.dram["tok_ln_f_b"].partition_broadcast(128)).then_inc(fin_landed, 16)
        wts.start(sp)
        with sp.Fori(0, DEPTH) as i:
            sp.wait_ge(dve_s.sem, dve_s.before("x_b2", i))
            sp.sem_inc(m.gate, 1)
            at = bass.ds(i, 1)
            sp.dma_start(wqkv[:], m.dram["tok_Wqkv"][at].rearrange("l c n -> c (l n)")).then_inc(wts.sem, 16)
            sp.dma_start(wo[:], m.dram["tok_Wo"][at].rearrange("l (h d) o -> d (l h) o", h=H)).then_inc(wts.sem, 16)
            sp.dma_start(w1[:], m.dram["tok_W1"][at].rearrange("l c n -> c (l n)")).then_inc(wts.sem, 16)
            sp.dma_start(w2[:], m.dram["tok_W2"][at].rearrange("l c n -> c (l n)")).then_inc(wts.sem, 16)
            for dst, src in ((ag, m.dram["tok_attn_ln_g"]), (ab, m.dram["tok_attn_ln_b"]), (fg, m.dram["tok_ff_ln_g"]), (fb, m.dram["tok_ff_ln_b"]), (b1, m.dram["tok_b1"])):
                sp.dma_start(dst[:], src[at].rearrange("l c -> c l")).then_inc(wts.sem, 16)
            for dst, src in ((bo, m.dram["tok_bo"]), (b2, m.dram["tok_b2"])):
                sp.dma_start(dst[:], src[at].rearrange("l c -> (l c)").partition_broadcast(128)).then_inc(wts.sem, 16)
        sp.wait_ge(dve_f.sem, dve_f.at("shift"))
        for j in range(4):
            sp.dma_start(m.dram["h_d"].rearrange("(g j t) c -> j t g c", j=4, t=T)[j, 0:NTOK], xh[32 * j:32 * j + NTOK]).then_inc(stored, 16)
        sp.wait_ge(stored, 16 * 4)
        phase_end(m, sp, ph)

    def tensor(pe):
        pe_s.start(pe)
        banks = lambda s: range(4 * s, 4 * s + 4)
        with pe.Fori(0, DEPTH) as i:
            pe.wait_ge(wts.sem, wts.at(i))
            pe.wait_ge(dve_s.sem, dve_s.before("x_mlp", i))
            pe.wait_ge(act_s.sem, act_s.before("gelu", i))
            pe.sem_inc(m.gate, 1)
            for k in range(3 * H):
                mm = pe.transpose(ps[0:DH, k // 8, k % 8 * C:(k % 8 + 1) * C], wqkv[:, k * DH:(k + 1) * DH], m.ident[0:C, 0:C])
            mm.then_inc(pe_s.mark("w_turned"), 1)
            pe.wait_ge(act_s.sem, act_s.at("w_copied", i))
            pe.sem_inc(m.gate, 1)
            for h in range(H):
                pe.matmul(ps[0:C, 2, h * C:(h + 1) * C], wT[:, h, :], wT[:, H + h, :], start=True, stop=True)
                mm = pe.matmul(ps[0:C, 3, h * C:(h + 1) * C], wT[:, 2 * H + h, :], wo[:, h, :], start=True, stop=True)
            mm.then_inc(pe_s.mark("combined"), 1)
            pe.wait_ge(dve_s.sem, dve_s.at("a_xh", i))
            pe.sem_inc(m.gate, 1)
            for g in range(G):
                mm = pe.transpose(ps[0:C, 4 + g // 4, g % 4 * 128:(g % 4 + 1) * 128], xh[:, g, :], m.ident[:])
            mm.then_inc(pe_s.mark("h_turned"), 1)
            for q in range(4):
                if q == 0:
                    pe.wait_ge(act_s.sem, act_s.at("wvo_copied", i))
                    pe.wait_ge(act_s.sem, act_s.at("ha3", i))
                elif q == 2:
                    pe.wait_ge(act_s.sem, act_s.at("t0", i))
                elif q == 3:
                    pe.wait_ge(dve_s.sem, dve_s.at("t1", i))
                pe.sem_inc(m.gate, 1)
                for h in range(H):
                    mm = pe.matmul(ps[0:C, 4 * (q % 2) + h, 0:16 * NTOK], wqk[:, h, :], hT[:, 16 * q:16 * q + 16, 0:NTOK], start=True, stop=True)
                mm.then_inc(pe_s.mark(f"t_proj{q}"), 1)
            for q in range(2):
                if q == 0:
                    pe.wait_ge(act_s.sem, act_s.at("t2", i))
                else:
                    pe.wait_ge(dve_s.sem, dve_s.at("t3", i))
                pe.sem_inc(m.gate, 1)
                for k in range(8):
                    g = 8 * q + k
                    mm = pe.matmul(ps[:, 4 * q + k // 2, k % 2 * 256:k % 2 * 256 + 256], hT[:, 4 * g:4 * g + 4, :].rearrange("c b r -> c (b r)"), wvo[:], start=True, stop=True)
                mm.then_inc(pe_s.mark(f"v_proj{q}"), 1)
            for q in range(4):
                if q < 2:
                    pe.wait_ge(act_s.sem, act_s.at(f"v{q}", i))
                else:
                    pe.wait_ge(act_s.sem, act_s.at(f"sc{q - 2}1", i))
                    pe.wait_ge(dve_s.sem, dve_s.at(f"sc{q - 2}3", i))
                pe.sem_inc(m.gate, 1)
                for k in range(4):
                    g = 4 * q + k
                    for h in range(H):
                        mm = pe.matmul(ps[:, 4 * (q % 2) + k, h * 68:(h + 1) * 68], tT[:, h, 4 * g:4 * g + 4, :].rearrange("c b r -> c (b r)"),
                                       hT[:, 4 * g:4 * g + 4, 0:NTOK], start=True, stop=True)
                mm.then_inc(pe_s.mark(f"scores{q}"), 1)
            pe.wait_ge(dve_s.sem, dve_s.at("diag1", i))
            pe.wait_ge(pool_s.sem, pool_s.at("diag3", i))
            pe.sem_inc(m.gate, 1)
            for g in range(G):
                for h in range(H):
                    mm = pe.matmul(ps[:, g // 8, g % 8 * C:(g % 8 + 1) * C], pd[:, g * H + h, :], vv[:, g, h * C:(h + 1) * C], start=h == 0, stop=h == H - 1)
            mm.then_inc(pe_s.mark("attended"), 1)
            pe.wait_ge(dve_s.sem, dve_s.at("f_xh", i))
            pe.sem_inc(m.gate, 1)
            for g in range(G):
                mm = pe.transpose(ps[0:C, 4 + g // 4, g % 4 * 128:(g % 4 + 1) * 128], xh[:, g, :], m.ident[:])
            mm.then_inc(pe_s.mark("f_turned"), 1)
            pe.wait_ge(act_s.sem, act_s.at("hf3", i))
            pe.sem_inc(m.gate, 1)
            for q in range(4):
                mm = pe.matmul(ps[:, q, 0:16 * NTOK], w1[:], hT[:, 16 * q:16 * q + 16, 0:NTOK], start=True, stop=True)
            mm.then_inc(pe_s.mark("mlp1"), 1)
            pe.wait_ge(act_s.sem, act_s.at("gelu", i))
            pe.sem_inc(m.gate, 1)
            for g in range(G):
                mm = pe.matmul(ps[:, 4 + g // 8, g % 8 * C:(g % 8 + 1) * C], gl[:, 4 * g:4 * g + 4, :].rearrange("c b r -> c (b r)"), w2[:], start=True, stop=True)
            mm.then_inc(pe_s.mark("mlp2"), 1)
        phase_end(m, pe, ph)

    def scalar(act):
        act_s.start(act)
        act_f.start(act)
        act.wait_ge(dve_c.sem, dve_c.at("clear"))
        with act.Fori(0, DEPTH) as i:
            act.wait_ge(wts.sem, wts.at(i))
            act.wait_ge(pe_s.sem, pe_s.at("w_turned", i))
            act.activation(wT[:, 0:8, :], ps[0:DH, 0, :].rearrange("c (k o) -> c k o", o=C), ACT.Copy)
            act.activation(wT[:, 8:12, :], ps[0:DH, 1, 0:256].rearrange("c (k o) -> c k o", o=C), ACT.Copy).then_inc(act_s.mark("w_copied"), 1)
            act.wait_ge(pe_s.sem, pe_s.at("combined", i))
            act.activation(wqk[:].rearrange("c h o -> c (h o)"), ps[0:C, 2, 0:H * C], ACT.Copy, scale=DH ** -0.5).then_inc(act_s.mark("wqk_copied"), 1)
            act.activation(wvo[:], ps[0:C, 3, 0:H * C], ACT.Copy).then_inc(act_s.mark("wvo_copied"), 1)
            act.wait_ge(dve_s.sem, dve_s.at("a_ss", i))
            act.activation(rstd[:], ss[:], ACT.Sqrt, bias=eps[:], scale=1.0 / C).then_inc(act_s.mark("std_a"), 1)
            act.wait_ge(pe_s.sem, pe_s.at("h_turned", i))
            for q in range(4):
                act.activation(hT[:, 16 * q:16 * q + 16, :].rearrange("c b r -> c (b r)"), ps[0:C, 4 + q, :], ACT.Identity,
                               bias=ab[:], scale=ag[:]).then_inc(act_s.mark(f"ha{q}"), 1)
            for q in (0, 2):
                act.wait_ge(pe_s.sem, pe_s.at(f"t_proj{q}", i))
                act.activation(tT[:, :, 16 * q:16 * q + 16, 0:NTOK], ps[0:C, 0:4, 0:16 * NTOK].rearrange("c h (b r) -> c h b r", b=16),
                               ACT.Copy).then_inc(act_s.mark(f"t{q}"), 1)
            for q in range(2):
                act.wait_ge(pe_s.sem, pe_s.at(f"v_proj{q}", i))
                act.activation(vv[:, 8 * q:8 * q + 8, :].rearrange("p g n -> p (g n)"), ps[:, 4 * q:4 * q + 4, :].rearrange("p b n -> p (b n)"),
                               ACT.Copy).then_inc(act_s.mark(f"v{q}"), 1)
            for q in range(4):
                act.wait_ge(pe_s.sem, pe_s.at(f"scores{q}", i))
                for j in range(2):
                    act.activation(sc[32 * j:32 * j + 32, 16 * q:16 * q + 16, :].rearrange("p (g h) n -> p g h n", g=4),
                                   ps[32 * j:32 * j + 32, 4 * (q % 2):4 * (q % 2) + 4, 0:4 * 68].rearrange("p g (h n) -> p g h n", h=4)[:, :, :, NTOK * j:NTOK * j + NTOK],
                                   ACT.Copy).then_inc(act_s.mark(f"sc{q}{j}"), 1)
            act.wait_ge(dve_s.sem, dve_s.at("minus", i))
            act.activation(ex[:], sc[:], ACT.Exp).then_inc(act_s.mark("exp"), 1)
            act.wait_ge(dve_s.sem, dve_s.at("f_ss", i))
            act.activation(rstd[:], ss[:], ACT.Sqrt, bias=eps[:], scale=1.0 / C).then_inc(act_s.mark("std_f"), 1)
            act.wait_ge(pe_s.sem, pe_s.at("f_turned", i))
            for q in range(4):
                act.activation(hT[:, 16 * q:16 * q + 16, :].rearrange("c b r -> c (b r)"), ps[0:C, 4 + q, :], ACT.Identity,
                               bias=fb[:], scale=fg[:]).then_inc(act_s.mark(f"hf{q}"), 1)
            act.wait_ge(pe_s.sem, pe_s.at("mlp1", i))
            act.activation(gl[:, :, 0:NTOK].rearrange("p (q b) r -> p q b r", q=4), ps[:, 0:4, 0:16 * NTOK].rearrange("p q (b r) -> p q b r", b=16),
                           ACT.Gelu, bias=b1[:]).then_inc(act_s.mark("gelu"), 1)
        act.wait_ge(dve_f.sem, dve_f.at("z_ss"))
        act.activation(rstd[:], ss[:], ACT.Sqrt, bias=eps[:], scale=1.0 / C).then_inc(act_f.mark("std_z"), 1)
        phase_end(m, act, ph)

    def norm(dve, S, k, i, std_sem, std_at):
        wide = lambda v: cols(v[:].unsqueeze(2), C)
        dve.tensor_reduce(mean[:], X4[:], X, ALU.add).then_inc(S.mark(f"{k}_sum"), 1)
        dve.wait_ge(S.sem, S.at(f"{k}_sum", i))
        dve.tensor_scalar(mean[:], mean[:], 1.0 / C, None, ALU.mult).then_inc(S.mark(f"{k}_mean"), 1)
        dve.wait_ge(S.sem, S.at(f"{k}_mean", i))
        dve.tensor_tensor(cent[:], X4[:], wide(mean), ALU.subtract).then_inc(S.mark(f"{k}_cent"), 1)
        dve.wait_ge(S.sem, S.at(f"{k}_cent", i))
        dve.tensor_tensor(sq[:], cent[:], cent[:], ALU.mult).then_inc(S.mark(f"{k}_sq"), 1)
        dve.wait_ge(S.sem, S.at(f"{k}_sq", i))
        dve.tensor_reduce(ss[:], sq[:], X, ALU.add).then_inc(S.mark(f"{k}_ss"), 1)
        dve.wait_ge(std_sem, std_at)
        dve.reciprocal(mean[:], rstd[:]).then_inc(S.mark(f"{k}_recip"), 1)
        dve.wait_ge(S.sem, S.at(f"{k}_recip", i))
        dve.tensor_tensor(xh[:], cent[:], wide(mean), ALU.mult).then_inc(S.mark(f"{k}_xh"), 1)

    def vector(dve):
        dve_c.start(dve)
        dve_s.start(dve)
        dve_f.start(dve)
        dve.memset(eps[:], EPS)
        for z in (tT, pr, pd, gl):
            ins = dve.memset(z[:], 0.0)
        ins.then_inc(dve_c.mark("clear"), 1)
        dve.wait_ge(dve_c.sem, dve_c.at("clear"))
        S = dve_s
        with dve.Fori(0, DEPTH) as i:
            dve.wait_ge(S.sem, S.before("x_b2", i))
            norm(dve, S, "a", i, act_s.sem, act_s.at("std_a", i))
            for q in (1, 3):
                dve.wait_ge(pe_s.sem, pe_s.at(f"t_proj{q}", i))
                dve.tensor_copy(tT[:, :, 16 * q:16 * q + 16, 0:NTOK], ps[0:C, 4:8, 0:16 * NTOK].rearrange("c h (b r) -> c h b r", b=16)
                                ).then_inc(S.mark(f"t{q}"), 1)
            for q in range(4):
                dve.wait_ge(pe_s.sem, pe_s.at(f"scores{q}", i))
                for j in (2, 3):
                    dve.tensor_copy(sc[32 * j:32 * j + 32, 16 * q:16 * q + 16, :].rearrange("p (g h) n -> p g h n", g=4),
                                    ps[32 * j:32 * j + 32, 4 * (q % 2):4 * (q % 2) + 4, 0:4 * 68].rearrange("p g (h n) -> p g h n", h=4)[:, :, :, NTOK * j:NTOK * j + NTOK]
                                    ).then_inc(S.mark(f"sc{q}{j}"), 1)
            dve.wait_ge(act_s.sem, act_s.at("sc31", i))
            dve.wait_ge(S.sem, S.at("sc33", i))
            dve.tensor_reduce(mx[:], sc[:], X, ALU.max).then_inc(S.mark("max"), 1)
            dve.wait_ge(S.sem, S.at("max", i))
            dve.tensor_tensor(sc[:], sc[:], cols(mx[:].unsqueeze(2), NTOK), ALU.subtract).then_inc(S.mark("minus"), 1)
            dve.wait_ge(act_s.sem, act_s.at("exp", i))
            dve.tensor_reduce(rs[:], ex[:], X, ALU.add).then_inc(S.mark("rsum"), 1)
            dve.wait_ge(S.sem, S.at("rsum", i))
            dve.reciprocal(mx[:], rs[:]).then_inc(S.mark("rrecip"), 1)
            dve.wait_ge(S.sem, S.at("rrecip", i))
            dve.tensor_tensor(pr[:, :, 0:NTOK], ex[:], cols(mx[:].unsqueeze(2), NTOK), ALU.mult).then_inc(S.mark("probs"), 1)
            dve.wait_ge(S.sem, S.at("probs", i))
            dve.wait_ge(pool_s.sem, pool_s.before("diag3", i))
            dve.transpose(prT[:].rearrange("p k r -> p (k r)"), pr[:].rearrange("p k r -> p (k r)")).then_inc(S.mark("probs_t"), 1)
            dve.wait_ge(S.sem, S.at("probs_t", i))
            for j in range(2):
                dve.tensor_copy(pd[32 * j:32 * j + 32, :, 32 * j:32 * j + NTOK], prT[32 * j:32 * j + 32, :, 0:NTOK]).then_inc(S.mark(f"diag{j}"), 1)
            dve.wait_ge(pe_s.sem, pe_s.at("attended", i))
            dve.tensor_tensor(X4[:].rearrange("p g c -> p (g c)"), ps[:, 0:2, :].rearrange("p b n -> p (b n)"), X4[:].rearrange("p g c -> p (g c)"), ALU.add).then_inc(S.mark("x_attn"), 1)
            dve.wait_ge(wts.sem, wts.at(i))
            dve.wait_ge(S.sem, S.at("x_attn", i))
            dve.tensor_tensor(X4[:], X4[:], bo[:].unsqueeze(1).broadcast_to([128, G, C]), ALU.add).then_inc(S.mark("x_bo"), 1)
            dve.wait_ge(S.sem, S.at("x_bo", i))
            norm(dve, S, "f", i, act_s.sem, act_s.at("std_f", i))
            dve.wait_ge(pe_s.sem, pe_s.at("mlp2", i))
            dve.tensor_tensor(X4[:].rearrange("p g c -> p (g c)"), ps[:, 4:6, :].rearrange("p b n -> p (b n)"), X4[:].rearrange("p g c -> p (g c)"), ALU.add).then_inc(S.mark("x_mlp"), 1)
            dve.wait_ge(S.sem, S.at("x_mlp", i))
            dve.tensor_tensor(X4[:], X4[:], b2[:].unsqueeze(1).broadcast_to([128, G, C]), ALU.add).then_inc(S.mark("x_b2"), 1)
        dve.wait_ge(S.sem, S.at("x_b2", DEPTH - 1))
        norm(dve, dve_f, "z", 0, act_f.sem, act_f.at("std_z"))
        dve.wait_ge(fin_landed, 32)
        dve.wait_ge(dve_f.sem, dve_f.at("z_xh"))
        dve.tensor_tensor(xh[:], xh[:], lfg[:].unsqueeze(1).broadcast_to([128, G, C]), ALU.mult).then_inc(dve_f.mark("gain"), 1)
        dve.wait_ge(dve_f.sem, dve_f.at("gain"))
        dve.tensor_tensor(xh[:], xh[:], lfb[:].unsqueeze(1).broadcast_to([128, G, C]), ALU.add).then_inc(dve_f.mark("shift"), 1)
        phase_end(m, dve, ph)

    def gpsimd(pool):
        pool_s.start(pool)
        with pool.Fori(0, DEPTH) as i:
            pool.wait_ge(dve_s.sem, dve_s.at("probs_t", i))
            pool.sem_inc(m.gate, 1)
            for j in (2, 3):
                pool.tensor_copy(pd[32 * j:32 * j + 32, :, 32 * j:32 * j + NTOK], prT[32 * j:32 * j + 32, :, 0:NTOK]).then_inc(pool_s.mark(f"diag{j}"), 1)
        phase_end(m, pool, ph)

    return dict(sync=sync, tensor=tensor, scalar=scalar, vector=vector, gpsimd=gpsimd)


def text_phase(nc, m, st, ph):
    D, V, CH, NCH, WIN, HID, ROUNDS = 128, 64, 8, 16, 4, 256, 3
    CP = CH // 2
    K = NB * NCH
    KT = K // 128
    sb = lambda n, s, d=F32: st.enter_context(nc.sbuf_tensor(n, s, d))
    w = {n: sb(f"x_{n}", s) for n, s in {
        "h0": [128, CP, D], "pos": [128, CP, D], "lln_g": [D, 1], "lln_b": [D, 1], "lw1": [D, HID], "lb1": [D, 2], "lw2": [D, 2, D],
        "lb2": [128, D], "pool_w": [D, D], "pool_b": [D, 1], "msg_w1": [D, 2, D], "msg_b1": [D, 1], "msg_w2": [D, D], "msg_b2": [D, 1],
        "upd_w1": [D, 2, D], "upd_b1": [D, 1], "upd_w2": [D, D], "upd_b2": [D, 1], "mln_g": [D, 1], "mln_b": [D, 1],
        "bc_w": [D, D], "bc_b": [128, D], "fln_g": [D, 1], "fln_b": [D, 1], "head_w": [D, V], "inv_count": [128, NCH],
        "id_col": [128, 1], "id_row": [128, V]}.items()}
    tok = sb("x_tok", [128, K * CH], I32)
    tokr, tokf = sb("x_tok_rows", [128, KT, CH], I32), sb("x_tok_rows_f", [128, KT, CH])
    hot = sb("x_hot", [128, CP, K])
    local, xh0, sq0 = sb("x_local", [128, CP, D]), sb("x_xh0", [128, CP, D]), sb("x_sq0", [128, CP, D])
    st4, st4b, eps = sb("x_st4", [128, CP]), sb("x_st4b", [128, CP]), sb("x_eps", [128, 1])
    hT0, gl0 = sb("x_ht0", [D, CP * 128]), sb("x_gl0", [D, 2, CP * 128])
    pooled = sb("x_pooled", [128, CP, D])
    hm = sb("x_hm", [D, NB, NCH])
    a, b = sb("x_a", [D, NB, NCH]), sb("x_b", [D, NB, NCH])
    z = [sb(f"x_z{d}", [D, NB, NCH]) for d in range(WIN + 1)]
    agg, u = sb("x_agg", [D, K]), sb("x_u", [D, K])
    r, cent, sq, xh = sb("x_r", [D, K]), sb("x_cent", [128, KT, D]), sb("x_sq", [128, KT, D]), sb("x_xh", [128, KT, D])
    mean, ss, std = sb("x_mean", [128, KT]), sb("x_ss", [128, KT]), sb("x_std", [128, KT])
    ltT, ltT2, ltsq = sb("x_ltt", [D, CP * 128]), sb("x_ltt2", [D, CP * 128]), sb("x_ltsq", [D, CP * 128])
    bcT = sb("x_bct", [D, KT, 128])
    hwg = sb("x_hwg", [D, V])
    th = sb("x_th", [128, CP, 2, V])
    ones, fb = sb("x_ones", [D, 128]), sb("x_fb", [D, 128])
    lb = sb("x_lb", [128, V])
    hotr = [sb(f"x_hotr{k}", [128, CH, V]) for k in range(2)]
    pick = [sb(f"x_pick{k}", [128, CH, V]) for k in range(2)]
    var, dev, rstd = sb("x_var", [128, KT, CH]), sb("x_dev", [128, KT, CH]), sb("x_rstd", [128, KT, CH])
    lg = [sb(f"x_lg{k}", [128, CH, V]) for k in range(2)]
    ps = m.psum
    flat = lambda t: t[:].rearrange("d n c -> d (n c)")
    landed = m.whole.enter_context(nc.semaphore("text_landed"))
    stored = [m.whole.enter_context(nc.semaphore(f"text_stored{k}")) for k in range(2)]
    nload = 0

    tiles = range(KT)
    pe_c = Steps(nc, m.whole, "text_pe_setup", ["h0_turned", "mlp1", "mlp2", "local_turned", "pooled", "summ"])
    act_c = Steps(nc, m.whole, "text_act_setup", ["std0", "h0_copied", "gelu0", "gelu1", "local_copied", "pooled_copied", "summ_copied"])
    ln0 = ["sum", "mean", "cent", "sq", "ss", "recip", "xh"]
    dve_c = Steps(nc, m.whole, "text_dve_setup", ["eps", "h0"] + ln0 + ["hot0", "hot1", "local_h", "local"])
    pe_r = Steps(nc, m.whole, "text_pe_round", ["pre_a", "pre_b", "msg", "upd1", "upd2", "r_turned", "xh_turned"])
    act_r = Steps(nc, m.whole, "text_act_round", ["a"] + [f"gelu{d}" for d in range(WIN + 1)] + ["agg", "u", "std", "hm"])
    dve_r = Steps(nc, m.whole, "text_dve_round", ["b"] + [f"z{d}" for d in range(WIN + 1)] + [f"sum{d}" for d in range(1, WIN + 1)]
                  + ["scaled", "r"] + ["lsum", "mean", "cent", "sq", "ss", "recip", "xh"])
    pe_f = Steps(nc, m.whole, "text_pe_final", ["bc", "ltc_turned", "bcc_turned", "th", "lb"] + [f"var{t}" for t in tiles] + [f"logits{t}" for t in tiles])
    act_f = Steps(nc, m.whole, "text_act_final", ["ltt", "ltt2", "ltsq", "bct", "std"])
    dve_f = Steps(nc, m.whole, "text_dve_final", ["ones", "th_clear", "fb", "hwg", "tokf", "tsum", "tmean", "ltc", "bc", "bsum", "bmean", "bcc", "bsq", "bss", "th0", "th1", "lb"]
                  + [f"{n}{t}" for t in tiles for n in ("hotr", "pick", "var")] + ["var_all", "recip"]
                  + [f"{n}{t}" for t in tiles for n in ("scaled", "logits")])

    loads = []
    for c2 in range(2):
        rows = slice(64 * c2, 64 * c2 + 64)
        loads.append((w["h0"][rows], m.dram["txt_emb"].unsqueeze(1).broadcast_to([V, CP, D])))
        loads.append((w["pos"][rows], m.dram["txt_pos"].rearrange("(cp c2) d -> c2 cp d", c2=2)[c2].partition_broadcast(64)))
    col = lambda ap: ap.rearrange("(c o) -> c o", o=1)
    for n in ("lln_g", "lln_b", "pool_b", "msg_b1", "msg_b2", "upd_b1", "upd_b2", "mln_g", "mln_b", "fln_g", "fln_b"):
        loads.append((w[n][:], col(m.dram[f"txt_{n}"])))
    for n in ("lw1", "pool_w", "msg_w2", "upd_w2", "bc_w", "head_w"):
        loads.append((w[n][:], m.dram[f"txt_{n}"]))
    for n in ("msg_w1", "upd_w1", "lw2"):
        loads.append((w[n][:], m.dram[f"txt_{n}"].rearrange("(k c) o -> c k o", k=2)))
    for k in range(2):
        loads.append((w["lb1"][:, k:k + 1], col(m.dram["txt_lb1"][D * k:D * k + D])))
    for n, src in (("lb2", m.dram["txt_lb2"]), ("bc_b", m.dram["txt_bc_b"]), ("inv_count", m.dram["inv_count"]), ("id_row", m.dram["id_row"])):
        loads.append((w[n][:], src.partition_broadcast(128)))
    loads.append((w["id_col"][:], m.dram["id_col"]))

    def sync(sp):
        for dst, src in loads:
            sp.dma_start(dst, src).then_inc(landed, 16)
        for b8 in range(8):
            sp.dma_start(tokr[16 * b8:16 * b8 + 16], m.dram["x_txt"].rearrange("(t b) (i c) -> b i t c", b=8, c=CH)[b8]).then_inc(landed, 16)
        sp.dma_start(tok[:], m.dram["x_txt"].rearrange("b t -> (b t)").partition_broadcast(128)).then_inc(landed, 16)
        for t in tiles:
            sp.wait_ge(dve_f.sem, dve_f.at(f"logits{t}"))
            dst = m.dram["h_d"].rearrange("(b t) c -> b (t c)", t=T)[8 * t:8 * t + 8, NTOK * C:].rearrange("b (i n) -> b i n", i=NCH)
            sp.dma_start(dst, lg[t % 2][:].rearrange("p c v -> p (c v)")).then_inc(stored[t % 2], 16)
        for k in range(2):
            sp.wait_ge(stored[k], 16 * KT // 2)
        phase_end(m, sp, ph)
    all_landed = 16 * (len(loads) + 9)

    def tensor(pe):
        for s in (pe_c, pe_r, pe_f):
            s.start(pe)
        S = pe_c
        pe.wait_ge(landed, all_landed)
        pe.wait_ge(dve_c.sem, dve_c.at("xh"))
        for k in range(CP):
            mm = pe.transpose(ps[:, 0, 128 * k:128 * k + 128], xh0[:, k, :], m.ident[:])
        mm.then_inc(S.mark("h0_turned"), 1)
        pe.wait_ge(act_c.sem, act_c.at("h0_copied"))
        for k in range(2):
            mm = pe.matmul(ps[:, 1 + k, :], w["lw1"][:, k * D:(k + 1) * D], hT0[:], start=True, stop=True)
        mm.then_inc(S.mark("mlp1"), 1)
        pe.wait_ge(act_c.sem, act_c.at("gelu1"))
        for k in range(CP):
            for h in range(2):
                mm = pe.matmul(ps[:, 3, 128 * k:128 * k + 128], gl0[:, h, 128 * k:128 * k + 128], w["lw2"][:, h, :], start=h == 0, stop=h == 1)
        mm.then_inc(S.mark("mlp2"), 1)
        pe.wait_ge(dve_c.sem, dve_c.at("local"))
        for k in range(CP):
            mm = pe.transpose(ps[:, 0, 128 * k:128 * k + 128], local[:, k, :], m.ident[:])
        mm.then_inc(S.mark("local_turned"), 1)
        pe.wait_ge(act_c.sem, act_c.at("local_copied"))
        for k in range(CP):
            mm = pe.matmul(ps[:, 1, 128 * k:128 * k + 128], hT0[:, 128 * k:128 * k + 128], w["pool_w"][:], start=True, stop=True)
        mm.then_inc(S.mark("pooled"), 1)
        pe.wait_ge(act_c.sem, act_c.at("pooled_copied"))
        pe.wait_ge(dve_c.sem, dve_c.at("hot1"))
        for half in range(2):
            for k in range(CP):
                mm = pe.matmul(ps[:, 2 + half, :], pooled[:, k, :], hot[:, k, 512 * half:512 * half + 512], start=k == 0, stop=k == CP - 1)
        mm.then_inc(S.mark("summ"), 1)
        pe.wait_ge(act_c.sem, act_c.at("summ_copied"))
        S = pe_r
        with pe.Fori(0, ROUNDS) as i:
            pe.wait_ge(act_r.sem, act_r.before("hm", i))
            pe.sem_inc(m.gate, 1)
            for k, name in ((0, "pre_a"), (1, "pre_b")):
                for half in range(2):
                    mm = pe.matmul(ps[:, 2 * k + half, :], w["msg_w1"][:, k, :], flat(hm)[:, 512 * half:512 * half + 512], start=True, stop=True)
                mm.then_inc(S.mark(name), 1)
            pe.wait_ge(dve_r.sem, dve_r.at("scaled", i))
            pe.sem_inc(m.gate, 1)
            for half in range(2):
                mm = pe.matmul(ps[:, 4 + half, :], w["msg_w2"][:], flat(z[0])[:, 512 * half:512 * half + 512], start=True, stop=True)
            mm.then_inc(S.mark("msg"), 1)
            pe.wait_ge(act_r.sem, act_r.at("agg", i))
            pe.sem_inc(m.gate, 1)
            for half in range(2):
                c = slice(512 * half, 512 * half + 512)
                pe.matmul(ps[:, 6 + half, :], w["upd_w1"][:, 0, :], flat(hm)[:, c], start=True, stop=False)
                mm = pe.matmul(ps[:, 6 + half, :], w["upd_w1"][:, 1, :], agg[:, c], start=False, stop=True)
            mm.then_inc(S.mark("upd1"), 1)
            pe.wait_ge(act_r.sem, act_r.at("u", i))
            pe.sem_inc(m.gate, 1)
            for half in range(2):
                c = slice(512 * half, 512 * half + 512)
                mm = pe.matmul(ps[:, half, :], w["upd_w2"][:], u[:, c], start=True, stop=True)
            mm.then_inc(S.mark("upd2"), 1)
            pe.wait_ge(dve_r.sem, dve_r.at("r", i))
            pe.sem_inc(m.gate, 1)
            for t in tiles:
                mm = pe.transpose(ps[:, 2 + t // 4, t % 4 * 128:t % 4 * 128 + 128], r[:, 128 * t:128 * t + 128], m.ident[:])
            mm.then_inc(S.mark("r_turned"), 1)
            pe.wait_ge(dve_r.sem, dve_r.at("xh", i))
            pe.sem_inc(m.gate, 1)
            for t in tiles:
                mm = pe.transpose(ps[:, 4 + t // 4, t % 4 * 128:t % 4 * 128 + 128], xh[:, t, :], m.ident[:])
            mm.then_inc(S.mark("xh_turned"), 1)
        S = pe_f
        pe.wait_ge(act_r.sem, act_r.at("hm", ROUNDS - 1))
        for t in tiles:
            mm = pe.matmul(ps[:, t // 4, t % 4 * 128:t % 4 * 128 + 128], flat(hm)[:, 128 * t:128 * t + 128], w["bc_w"][:], start=True, stop=True)
        mm.then_inc(S.mark("bc"), 1)
        pe.wait_ge(dve_f.sem, dve_f.at("ltc"))
        for k in range(CP):
            mm = pe.transpose(ps[:, 4, 128 * k:128 * k + 128], xh0[:, k, :], m.ident[:])
        mm.then_inc(S.mark("ltc_turned"), 1)
        pe.wait_ge(dve_f.sem, dve_f.at("bcc"))
        for t in tiles:
            mm = pe.transpose(ps[:, 2 + t // 4, t % 4 * 128:t % 4 * 128 + 128], cent[:, t, :], m.ident[:])
        mm.then_inc(S.mark("bcc_turned"), 1)
        pe.wait_ge(act_f.sem, act_f.at("ltt"))
        pe.wait_ge(dve_f.sem, dve_f.at("hwg"))
        for k in range(CP):
            mm = pe.matmul(ps[:, 5, V * k:V * k + V], ltT[:, 128 * k:128 * k + 128], hwg[:], start=True, stop=True)
        mm.then_inc(S.mark("th"), 1)
        pe.matmul(ps[:, 6, 0:V], fb[:], w["head_w"][:], start=True, stop=True).then_inc(S.mark("lb"), 1)
        pe.wait_ge(act_f.sem, act_f.at("bct"))
        for t in tiles:
            if t >= 2:
                pe.wait_ge(dve_f.sem, dve_f.at(f"pick{t - 2}"))
            pe.matmul(ps[:, t % 2, :], bcT[:, t, :], ltT2[:], start=True, stop=False)
            pe.matmul(ps[:, t % 2, :], ones[:], ltsq[:], start=False, stop=True).then_inc(S.mark(f"var{t}"), 1)
        pe.wait_ge(dve_f.sem, dve_f.at("th1"))
        for t in tiles:
            if t >= 2:
                pe.wait_ge(dve_f.sem, dve_f.at(f"scaled{t - 2}"))
            pe.matmul(ps[:, 2 + t % 2, :], bcT[:, t, :], hwg[:].unsqueeze(1).broadcast_to([D, CH, V]), start=True, stop=False)
            for k in range(CP):
                mm = pe.matmul(ps[:, 2 + t % 2, 128 * k:128 * k + 128], hot[:, k, 128 * t:128 * t + 128], th[:, k].rearrange("p c v -> p (c v)"),
                               start=False, stop=k == CP - 1)
            mm.then_inc(S.mark(f"logits{t}"), 1)
        phase_end(m, pe, ph)

    def scalar(act):
        for s in (act_c, act_r, act_f):
            s.start(act)
        S = act_c
        act.wait_ge(landed, all_landed)
        act.wait_ge(dve_c.sem, dve_c.at("ss"))
        act.activation(st4b[:], st4[:], ACT.Sqrt, bias=eps[:], scale=1.0 / D).then_inc(S.mark("std0"), 1)
        act.wait_ge(pe_c.sem, pe_c.at("h0_turned"))
        act.activation(hT0[:], ps[:, 0, :], ACT.Identity, bias=w["lln_b"][:], scale=w["lln_g"][:]).then_inc(S.mark("h0_copied"), 1)
        act.wait_ge(pe_c.sem, pe_c.at("mlp1"))
        for k in range(2):
            act.activation(gl0[:, k, :], ps[:, 1 + k, :], ACT.Gelu, bias=w["lb1"][:, k:k + 1]).then_inc(S.mark(f"gelu{k}"), 1)
        act.wait_ge(pe_c.sem, pe_c.at("local_turned"))
        act.activation(hT0[:], ps[:, 0, :], ACT.Copy).then_inc(S.mark("local_copied"), 1)
        act.wait_ge(pe_c.sem, pe_c.at("pooled"))
        act.activation(pooled[:].rearrange("p k d -> p (k d)"), ps[:, 1, :], ACT.Copy, scale=1.0 / CH).then_inc(S.mark("pooled_copied"), 1)
        act.wait_ge(pe_c.sem, pe_c.at("summ"))
        act.activation(flat(hm), ps[:, 2:4, :].rearrange("p b n -> p (b n)"), ACT.Identity, bias=w["pool_b"][:]).then_inc(S.mark("summ_copied"), 1)
        S = act_r
        with act.Fori(0, ROUNDS) as i:
            act.wait_ge(pe_r.sem, pe_r.at("pre_a", i))
            act.activation(flat(a), ps[:, 0:2, :].rearrange("p b n -> p (b n)"), ACT.Identity, bias=w["msg_b1"][:]).then_inc(S.mark("a"), 1)
            for d in range(WIN + 1):
                act.wait_ge(dve_r.sem, dve_r.at(f"z{d}", i))
                act.activation(z[d][:, :, d:], z[d][:, :, d:], ACT.Gelu).then_inc(S.mark(f"gelu{d}"), 1)
            act.wait_ge(pe_r.sem, pe_r.at("msg", i))
            act.activation(agg[:], ps[:, 4:6, :].rearrange("p b n -> p (b n)"), ACT.Identity, bias=w["msg_b2"][:]).then_inc(S.mark("agg"), 1)
            act.wait_ge(pe_r.sem, pe_r.at("upd1", i))
            act.activation(u[:], ps[:, 6:8, :].rearrange("p b n -> p (b n)"), ACT.Gelu, bias=w["upd_b1"][:]).then_inc(S.mark("u"), 1)
            act.wait_ge(dve_r.sem, dve_r.at("ss", i))
            act.activation(std[:], ss[:], ACT.Sqrt, bias=eps[:], scale=1.0 / D).then_inc(S.mark("std"), 1)
            act.wait_ge(pe_r.sem, pe_r.at("xh_turned", i))
            act.activation(flat(hm), ps[:, 4:6, :].rearrange("p b n -> p (b n)"), ACT.Identity, bias=w["mln_b"][:], scale=w["mln_g"][:]).then_inc(S.mark("hm"), 1)
        S = act_f
        act.wait_ge(pe_f.sem, pe_f.at("ltc_turned"))
        act.activation(ltT[:], ps[:, 4, :], ACT.Copy).then_inc(S.mark("ltt"), 1)
        act.activation(ltT2[:], ps[:, 4, :], ACT.Copy, scale=2.0).then_inc(S.mark("ltt2"), 1)
        act.activation(ltsq[:], ps[:, 4, :], ACT.Square).then_inc(S.mark("ltsq"), 1)
        act.wait_ge(pe_f.sem, pe_f.at("bcc_turned"))
        act.activation(flat(bcT), ps[:, 2:4, :].rearrange("p b n -> p (b n)"), ACT.Copy).then_inc(S.mark("bct"), 1)
        act.wait_ge(dve_f.sem, dve_f.at("var_all"))
        act.activation(dev[:], var[:], ACT.Sqrt, bias=eps[:], scale=1.0 / D).then_inc(S.mark("std"), 1)
        phase_end(m, act, ph)

    def vector(dve):
        for s in (dve_c, dve_r, dve_f):
            s.start(dve)
        S = dve_c
        wide = lambda v, n=D: cols(v.unsqueeze(2), n)
        dve.memset(eps[:], EPS).then_inc(S.mark("eps"), 1)
        dve.wait_ge(landed, all_landed)
        dve.tensor_tensor(w["h0"][:], w["h0"][:], w["pos"][:], ALU.add).then_inc(S.mark("h0"), 1)
        dve.wait_ge(S.sem, S.at("h0"))
        dve.tensor_reduce(st4[:], w["h0"][:], X, ALU.add).then_inc(S.mark("sum"), 1)
        dve.wait_ge(S.sem, S.at("sum"))
        dve.tensor_scalar(st4b[:], st4[:], 1.0 / D, None, ALU.mult).then_inc(S.mark("mean"), 1)
        dve.wait_ge(S.sem, S.at("mean"))
        dve.tensor_tensor(xh0[:], w["h0"][:], wide(st4b[:]), ALU.subtract).then_inc(S.mark("cent"), 1)
        dve.wait_ge(S.sem, S.at("cent"))
        dve.tensor_tensor(sq0[:], xh0[:], xh0[:], ALU.mult).then_inc(S.mark("sq"), 1)
        dve.wait_ge(S.sem, S.at("sq"))
        dve.tensor_reduce(st4[:], sq0[:], X, ALU.add).then_inc(S.mark("ss"), 1)
        dve.wait_ge(act_c.sem, act_c.at("std0"))
        dve.reciprocal(st4[:], st4b[:]).then_inc(S.mark("recip"), 1)
        dve.wait_ge(S.sem, S.at("recip"))
        dve.tensor_tensor(xh0[:], xh0[:], wide(st4[:]), ALU.mult).then_inc(S.mark("xh"), 1)
        for c2 in range(2):
            rows = slice(64 * c2, 64 * c2 + 64)
            dve.tensor_scalar(hot[rows], tok[rows].rearrange("p (k cp c) -> p c cp k", cp=CP, c=2)[:, c2], w["id_col"][rows], None, ALU.is_equal
                              ).then_inc(S.mark(f"hot{c2}"), 1)
        dve.wait_ge(pe_c.sem, pe_c.at("mlp2"))
        dve.tensor_tensor(local[:].rearrange("p k d -> p (k d)"), ps[:, 3, :], w["h0"][:].rearrange("p k d -> p (k d)"), ALU.add).then_inc(S.mark("local_h"), 1)
        dve.wait_ge(S.sem, S.at("local_h"))
        dve.tensor_tensor(local[:], local[:], w["lb2"][:].unsqueeze(1).broadcast_to([128, CP, D]), ALU.add).then_inc(S.mark("local"), 1)
        S = dve_r
        with dve.Fori(0, ROUNDS) as i:
            dve.wait_ge(pe_r.sem, pe_r.at("pre_b", i))
            dve.tensor_copy(flat(b), ps[:, 2:4, :].rearrange("p b n -> p (b n)")).then_inc(S.mark("b"), 1)
            dve.wait_ge(act_r.sem, act_r.at("a", i))
            dve.wait_ge(S.sem, S.at("b", i))
            for d in range(WIN + 1):
                dve.tensor_tensor(z[d][:, :, d:], a[:, :, d:], b[:, :, 0:NCH - d], ALU.add).then_inc(S.mark(f"z{d}"), 1)
            for d in range(1, WIN + 1):
                dve.wait_ge(act_r.sem, act_r.at(f"gelu{d}", i))
                if d > 1:
                    dve.wait_ge(S.sem, S.at(f"sum{d - 1}", i))
                dve.tensor_tensor(z[0][:, :, d:], z[0][:, :, d:], z[d][:, :, d:], ALU.add).then_inc(S.mark(f"sum{d}"), 1)
            dve.wait_ge(S.sem, S.at(f"sum{WIN}", i))
            dve.tensor_tensor(z[0][:], z[0][:], w["inv_count"][:].unsqueeze(1).broadcast_to([D, NB, NCH]), ALU.mult).then_inc(S.mark("scaled"), 1)
            dve.wait_ge(pe_r.sem, pe_r.at("upd2", i))
            dve.scalar_tensor_tensor(out=r[:], in0=ps[:, 0:2, :].rearrange("p b n -> p (b n)"), scalar=w["upd_b2"][:], in1=flat(hm), op0=ALU.add, op1=ALU.add
                                     ).then_inc(S.mark("r"), 1)
            dve.wait_ge(pe_r.sem, pe_r.at("r_turned", i))
            rows = ps[:, 2:4, :].rearrange("p b (t d) -> p (b t) d", d=D)
            dve.tensor_reduce(ss[:], rows, X, ALU.add).then_inc(S.mark("lsum"), 1)
            dve.wait_ge(S.sem, S.at("lsum", i))
            dve.tensor_scalar(mean[:], ss[:], 1.0 / D, None, ALU.mult).then_inc(S.mark("mean"), 1)
            dve.wait_ge(S.sem, S.at("mean", i))
            dve.tensor_tensor(cent[:], rows, wide(mean[:]), ALU.subtract).then_inc(S.mark("cent"), 1)
            dve.wait_ge(S.sem, S.at("cent", i))
            dve.tensor_tensor(sq[:], cent[:], cent[:], ALU.mult).then_inc(S.mark("sq"), 1)
            dve.wait_ge(S.sem, S.at("sq", i))
            dve.tensor_reduce(ss[:], sq[:], X, ALU.add).then_inc(S.mark("ss"), 1)
            dve.wait_ge(act_r.sem, act_r.at("std", i))
            dve.reciprocal(mean[:], std[:]).then_inc(S.mark("recip"), 1)
            dve.wait_ge(S.sem, S.at("recip", i))
            dve.tensor_tensor(xh[:], cent[:], wide(mean[:]), ALU.mult).then_inc(S.mark("xh"), 1)
        S = dve_f
        dve.memset(ones[:], 1.0).then_inc(S.mark("ones"), 1)
        dve.memset(th[:], 0.0).then_inc(S.mark("th_clear"), 1)
        dve.tensor_copy(fb[:], w["fln_b"][:].broadcast_to([D, 128])).then_inc(S.mark("fb"), 1)
        dve.tensor_scalar(hwg[:], w["head_w"][:], w["fln_g"][:], None, ALU.mult).then_inc(S.mark("hwg"), 1)
        dve.tensor_copy(tokf[:], tokr[:]).then_inc(S.mark("tokf"), 1)
        dve.tensor_reduce(st4[:], local[:], X, ALU.add).then_inc(S.mark("tsum"), 1)
        dve.wait_ge(S.sem, S.at("tsum"))
        dve.tensor_scalar(st4b[:], st4[:], 1.0 / D, None, ALU.mult).then_inc(S.mark("tmean"), 1)
        dve.wait_ge(S.sem, S.at("tmean"))
        dve.tensor_tensor(xh0[:], local[:], wide(st4b[:]), ALU.subtract).then_inc(S.mark("ltc"), 1)
        dve.wait_ge(pe_f.sem, pe_f.at("bc"))
        dve.tensor_tensor(cent[:], ps[:, 0:2, :].rearrange("p b (t d) -> p (b t) d", d=D), w["bc_b"][:].unsqueeze(1).broadcast_to([128, KT, D]), ALU.add).then_inc(S.mark("bc"), 1)
        dve.wait_ge(S.sem, S.at("bc"))
        dve.tensor_reduce(ss[:], cent[:], X, ALU.add).then_inc(S.mark("bsum"), 1)
        dve.wait_ge(S.sem, S.at("bsum"))
        dve.tensor_scalar(mean[:], ss[:], 1.0 / D, None, ALU.mult).then_inc(S.mark("bmean"), 1)
        dve.wait_ge(S.sem, S.at("bmean"))
        dve.tensor_tensor(cent[:], cent[:], wide(mean[:]), ALU.subtract).then_inc(S.mark("bcc"), 1)
        dve.wait_ge(S.sem, S.at("bcc"))
        dve.tensor_tensor(sq[:], cent[:], cent[:], ALU.mult).then_inc(S.mark("bsq"), 1)
        dve.wait_ge(S.sem, S.at("bsq"))
        dve.tensor_reduce(ss[:], sq[:], X, ALU.add).then_inc(S.mark("bss"), 1)
        dve.wait_ge(pe_f.sem, pe_f.at("th"))
        for c2 in range(2):
            rows = slice(64 * c2, 64 * c2 + 64)
            dve.tensor_copy(th[rows, :, c2, :], ps[rows, 5, 0:CP * V].rearrange("p (k v) -> p k v", v=V)).then_inc(S.mark(f"th{c2}"), 1)
        dve.wait_ge(pe_f.sem, pe_f.at("lb"))
        dve.tensor_copy(lb[:], ps[:, 6, 0:V]).then_inc(S.mark("lb"), 1)
        for t in tiles:
            dve.tensor_tensor(hotr[t % 2][:], wide(tokf[:, t, :], V), w["id_row"][:].unsqueeze(1).broadcast_to([128, CH, V]), ALU.is_equal).then_inc(S.mark(f"hotr{t}"), 1)
            dve.wait_ge(pe_f.sem, pe_f.at(f"var{t}"))
            dve.wait_ge(S.sem, S.at(f"hotr{t}"))
            dve.tensor_tensor(pick[t % 2][:], ps[:, t % 2, :].rearrange("p (c v) -> p c v", v=V), hotr[t % 2][:], ALU.mult).then_inc(S.mark(f"pick{t}"), 1)
            dve.wait_ge(S.sem, S.at(f"pick{t}"))
            dve.tensor_reduce(var[:, t, :], pick[t % 2][:], X, ALU.add).then_inc(S.mark(f"var{t}"), 1)
        dve.wait_ge(S.sem, S.at(f"var{KT - 1}"))
        dve.tensor_tensor(var[:], var[:], wide(ss[:], CH), ALU.add).then_inc(S.mark("var_all"), 1)
        dve.wait_ge(act_f.sem, act_f.at("std"))
        dve.reciprocal(rstd[:], dev[:]).then_inc(S.mark("recip"), 1)
        dve.wait_ge(S.sem, S.at("recip"))
        for t in tiles:
            dve.wait_ge(pe_f.sem, pe_f.at(f"logits{t}"))
            if t >= 2:
                dve.wait_ge(stored[t % 2], 16 * (t // 2))
            dve.tensor_tensor(lg[t % 2][:], ps[:, 2 + t % 2, :].rearrange("p (c v) -> p c v", v=V), wide(rstd[:, t, :], V), ALU.mult).then_inc(S.mark(f"scaled{t}"), 1)
            dve.wait_ge(S.sem, S.at(f"scaled{t}"))
            dve.tensor_tensor(lg[t % 2][:], lg[t % 2][:], lb[:].unsqueeze(1).broadcast_to([128, CH, V]), ALU.add).then_inc(S.mark(f"logits{t}"), 1)
        phase_end(m, dve, ph)

    def gpsimd(pool):
        phase_end(m, pool, ph)

    return dict(sync=sync, tensor=tensor, scalar=scalar, vector=vector, gpsimd=gpsimd)


def token_norm(dve, S, i, act_s, pre, src, cent, sq, mean, ss):
    J = NB * T // TM
    wide = lambda v: cols(v[:].unsqueeze(2), C)
    dve.tensor_reduce(ss[:], src[:], X, ALU.add).then_inc(S.mark(f"{pre}_sum"), 1)
    dve.wait_ge(S.sem, S.at(f"{pre}_sum"))
    dve.tensor_scalar(mean[:], ss[:], 1.0 / C, None, ALU.mult).then_inc(S.mark(f"{pre}_mean"), 1)
    dve.wait_ge(S.sem, S.at(f"{pre}_mean"))
    for k in range(4):
        j = slice(J // 4 * k, J // 4 * (k + 1))
        dve.tensor_tensor(cent[:, j], src[:, j], cols(mean[:, j].unsqueeze(2), C), ALU.subtract).then_inc(S.mark(f"{pre}_cent{k}"), 1)
    for k in range(4):
        j = slice(J // 4 * k, J // 4 * (k + 1))
        dve.wait_ge(act_s.sem, act_s.at(f"{pre}_sq{k}"))
        dve.tensor_reduce(ss[:, j], sq[k % 2][:], X, ALU.add).then_inc(S.mark(f"{pre}_ss{k}"), 1)
    dve.wait_ge(act_s.sem, act_s.at(f"{pre}_std"))
    dve.reciprocal(ss[:], mean[:]).then_inc(S.mark(f"{pre}_recip"), 1)
    dve.wait_ge(S.sem, S.at(f"{pre}_recip"))


NORM_DVE = ["sum", "mean"] + [f"cent{k}" for k in range(4)] + [f"ss{k}" for k in range(4)] + ["recip"]
NORM_ACT = [f"sq{k}" for k in range(4)] + ["std"]


def token_norm_squares(act, S, dve_s, pre, cent, sq, mean, ss, eps, ready):
    J = NB * T // TM
    for k in range(4):
        j = slice(J // 4 * k, J // 4 * (k + 1))
        act.wait_ge(dve_s.sem, dve_s.at(ready.format(k=k)))
        if k >= 2:
            act.wait_ge(dve_s.sem, dve_s.at(f"{pre}_ss{k - 2}"))
        act.activation(sq[k % 2][:], cent[:, j], ACT.Square).then_inc(S.mark(f"{pre}_sq{k}"), 1)
    act.wait_ge(dve_s.sem, dve_s.at(f"{pre}_ss3"))
    act.activation(mean[:], ss[:], ACT.Sqrt, bias=eps[0:TM], scale=1.0 / C).then_inc(S.mark(f"{pre}_std"), 1)


def joint_in_phase(nc, m, st, ph):
    J = NB * T // TM
    sb = lambda n, s, d=F32: st.enter_context(nc.sbuf_tensor(n, s, d))
    cent = sb("ji_cent", [TM, J, C])
    sq = [sb(f"ji_sq{k}", [TM, J // 4, C]) for k in range(2)]
    mean, ss, eps = sb("ji_mean", [TM, J]), sb("ji_ss", [TM, J]), sb("ji_eps", [128, 1])
    wv, wvT = sb("ji_wv", [C, C]), sb("ji_wvt", [C, C])
    xh = [sb(f"ji_xh{s}", [TM, GJ, C]) for s in range(2)]
    xT = [sb(f"ji_xt{s}", [C, GT]) for s in range(2)]
    vT = [sb(f"ji_vt{s}", [C, GT]) for s in range(2)]
    ps = m.psum
    landed = m.whole.enter_context(nc.semaphore("ji_landed"))
    stored = [Landed(nc, m.whole, f"ji_stored{s}", 2) for s in range(2)]
    dve_n = Steps(nc, m.whole, "ji_dve_norm", ["eps"] + [f"n_{k}" for k in NORM_DVE] + ["wvt"])
    act_n = Steps(nc, m.whole, "ji_act_norm", [f"n_{k}" for k in NORM_ACT])
    pe_n = Steps(nc, m.whole, "ji_pe_w", ["wvt"])
    pe_s = Steps(nc, m.whole, "ji_pe", [f"{k}{s}" for s in range(2) for k in ("turned", "v")])
    act_s = Steps(nc, m.whole, "ji_act", ["xt0", "xt1"])
    dve_s = Steps(nc, m.whole, "ji_dve", [f"{k}{s}" for s in range(2) for k in ("xh", "vt")])
    P = NG // 2

    def sync(sp):
        for s in range(2):
            stored[s].start(sp)
        sp.dma_start(wv[:], m.dram["attn_Wv"]).then_inc(landed, 16)
        rows = m.dram["h_d"].rearrange("(j p) c -> p j c", p=TM)
        for p0, p1 in ((0, 112), (112, TM)):
            sp.dma_start(m.h[p0:p1], rows[p0:p1]).then_inc(landed, 16)
        with sp.Fori(0, P) as i:
            for s in range(2):
                sp.wait_ge(act_s.sem, act_s.at(f"xt{s}", i))
                sp.sem_inc(m.gate, 1)
                sp.dma_start(m.dram["xt_d"][:, bass.ds(i * 2 * GT + s * GT, GT)], xT[s][:]).then_inc(stored[s].sem, 16)
                sp.wait_ge(dve_s.sem, dve_s.at(f"vt{s}", i))
                sp.sem_inc(m.gate, 1)
                sp.dma_start(m.dram["v_d"][bass.ds(i * 2 * GB + s * GB, GB)].rearrange("b (o s) -> o b s", o=C),
                             vT[s][:].rearrange("o (b s) -> o b s", b=GB)).then_inc(stored[s].sem, 16)
        for s in range(2):
            sp.wait_ge(stored[s].sem, stored[s].at(P - 1))
        phase_end(m, sp, ph)

    def tensor(pe):
        pe_n.start(pe)
        pe_s.start(pe)
        pe.wait_ge(landed, 48)
        pe.transpose(ps[0:C, 0, 0:C], wv[:], m.ident[0:C, 0:C]).then_inc(pe_n.mark("wvt"), 1)
        pe.wait_ge(dve_n.sem, dve_n.at("wvt"))
        with pe.Fori(0, P) as i:
            for s in range(2):
                pe.wait_ge(dve_s.sem, dve_s.at(f"xh{s}", i))
                pe.wait_ge(act_s.sem, act_s.before(f"xt{s}", i))
                pe.sem_inc(m.gate, 1)
                for j in range(GJ):
                    mm = pe.transpose(ps[0:C, 2 * s + j // 4, j % 4 * TM:j % 4 * TM + TM], xh[s][:, j, :], m.ident[0:TM, 0:TM])
                mm.then_inc(pe_s.mark(f"turned{s}"), 1)
                pe.wait_ge(act_s.sem, act_s.at(f"xt{s}", i))
                pe.wait_ge(dve_s.sem, dve_s.before(f"vt{s}", i))
                pe.sem_inc(m.gate, 1)
                for k in range(2):
                    mm = pe.matmul(ps[0:C, 4 + 2 * s + k, 0:GT // 2], wvT[:], xT[s][:, GT // 2 * k:GT // 2 * (k + 1)], start=True, stop=True)
                mm.then_inc(pe_s.mark(f"v{s}"), 1)
        phase_end(m, pe, ph)

    def scalar(act):
        act_n.start(act)
        act_s.start(act)
        token_norm_squares(act, act_n, dve_n, "n", cent, sq, mean, ss, eps, "n_cent{k}")
        with act.Fori(0, P) as i:
            for s in range(2):
                act.wait_ge(pe_s.sem, pe_s.at(f"turned{s}", i))
                act.wait_ge(pe_s.sem, pe_s.before(f"v{s}", i))
                act.wait_ge(stored[s].sem, stored[s].before(i))
                act.activation(xT[s][:, 0:4 * TM], ps[0:C, 2 * s, 0:4 * TM], ACT.Copy)
                act.activation(xT[s][:, 4 * TM:GT], ps[0:C, 2 * s + 1, 0:TM], ACT.Copy).then_inc(act_s.mark(f"xt{s}"), 1)
        phase_end(m, act, ph)

    def vector(dve):
        dve_n.start(dve)
        dve_s.start(dve)
        dve.memset(eps[:], EPS).then_inc(dve_n.mark("eps"), 1)
        dve.wait_ge(landed, 48)
        token_norm(dve, dve_n, 0, act_n, "n", m.h, cent, sq, mean, ss)
        dve.wait_ge(pe_n.sem, pe_n.at("wvt"))
        dve.tensor_copy(wvT[:], ps[0:C, 0, 0:C]).then_inc(dve_n.mark("wvt"), 1)
        with dve.Fori(0, P) as i:
            for s in range(2):
                dve.wait_ge(pe_s.sem, pe_s.before(f"turned{s}", i))
                at = bass.ds(i * 2 * GJ + s * GJ, GJ)
                dve.tensor_tensor(xh[s][:], cent[:, at, :], cols(ss[:, at].unsqueeze(2), C), ALU.mult).then_inc(dve_s.mark(f"xh{s}"), 1)
                dve.wait_ge(pe_s.sem, pe_s.at(f"v{s}", i))
                dve.wait_ge(stored[s].sem, stored[s].before(i))
                dve.tensor_copy(vT[s][:].rearrange("o (k n) -> o k n", k=2), ps[0:C, 4 + 2 * s:6 + 2 * s, 0:GT // 2]).then_inc(dve_s.mark(f"vt{s}"), 1)
        phase_end(m, dve, ph)

    def gpsimd(pool):
        phase_end(m, pool, ph)

    return dict(sync=sync, tensor=tensor, scalar=scalar, vector=vector, gpsimd=gpsimd)


def joint_phase(nc, m, st, ph):
    H, KD, U, TC = 8, 64, 5, 73
    sb = lambda n, s, d=F32: st.enter_context(nc.sbuf_tensor(n, s, d))
    wq, wk = sb("jo_wq", [KD, H, C]), sb("jo_wk", [KD, C])
    wqk = sb("jo_wqk", [C, H, C])
    xs = [sb(f"jo_x{s}", [128, T]) for s in range(2)]
    v = [sb(f"jo_v{s}", [TC, 2, KD + 1]) for s in range(2)]
    q = [sb(f"jo_q{s}", [128, T, H // 2]) for s in range(2)]
    mx = [sb(f"jo_max{u}", [TM, U]) for u in range(2)]
    sc = [sb(f"jo_sc{u}", [TM, U, T]) for u in range(2)]
    pr = [sb(f"jo_pr{u}", [TM, U, T]) for u in range(2)]
    pT = [sb(f"jo_pt{u}", [TC, 2 * U, TM]) for u in range(2)]
    rs = [sb(f"jo_rs{u}", [TM, U]) for u in range(2)]
    ctx = [sb(f"jo_ctx{s}", [TM, 2 * U, KD]) for s in range(2)]
    ps = m.psum
    NP = NB // 2
    wl = m.whole.enter_context(nc.semaphore("jo_weights_landed"))
    xl = [Landed(nc, m.whole, f"jo_x_landed{s}", 4) for s in range(2)]
    stored = [Landed(nc, m.whole, f"jo_ctx_stored{s}", 2) for s in range(2)]
    S1 = lambda n, steps: Steps(nc, m.whole, n, steps)
    pe_w, act_w, dve_w = S1("jo_pe_w", ["wqk"]), S1("jo_act_w", ["wqk"]), S1("jo_dve_w", ["v_ones0", "v_ones1", "v_ready"])
    units = [(s, u) for s in range(2) for u in range(2)]
    pe_q = S1("jo_queries", [f"q{s}{k}" for s in range(2) for k in range(2)])
    act_q = S1("jo_queries_copied", [f"q{s}{k}" for s in range(2) for k in range(2)])
    pe_sc = S1("jo_scores", [f"s{s}{u}{k}" for s, u in units for k in range(2)])
    dve_sc = S1("jo_shifted", [f"{n}{s}{u}{k}" for s, u in units for k in range(2) for n in ("max", "minus")])
    act_e = S1("jo_exp", [f"e{s}{u}{k}" for s, u in units for k in range(2)])
    pe_t = S1("jo_turned", [f"t{s}{u}{k}" for s, u in units for k in range(3)])
    act_t = S1("jo_turned_copied", [f"t{s}{u}{k}" for s, u in units for k in range(3)])
    pe_v = S1("jo_attended", [f"v{s}{u}" for s, u in units])
    dve_v = S1("jo_normed", [f"{n}{s}{u}" for s, u in units for n in ("recip", "ctx")])
    nxt = {(0, 0): (0, 1, 0), (0, 1): (1, 0, 0), (1, 0): (1, 1, 0), (1, 1): (0, 0, 1)}
    prv = {(0, 0): (1, 1), (0, 1): (0, 0), (1, 0): (0, 1), (1, 1): (1, 0)}
    banks3 = [(0, 4), (4, 8), (8, 10)]

    def prev_at(S, fmt, s, u, i):
        ps_, pu = prv[s, u]
        return S.before(fmt.format(s=ps_, u=pu), i) if (s, u) == (0, 0) else S.at(fmt.format(s=ps_, u=pu), i)

    def sync(sp):
        for s in range(2):
            xl[s].start(sp)
            stored[s].start(sp)
        sp.dma_start(wq[:], m.dram["attn_Wq"].rearrange("(h d) c -> d h c", h=H)).then_inc(wl, 16)
        sp.dma_start(wk[:], m.dram["attn_Wk"]).then_inc(wl, 16)
        sp.wait_ge(dve_w.sem, dve_w.at("v_ready"))

        def load(s, i):
            sp.wait_ge(pe_v.sem, pe_v.before(f"v{s}1", i))
            sp.sem_inc(m.gate, 1)
            t0 = i * 2 * T + s * T
            for par in range(2):
                sp.dma_start(xs[s][C * par:C * par + C], m.dram["xt_d"][:, bass.ds(t0, T)]).then_inc(xl[s].sem, 16)
            rows = m.dram["v_d"][bass.ds(i * 2 + s, 1)].rearrange("b (t d) -> t (b d)", d=KD)
            sp.dma_start(v[s][0:TC, 0, 0:KD], rows[0:TC]).then_inc(xl[s].sem, 16)
            sp.dma_start(v[s][1:TC, 1, 0:KD], rows[TC:T]).then_inc(xl[s].sem, 16)

        def store(s, i, ready):
            sp.wait_ge(dve_v.sem, ready)
            sp.sem_inc(m.gate, 1)
            dst = m.dram["ctx_d"][bass.ds(i * 2 + s, 1)].rearrange("b (p n) -> p (b n)", p=TM)
            src = ctx[s][:].rearrange("p n d -> p (n d)")
            for p0, p1 in ((0, 112), (112, TM)):
                sp.dma_start(dst[p0:p1], src[p0:p1]).then_inc(stored[s].sem, 16)

        for s in range(2):
            load(s, 0)
        with sp.Fori(1, NP) as i:
            for s in range(2):
                load(s, i)
                store(s, i - 1, dve_v.before(f"ctx{s}1", i))
        for s in range(2):
            store(s, NP - 1, dve_v.at(f"ctx{s}1", NP - 1))
        for s in range(2):
            sp.wait_ge(stored[s].sem, stored[s].at(NP - 1))
        phase_end(m, sp, ph)

    def tensor(pe):
        for S in (pe_w, pe_q, pe_sc, pe_t, pe_v):
            S.start(pe)
        pe.wait_ge(wl, 32)
        for h in range(H):
            mm = pe.matmul(ps[0:C, 0, h * C:(h + 1) * C], wq[:, h, :], wk[:], start=True, stop=True)
        mm.then_inc(pe_w.mark("wqk"), 1)
        pe.wait_ge(act_w.sem, act_w.at("wqk"))

        def queries(s, i):
            pe.wait_ge(xl[s].sem, xl[s].at(i))
            for k in range(2):
                before = act_q.at(f"q{s}0", i) if k else (act_q.at("q01", i) if s else act_q.before("q11", i))
                pe.wait_ge(act_q.sem, before)
                pe.sem_inc(m.gate, 1)
                for h2 in range(2):
                    mm = pe.matmul(ps[:, 7, h2 * T:(h2 + 1) * T], wqk[:, 4 * k + 2 * h2:4 * k + 2 * h2 + 2, :].rearrange("c h o -> c (h o)"), xs[s][0:C],
                                   start=True, stop=True)
                mm.then_inc(pe_q.mark(f"q{s}{k}"), 1)

        def scores(s, u, i):
            if u == 0:
                pe.wait_ge(act_q.sem, act_q.at(f"q{s}1", i))
            other = dve_sc.at(f"minus0{u}1", i) if s else dve_sc.before(f"minus1{u}1", i)
            pe.wait_ge(dve_sc.sem, other)
            pe.sem_inc(m.gate, 1)
            rows = q[s][C * u:C * u + C].rearrange("c s h -> c (s h)")
            for j in range(U):
                k = j // 3
                mm = pe.matmul(ps[0:TM, 2 * u + k, (j - 3 * k) * T:(j - 3 * k + 1) * T], rows[:, j::U], xs[s][C * u:C * u + C], start=True, stop=True)
                if j in (2, 4):
                    mm.then_inc(pe_sc.mark(f"s{s}{u}{k}"), 1)

        def attend(s, u, i):
            pe.wait_ge(act_e.sem, act_e.at(f"e{s}{u}1", i))
            for k, (a, b) in enumerate(banks3):
                if k == 2:
                    pe.wait_ge(act_t.sem, act_t.at(f"t{s}{u}0", i))
                else:
                    pe.wait_ge(act_t.sem, prev_at(act_t, "t{s}{u}2", s, u, i))
                pe.sem_inc(m.gate, 1)
                for n in range(a, b):
                    c, j = divmod(n, U)
                    mm = pe.transpose(ps[0:TC, 4 + k % 2, (n - a) * TM:(n - a + 1) * TM], pr[u][:, j, 72 * c:72 * c + TC], m.ident[0:TM, 0:TM])
                mm.then_inc(pe_t.mark(f"t{s}{u}{k}"), 1)
            pe.wait_ge(act_t.sem, act_t.at(f"t{s}{u}2", i))
            pe.wait_ge(dve_v.sem, prev_at(dve_v, "ctx{s}{u}", s, u, i))
            pe.sem_inc(m.gate, 1)
            for j in range(U):
                for c in range(2):
                    mm = pe.matmul(ps[0:TM, 6, j * (KD + 1):(j + 1) * (KD + 1)], pT[u][:, U * c + j, :], v[s][:, c, :], start=c == 0, stop=c == 1)
            mm.then_inc(pe_v.mark(f"v{s}{u}"), 1)

        def one_pass(i, last=False):
            for s, u in units:
                s2, u2, more = nxt[s, u]
                if not (last and more):
                    if u2 == 0:
                        queries(s2, i + more)
                    scores(s2, u2, i + more)
                attend(s, u, i)

        queries(0, 0)
        scores(0, 0, 0)
        with pe.Fori(0, NP - 1) as i:
            one_pass(i)
        one_pass(NP - 1, last=True)
        phase_end(m, pe, ph)

    def scalar(act):
        for S in (act_w, act_q, act_e, act_t):
            S.start(act)
        act.wait_ge(pe_w.sem, pe_w.at("wqk"))
        act.activation(wqk[:].rearrange("c h o -> c (h o)"), ps[0:C, 0, :], ACT.Copy, scale=H ** -0.5).then_inc(act_w.mark("wqk"), 1)
        act.preload_act_table(ACT.Exp)

        def copy_queries(s, i):
            for k in range(2):
                act.wait_ge(pe_q.sem, pe_q.at(f"q{s}{k}", i))
                if k == 0:
                    act.wait_ge(pe_sc.sem, pe_sc.before(f"s{s}11", i))
                act.activation(q[s][:, :, 2 * k:2 * k + 2].rearrange("p s h -> p h s"), ps[:, 7, 0:2 * T].rearrange("p (h s) -> p h s", h=2),
                               ACT.Copy).then_inc(act_q.mark(f"q{s}{k}"), 1)

        def exp(s, u, i):
            for k, (a, b) in enumerate(((0, 3), (3, 5))):
                act.wait_ge(dve_sc.sem, dve_sc.at(f"minus{s}{u}{k}", i))
                if k == 0:
                    act.wait_ge(pe_t.sem, pe_t.at(f"t0{u}2", i) if s else pe_t.before(f"t1{u}2", i))
                act.activation(pr[u][:, a:b], sc[u][:, a:b], ACT.Exp).then_inc(act_e.mark(f"e{s}{u}{k}"), 1)

        def copy_turned(s, u, i):
            for k, (a, b) in enumerate(banks3):
                act.wait_ge(pe_t.sem, pe_t.at(f"t{s}{u}{k}", i))
                if k == 0:
                    act.wait_ge(pe_v.sem, pe_v.at(f"v0{u}", i) if s else pe_v.before(f"v1{u}", i))
                act.activation(pT[u][:, a:b].rearrange("p n m -> p (n m)"), ps[0:TC, 4 + k % 2, 0:(b - a) * TM], ACT.Copy).then_inc(act_t.mark(f"t{s}{u}{k}"), 1)

        def one_pass(i, last=False):
            for s, u in units:
                s2, u2, more = nxt[s, u]
                if u2 == 0 and not (last and more):
                    copy_queries(s2, i + more)
                copy_turned(s, u, i)
                if not (last and more):
                    exp(s2, u2, i + more)

        copy_queries(0, 0)
        exp(0, 0, 0)
        with act.Fori(0, NP - 1) as i:
            one_pass(i)
        one_pass(NP - 1, last=True)
        phase_end(m, act, ph)

    def vector(dve):
        for S in (dve_w, dve_sc, dve_v):
            S.start(dve)
        for s in range(2):
            dve.memset(v[s][:, :, KD:KD + 1], 1.0).then_inc(dve_w.mark(f"v_ones{s}"), 1)
        dve.wait_ge(dve_w.sem, dve_w.at("v_ones1"))
        for s in range(2):
            last = dve.memset(v[s][0:1, 1, :], 0.0)
        last.then_inc(dve_w.mark("v_ready"), 1)

        def shift(s, u, i):
            for k, (a, b) in enumerate(((0, 3), (3, 5))):
                bank = ps[0:TM, 2 * u + k, 0:(b - a) * T].rearrange("p (j t) -> p j t", t=T)
                dve.wait_ge(pe_sc.sem, pe_sc.at(f"s{s}{u}{k}", i))
                dve.tensor_reduce(mx[u][:, a:b], bank, X, ALU.max).then_inc(dve_sc.mark(f"max{s}{u}{k}"), 1)
                dve.wait_ge(dve_sc.sem, dve_sc.at(f"max{s}{u}{k}", i))
                if k == 0:
                    dve.wait_ge(act_e.sem, act_e.at(f"e0{u}1", i) if s else act_e.before(f"e1{u}1", i))
                dve.tensor_tensor(sc[u][:, a:b], bank, cols(mx[u][:, a:b].unsqueeze(2), T), ALU.subtract).then_inc(dve_sc.mark(f"minus{s}{u}{k}"), 1)

        def normalise(s, u, i):
            o = ps[0:TM, 6, 0:U * (KD + 1)].rearrange("p (j d) -> p j d", j=U)
            dve.wait_ge(pe_v.sem, pe_v.at(f"v{s}{u}", i))
            dve.reciprocal(rs[u][:], o[:, :, KD]).then_inc(dve_v.mark(f"recip{s}{u}"), 1)
            dve.wait_ge(dve_v.sem, dve_v.at(f"recip{s}{u}", i))
            if u == 0:
                dve.wait_ge(stored[s].sem, stored[s].before(i))
            dve.tensor_tensor(ctx[s][:, u::2, :], o[:, :, 0:KD], cols(rs[u][:].unsqueeze(2), KD), ALU.mult).then_inc(dve_v.mark(f"ctx{s}{u}"), 1)

        def one_pass(i, last=False):
            for s, u in units:
                s2, u2, more = nxt[s, u]
                if not (last and more):
                    shift(s2, u2, i + more)
                normalise(s, u, i)

        shift(0, 0, 0)
        with dve.Fori(0, NP - 1) as i:
            one_pass(i)
        one_pass(NP - 1, last=True)
        phase_end(m, dve, ph)

    def gpsimd(pool):
        phase_end(m, pool, ph)

    return dict(sync=sync, tensor=tensor, scalar=scalar, vector=vector, gpsimd=gpsimd)


def joint_out_phase(nc, m, st, ph):
    J, KT = NB * T // TM, 4
    sb = lambda n, s, d=F32: st.enter_context(nc.sbuf_tensor(n, s, d))
    wo, woT = sb("po_wo", [C, 128, KT]), sb("po_wot", [128, KT, C])
    cx = [sb(f"po_cx{s}", [128, GB, KT, T]) for s in range(2)]
    oT = [sb(f"po_ot{s}", [C, GT]) for s in range(2)]
    sq = [sb(f"po_sq{k}", [TM, J // 4, C]) for k in range(2)]
    mean, ss, eps, eps_rms = sb("po_mean", [TM, J]), sb("po_ss", [TM, J]), sb("po_eps", [128, 1]), sb("po_eps_rms", [128, 1])
    zt = [sb(f"po_z{s}", [TM, GJ, C]) for s in range(2)]
    zT = [sb(f"po_zt{s}", [C, GT]) for s in range(2)]
    ps = m.psum
    P = NG // 2
    S1 = lambda n, steps: Steps(nc, m.whole, n, steps)
    wl = m.whole.enter_context(nc.semaphore("po_weights_landed"))
    cl = [Landed(nc, m.whole, f"po_ctx_landed{s}", GB) for s in range(2)]
    stored = [Landed(nc, m.whole, f"po_z_stored{s}", 1) for s in range(2)]
    pe_w, dve_w = S1("po_pe_w", ["wot"]), S1("po_dve_w", ["eps", "wot"])
    pe_s = S1("po_pe", [f"{k}{s}" for s in range(2) for k in ("out", "turned")])
    act_s = S1("po_act", ["ot0", "ot1"])
    dve_s = S1("po_dve", ["h0", "h1"])
    dve_n = S1("po_dve_norm", [f"n_{k}" for k in NORM_DVE] + [f"y{k}" for k in range(4)] + [f"r_ss{k}" for k in range(4)] + ["r_recip"])
    act_n = S1("po_act_norm", [f"n_{k}" for k in NORM_ACT] + [f"r_{k}" for k in NORM_ACT])
    pe_z, act_z, dve_z = S1("po_pe_z", ["z0", "z1"]), S1("po_act_z", ["z0", "z1"]), S1("po_dve_z", ["z0", "z1"])

    def sync(sp):
        for s in range(2):
            cl[s].start(sp)
            stored[s].start(sp)
        sp.dma_start(wo[:], m.dram["attn_Wo"].rearrange("o (p k) -> o p k", k=KT)).then_inc(wl, 16)
        with sp.Fori(0, P) as i:
            for s in range(2):
                sp.wait_ge(pe_s.sem, pe_s.before(f"out{s}", i))
                sp.sem_inc(m.gate, 1)
                for b in range(GB):
                    sp.dma_start(cx[s][:, b].rearrange("p k t -> p (k t)"),
                                 m.dram["ctx_d"][bass.ds(i * 2 * GB + (s * GB + b), 1)].rearrange("b (p n) -> p (b n)", p=128)).then_inc(cl[s].sem, 16)
        with sp.Fori(0, P) as i:
            for s in range(2):
                sp.wait_ge(act_z.sem, act_z.at(f"z{s}", i))
                sp.sem_inc(m.gate, 1)
                sp.dma_start(m.dram["zt_d"][:, bass.ds(i * 2 * GT + s * GT, GT)], zT[s][:]).then_inc(stored[s].sem, 16)
        for s in range(2):
            sp.wait_ge(stored[s].sem, stored[s].at(P - 1))
        phase_end(m, sp, ph)

    def tensor(pe):
        for S in (pe_w, pe_s, pe_z):
            S.start(pe)
        pe.wait_ge(wl, 16)
        for k in range(KT):
            mm = pe.transpose(ps[:, 0, k * C:(k + 1) * C], wo[:, :, k], m.ident[0:C, 0:C])
        mm.then_inc(pe_w.mark("wot"), 1)
        pe.wait_ge(dve_w.sem, dve_w.at("wot"))
        with pe.Fori(0, P) as i:
            for s in range(2):
                pe.wait_ge(cl[s].sem, cl[s].at(i))
                pe.wait_ge(act_s.sem, act_s.before(f"ot{s}", i))
                pe.sem_inc(m.gate, 1)
                for half in range(2):
                    for k in range(KT):
                        mm = pe.matmul(ps[0:C, 2 * s + half, 0:2 * T], woT[:, k, :], cx[s][:, 2 * half:2 * half + 2, k, :], start=k == 0, stop=k == KT - 1)
                mm.then_inc(pe_s.mark(f"out{s}"), 1)
                pe.wait_ge(act_s.sem, act_s.at(f"ot{s}", i))
                pe.wait_ge(dve_s.sem, dve_s.before(f"h{s}", i))
                pe.sem_inc(m.gate, 1)
                for j in range(GJ):
                    mm = pe.transpose(ps[0:TM, 4 + s, j * C:(j + 1) * C], oT[s][:, j * TM:(j + 1) * TM], m.ident[0:C, 0:C])
                mm.then_inc(pe_s.mark(f"turned{s}"), 1)
        turn_groups(m, pe, P, pe_z, dve_z, act_z, zt, C)
        phase_end(m, pe, ph)

    def scalar(act):
        for S in (act_s, act_n, act_z):
            S.start(act)
        with act.Fori(0, P) as i:
            for s in range(2):
                act.wait_ge(pe_s.sem, pe_s.at(f"out{s}", i))
                act.wait_ge(pe_s.sem, pe_s.before(f"turned{s}", i))
                act.activation(oT[s][:].rearrange("c (h n) -> c h n", h=2), ps[0:C, 2 * s:2 * s + 2, 0:2 * T], ACT.Copy).then_inc(act_s.mark(f"ot{s}"), 1)
        token_norm_squares(act, act_n, dve_n, "n", m.y, sq, mean, ss, eps, "n_cent{k}")
        token_norm_squares(act, act_n, dve_n, "r", m.y, sq, mean, ss, eps_rms, "y{k}")
        with act.Fori(0, P) as i:
            for s in range(2):
                act.wait_ge(pe_z.sem, pe_z.at(f"z{s}", i))
                act.wait_ge(stored[s].sem, stored[s].before(i))
                act.activation(zT[s][:, 0:4 * TM], ps[0:C, 2 * s, 0:4 * TM], ACT.Copy)
                act.activation(zT[s][:, 4 * TM:GT], ps[0:C, 2 * s + 1, 0:TM], ACT.Copy).then_inc(act_z.mark(f"z{s}"), 1)
        phase_end(m, act, ph)

    def vector(dve):
        for S in (dve_w, dve_s, dve_n, dve_z):
            S.start(dve)
        dve.memset(eps[:], EPS)
        dve.memset(eps_rms[:], 1e-6).then_inc(dve_w.mark("eps"), 1)
        dve.wait_ge(pe_w.sem, pe_w.at("wot"))
        dve.tensor_copy(woT[:], ps[:, 0, 0:KT * C].rearrange("p (k o) -> p k o", k=KT)).then_inc(dve_w.mark("wot"), 1)
        with dve.Fori(0, P) as i:
            for s in range(2):
                at = bass.ds(i * 2 * GJ + s * GJ, GJ)
                dve.wait_ge(pe_s.sem, pe_s.at(f"turned{s}", i))
                dve.tensor_tensor(m.h[:, at, :], ps[0:TM, 4 + s, 0:GJ * C].rearrange("p (j c) -> p j c", c=C), m.h[:, at, :], ALU.add).then_inc(dve_s.mark(f"h{s}"), 1)
        dve.wait_ge(dve_s.sem, dve_s.at("h1", P - 1))
        token_norm(dve, dve_n, 0, act_n, "n", m.h, m.y, sq, mean, ss)
        for k in range(4):
            j = slice(J // 4 * k, J // 4 * (k + 1))
            dve.tensor_tensor(m.y[:, j], m.y[:, j], cols(ss[:, j].unsqueeze(2), C), ALU.mult).then_inc(dve_n.mark(f"y{k}"), 1)
        root_mean_square(dve, dve_n, act_n, sq, mean, ss, "y3")
        scale_groups(dve, P, dve_z, pe_z, zt, m.y, ss)
        phase_end(m, dve, ph)

    def gpsimd(pool):
        phase_end(m, pool, ph)

    return dict(sync=sync, tensor=tensor, scalar=scalar, vector=vector, gpsimd=gpsimd)


def root_mean_square(dve, S, act_s, sq, mean, ss, last_use):
    J = NB * T // TM
    dve.wait_ge(S.sem, S.at(last_use))
    for k in range(4):
        j = slice(J // 4 * k, J // 4 * (k + 1))
        dve.wait_ge(act_s.sem, act_s.at(f"r_sq{k}"))
        dve.tensor_reduce(ss[:, j], sq[k % 2][:], X, ALU.add).then_inc(S.mark(f"r_ss{k}"), 1)
    dve.wait_ge(act_s.sem, act_s.at("r_std"))
    dve.reciprocal(ss[:], mean[:]).then_inc(S.mark("r_recip"), 1)
    dve.wait_ge(S.sem, S.at("r_recip"))


def scale_groups(dve, passes, S, pe_s, dst, src, factor):
    with dve.Fori(0, passes) as i:
        for s in range(2):
            dve.wait_ge(pe_s.sem, pe_s.before(f"z{s}", i))
            at = bass.ds(i * 2 * GJ + s * GJ, GJ)
            dve.tensor_tensor(dst[s][:], src[:, at, :], cols(factor[:, at].unsqueeze(2), C), ALU.mult).then_inc(S.mark(f"z{s}"), 1)


def turn_groups(m, pe, passes, S, dve_s, act_s, src, rows):
    with pe.Fori(0, passes) as i:
        for s in range(2):
            pe.wait_ge(dve_s.sem, dve_s.at(f"z{s}", i))
            pe.wait_ge(act_s.sem, act_s.before(f"z{s}", i))
            pe.sem_inc(m.gate, 1)
            for j in range(GJ):
                mm = pe.transpose(m.psum[0:rows, 2 * s + j // 4, j % 4 * TM:j % 4 * TM + TM], src[s][:, j, :], m.ident[0:TM, 0:TM])
            mm.then_inc(S.mark(f"z{s}"), 1)


def causal_phase(nc, m, st, ph):
    H, HD, KV, R, Q = 4, 16, 2, 32, 73
    W = Q + T
    sb = lambda n, s, d=F32: st.enter_context(nc.sbuf_tensor(n, s, d))
    w4, wT = sb("ca_w4", [128, 4, C]), sb("ca_wt", [C, 4, 128])
    wv, wvT = sb("ca_wv", [KV * HD, C]), sb("ca_wvt", [C, KV * HD])
    l1 = sb("ca_ln1", [C, 1])
    cos, sin, mask = sb("ca_cos", [128, 2 * T]), sb("ca_sin", [128, 2 * T]), sb("ca_mask", [Q, W])
    z = [sb(f"ca_z{s}", [C, T]) for s in range(2)]
    t1, t2 = ([sb(f"ca_{n}{s}", [128, 2 * T]) for s in range(2)] for n in ("t1", "t2"))
    qz = [sb(f"ca_q{s}", [128, H, T]) for s in range(2)]
    kk = [sb(f"ca_k{s}", [128, T]) for s in range(2)]
    v = [sb(f"ca_v{s}", [Q, 2, KV, HD + 1]) for s in range(2)]
    sc = [sb(f"ca_sc{s}", [Q, H, W]) for s in range(2)]
    pr = [sb(f"ca_pr{s}", [Q, H, W]) for s in range(2)]
    mx = [sb(f"ca_mx{s}", [Q, 2, H]) for s in range(2)]
    pT = [sb(f"ca_pt{s}", [Q, 3, H, Q]) for s in range(2)]
    rs = [sb(f"ca_rs{s}", [Q, 2 * H]) for s in range(2)]
    y = [sb(f"ca_y{s}", [Q, 2, H * HD]) for s in range(2)]
    yT = [sb(f"ca_yt{s}", [C, T]) for s in range(2)]
    ps = m.psum
    NP = NB // 2
    SEG = ((0, 0, Q), (1, Q, W))
    VC = 2 * T
    S1 = lambda n, steps: Steps(nc, m.whole, n, steps)
    two = lambda *names: [f"{n}{s}" for s in range(2) for n in names]
    wl = m.whole.enter_context(nc.semaphore("ca_weights_landed"))
    zl = [Landed(nc, m.whole, f"ca_z_landed{s}", 1) for s in range(2)]
    stored = [Landed(nc, m.whole, f"ca_y_stored{s}", 1) for s in range(2)]
    dve_w, pe_w, act_w = S1("ca_dve_w", ["ones", "clear"]), S1("ca_pe_w", ["turned"]), S1("ca_act_w", ["wt", "wvt"])
    pe_q, pe_sc, pe_t, pe_v, pe_y = (S1(f"ca_pe_{n}", x) for n, x in (
        ("qkv", two("qkv")), ("scores", two("s")), ("turned", two("ta", "tb", "tc")), ("attended", two("o")), ("y", two("y"))))
    dve_r = S1("ca_dve_rope", two("cos", "va", "v", "sin"))
    pool_r = S1("ca_pool_rope", two(*[f"q{h}_" for h in range(H)], "k"))
    dve_sc = S1("ca_dve_scores", two("mask", "max0_", "max1_", "minus0_", "minus1_"))
    dve_o = S1("ca_dve_out", two("recip", "y"))
    act_e, act_t, act_y = (S1(f"ca_act_{n}", x) for n, x in (
        ("exp", two("e")), ("turned", two("ta", "tb", "tc")), ("y", two("y"))))

    def last(S, name, s, i):
        return S.at(name + "0", i) if s else S.before(name + "1", i)

    def sync(sp):
        for s in range(2):
            zl[s].start(sp)
            stored[s].start(sp)
        sp.dma_start(l1[:], m.dram["ffn_ln1_w"].rearrange("(c o) -> c o", o=1)).then_inc(wl, 16)
        sp.dma_start(wv[:], m.dram["ffn_wv"]).then_inc(wl, 16)
        sp.dma_start(cos[:], m.dram["rope_cos"]).then_inc(wl, 16)
        sp.dma_start(sin[:], m.dram["rope_sin"]).then_inc(wl, 16)
        sp.dma_start(mask[:], m.dram["causal_mask"]).then_inc(wl, 16)
        sp.wait_ge(dve_w.sem, dve_w.at("clear"))
        for h in range(H):
            for k, src, r0 in ((0, m.dram["ffn_wq"], HD * h), (2, m.dram["ffn_wk"], HD * (h // 2))):
                sp.dma_start(w4[R * h:R * h + HD, k, :], src[r0:r0 + HD]).then_inc(wl, 16)
                sp.dma_start(w4[R * h:R * h + HD // 2, k + 1, :], src[r0 + HD // 2:r0 + HD]).then_inc(wl, 16)
                sp.dma_start(w4[R * h + HD // 2:R * h + HD, k + 1, :], src[r0:r0 + HD // 2]).then_inc(wl, 16)

        def load(s, i):
            sp.wait_ge(pe_q.sem, pe_q.before(f"qkv{s}", i))
            sp.sem_inc(m.gate, 1)
            sp.dma_start(z[s][:], m.dram["zt_d"][:, bass.ds(i * 2 * T + s * T, T)]).then_inc(zl[s].sem, 16)

        def store(s, i, ready):
            sp.wait_ge(act_y.sem, ready)
            sp.sem_inc(m.gate, 1)
            sp.dma_start(m.dram["yt_d"][:, bass.ds(i * 2 * T + s * T, T)], yT[s][:]).then_inc(stored[s].sem, 16)

        for s in range(2):
            load(s, 0)
        with sp.Fori(1, NP) as i:
            for s in range(2):
                load(s, i)
                store(s, i - 1, act_y.before(f"y{s}", i))
        for s in range(2):
            store(s, NP - 1, act_y.at(f"y{s}", NP - 1))
        for s in range(2):
            sp.wait_ge(stored[s].sem, stored[s].at(NP - 1))
        phase_end(m, sp, ph)

    def tensor(pe):
        for S in (pe_w, pe_q, pe_sc, pe_t, pe_v, pe_y):
            S.start(pe)
        pe.wait_ge(wl, 16 * 29)
        for k in range(4):
            pe.transpose(ps[0:C, 0, 128 * k:128 * k + 128], w4[:, k, :], m.ident[:])
        pe.transpose(ps[0:C, 1, 0:KV * HD], wv[:], m.ident[0:KV * HD, 0:KV * HD]).then_inc(pe_w.mark("turned"), 1)
        pe.wait_ge(act_w.sem, act_w.at("wvt"))

        def project(s, i):
            pe.wait_ge(zl[s].sem, zl[s].at(i))
            pe.wait_ge(dve_r.sem, last(dve_r, "sin", s, i))
            pe.sem_inc(m.gate, 1)
            for k in range(4):
                pe.matmul(ps[:, 6 + k % 2, k // 2 * T:(k // 2 + 1) * T], wT[:, k, :], z[s][:], start=True, stop=True)
            pe.matmul(ps[0:Q, 6, VC:VC + 32], z[s][:, 0:Q], wvT[:], start=True, stop=True)
            pe.matmul(ps[0:T - Q, 6, VC + 32:VC + 64], z[s][:, Q:T], wvT[:], start=True, stop=True).then_inc(pe_q.mark(f"qkv{s}"), 1)

        def scores(s, i):
            pe.wait_ge(pool_r.sem, pool_r.at(f"k{s}", i))
            pe.wait_ge(dve_o.sem, dve_o.before(f"y{s}", i))
            pe.sem_inc(m.gate, 1)
            for h in range(H):
                bank, c0 = 2 * s + h // 2, h % 2 * W
                pe.matmul(ps[0:Q, bank, c0:c0 + Q], qz[s][:, h, 0:Q], kk[s][:, 0:Q], start=True, stop=True)
                mm = pe.matmul(ps[0:Q, bank, c0 + Q:c0 + W], qz[s][:, h, Q - 1:T], kk[s][:], start=True, stop=True)
            mm.then_inc(pe_sc.mark(f"s{s}"), 1)

        turns = (("ta", 0, Q), ("tb", Q, Q), ("tc", 2 * Q, T - Q))

        def turn(s, i):
            pe.wait_ge(act_e.sem, act_e.at(f"e{s}", i))
            for k, (name, c0, n) in enumerate(turns):
                if k == 1:
                    pe.wait_ge(act_y.sem, last(act_y, "y", s, i))
                else:
                    pe.wait_ge(act_t.sem, act_t.at(f"ta{s}", i) if k == 2 else last(act_t, "tc", s, i))
                pe.sem_inc(m.gate, 1)
                for h in range(H):
                    mm = pe.transpose(ps[0:n, 4 + k % 2, h * Q:(h + 1) * Q], pr[s][:, h, c0:c0 + n], m.ident[0:Q, 0:Q])
                mm.then_inc(pe_t.mark(f"{name}{s}"), 1)

        def attend(s, i):
            pe.wait_ge(act_t.sem, act_t.at(f"tc{s}", i))
            pe.wait_ge(dve_r.sem, dve_r.at(f"v{s}", i))
            pe.wait_ge(dve_sc.sem, dve_sc.at(f"mask{s}", i))
            pe.sem_inc(m.gate, 1)
            for h in range(H):
                o = lambda tile: ps[0:Q, 2 * s, (tile * H + h) * (HD + 1):(tile * H + h + 1) * (HD + 1)]
                pe.matmul(o(0), pT[s][:, 0, h, :], v[s][:, 0, h // 2, :], start=True, stop=True)
                pe.matmul(o(1), pT[s][:, 1, h, :], v[s][:, 0, h // 2, :], start=True, stop=False)
                mm = pe.matmul(o(1), pT[s][0:T - Q, 2, h, :], v[s][0:T - Q, 1, h // 2, :], start=False, stop=True)
            mm.then_inc(pe_v.mark(f"o{s}"), 1)

        def turn_y(s, i):
            pe.wait_ge(dve_o.sem, dve_o.at(f"y{s}", i))
            pe.wait_ge(act_t.sem, act_t.at(f"tb{s}", i))
            pe.sem_inc(m.gate, 1)
            pe.transpose(ps[0:C, 5, 0:Q], y[s][:, 0, :], m.ident[0:Q, 0:Q])
            pe.transpose(ps[0:C, 5, Q - 1:T], y[s][:, 1, :], m.ident[0:Q, 0:Q]).then_inc(pe_y.mark(f"y{s}"), 1)

        def one_pass(i, end=False):
            project(1, i)
            turn(0, i)
            scores(1, i)
            attend(0, i)
            if not end:
                project(0, i + 1)
            turn_y(0, i)
            turn(1, i)
            if not end:
                scores(0, i + 1)
            attend(1, i)
            turn_y(1, i)

        project(0, 0)
        scores(0, 0)
        with pe.Fori(0, NP - 1) as i:
            one_pass(i)
        one_pass(NP - 1, end=True)
        phase_end(m, pe, ph)

    def scalar(act):
        for S in (act_w, act_e, act_t, act_y):
            S.start(act)
        act.wait_ge(wl, 16 * 29)
        act.wait_ge(pe_w.sem, pe_w.at("turned"))
        act.activation(wT[:].rearrange("c k n -> c (k n)"), ps[0:C, 0, :], ACT.Copy, scale=l1[:]).then_inc(act_w.mark("wt"), 1)
        act.activation(wvT[:], ps[0:C, 1, 0:KV * HD], ACT.Copy, scale=l1[:]).then_inc(act_w.mark("wvt"), 1)
        act.preload_act_table(ACT.Exp)

        def exp(s, i):
            act.wait_ge(dve_sc.sem, dve_sc.at(f"minus1_{s}", i))
            act.wait_ge(pe_t.sem, pe_t.before(f"tc{s}", i))
            act.activation(pr[s][:], sc[s][:], ACT.Exp).then_inc(act_e.mark(f"e{s}"), 1)

        def turned(s, i):
            for k, (name, n) in enumerate((("ta", Q), ("tb", Q), ("tc", T - Q))):
                act.wait_ge(pe_t.sem, pe_t.at(f"{name}{s}", i))
                if k == 0:
                    act.wait_ge(pe_v.sem, pe_v.before(f"o{s}", i))
                act.activation(pT[s][0:n, k].rearrange("p h q -> p (h q)"), ps[0:n, 4 + k % 2, 0:H * Q], ACT.Copy).then_inc(act_t.mark(f"{name}{s}"), 1)

        def copy_y(s, i):
            act.wait_ge(pe_y.sem, pe_y.at(f"y{s}", i))
            act.wait_ge(stored[s].sem, stored[s].before(i))
            act.activation(yT[s][:], ps[0:C, 5, 0:T], ACT.Copy).then_inc(act_y.mark(f"y{s}"), 1)

        def one_pass(i, end=False):
            turned(0, i)
            exp(1, i)
            copy_y(0, i)
            turned(1, i)
            if not end:
                exp(0, i + 1)
            copy_y(1, i)

        exp(0, 0)
        with act.Fori(0, NP - 1) as i:
            one_pass(i)
        one_pass(NP - 1, end=True)
        phase_end(m, act, ph)

    def vector(dve):
        for S in (dve_w, dve_r, dve_sc, dve_o):
            S.start(dve)
        for s in range(2):
            dve.memset(v[s][:], 1.0)
            ins = dve.memset(qz[s][:], 0.0)
        ins.then_inc(dve_w.mark("ones"), 1)
        dve.memset(w4[:], 0.0).then_inc(dve_w.mark("clear"), 1)
        dve.wait_ge(wl, 16 * 29)
        dve.wait_ge(dve_w.sem, dve_w.at("ones"))

        def rotate(s, i):
            dve.wait_ge(pe_q.sem, pe_q.at(f"qkv{s}", i))
            dve.wait_ge(pool_r.sem, pool_r.before(f"k{s}", i))
            dve.tensor_tensor(t1[s][:], ps[:, 6, 0:2 * T], cos[:], ALU.mult).then_inc(dve_r.mark(f"cos{s}"), 1)
            dve.wait_ge(pe_v.sem, pe_v.before(f"o{s}", i))
            dve.tensor_copy(v[s][0:Q, 0, :, 0:HD], ps[0:Q, 6, VC:VC + 32].rearrange("p (k d) -> p k d", k=KV)).then_inc(dve_r.mark(f"va{s}"), 1)
            dve.tensor_copy(v[s][0:T - Q, 1, :, 0:HD], ps[0:T - Q, 6, VC + 32:VC + 64].rearrange("p (k d) -> p k d", k=KV)).then_inc(dve_r.mark(f"v{s}"), 1)
            dve.tensor_tensor(t2[s][:], ps[:, 7, 0:2 * T], sin[:], ALU.mult).then_inc(dve_r.mark(f"sin{s}"), 1)

        def shift(s, i):
            bank = ps[0:Q, 2 * s:2 * s + 2, 0:2 * W].rearrange("p b (h w) -> p b h w", h=2)
            dve.wait_ge(pe_sc.sem, pe_sc.at(f"s{s}", i))
            dve.wait_ge(act_e.sem, act_e.before(f"e{s}", i))
            dve.tensor_tensor(sc[s][:].rearrange("p (b h) w -> p b h w", b=2), bank,
                              mask[:].unsqueeze(1).unsqueeze(1).broadcast_to([Q, 2, 2, W]), ALU.add).then_inc(dve_sc.mark(f"mask{s}"), 1)
            dve.wait_ge(dve_sc.sem, dve_sc.at(f"mask{s}", i))
            for k, a, b in SEG:
                dve.tensor_reduce(mx[s][:, k], sc[s][:, :, a:b], X, ALU.max).then_inc(dve_sc.mark(f"max{k}_{s}"), 1)
            for k, a, b in SEG:
                dve.wait_ge(dve_sc.sem, dve_sc.at(f"max{k}_{s}", i))
                dve.tensor_tensor(sc[s][:, :, a:b], sc[s][:, :, a:b], cols(mx[s][:, k].unsqueeze(2), b - a), ALU.subtract).then_inc(dve_sc.mark(f"minus{k}_{s}"), 1)

        def normalise(s, i):
            o = ps[0:Q, 2 * s, 0:2 * H * (HD + 1)].rearrange("p (n d) -> p n d", d=HD + 1)
            dve.wait_ge(pe_v.sem, pe_v.at(f"o{s}", i))
            dve.reciprocal(rs[s][:], o[:, :, HD]).then_inc(dve_o.mark(f"recip{s}"), 1)
            dve.wait_ge(dve_o.sem, dve_o.at(f"recip{s}", i))
            dve.wait_ge(pe_y.sem, pe_y.before(f"y{s}", i))
            dve.tensor_tensor(y[s][:].rearrange("p t (h d) -> p (t h) d", d=HD), o[:, :, 0:HD], cols(rs[s][:].unsqueeze(2), HD), ALU.mult).then_inc(dve_o.mark(f"y{s}"), 1)

        def one_pass(i, end=False):
            rotate(1, i)
            shift(1, i)
            normalise(0, i)
            if not end:
                rotate(0, i + 1)
                shift(0, i + 1)
            normalise(1, i)

        rotate(0, 0)
        shift(0, 0)
        with dve.Fori(0, NP - 1) as i:
            one_pass(i)
        one_pass(NP - 1, end=True)
        phase_end(m, dve, ph)

    def gpsimd(pool):
        pool_r.start(pool)
        pool.wait_ge(dve_w.sem, dve_w.at("ones"))
        with pool.Fori(0, NP) as i:
            for s in range(2):
                pool.wait_ge(dve_r.sem, dve_r.at(f"sin{s}", i))
                pool.wait_ge(pe_sc.sem, pe_sc.before(f"s{s}", i))
                pool.wait_ge(pool_r.sem, last(pool_r, "k", s, i))
                pool.sem_inc(m.gate, 1)
                for h in range(H):
                    r = slice(R * h, R * h + R)
                    pool.tensor_tensor(qz[s][r, h, :], t1[s][r, 0:T], t2[s][r, 0:T], ALU.add).then_inc(pool_r.mark(f"q{h}_{s}"), 1)
                pool.wait_ge(pool_r.sem, pool_r.at(f"q{H - 1}_{s}", i))
                pool.tensor_tensor(kk[s][:], t1[s][:, T:2 * T], t2[s][:, T:2 * T], ALU.add).then_inc(pool_r.mark(f"k{s}"), 1)
        phase_end(m, pool, ph)

    return dict(sync=sync, tensor=tensor, scalar=scalar, vector=vector, gpsimd=gpsimd)


def causal_out_phase(nc, m, st, ph):
    J, NE = NB * T // TM, 8
    sb = lambda n, s, d=F32: st.enter_context(nc.sbuf_tensor(n, s, d))
    wo, woT = sb("fo_wo", [C, C]), sb("fo_wot", [C, C])
    rw, rT, l2 = sb("fo_router", [NE, C]), sb("fo_router_t", [C, NE]), sb("fo_ln2", [C, 1])
    yt = [sb(f"fo_yt{s}", [C, GT]) for s in range(2)]
    sq = [sb(f"fo_sq{k}", [TM, J // 4, C]) for k in range(2)]
    mean, ss, eps_rms = sb("fo_mean", [TM, J]), sb("fo_ss", [TM, J]), sb("fo_eps_rms", [128, 1])
    zt = [sb(f"fo_z{s}", [TM, GJ, C]) for s in range(2)]
    zT = [sb(f"fo_zt{s}", [C, GT]) for s in range(2)]
    lg, pr, eq, one1, one2 = (sb(f"fo_{n}", [TM, J, NE]) for n in ("logits", "probs", "eq", "one1", "one2"))
    desc = sb("fo_desc", [TM, NE])
    mx, rs, p2, ws = (sb(f"fo_{n}", [TM, J]) for n in ("mx", "rs", "p2", "ws"))
    ps = m.psum
    P = NG // 2
    S1 = lambda n, steps: Steps(nc, m.whole, n, steps)
    wl = m.whole.enter_context(nc.semaphore("fo_weights_landed"))
    yl = [Landed(nc, m.whole, f"fo_y_landed{s}", 1) for s in range(2)]
    stored = [Landed(nc, m.whole, f"fo_z_stored{s}", 1) for s in range(2)]
    pe_w, act_w, dve_w = S1("fo_pe_w", ["wot", "rt"]), S1("fo_act_w", ["wot", "rt"]), S1("fo_dve_w", ["eps"])
    pe_s, dve_s = S1("fo_pe", ["o0", "o1"]), S1("fo_dve", ["y0", "y1"])
    dve_n = S1("fo_dve_norm", [f"r_ss{k}" for k in range(4)] + ["r_recip", "h"])
    act_n = S1("fo_act_norm", [f"r_{k}" for k in NORM_ACT])
    pe_z, act_z, dve_z = S1("fo_pe_z", ["z0", "z1"]), S1("fo_act_z", ["z0", "z1"]), S1("fo_dve_z", ["z0", "z1"])
    pe_l, dve_l = S1("fo_pe_logits", ["l0", "l1"]), S1("fo_dve_logits", ["l0", "l1"])
    dve_g = S1("fo_dve_gates", ["max", "minus", "sum", "recip", "probs", "p1", "eq1", "cand1", "best1", "one1", "rest", "p2",
                                "eq2", "cand2", "best2", "one2", "wsum", "wrecip", "both", "picked", "gates"])
    act_g = S1("fo_act_gates", ["exp"])

    def sync(sp):
        for s in range(2):
            yl[s].start(sp)
            stored[s].start(sp)
        sp.dma_start(wo[:], m.dram["ffn_wo"]).then_inc(wl, 16)
        sp.dma_start(rw[:], m.dram["ffn_router_w"]).then_inc(wl, 16)
        sp.dma_start(l2[:], m.dram["ffn_ln2_w"].rearrange("(c o) -> c o", o=1)).then_inc(wl, 16)
        sp.dma_start(desc[:], m.dram["descending"].partition_broadcast(TM)).then_inc(wl, 16)
        with sp.Fori(0, P) as i:
            for s in range(2):
                sp.wait_ge(pe_s.sem, pe_s.before(f"o{s}", i))
                sp.sem_inc(m.gate, 1)
                sp.dma_start(yt[s][:], m.dram["yt_d"][:, bass.ds(i * 2 * GT + s * GT, GT)]).then_inc(yl[s].sem, 16)
        with sp.Fori(0, P) as i:
            for s in range(2):
                sp.wait_ge(act_z.sem, act_z.at(f"z{s}", i))
                sp.sem_inc(m.gate, 1)
                sp.dma_start(m.dram["zt_d"][:, bass.ds(i * 2 * GT + s * GT, GT)], zT[s][:]).then_inc(stored[s].sem, 16)
        for s in range(2):
            sp.wait_ge(stored[s].sem, stored[s].at(P - 1))
        phase_end(m, sp, ph)

    def tensor(pe):
        for S in (pe_w, pe_s, pe_z, pe_l):
            S.start(pe)
        pe.wait_ge(wl, 64)
        pe.transpose(ps[0:C, 0, 0:C], wo[:], m.ident[0:C, 0:C]).then_inc(pe_w.mark("wot"), 1)
        pe.transpose(ps[0:C, 1, 0:NE], rw[:], m.ident[0:NE, 0:NE]).then_inc(pe_w.mark("rt"), 1)
        pe.wait_ge(act_w.sem, act_w.at("rt"))
        with pe.Fori(0, P) as i:
            for s in range(2):
                pe.wait_ge(yl[s].sem, yl[s].at(i))
                pe.wait_ge(dve_s.sem, dve_s.before(f"y{s}", i))
                pe.sem_inc(m.gate, 1)
                for j in range(GJ):
                    mm = pe.matmul(ps[0:TM, s, j * C:(j + 1) * C], yt[s][:, j * TM:(j + 1) * TM], woT[:], start=True, stop=True)
                mm.then_inc(pe_s.mark(f"o{s}"), 1)
        with pe.Fori(0, P) as i:
            for s in range(2):
                pe.wait_ge(dve_z.sem, dve_z.at(f"z{s}", i))
                pe.wait_ge(act_z.sem, act_z.before(f"z{s}", i))
                pe.sem_inc(m.gate, 1)
                for j in range(GJ):
                    mm = pe.transpose(ps[0:C, 2 * s + j // 4, j % 4 * TM:j % 4 * TM + TM], zt[s][:, j, :], m.ident[0:TM, 0:TM])
                mm.then_inc(pe_z.mark(f"z{s}"), 1)
                pe.wait_ge(act_z.sem, act_z.at(f"z{s}", i))
                pe.wait_ge(dve_l.sem, dve_l.before(f"l{s}", i))
                pe.sem_inc(m.gate, 1)
                for j in range(GJ):
                    mm = pe.matmul(ps[0:TM, 4 + s, j * NE:(j + 1) * NE], zT[s][:, j * TM:(j + 1) * TM], rT[:], start=True, stop=True)
                mm.then_inc(pe_l.mark(f"l{s}"), 1)
        phase_end(m, pe, ph)

    def scalar(act):
        for S in (act_w, act_n, act_z, act_g):
            S.start(act)
        act.wait_ge(wl, 64)
        act.wait_ge(pe_w.sem, pe_w.at("rt"))
        act.activation(woT[:], ps[0:C, 0, 0:C], ACT.Copy).then_inc(act_w.mark("wot"), 1)
        act.activation(rT[:], ps[0:C, 1, 0:NE], ACT.Copy, scale=l2[:]).then_inc(act_w.mark("rt"), 1)
        act.wait_ge(dve_s.sem, dve_s.at("y1", P - 1))
        for k in range(4):
            j = slice(J // 4 * k, J // 4 * (k + 1))
            if k >= 2:
                act.wait_ge(dve_n.sem, dve_n.at(f"r_ss{k - 2}"))
            act.activation(sq[k % 2][:], m.y[:, j], ACT.Square).then_inc(act_n.mark(f"r_sq{k}"), 1)
        act.wait_ge(dve_n.sem, dve_n.at("r_ss3"))
        act.activation(mean[:], ss[:], ACT.Sqrt, bias=eps_rms[0:TM], scale=1.0 / C).then_inc(act_n.mark("r_std"), 1)
        with act.Fori(0, P) as i:
            for s in range(2):
                act.wait_ge(pe_z.sem, pe_z.at(f"z{s}", i))
                act.wait_ge(stored[s].sem, stored[s].before(i))
                act.wait_ge(pe_l.sem, pe_l.before(f"l{s}", i))
                act.activation(zT[s][:, 0:4 * TM], ps[0:C, 2 * s, 0:4 * TM], ACT.Copy)
                act.activation(zT[s][:, 4 * TM:GT], ps[0:C, 2 * s + 1, 0:TM], ACT.Copy).then_inc(act_z.mark(f"z{s}"), 1)
        act.wait_ge(dve_g.sem, dve_g.at("minus"))
        act.activation(pr[:], lg[:], ACT.Exp).then_inc(act_g.mark("exp"), 1)
        phase_end(m, act, ph)

    def vector(dve):
        for S in (dve_w, dve_s, dve_n, dve_z, dve_l, dve_g):
            S.start(dve)
        dve.memset(eps_rms[:], 1e-6).then_inc(dve_w.mark("eps"), 1)
        with dve.Fori(0, P) as i:
            for s in range(2):
                at = bass.ds(i * 2 * GJ + s * GJ, GJ)
                dve.wait_ge(pe_s.sem, pe_s.at(f"o{s}", i))
                dve.tensor_tensor(m.y[:, at, :], ps[0:TM, s, 0:GJ * C].rearrange("p (j c) -> p j c", c=C), m.y[:, at, :], ALU.add).then_inc(dve_s.mark(f"y{s}"), 1)
        dve.wait_ge(dve_s.sem, dve_s.at("y1", P - 1))
        for k in range(4):
            j = slice(J // 4 * k, J // 4 * (k + 1))
            dve.wait_ge(act_n.sem, act_n.at(f"r_sq{k}"))
            dve.tensor_reduce(ss[:, j], sq[k % 2][:], X, ALU.add).then_inc(dve_n.mark(f"r_ss{k}"), 1)
        dve.wait_ge(act_n.sem, act_n.at("r_std"))
        dve.reciprocal(ss[:], mean[:]).then_inc(dve_n.mark("r_recip"), 1)
        dve.tensor_tensor(m.h[:], m.h[:], m.y[:], ALU.add).then_inc(dve_n.mark("h"), 1)
        dve.wait_ge(dve_n.sem, dve_n.at("h"))
        with dve.Fori(0, P) as i:
            for s in range(2):
                at = bass.ds(i * 2 * GJ + s * GJ, GJ)
                dve.wait_ge(pe_z.sem, pe_z.before(f"z{s}", i))
                dve.tensor_tensor(zt[s][:], m.y[:, at, :], cols(ss[:, at].unsqueeze(2), C), ALU.mult).then_inc(dve_z.mark(f"z{s}"), 1)
                dve.wait_ge(pe_l.sem, pe_l.at(f"l{s}", i))
                dve.tensor_scalar(lg[:, at, :], ps[0:TM, 4 + s, 0:GJ * NE].rearrange("p (j e) -> p j e", e=NE), 1.0, None, ALU.mult).then_inc(dve_l.mark(f"l{s}"), 1)
        S = dve_g
        wide = lambda v: cols(v[:].unsqueeze(2), NE)
        place = desc[:].unsqueeze(1).broadcast_to([TM, J, NE])
        dve.wait_ge(wl, 64)
        dve.wait_ge(dve_l.sem, dve_l.at("l1", P - 1))
        dve.tensor_reduce(mx[:], lg[:], X, ALU.max).then_inc(S.mark("max"), 1)
        dve.wait_ge(S.sem, S.at("max"))
        dve.tensor_tensor(lg[:], lg[:], wide(mx), ALU.subtract).then_inc(S.mark("minus"), 1)
        dve.wait_ge(act_g.sem, act_g.at("exp"))
        dve.tensor_reduce(rs[:], pr[:], X, ALU.add).then_inc(S.mark("sum"), 1)
        dve.wait_ge(S.sem, S.at("sum"))
        dve.reciprocal(mx[:], rs[:]).then_inc(S.mark("recip"), 1)
        dve.wait_ge(S.sem, S.at("recip"))
        dve.tensor_tensor(pr[:], pr[:], wide(mx), ALU.mult).then_inc(S.mark("probs"), 1)
        dve.wait_ge(S.sem, S.at("probs"))
        dve.tensor_reduce(mx[:], pr[:], X, ALU.max).then_inc(S.mark("p1"), 1)
        dve.wait_ge(S.sem, S.at("p1"))
        dve.tensor_tensor(eq[:], pr[:], wide(mx), ALU.is_equal).then_inc(S.mark("eq1"), 1)
        dve.wait_ge(S.sem, S.at("eq1"))
        dve.tensor_tensor(eq[:], eq[:], place, ALU.mult).then_inc(S.mark("cand1"), 1)
        dve.wait_ge(S.sem, S.at("cand1"))
        dve.tensor_reduce(rs[:], eq[:], X, ALU.max).then_inc(S.mark("best1"), 1)
        dve.wait_ge(S.sem, S.at("best1"))
        dve.tensor_tensor(one1[:], place, wide(rs), ALU.is_equal).then_inc(S.mark("one1"), 1)
        dve.wait_ge(S.sem, S.at("one1"))
        dve.scalar_tensor_tensor(out=lg[:], in0=one1[:], scalar=-2.0, in1=pr[:], op0=ALU.mult, op1=ALU.add).then_inc(S.mark("rest"), 1)
        dve.wait_ge(S.sem, S.at("rest"))
        dve.tensor_reduce(p2[:], lg[:], X, ALU.max).then_inc(S.mark("p2"), 1)
        dve.wait_ge(S.sem, S.at("p2"))
        dve.tensor_tensor(eq[:], lg[:], wide(p2), ALU.is_equal).then_inc(S.mark("eq2"), 1)
        dve.wait_ge(S.sem, S.at("eq2"))
        dve.tensor_tensor(eq[:], eq[:], place, ALU.mult).then_inc(S.mark("cand2"), 1)
        dve.wait_ge(S.sem, S.at("cand2"))
        dve.tensor_reduce(rs[:], eq[:], X, ALU.max).then_inc(S.mark("best2"), 1)
        dve.wait_ge(S.sem, S.at("best2"))
        dve.tensor_tensor(one2[:], place, wide(rs), ALU.is_equal).then_inc(S.mark("one2"), 1)
        dve.scalar_tensor_tensor(out=ws[:], in0=mx[:], scalar=1e-9, in1=p2[:], op0=ALU.add, op1=ALU.add).then_inc(S.mark("wsum"), 1)
        dve.wait_ge(S.sem, S.at("wsum"))
        dve.reciprocal(rs[:], ws[:]).then_inc(S.mark("wrecip"), 1)
        dve.wait_ge(S.sem, S.at("wrecip"))
        dve.tensor_tensor(one1[:], one1[:], one2[:], ALU.add).then_inc(S.mark("both"), 1)
        dve.wait_ge(S.sem, S.at("both"))
        dve.tensor_tensor(one1[:], one1[:], pr[:], ALU.mult).then_inc(S.mark("picked"), 1)
        dve.wait_ge(S.sem, S.at("picked"))
        dve.tensor_tensor(m.gates[:], one1[:], wide(rs), ALU.mult).then_inc(S.mark("gates"), 1)
        phase_end(m, dve, ph)

    def gpsimd(pool):
        phase_end(m, pool, ph)

    return dict(sync=sync, tensor=tensor, scalar=scalar, vector=vector, gpsimd=gpsimd)


def experts_phase(nc, m, st, ph):
    NE, HID, KH, N = 8, 170, 85, 2 * TM
    J = NB * T // TM
    sb = lambda n, s, d=F32: st.enter_context(nc.sbuf_tensor(n, s, d))
    w1, w3, w2 = sb("ex_w1", [KH, NE, 2, C]), sb("ex_w3", [KH, NE, 2, C]), sb("ex_w2", [C, NE, HID])
    w1T, w3T, w2T = sb("ex_w1t", [C, NE, 2, KH]), sb("ex_w3t", [C, NE, 2, KH]), sb("ex_w2t", [KH, NE, 2, C])
    l2 = sb("ex_ln2", [C, 1])
    z = [sb(f"ex_z{s}", [C, N]) for s in range(2)]
    act1 = [sb(f"ex_silu{k}", [KH, 2 * N]) for k in range(2)]
    hid = [sb(f"ex_hid{k}", [KH, 2, N]) for k in range(2)]
    gated = [sb(f"ex_gated{s}", [TM, 2, NE, C]) for s in range(2)]
    summed = [sb(f"ex_sum{s}", [TM, 2, C]) for s in range(2)]
    res = [sb(f"ex_out{s}", [TM, 2, C]) for s in range(2)]
    ps = m.psum
    P = J // 4
    S1 = lambda n, steps: Steps(nc, m.whole, n, steps)
    wl = m.whole.enter_context(nc.semaphore("ex_weights_landed"))
    zl = [Landed(nc, m.whole, f"ex_z_landed{s}", 1) for s in range(2)]
    stored = [Landed(nc, m.whole, f"ex_stored{s}", 2) for s in range(2)]
    pe_w, act_w = S1("ex_pe_w", [f"w{e}" for e in range(NE)]), S1("ex_act_w", [f"w{e}" for e in range(NE)])
    units = [(s, e) for s in range(2) for e in range(NE)]
    name = [f"{s}{e}" for s, e in units]
    pe_u, pe_d = S1("ex_pe_up", [f"{g}{n}" for n in name for g in ("gate", "up")]), S1("ex_pe_down", ["d" + n for n in name])
    act_s, dve_h = S1("ex_act_silu", ["s" + n for n in name]), S1("ex_dve_hidden", ["h" + n for n in name])
    dve_o = S1("ex_dve_out", [f"{n}{s}" for s in range(2) for n in ("gated", "sum", "out")])

    def before_unit(S, k, s, e, i, back):
        n = s * NE + e - back
        return S.at(k + name[n], i) if n >= 0 else S.before(k + name[n], i)

    def sync(sp):
        for s in range(2):
            zl[s].start(sp)
            stored[s].start(sp)
        for t in range(2):
            sp.dma_start(w1[:, :, t], m.dram["ffn_w1"][:, t * KH:(t + 1) * KH].rearrange("e k c -> k e c")).then_inc(wl, 16)
            sp.dma_start(w3[:, :, t], m.dram["ffn_w3"][:, t * KH:(t + 1) * KH].rearrange("e k c -> k e c")).then_inc(wl, 16)
        sp.dma_start(w2[:], m.dram["ffn_w2"].rearrange("e c k -> c e k")).then_inc(wl, 16)
        sp.dma_start(l2[:], m.dram["ffn_ln2_w"].rearrange("(c o) -> c o", o=1)).then_inc(wl, 16)

        def load(s, i):
            sp.wait_ge(pe_u.sem, pe_u.before(f"up{s}{NE - 1}", i))
            sp.sem_inc(m.gate, 1)
            sp.dma_start(z[s][:], m.dram["zt_d"][:, bass.ds(i * 2 * N + s * N, N)]).then_inc(zl[s].sem, 16)

        def store(s, i, ready):
            sp.wait_ge(dve_o.sem, ready)
            sp.sem_inc(m.gate, 1)
            dst = m.out.rearrange("b t c -> (b t) c")[bass.ds(i * 2 * N + s * N, N)].rearrange("(j p) c -> p j c", p=TM)
            for p0, p1 in ((0, 112), (112, TM)):
                sp.dma_start(dst[p0:p1], res[s][p0:p1]).then_inc(stored[s].sem, 16)

        for s in range(2):
            load(s, 0)
        with sp.Fori(1, P) as i:
            for s in range(2):
                load(s, i)
                store(s, i - 1, dve_o.before(f"out{s}", i))
        for s in range(2):
            store(s, P - 1, dve_o.at(f"out{s}", P - 1))
        for s in range(2):
            sp.wait_ge(stored[s].sem, stored[s].at(P - 1))
        phase_end(m, sp, ph)

    def tensor(pe):
        for S in (pe_w, pe_u, pe_d):
            S.start(pe)
        pe.wait_ge(wl, 16 * 6)
        for e in range(NE):
            if e >= 2:
                pe.wait_ge(act_w.sem, act_w.at(f"w{e - 2}"))
            b = 2 * (e % 2)
            for t in range(2):
                pe.transpose(ps[0:C, b, t * KH:(t + 1) * KH], w1[:, e, t, :], m.ident[0:KH, 0:KH])
                pe.transpose(ps[0:C, b, (2 + t) * KH:(3 + t) * KH], w3[:, e, t, :], m.ident[0:KH, 0:KH])
                mm = pe.transpose(ps[0:KH, b + 1, t * C:(t + 1) * C], w2[:, e, t * KH:(t + 1) * KH], m.ident[0:C, 0:C])
            mm.then_inc(pe_w.mark(f"w{e}"), 1)
        pe.wait_ge(act_w.sem, act_w.at(f"w{NE - 1}"))

        def up(s, e, i):
            if e == 0:
                pe.wait_ge(zl[s].sem, zl[s].at(i))
            pe.wait_ge(dve_h.sem, before_unit(dve_h, "h", s, e, i, 2))
            pe.sem_inc(m.gate, 1)
            for k, (w, g) in enumerate(((w1T, "gate"), (w3T, "up"))):
                for t in range(2):
                    mm = pe.matmul(ps[0:KH, 2 * (e % 2) + k, t * N:(t + 1) * N], w[:, e, t, :], z[s][:], start=True, stop=True)
                mm.then_inc(pe_u.mark(f"{g}{s}{e}"), 1)

        def down(s, e, i):
            pe.wait_ge(dve_h.sem, dve_h.at(f"h{s}{e}", i))
            if e == 0:
                pe.wait_ge(dve_o.sem, dve_o.before(f"gated{s}", i))
            pe.sem_inc(m.gate, 1)
            for j in range(2):
                for t in range(2):
                    mm = pe.matmul(ps[0:TM, 4 + 2 * s + j, e * C:(e + 1) * C], hid[e % 2][:, t, j * TM:(j + 1) * TM], w2T[:, e, t, :], start=t == 0, stop=t == 1)
            mm.then_inc(pe_d.mark(f"d{s}{e}"), 1)

        def one_pass(i, end=False):
            for n, (s, e) in enumerate(units):
                if n + 1 < len(units):
                    up(*units[n + 1], i)
                elif not end:
                    up(0, 0, i + 1)
                down(s, e, i)

        up(0, 0, 0)
        with pe.Fori(0, P - 1) as i:
            one_pass(i)
        one_pass(P - 1, end=True)
        phase_end(m, pe, ph)

    def scalar(act):
        for S in (act_w, act_s):
            S.start(act)
        act.wait_ge(wl, 16 * 6)
        for e in range(NE):
            b = 2 * (e % 2)
            act.wait_ge(pe_w.sem, pe_w.at(f"w{e}"))
            act.activation(w1T[:, e], ps[0:C, b, 0:2 * KH].rearrange("c (t k) -> c t k", t=2), ACT.Copy, scale=l2[:])
            act.activation(w3T[:, e], ps[0:C, b, 2 * KH:4 * KH].rearrange("c (t k) -> c t k", t=2), ACT.Copy, scale=l2[:])
            act.activation(w2T[:, e], ps[0:KH, b + 1, 0:2 * C].rearrange("c (t k) -> c t k", t=2), ACT.Copy).then_inc(act_w.mark(f"w{e}"), 1)
        act.preload_act_table(ACT.Silu)
        with act.Fori(0, P) as i:
            for s, e in units:
                act.wait_ge(pe_u.sem, pe_u.at(f"gate{s}{e}", i))
                act.wait_ge(dve_h.sem, before_unit(dve_h, "h", s, e, i, 2))
                act.activation(act1[e % 2][:], ps[0:KH, 2 * (e % 2), 0:2 * N], ACT.Silu).then_inc(act_s.mark(f"s{s}{e}"), 1)
        phase_end(m, act, ph)

    def vector(dve):
        for S in (dve_h, dve_o):
            S.start(dve)

        def combine(s, i):
            at = bass.ds(i * 4 + 2 * s, 2)
            dve.wait_ge(pe_d.sem, pe_d.at(f"d{s}{NE - 1}", i))
            dve.tensor_tensor(gated[s][:].rearrange("p j e c -> p (j e) c"), ps[0:TM, 4 + 2 * s:6 + 2 * s, :].rearrange("p j (e c) -> p (j e) c", c=C),
                              cols(m.gates[:, at, :].rearrange("p j e -> p (j e)").unsqueeze(2), C), ALU.mult).then_inc(dve_o.mark(f"gated{s}"), 1)
            dve.wait_ge(dve_o.sem, dve_o.at(f"gated{s}", i))
            dve.tensor_reduce(summed[s][:], gated[s][:].rearrange("p j e c -> p j c e"), X, ALU.add).then_inc(dve_o.mark(f"sum{s}"), 1)
            dve.wait_ge(dve_o.sem, dve_o.at(f"sum{s}", i))
            dve.wait_ge(stored[s].sem, stored[s].before(i))
            dve.tensor_tensor(res[s][:], summed[s][:], m.h[:, at, :], ALU.add).then_inc(dve_o.mark(f"out{s}"), 1)

        def hidden(s, e, i):
            dve.wait_ge(act_s.sem, act_s.at(f"s{s}{e}", i))
            dve.wait_ge(pe_u.sem, pe_u.at(f"up{s}{e}", i))
            dve.wait_ge(pe_d.sem, before_unit(pe_d, "d", s, e, i, 2))
            dve.tensor_tensor(hid[e % 2][:].rearrange("k t n -> k (t n)"), ps[0:KH, 2 * (e % 2) + 1, 0:2 * N], act1[e % 2][:], ALU.mult).then_inc(dve_h.mark(f"h{s}{e}"), 1)

        def one_pass(i, end=False):
            for n, (s, e) in enumerate(units):
                if n + 1 < len(units):
                    hidden(*units[n + 1], i)
                elif not end:
                    hidden(0, 0, i + 1)
                if e == NE - 1:
                    combine(s, i)

        hidden(0, 0, 0)
        with dve.Fori(0, P - 1) as i:
            one_pass(i)
        one_pass(P - 1, end=True)
        phase_end(m, dve, ph)

    def gpsimd(pool):
        phase_end(m, pool, ph)

    return dict(sync=sync, tensor=tensor, scalar=scalar, vector=vector, gpsimd=gpsimd)


PHASES = [patch_phase, vit_phase, text_phase, joint_in_phase, joint_phase, joint_out_phase, causal_phase, causal_out_phase, experts_phase]
DEBUG = False





def program(nc, dram, scratch, out):
    with ExitStack() as whole:
        m = Shared({**dram, **scratch})
        m.out = out
        m.whole = whole
        m.psum = whole.enter_context(nc.psum_tensor("banks", [128, 8, BANK], F32))
        m.ident = whole.enter_context(nc.sbuf_tensor("ident", [128, 128], F32))
        m.phase_done = whole.enter_context(nc.semaphore("phase_done"))
        m.gate = whole.enter_context(nc.semaphore("gate"))
        m.ident_landed = whole.enter_context(nc.semaphore("ident_landed"))
        m.vit_x = whole.enter_context(nc.sbuf_tensor("vit_x", [128, 16, C], F32))
        m.pos_tile = whole.enter_context(nc.sbuf_tensor("pos_tile", [128, C], F32))
        m.h = whole.enter_context(nc.sbuf_tensor("h", [TM, NB * T // TM, C], F32))
        m.y = whole.enter_context(nc.sbuf_tensor("y", [TM, NB * T // TM, C], F32))
        m.gates = whole.enter_context(nc.sbuf_tensor("gates", [TM, NB * T // TM, 8], F32))
        phases = []
        for ph, build in enumerate(PHASES):
            with ExitStack() as st:
                phases.append(build(nc, m, st, ph))
        block = whole.enter_context(nc.Block())

        @block.sync
        def _(sp):
            sp.dma_start(m.ident[:], m.dram["identity"]).then_inc(m.ident_landed, 16)
            for p in phases:
                p["sync"](sp)

        @block.tensor
        def _(pe):
            pe.wait_ge(m.ident_landed, 16)
            for p in phases:
                p["tensor"](pe)

        @block.scalar
        def _(act):
            for p in phases:
                p["scalar"](act)

        @block.vector
        def _(dve):
            for p in phases:
                p["vector"](dve)

        @block.gpsimd
        def _(pool):
            for p in phases:
                p["gpsimd"](pool)


def _constants(np):
    f = np.float32
    freqs = np.outer(np.arange(T, dtype=f), 1.0 / 10000.0 ** (np.arange(0, 16, 2, dtype=f) / 16)).astype(f)
    sign = np.repeat(np.array([-1, 1], f), 8)[:, None]
    cos, sin = np.cos(np.tile(freqs, 2)).T, sign * np.sin(np.tile(freqs, 2)).T
    table = lambda t: np.tile(np.concatenate([np.concatenate([0.25 * t, t], 1), np.zeros((16, 2 * T), f)]), (4, 1)).astype(f)
    q = np.arange(73)[:, None]
    mask = np.concatenate([np.where(np.arange(73) <= q, 0, MASKED), np.where(np.arange(T) <= q + 72, 0, MASKED)], 1).astype(f)
    return {
        "rope_cos": table(cos),
        "rope_sin": table(sin),
        "causal_mask": mask,
        "descending": np.arange(8, 0, -1).astype(f),
        "identity": np.eye(128, dtype=f),
        "inv_count": (1 / np.minimum(np.arange(16) + 1, 5)).astype(f),
        "id_col": (np.arange(128) % 64).astype(f)[:, None],
        "id_row": np.arange(64).astype(f),
    }


_SCRATCH = {"h_d": (NB * T, C), "xt_d": (C, NB * T), "v_d": (NB, T * C), "ctx_d": (NB, T * 8 * C),
            "zt_d": (C, NB * T), "yt_d": (C, NB * T)}


def kernel(**inputs):
    import numpy as _np
    import concourse.bacc as _bacc
    from concourse import mybir as _mybir
    from concourse.bass_utils import run_bass_kernel_spmd as _run

    nc = _bacc.Bacc("TRN2", target_bir_lowering=False, num_devices=1)
    arrays, dram = {}, {}
    for name, a in {**inputs, **_constants(_np)}.items():
        a = _np.ascontiguousarray(a)
        arrays[f"in_{name}"] = a
        dram[name.removeprefix("L0_")] = nc.dram_tensor(f"in_{name}", a.shape, _mybir.dt.from_np(a.dtype), kind="ExternalInput").ap()
    scratch = {n: nc.dram_tensor(n, s, _mybir.dt.float32, kind="ExternalOutput" if DEBUG else "Internal").ap() for n, s in _SCRATCH.items()}
    out = nc.dram_tensor("fused_out", (NB, T, C), _mybir.dt.float32, kind="ExternalOutput").ap()
    program(nc, dram, scratch, out)
    r = _run(nc, [arrays], core_ids=[0])
    return r.results[0]["fused_out"]
```

```python
from contextlib import ExitStack

import concourse.bass as bass
from concourse import mybir

F32 = mybir.dt.float32
BF16 = mybir.dt.bfloat16
I32 = mybir.dt.int32
ALU = mybir.AluOpType
ACT = mybir.ActivationFunctionType
X = mybir.AxisListType.X

NB = 64
C = 64
NTOK = 17
T = 145
TOKENS = NB * T
TM = 116
GB = 4
GT = GB * T
GJ = GT // TM
NG = NB // GB
EPS = 1e-5
MASKED = -1e30
BANK = 512


class Steps:

    def __init__(self, nc, stack, name, steps):
        self.sem = stack.enter_context(nc.semaphore(name))
        self.steps = steps
        self.n = len(steps)
        self.next = 0

    def start(self, eng):
        eng.sem_inc(self.sem, self.n)

    def mark(self, step):
        assert self.steps[self.next % self.n] == step, (step, self.steps[self.next % self.n])
        self.next += 1
        return self.sem

    def at(self, step, i=0):
        return i * self.n + (self.n + self.steps.index(step) + 1)

    def before(self, step, i=0):
        return i * self.n + (self.steps.index(step) + 1)


class Landed:

    def __init__(self, nc, stack, name, k):
        self.sem = stack.enter_context(nc.semaphore(name))
        self.k = 16 * k

    def start(self, eng):
        eng.sem_inc(self.sem, self.k)

    def at(self, i=0):
        return i * self.k + 2 * self.k

    def before(self, i=0):
        return i * self.k + self.k


class Shared:

    def __init__(self, dram):
        self.dram = dram


def cols(ap, n):
    return ap.broadcast_to(list(ap.shape[:-1]) + [n])


def phase_end(m, eng, phase):
    eng.drain().then_inc(m.phase_done, 1)
    eng.wait_ge(m.phase_done, 5 * (phase + 1))
    eng.sem_inc(m.gate, 1)


def patch_phase(nc, m, st, ph):
    IMG, P, GRID, DIM = 128, 32, 4, 64
    CH = 3
    K = CH * P
    B8 = 8
    NI = NB // B8
    NP = B8 * GRID * GRID
    PD = CH * P * P
    sb = lambda n, s, d=F32: st.enter_context(nc.sbuf_tensor(n, s, d))
    img = [sb(f"img{s}", [K, B8, GRID, IMG]) for s in range(2)]
    sq = [sb(f"img_sq{s}", [K, NP // 4, 4 * P]) for s in range(2)]
    sqsum = [sb(f"sqsum{s}", [K, NP]) for s in range(2)]
    proj = [sb(f"proj{s}", [DIM + 1, NP]) for s in range(2)]
    w = sb("w_patch", [K, P, DIM])
    wg = sb("w_patch_gained", [K, P, DIM + 1])
    wb = sb("w_patch_biased", [K, P, DIM])
    gain, shift = sb("patch_gain", [K, P]), sb("patch_shift", [K, P])
    wsum, wbsum = sb("w_gained_sum", [K, DIM]), sb("w_biased_sum", [K, DIM])
    ones = sb("ones_patch", [K, 128])
    colsum, bias = sb("colsum", [128, DIM]), sb("bias_p", [128, DIM])
    bp = sb("b_patch_rows", [128, DIM])
    g2, b2 = sb("ln_p2_g_rows", [128, DIM]), sb("ln_p2_b_rows", [128, DIM])
    pos = sb("pos_rows", [128, DIM])
    cls = sb("cls_rows", [128, DIM])
    raw = sb("raw_tokens", [128, NI, DIM + 2])
    y, t = sb("patch_y", [128, NI, DIM]), sb("patch_t", [128, NI, DIM])
    mean, var, tmp = sb("p_mean", [128, NI]), sb("p_var", [128, NI]), sb("p_tmp", [128, NI])
    eps = sb("p_eps", [128, 1])
    ps = m.psum
    sem = lambda n: m.whole.enter_context(nc.semaphore(n))
    consts = sem("patch_consts_landed")
    placed = sem("patch_tokens_placed")
    imgs = [Landed(nc, m.whole, f"img_landed{s}", CH * GRID) for s in range(2)]
    pe_s = Steps(nc, m.whole, "patch_pe", [f"{k}{s}" for s in range(2) for k in ("projected", "squares", "turned")])
    act_s = Steps(nc, m.whole, "patch_act", [f"{k}{s}" for s in range(2) for k in ("squared", "proj_copied")])
    dve_s = Steps(nc, m.whole, "patch_dve", [f"{k}{s}" for s in range(2) for k in ("sq_reduced", "raw_copied", "sumsq_copied")])
    pe_w = Steps(nc, m.whole, "patch_pe_w", ["sums"])
    dve_w = Steps(nc, m.whole, "patch_dve_w", ["ones", "gained", "ones_col", "biased", "wsum", "wbsum", "colsum", "bias", "eps", "x_clear"])
    fin = ["mean", "msq", "ex2", "var", "recip", "mu_w", "minus", "scaled", "biased", "sum", "mean2", "cent",
           "sq2", "ss2", "recip2", "norm2", "gain2", "shift2", "pos_added"]
    dve_f = Steps(nc, m.whole, "patch_dve_f", fin)
    act_f = Steps(nc, m.whole, "patch_act_f", ["std", "std2"])

    def sync(sp):
        sp.dma_start(w[:], m.dram["tok_W_patch"].rearrange("(p x) o -> p x o", x=P)).then_inc(consts, 16)
        sp.dma_start(gain[:], m.dram["tok_ln_p1_g"].rearrange("(p x) -> p x", x=P)).then_inc(consts, 16)
        sp.dma_start(shift[:], m.dram["tok_ln_p1_b"].rearrange("(p x) -> p x", x=P)).then_inc(consts, 16)
        sp.dma_start(bp[:], m.dram["tok_b_patch"].partition_broadcast(128)).then_inc(consts, 16)
        sp.dma_start(g2[:], m.dram["tok_ln_p2_g"].partition_broadcast(128)).then_inc(consts, 16)
        sp.dma_start(b2[:], m.dram["tok_ln_p2_b"].partition_broadcast(128)).then_inc(consts, 16)
        for s in range(2):
            imgs[s].start(sp)
        with sp.Fori(0, NI // 2) as i:
            for s in range(2):
                sp.wait_ge(pe_s.sem, pe_s.before(f"projected{s}", i))
                sp.sem_inc(m.gate, 1)
                sp.wait_ge(act_s.sem, act_s.before(f"squared{s}", i))
                sp.sem_inc(m.gate, 1)
                for c in range(CH):
                    for g in range(GRID):
                        sp.dma_start(img[s][c * P:(c + 1) * P, :, g, :],
                                     m.dram["x"][bass.ds(i * 2 * B8 + s * B8, B8), c, g * P:(g + 1) * P].rearrange("b r w -> r b w")
                                     ).then_inc(imgs[s].sem, 16)
        sp.wait_ge(dve_w.sem, dve_w.at("x_clear"))
        for j in range(4):
            sp.dma_start(m.pos_tile[32 * j:32 * j + NTOK], m.dram["tok_pos"][0]).then_inc(consts, 16)
            sp.dma_start(m.vit_x[32 * j:32 * j + 1], m.dram["tok_cls"][0, 0:1].unsqueeze(1).broadcast_to([1, 16, DIM])).then_inc(placed, 16)
        sp.wait_ge(dve_f.sem, dve_f.at("shift2"))
        for j in range(4):
            for half in range(2):
                p0 = (4 * half + j) * 16
                sp.dma_start(m.vit_x[32 * j + 1:32 * j + NTOK, half::2, :], y[p0:p0 + 16]).then_inc(placed, 16)
        sp.wait_ge(placed, 16 * 12)
        phase_end(m, sp, ph)

    def tensor(pe):
        pe_w.start(pe)
        pe_s.start(pe)
        pe.wait_ge(dve_w.sem, dve_w.at("wbsum"))
        pe.matmul(ps[:, 0, 0:DIM], ones[:], wsum[:], start=True, stop=True)
        pe.matmul(ps[:, 1, 0:DIM], ones[:], wbsum[:], start=True, stop=True).then_inc(pe_w.mark("sums"), 1)
        with pe.Fori(0, NI // 2) as i:
            for s in range(2):
                pe.wait_ge(imgs[s].sem, imgs[s].at(i))
                pe.wait_ge(act_s.sem, act_s.before(f"proj_copied{s}", i))
                pe.sem_inc(m.gate, 1)
                for px in range(P):
                    mm = pe.matmul(ps[0:DIM + 1, 2 + s, 0:NP], wg[:, px, :],
                                   img[s][:].rearrange("k b g (h x) -> k (b g h) x", x=P)[:, :, px],
                                   start=px == 0, stop=px == P - 1)
                mm.then_inc(pe_s.mark(f"projected{s}"), 1)
                pe.wait_ge(dve_s.sem, dve_s.at(f"sq_reduced{s}", i))
                pe.wait_ge(dve_s.sem, dve_s.before(f"sumsq_copied{s}", i))
                pe.sem_inc(m.gate, 1)
                pe.matmul(ps[:, 4 + s, 0:1], sqsum[s][:], ones[:, 0:1], start=True, stop=True).then_inc(pe_s.mark(f"squares{s}"), 1)
                pe.wait_ge(act_s.sem, act_s.at(f"proj_copied{s}", i))
                pe.sem_inc(m.gate, 1)
                pe.transpose(ps[:, 6 + s, 0:DIM + 1], proj[s][:], m.ident[0:DIM + 1, 0:DIM + 1]).then_inc(pe_s.mark(f"turned{s}"), 1)
        phase_end(m, pe, ph)

    def scalar(act):
        act_s.start(act)
        act_f.start(act)
        with act.Fori(0, NI // 2) as i:
            for s in range(2):
                act.wait_ge(imgs[s].sem, imgs[s].at(i))
                act.wait_ge(dve_s.sem, dve_s.before(f"sq_reduced{s}", i))
                act.activation(sq[s][:].rearrange("k n (g p) -> k (n g p)", g=4), img[s][:].rearrange("k b g w -> k (b g w)"),
                               ACT.Square).then_inc(act_s.mark(f"squared{s}"), 1)
                act.wait_ge(pe_s.sem, pe_s.at(f"projected{s}", i))
                act.wait_ge(pe_s.sem, pe_s.before(f"turned{s}", i))
                act.activation(proj[s][:], ps[0:DIM + 1, 2 + s, 0:NP], ACT.Copy).then_inc(act_s.mark(f"proj_copied{s}"), 1)
        act.wait_ge(dve_w.sem, dve_w.at("eps"))
        act.wait_ge(dve_f.sem, dve_f.at("var"))
        act.activation(tmp[:], var[:], ACT.Sqrt, bias=eps[:]).then_inc(act_f.mark("std"), 1)
        act.wait_ge(dve_f.sem, dve_f.at("ss2"))
        act.activation(tmp[:], var[:], ACT.Sqrt, bias=eps[:], scale=1.0 / DIM).then_inc(act_f.mark("std2"), 1)
        phase_end(m, act, ph)

    def vector(dve):
        dve_w.start(dve)
        dve_s.start(dve)
        dve_f.start(dve)
        dve.memset(ones[:], 1.0).then_inc(dve_w.mark("ones"), 1)
        dve.wait_ge(consts, 16 * 6)
        dve.tensor_tensor(wg[:, :, 0:DIM], w[:], cols(gain[:].unsqueeze(2), DIM), ALU.mult).then_inc(dve_w.mark("gained"), 1)
        dve.memset(wg[:, :, DIM:DIM + 1], 1.0).then_inc(dve_w.mark("ones_col"), 1)
        dve.tensor_tensor(wb[:], w[:], cols(shift[:].unsqueeze(2), DIM), ALU.mult).then_inc(dve_w.mark("biased"), 1)
        dve.wait_ge(dve_w.sem, dve_w.at("biased"))
        dve.tensor_reduce(wsum[:], wg[:, :, 0:DIM].rearrange("k x o -> k o x"), X, ALU.add).then_inc(dve_w.mark("wsum"), 1)
        dve.tensor_reduce(wbsum[:], wb[:].rearrange("k x o -> k o x"), X, ALU.add).then_inc(dve_w.mark("wbsum"), 1)
        dve.wait_ge(pe_w.sem, pe_w.at("sums"))
        dve.tensor_copy(colsum[:], ps[:, 0, 0:DIM]).then_inc(dve_w.mark("colsum"), 1)
        dve.tensor_tensor(bias[:], ps[:, 1, 0:DIM], bp[:], ALU.add).then_inc(dve_w.mark("bias"), 1)
        dve.memset(eps[:], EPS).then_inc(dve_w.mark("eps"), 1)
        dve.memset(m.pos_tile[:], 0.0)
        dve.memset(m.vit_x[:], 0.0).then_inc(dve_w.mark("x_clear"), 1)
        with dve.Fori(0, NI // 2) as i:
            for s in range(2):
                dve.wait_ge(act_s.sem, act_s.at(f"squared{s}", i))
                dve.wait_ge(pe_s.sem, pe_s.before(f"squares{s}", i))
                dve.tensor_reduce(sqsum[s][:], sq[s][:].rearrange("k n (g p) -> k (n g) p", g=4), X, ALU.add
                                  ).then_inc(dve_s.mark(f"sq_reduced{s}"), 1)
                dve.wait_ge(pe_s.sem, pe_s.at(f"turned{s}", i))
                dve.tensor_scalar(raw[:, bass.ds(2 * i + s, 1), 0:DIM + 1], ps[:, 6 + s, 0:DIM + 1].unsqueeze(1), 1.0, None, ALU.mult
                                  ).then_inc(dve_s.mark(f"raw_copied{s}"), 1)
                dve.tensor_scalar(raw[:, bass.ds(2 * i + s, 1), DIM + 1:DIM + 2], ps[:, 4 + s, 0:1].unsqueeze(1), 1.0, None, ALU.mult
                                  ).then_inc(dve_s.mark(f"sumsq_copied{s}"), 1)
        dve.wait_ge(dve_s.sem, dve_s.at("sumsq_copied1", NI // 2 - 1))
        F = dve_f
        dve.tensor_scalar(mean[:], raw[:, :, DIM], 1.0 / PD, None, ALU.mult).then_inc(F.mark("mean"), 1)
        dve.wait_ge(F.sem, F.at("mean"))
        dve.tensor_tensor(tmp[:], mean[:], mean[:], ALU.mult).then_inc(F.mark("msq"), 1)
        dve.tensor_scalar(var[:], raw[:, :, DIM + 1], 1.0 / PD, None, ALU.mult).then_inc(F.mark("ex2"), 1)
        dve.wait_ge(F.sem, F.at("ex2"))
        dve.tensor_tensor(var[:], var[:], tmp[:], ALU.subtract).then_inc(F.mark("var"), 1)
        dve.wait_ge(act_f.sem, act_f.at("std"))
        dve.reciprocal(var[:], tmp[:]).then_inc(F.mark("recip"), 1)
        dve.tensor_tensor(t[:], colsum[:].unsqueeze(1).broadcast_to([128, NI, DIM]), cols(mean[:].unsqueeze(2), DIM), ALU.mult).then_inc(F.mark("mu_w"), 1)
        dve.wait_ge(F.sem, F.at("mu_w"))
        dve.tensor_tensor(y[:], raw[:, :, 0:DIM], t[:], ALU.subtract).then_inc(F.mark("minus"), 1)
        dve.wait_ge(F.sem, F.at("minus"))
        dve.tensor_tensor(y[:], y[:], cols(var[:].unsqueeze(2), DIM), ALU.mult).then_inc(F.mark("scaled"), 1)
        dve.wait_ge(F.sem, F.at("scaled"))
        dve.tensor_tensor(y[:], y[:], bias[:].unsqueeze(1).broadcast_to([128, NI, DIM]), ALU.add).then_inc(F.mark("biased"), 1)
        dve.wait_ge(F.sem, F.at("biased"))
        dve.tensor_reduce(mean[:], y[:], X, ALU.add).then_inc(F.mark("sum"), 1)
        dve.wait_ge(F.sem, F.at("sum"))
        dve.tensor_scalar(mean[:], mean[:], 1.0 / DIM, None, ALU.mult).then_inc(F.mark("mean2"), 1)
        dve.wait_ge(F.sem, F.at("mean2"))
        dve.tensor_tensor(y[:], y[:], cols(mean[:].unsqueeze(2), DIM), ALU.subtract).then_inc(F.mark("cent"), 1)
        dve.wait_ge(F.sem, F.at("cent"))
        dve.tensor_tensor(t[:], y[:], y[:], ALU.mult).then_inc(F.mark("sq2"), 1)
        dve.wait_ge(F.sem, F.at("sq2"))
        dve.tensor_reduce(var[:], t[:], X, ALU.add).then_inc(F.mark("ss2"), 1)
        dve.wait_ge(act_f.sem, act_f.at("std2"))
        dve.reciprocal(mean[:], tmp[:]).then_inc(F.mark("recip2"), 1)
        dve.wait_ge(F.sem, F.at("recip2"))
        dve.tensor_tensor(y[:], y[:], cols(mean[:].unsqueeze(2), DIM), ALU.mult).then_inc(F.mark("norm2"), 1)
        dve.wait_ge(F.sem, F.at("norm2"))
        dve.tensor_tensor(y[:], y[:], g2[:].unsqueeze(1).broadcast_to([128, NI, DIM]), ALU.mult).then_inc(F.mark("gain2"), 1)
        dve.wait_ge(F.sem, F.at("gain2"))
        dve.tensor_tensor(y[:], y[:], b2[:].unsqueeze(1).broadcast_to([128, NI, DIM]), ALU.add).then_inc(F.mark("shift2"), 1)
        dve.wait_ge(placed, 16 * 12)
        dve.wait_ge(consts, 16 * 10)
        dve.tensor_tensor(m.vit_x[:], m.vit_x[:], m.pos_tile[:].unsqueeze(1).broadcast_to([128, 16, DIM]), ALU.add).then_inc(F.mark("pos_added"), 1)
        phase_end(m, dve, ph)

    def gpsimd(pool):
        phase_end(m, pool, ph)

    return dict(sync=sync, tensor=tensor, scalar=scalar, vector=vector, gpsimd=gpsimd)


def vit_phase(nc, m, st, ph):
    G, R, H, DH, MLP, DEPTH = 16, 32, 4, 64, 128, 4
    sb = lambda n, s, d=F32: st.enter_context(nc.sbuf_tensor(n, s, d))
    wqkv, wo, w1, w2 = sb("wqkv", [C, 3 * H * DH]), sb("wo_h", [DH, H, C]), sb("w1_v", [C, MLP]), sb("w2_v", [MLP, C])
    ag, ab, fg, fb = (sb(n, [C, 1]) for n in ("attn_g", "attn_b", "ff_g", "ff_b"))
    b1 = sb("b1_col", [MLP, 1])
    bo, b2 = sb("bo_rows", [128, C]), sb("b2_rows", [128, C])
    lfg, lfb = sb("ln_f_g_rows", [128, C]), sb("ln_f_b_rows", [128, C])
    wT = sb("wqkv_t", [DH, 3 * H, C])
    wqk = sb("wq_wk", [C, H, C])
    wvo = sb("wv_wo", [C, H * C])
    cent, sq, xh = sb("v_cent", [128, G, C]), sb("v_sq", [128, G, C]), sb("v_xh", [128, G, C])
    mean, ss, rstd = sb("v_mean", [128, G]), sb("v_ss", [128, G]), sb("v_rstd", [128, G])
    eps = sb("v_eps", [128, 1])
    hT = sb("v_ht", [C, G * 4, R])
    tT = sb("v_tt", [C, H, G * 4, R])
    vv = sb("v_vv", [128, G, H * C])
    sc, ex = sb("v_scores", [128, G * H, NTOK]), sb("v_exp", [128, G * H, NTOK])
    mx, rs = sb("v_max", [128, G * H]), sb("v_rs", [128, G * H])
    pr = sb("v_probs", [128, G * H, R])
    prT = sb("v_probs_t", [128, G * H, R])
    pd = sb("v_probs_diag", [128, G * H, 4 * R])
    gl = sb("v_gelu", [MLP, G * 4, R])
    ps = m.psum
    X4 = m.vit_x
    fin_landed = m.whole.enter_context(nc.semaphore("vit_final_landed"))
    stored = m.whole.enter_context(nc.semaphore("vit_stored"))
    NW = 11
    wts = Landed(nc, m.whole, "vit_weights_landed", NW)
    pe_s = Steps(nc, m.whole, "vit_pe", ["w_turned", "combined", "h_turned"] + [f"t_proj{q}" for q in range(4)]
                 + ["v_proj0", "v_proj1"] + [f"scores{q}" for q in range(4)] + ["attended", "f_turned", "mlp1", "mlp2"])
    act_s = Steps(nc, m.whole, "vit_act", ["w_copied", "wqk_copied", "wvo_copied", "std_a"] + [f"ha{q}" for q in range(4)]
                  + ["t0", "t2", "v0", "v1"] + [f"sc{q}{j}" for q in range(4) for j in range(2)] + ["exp", "std_f"]
                  + [f"hf{q}" for q in range(4)] + ["gelu"])
    ln = lambda k: [f"{k}_{n}" for n in ("sum", "mean", "cent", "sq", "ss", "recip", "xh")]
    dve_s = Steps(nc, m.whole, "vit_dve", ln("a") + ["t1", "t3"] + [f"sc{q}{j}" for q in range(4) for j in (2, 3)]
                  + ["max", "minus", "rsum", "rrecip", "probs", "probs_t", "diag0", "diag1", "x_attn", "x_bo"] + ln("f") + ["x_mlp", "x_b2"])
    pool_s = Steps(nc, m.whole, "vit_pool", ["diag2", "diag3"])
    dve_c = Steps(nc, m.whole, "vit_dve_c", ["clear"])
    dve_f = Steps(nc, m.whole, "vit_dve_f", ln("z") + ["gain", "shift"])
    act_f = Steps(nc, m.whole, "vit_act_f", ["std_z"])

    def sync(sp):
        sp.dma_start(lfg[:], m.dram["tok_ln_f_g"].partition_broadcast(128)).then_inc(fin_landed, 16)
        sp.dma_start(lfb[:], m.dram["tok_ln_f_b"].partition_broadcast(128)).then_inc(fin_landed, 16)
        wts.start(sp)
        with sp.Fori(0, DEPTH) as i:
            sp.wait_ge(dve_s.sem, dve_s.before("x_b2", i))
            sp.sem_inc(m.gate, 1)
            at = bass.ds(i, 1)
            sp.dma_start(wqkv[:], m.dram["tok_Wqkv"][at].rearrange("l c n -> c (l n)")).then_inc(wts.sem, 16)
            sp.dma_start(wo[:], m.dram["tok_Wo"][at].rearrange("l (h d) o -> d (l h) o", h=H)).then_inc(wts.sem, 16)
            sp.dma_start(w1[:], m.dram["tok_W1"][at].rearrange("l c n -> c (l n)")).then_inc(wts.sem, 16)
            sp.dma_start(w2[:], m.dram["tok_W2"][at].rearrange("l c n -> c (l n)")).then_inc(wts.sem, 16)
            for dst, src in ((ag, m.dram["tok_attn_ln_g"]), (ab, m.dram["tok_attn_ln_b"]), (fg, m.dram["tok_ff_ln_g"]), (fb, m.dram["tok_ff_ln_b"]), (b1, m.dram["tok_b1"])):
                sp.dma_start(dst[:], src[at].rearrange("l c -> c l")).then_inc(wts.sem, 16)
            for dst, src in ((bo, m.dram["tok_bo"]), (b2, m.dram["tok_b2"])):
                sp.dma_start(dst[:], src[at].rearrange("l c -> (l c)").partition_broadcast(128)).then_inc(wts.sem, 16)
        sp.wait_ge(dve_f.sem, dve_f.at("shift"))
        for j in range(4):
            sp.dma_start(m.dram["h_d"].rearrange("(g j t) c -> j t g c", j=4, t=T)[j, 0:NTOK], xh[32 * j:32 * j + NTOK]).then_inc(stored, 16)
        sp.wait_ge(stored, 16 * 4)
        phase_end(m, sp, ph)

    def tensor(pe):
        pe_s.start(pe)
        banks = lambda s: range(4 * s, 4 * s + 4)
        with pe.Fori(0, DEPTH) as i:
            pe.wait_ge(wts.sem, wts.at(i))
            pe.wait_ge(dve_s.sem, dve_s.before("x_mlp", i))
            pe.wait_ge(act_s.sem, act_s.before("gelu", i))
            pe.sem_inc(m.gate, 1)
            for k in range(3 * H):
                mm = pe.transpose(ps[0:DH, k // 8, k % 8 * C:(k % 8 + 1) * C], wqkv[:, k * DH:(k + 1) * DH], m.ident[0:C, 0:C])
            mm.then_inc(pe_s.mark("w_turned"), 1)
            pe.wait_ge(act_s.sem, act_s.at("w_copied", i))
            pe.sem_inc(m.gate, 1)
            for h in range(H):
                pe.matmul(ps[0:C, 2, h * C:(h + 1) * C], wT[:, h, :], wT[:, H + h, :], start=True, stop=True)
                mm = pe.matmul(ps[0:C, 3, h * C:(h + 1) * C], wT[:, 2 * H + h, :], wo[:, h, :], start=True, stop=True)
            mm.then_inc(pe_s.mark("combined"), 1)
            pe.wait_ge(dve_s.sem, dve_s.at("a_xh", i))
            pe.sem_inc(m.gate, 1)
            for g in range(G):
                mm = pe.transpose(ps[0:C, 4 + g // 4, g % 4 * 128:(g % 4 + 1) * 128], xh[:, g, :], m.ident[:])
            mm.then_inc(pe_s.mark("h_turned"), 1)
            for q in range(4):
                if q == 0:
                    pe.wait_ge(act_s.sem, act_s.at("wvo_copied", i))
                    pe.wait_ge(act_s.sem, act_s.at("ha3", i))
                elif q == 2:
                    pe.wait_ge(act_s.sem, act_s.at("t0", i))
                elif q == 3:
                    pe.wait_ge(dve_s.sem, dve_s.at("t1", i))
                pe.sem_inc(m.gate, 1)
                for h in range(H):
                    mm = pe.matmul(ps[0:C, 4 * (q % 2) + h, 0:16 * NTOK], wqk[:, h, :], hT[:, 16 * q:16 * q + 16, 0:NTOK], start=True, stop=True)
                mm.then_inc(pe_s.mark(f"t_proj{q}"), 1)
            for q in range(2):
                if q == 0:
                    pe.wait_ge(act_s.sem, act_s.at("t2", i))
                else:
                    pe.wait_ge(dve_s.sem, dve_s.at("t3", i))
                pe.sem_inc(m.gate, 1)
                for k in range(8):
                    g = 8 * q + k
                    mm = pe.matmul(ps[:, 4 * q + k // 2, k % 2 * 256:k % 2 * 256 + 256], hT[:, 4 * g:4 * g + 4, :].rearrange("c b r -> c (b r)"), wvo[:], start=True, stop=True)
                mm.then_inc(pe_s.mark(f"v_proj{q}"), 1)
            for q in range(4):
                if q < 2:
                    pe.wait_ge(act_s.sem, act_s.at(f"v{q}", i))
                else:
                    pe.wait_ge(act_s.sem, act_s.at(f"sc{q - 2}1", i))
                    pe.wait_ge(dve_s.sem, dve_s.at(f"sc{q - 2}3", i))
                pe.sem_inc(m.gate, 1)
                for k in range(4):
                    g = 4 * q + k
                    for h in range(H):
                        mm = pe.matmul(ps[:, 4 * (q % 2) + k, h * 68:(h + 1) * 68], tT[:, h, 4 * g:4 * g + 4, :].rearrange("c b r -> c (b r)"),
                                       hT[:, 4 * g:4 * g + 4, 0:NTOK], start=True, stop=True)
                mm.then_inc(pe_s.mark(f"scores{q}"), 1)
            pe.wait_ge(dve_s.sem, dve_s.at("diag1", i))
            pe.wait_ge(pool_s.sem, pool_s.at("diag3", i))
            pe.sem_inc(m.gate, 1)
            for g in range(G):
                for h in range(H):
                    mm = pe.matmul(ps[:, g // 8, g % 8 * C:(g % 8 + 1) * C], pd[:, g * H + h, :], vv[:, g, h * C:(h + 1) * C], start=h == 0, stop=h == H - 1)
            mm.then_inc(pe_s.mark("attended"), 1)
            pe.wait_ge(dve_s.sem, dve_s.at("f_xh", i))
            pe.sem_inc(m.gate, 1)
            for g in range(G):
                mm = pe.transpose(ps[0:C, 4 + g // 4, g % 4 * 128:(g % 4 + 1) * 128], xh[:, g, :], m.ident[:])
            mm.then_inc(pe_s.mark("f_turned"), 1)
            pe.wait_ge(act_s.sem, act_s.at("hf3", i))
            pe.sem_inc(m.gate, 1)
            for q in range(4):
                mm = pe.matmul(ps[:, q, 0:16 * NTOK], w1[:], hT[:, 16 * q:16 * q + 16, 0:NTOK], start=True, stop=True)
            mm.then_inc(pe_s.mark("mlp1"), 1)
            pe.wait_ge(act_s.sem, act_s.at("gelu", i))
            pe.sem_inc(m.gate, 1)
            for g in range(G):
                mm = pe.matmul(ps[:, 4 + g // 8, g % 8 * C:(g % 8 + 1) * C], gl[:, 4 * g:4 * g + 4, :].rearrange("c b r -> c (b r)"), w2[:], start=True, stop=True)
            mm.then_inc(pe_s.mark("mlp2"), 1)
        phase_end(m, pe, ph)

    def scalar(act):
        act_s.start(act)
        act_f.start(act)
        act.wait_ge(dve_c.sem, dve_c.at("clear"))
        with act.Fori(0, DEPTH) as i:
            act.wait_ge(wts.sem, wts.at(i))
            act.wait_ge(pe_s.sem, pe_s.at("w_turned", i))
            act.activation(wT[:, 0:8, :], ps[0:DH, 0, :].rearrange("c (k o) -> c k o", o=C), ACT.Copy)
            act.activation(wT[:, 8:12, :], ps[0:DH, 1, 0:256].rearrange("c (k o) -> c k o", o=C), ACT.Copy).then_inc(act_s.mark("w_copied"), 1)
            act.wait_ge(pe_s.sem, pe_s.at("combined", i))
            act.activation(wqk[:].rearrange("c h o -> c (h o)"), ps[0:C, 2, 0:H * C], ACT.Copy, scale=DH ** -0.5).then_inc(act_s.mark("wqk_copied"), 1)
            act.activation(wvo[:], ps[0:C, 3, 0:H * C], ACT.Copy).then_inc(act_s.mark("wvo_copied"), 1)
            act.wait_ge(dve_s.sem, dve_s.at("a_ss", i))
            act.activation(rstd[:], ss[:], ACT.Sqrt, bias=eps[:], scale=1.0 / C).then_inc(act_s.mark("std_a"), 1)
            act.wait_ge(pe_s.sem, pe_s.at("h_turned", i))
            for q in range(4):
                act.activation(hT[:, 16 * q:16 * q + 16, :].rearrange("c b r -> c (b r)"), ps[0:C, 4 + q, :], ACT.Identity,
                               bias=ab[:], scale=ag[:]).then_inc(act_s.mark(f"ha{q}"), 1)
            for q in (0, 2):
                act.wait_ge(pe_s.sem, pe_s.at(f"t_proj{q}", i))
                act.activation(tT[:, :, 16 * q:16 * q + 16, 0:NTOK], ps[0:C, 0:4, 0:16 * NTOK].rearrange("c h (b r) -> c h b r", b=16),
                               ACT.Copy).then_inc(act_s.mark(f"t{q}"), 1)
            for q in range(2):
                act.wait_ge(pe_s.sem, pe_s.at(f"v_proj{q}", i))
                act.activation(vv[:, 8 * q:8 * q + 8, :].rearrange("p g n -> p (g n)"), ps[:, 4 * q:4 * q + 4, :].rearrange("p b n -> p (b n)"),
                               ACT.Copy).then_inc(act_s.mark(f"v{q}"), 1)
            for q in range(4):
                act.wait_ge(pe_s.sem, pe_s.at(f"scores{q}", i))
                for j in range(2):
                    act.activation(sc[32 * j:32 * j + 32, 16 * q:16 * q + 16, :].rearrange("p (g h) n -> p g h n", g=4),
                                   ps[32 * j:32 * j + 32, 4 * (q % 2):4 * (q % 2) + 4, 0:4 * 68].rearrange("p g (h n) -> p g h n", h=4)[:, :, :, NTOK * j:NTOK * j + NTOK],
                                   ACT.Copy).then_inc(act_s.mark(f"sc{q}{j}"), 1)
            act.wait_ge(dve_s.sem, dve_s.at("minus", i))
            act.activation(ex[:], sc[:], ACT.Exp).then_inc(act_s.mark("exp"), 1)
            act.wait_ge(dve_s.sem, dve_s.at("f_ss", i))
            act.activation(rstd[:], ss[:], ACT.Sqrt, bias=eps[:], scale=1.0 / C).then_inc(act_s.mark("std_f"), 1)
            act.wait_ge(pe_s.sem, pe_s.at("f_turned", i))
            for q in range(4):
                act.activation(hT[:, 16 * q:16 * q + 16, :].rearrange("c b r -> c (b r)"), ps[0:C, 4 + q, :], ACT.Identity,
                               bias=fb[:], scale=fg[:]).then_inc(act_s.mark(f"hf{q}"), 1)
            act.wait_ge(pe_s.sem, pe_s.at("mlp1", i))
            act.activation(gl[:, :, 0:NTOK].rearrange("p (q b) r -> p q b r", q=4), ps[:, 0:4, 0:16 * NTOK].rearrange("p q (b r) -> p q b r", b=16),
                           ACT.Gelu, bias=b1[:]).then_inc(act_s.mark("gelu"), 1)
        act.wait_ge(dve_f.sem, dve_f.at("z_ss"))
        act.activation(rstd[:], ss[:], ACT.Sqrt, bias=eps[:], scale=1.0 / C).then_inc(act_f.mark("std_z"), 1)
        phase_end(m, act, ph)

    def norm(dve, S, k, i, std_sem, std_at):
        wide = lambda v: cols(v[:].unsqueeze(2), C)
        dve.tensor_reduce(mean[:], X4[:], X, ALU.add).then_inc(S.mark(f"{k}_sum"), 1)
        dve.wait_ge(S.sem, S.at(f"{k}_sum", i))
        dve.tensor_scalar(mean[:], mean[:], 1.0 / C, None, ALU.mult).then_inc(S.mark(f"{k}_mean"), 1)
        dve.wait_ge(S.sem, S.at(f"{k}_mean", i))
        dve.tensor_tensor(cent[:], X4[:], wide(mean), ALU.subtract).then_inc(S.mark(f"{k}_cent"), 1)
        dve.wait_ge(S.sem, S.at(f"{k}_cent", i))
        dve.tensor_tensor(sq[:], cent[:], cent[:], ALU.mult).then_inc(S.mark(f"{k}_sq"), 1)
        dve.wait_ge(S.sem, S.at(f"{k}_sq", i))
        dve.tensor_reduce(ss[:], sq[:], X, ALU.add).then_inc(S.mark(f"{k}_ss"), 1)
        dve.wait_ge(std_sem, std_at)
        dve.reciprocal(mean[:], rstd[:]).then_inc(S.mark(f"{k}_recip"), 1)
        dve.wait_ge(S.sem, S.at(f"{k}_recip", i))
        dve.tensor_tensor(xh[:], cent[:], wide(mean), ALU.mult).then_inc(S.mark(f"{k}_xh"), 1)

    def vector(dve):
        dve_c.start(dve)
        dve_s.start(dve)
        dve_f.start(dve)
        dve.memset(eps[:], EPS)
        for z in (tT, pr, pd, gl):
            ins = dve.memset(z[:], 0.0)
        ins.then_inc(dve_c.mark("clear"), 1)
        dve.wait_ge(dve_c.sem, dve_c.at("clear"))
        S = dve_s
        with dve.Fori(0, DEPTH) as i:
            dve.wait_ge(S.sem, S.before("x_b2", i))
            norm(dve, S, "a", i, act_s.sem, act_s.at("std_a", i))
            for q in (1, 3):
                dve.wait_ge(pe_s.sem, pe_s.at(f"t_proj{q}", i))
                dve.tensor_copy(tT[:, :, 16 * q:16 * q + 16, 0:NTOK], ps[0:C, 4:8, 0:16 * NTOK].rearrange("c h (b r) -> c h b r", b=16)
                                ).then_inc(S.mark(f"t{q}"), 1)
            for q in range(4):
                dve.wait_ge(pe_s.sem, pe_s.at(f"scores{q}", i))
                for j in (2, 3):
                    dve.tensor_copy(sc[32 * j:32 * j + 32, 16 * q:16 * q + 16, :].rearrange("p (g h) n -> p g h n", g=4),
                                    ps[32 * j:32 * j + 32, 4 * (q % 2):4 * (q % 2) + 4, 0:4 * 68].rearrange("p g (h n) -> p g h n", h=4)[:, :, :, NTOK * j:NTOK * j + NTOK]
                                    ).then_inc(S.mark(f"sc{q}{j}"), 1)
            dve.wait_ge(act_s.sem, act_s.at("sc31", i))
            dve.wait_ge(S.sem, S.at("sc33", i))
            dve.tensor_reduce(mx[:], sc[:], X, ALU.max).then_inc(S.mark("max"), 1)
            dve.wait_ge(S.sem, S.at("max", i))
            dve.tensor_tensor(sc[:], sc[:], cols(mx[:].unsqueeze(2), NTOK), ALU.subtract).then_inc(S.mark("minus"), 1)
            dve.wait_ge(act_s.sem, act_s.at("exp", i))
            dve.tensor_reduce(rs[:], ex[:], X, ALU.add).then_inc(S.mark("rsum"), 1)
            dve.wait_ge(S.sem, S.at("rsum", i))
            dve.reciprocal(mx[:], rs[:]).then_inc(S.mark("rrecip"), 1)
            dve.wait_ge(S.sem, S.at("rrecip", i))
            dve.tensor_tensor(pr[:, :, 0:NTOK], ex[:], cols(mx[:].unsqueeze(2), NTOK), ALU.mult).then_inc(S.mark("probs"), 1)
            dve.wait_ge(S.sem, S.at("probs", i))
            dve.wait_ge(pool_s.sem, pool_s.before("diag3", i))
            dve.transpose(prT[:].rearrange("p k r -> p (k r)"), pr[:].rearrange("p k r -> p (k r)")).then_inc(S.mark("probs_t"), 1)
            dve.wait_ge(S.sem, S.at("probs_t", i))
            for j in range(2):
                dve.tensor_copy(pd[32 * j:32 * j + 32, :, 32 * j:32 * j + NTOK], prT[32 * j:32 * j + 32, :, 0:NTOK]).then_inc(S.mark(f"diag{j}"), 1)
            dve.wait_ge(pe_s.sem, pe_s.at("attended", i))
            dve.tensor_tensor(X4[:].rearrange("p g c -> p (g c)"), ps[:, 0:2, :].rearrange("p b n -> p (b n)"), X4[:].rearrange("p g c -> p (g c)"), ALU.add).then_inc(S.mark("x_attn"), 1)
            dve.wait_ge(wts.sem, wts.at(i))
            dve.wait_ge(S.sem, S.at("x_attn", i))
            dve.tensor_tensor(X4[:], X4[:], bo[:].unsqueeze(1).broadcast_to([128, G, C]), ALU.add).then_inc(S.mark("x_bo"), 1)
            dve.wait_ge(S.sem, S.at("x_bo", i))
            norm(dve, S, "f", i, act_s.sem, act_s.at("std_f", i))
            dve.wait_ge(pe_s.sem, pe_s.at("mlp2", i))
            dve.tensor_tensor(X4[:].rearrange("p g c -> p (g c)"), ps[:, 4:6, :].rearrange("p b n -> p (b n)"), X4[:].rearrange("p g c -> p (g c)"), ALU.add).then_inc(S.mark("x_mlp"), 1)
            dve.wait_ge(S.sem, S.at("x_mlp", i))
            dve.tensor_tensor(X4[:], X4[:], b2[:].unsqueeze(1).broadcast_to([128, G, C]), ALU.add).then_inc(S.mark("x_b2"), 1)
        dve.wait_ge(S.sem, S.at("x_b2", DEPTH - 1))
        norm(dve, dve_f, "z", 0, act_f.sem, act_f.at("std_z"))
        dve.wait_ge(fin_landed, 32)
        dve.wait_ge(dve_f.sem, dve_f.at("z_xh"))
        dve.tensor_tensor(xh[:], xh[:], lfg[:].unsqueeze(1).broadcast_to([128, G, C]), ALU.mult).then_inc(dve_f.mark("gain"), 1)
        dve.wait_ge(dve_f.sem, dve_f.at("gain"))
        dve.tensor_tensor(xh[:], xh[:], lfb[:].unsqueeze(1).broadcast_to([128, G, C]), ALU.add).then_inc(dve_f.mark("shift"), 1)
        phase_end(m, dve, ph)

    def gpsimd(pool):
        pool_s.start(pool)
        with pool.Fori(0, DEPTH) as i:
            pool.wait_ge(dve_s.sem, dve_s.at("probs_t", i))
            pool.sem_inc(m.gate, 1)
            for j in (2, 3):
                pool.tensor_copy(pd[32 * j:32 * j + 32, :, 32 * j:32 * j + NTOK], prT[32 * j:32 * j + 32, :, 0:NTOK]).then_inc(pool_s.mark(f"diag{j}"), 1)
        phase_end(m, pool, ph)

    return dict(sync=sync, tensor=tensor, scalar=scalar, vector=vector, gpsimd=gpsimd)


def text_phase(nc, m, st, ph):
    D, V, CH, NCH, WIN, HID, ROUNDS = 128, 64, 8, 16, 4, 256, 3
    CP = CH // 2
    K = NB * NCH
    KT = K // 128
    sb = lambda n, s, d=F32: st.enter_context(nc.sbuf_tensor(n, s, d))
    w = {n: sb(f"x_{n}", s) for n, s in {
        "h0": [128, CP, D], "pos": [128, CP, D], "lln_g": [D, 1], "lln_b": [D, 1], "lw1": [D, HID], "lb1": [D, 2], "lw2": [D, 2, D],
        "lb2": [128, D], "pool_w": [D, D], "pool_b": [D, 1], "msg_w1": [D, 2, D], "msg_b1": [D, 1], "msg_w2": [D, D], "msg_b2": [D, 1],
        "upd_w1": [D, 2, D], "upd_b1": [D, 1], "upd_w2": [D, D], "upd_b2": [D, 1], "mln_g": [D, 1], "mln_b": [D, 1],
        "bc_w": [D, D], "bc_b": [128, D], "fln_g": [D, 1], "fln_b": [D, 1], "head_w": [D, V], "inv_count": [128, NCH],
        "id_col": [128, 1], "id_row": [128, V]}.items()}
    tok = sb("x_tok", [128, K * CH], I32)
    tokr, tokf = sb("x_tok_rows", [128, KT, CH], I32), sb("x_tok_rows_f", [128, KT, CH])
    hot = sb("x_hot", [128, CP, K])
    local, xh0, sq0 = sb("x_local", [128, CP, D]), sb("x_xh0", [128, CP, D]), sb("x_sq0", [128, CP, D])
    st4, st4b, eps = sb("x_st4", [128, CP]), sb("x_st4b", [128, CP]), sb("x_eps", [128, 1])
    hT0, gl0 = sb("x_ht0", [D, CP * 128]), sb("x_gl0", [D, 2, CP * 128])
    pooled = sb("x_pooled", [128, CP, D])
    hm = sb("x_hm", [D, NB, NCH])
    a, b = sb("x_a", [D, NB, NCH]), sb("x_b", [D, NB, NCH])
    z = [sb(f"x_z{d}", [D, NB, NCH]) for d in range(WIN + 1)]
    agg, u = sb("x_agg", [D, K]), sb("x_u", [D, K])
    r, cent, sq, xh = sb("x_r", [D, K]), sb("x_cent", [128, KT, D]), sb("x_sq", [128, KT, D]), sb("x_xh", [128, KT, D])
    mean, ss, std = sb("x_mean", [128, KT]), sb("x_ss", [128, KT]), sb("x_std", [128, KT])
    ltT, ltT2, ltsq = sb("x_ltt", [D, CP * 128]), sb("x_ltt2", [D, CP * 128]), sb("x_ltsq", [D, CP * 128])
    bcT = sb("x_bct", [D, KT, 128])
    hwg = sb("x_hwg", [D, V])
    th = sb("x_th", [128, CP, 2, V])
    ones, fb = sb("x_ones", [D, 128]), sb("x_fb", [D, 128])
    lb = sb("x_lb", [128, V])
    hotr = [sb(f"x_hotr{k}", [128, CH, V]) for k in range(2)]
    pick = [sb(f"x_pick{k}", [128, CH, V]) for k in range(2)]
    var, dev, rstd = sb("x_var", [128, KT, CH]), sb("x_dev", [128, KT, CH]), sb("x_rstd", [128, KT, CH])
    lg = [sb(f"x_lg{k}", [128, CH, V]) for k in range(2)]
    ps = m.psum
    flat = lambda t: t[:].rearrange("d n c -> d (n c)")
    landed = m.whole.enter_context(nc.semaphore("text_landed"))
    stored = [m.whole.enter_context(nc.semaphore(f"text_stored{k}")) for k in range(2)]
    nload = 0

    tiles = range(KT)
    pe_c = Steps(nc, m.whole, "text_pe_setup", ["h0_turned", "mlp1", "mlp2", "local_turned", "pooled", "summ"])
    act_c = Steps(nc, m.whole, "text_act_setup", ["std0", "h0_copied", "gelu0", "gelu1", "local_copied", "pooled_copied", "summ_copied"])
    ln0 = ["sum", "mean", "cent", "sq", "ss", "recip", "xh"]
    dve_c = Steps(nc, m.whole, "text_dve_setup", ["eps", "h0"] + ln0 + ["hot0", "hot1", "local_h", "local"])
    pe_r = Steps(nc, m.whole, "text_pe_round", ["pre_a", "pre_b", "msg", "upd1", "upd2", "r_turned", "xh_turned"])
    act_r = Steps(nc, m.whole, "text_act_round", ["a"] + [f"gelu{d}" for d in range(WIN + 1)] + ["agg", "u", "std", "hm"])
    dve_r = Steps(nc, m.whole, "text_dve_round", ["b"] + [f"z{d}" for d in range(WIN + 1)] + [f"sum{d}" for d in range(1, WIN + 1)]
                  + ["scaled", "r"] + ["lsum", "mean", "cent", "sq", "ss", "recip", "xh"])
    pe_f = Steps(nc, m.whole, "text_pe_final", ["bc", "ltc_turned", "bcc_turned", "th", "lb"] + [f"var{t}" for t in tiles] + [f"logits{t}" for t in tiles])
    act_f = Steps(nc, m.whole, "text_act_final", ["ltt", "ltt2", "ltsq", "bct", "std"])
    dve_f = Steps(nc, m.whole, "text_dve_final", ["ones", "th_clear", "fb", "hwg", "tokf", "tsum", "tmean", "ltc", "bc", "bsum", "bmean", "bcc", "bsq", "bss", "th0", "th1", "lb"]
                  + [f"{n}{t}" for t in tiles for n in ("hotr", "pick", "var")] + ["var_all", "recip"]
                  + [f"{n}{t}" for t in tiles for n in ("scaled", "logits")])

    loads = []
    for c2 in range(2):
        rows = slice(64 * c2, 64 * c2 + 64)
        loads.append((w["h0"][rows], m.dram["txt_emb"].unsqueeze(1).broadcast_to([V, CP, D])))
        loads.append((w["pos"][rows], m.dram["txt_pos"].rearrange("(cp c2) d -> c2 cp d", c2=2)[c2].partition_broadcast(64)))
    col = lambda ap: ap.rearrange("(c o) -> c o", o=1)
    for n in ("lln_g", "lln_b", "pool_b", "msg_b1", "msg_b2", "upd_b1", "upd_b2", "mln_g", "mln_b", "fln_g", "fln_b"):
        loads.append((w[n][:], col(m.dram[f"txt_{n}"])))
    for n in ("lw1", "pool_w", "msg_w2", "upd_w2", "bc_w", "head_w"):
        loads.append((w[n][:], m.dram[f"txt_{n}"]))
    for n in ("msg_w1", "upd_w1", "lw2"):
        loads.append((w[n][:], m.dram[f"txt_{n}"].rearrange("(k c) o -> c k o", k=2)))
    for k in range(2):
        loads.append((w["lb1"][:, k:k + 1], col(m.dram["txt_lb1"][D * k:D * k + D])))
    for n, src in (("lb2", m.dram["txt_lb2"]), ("bc_b", m.dram["txt_bc_b"]), ("inv_count", m.dram["inv_count"]), ("id_row", m.dram["id_row"])):
        loads.append((w[n][:], src.partition_broadcast(128)))
    loads.append((w["id_col"][:], m.dram["id_col"]))

    def sync(sp):
        for dst, src in loads:
            sp.dma_start(dst, src).then_inc(landed, 16)
        for b8 in range(8):
            sp.dma_start(tokr[16 * b8:16 * b8 + 16], m.dram["x_txt"].rearrange("(t b) (i c) -> b i t c", b=8, c=CH)[b8]).then_inc(landed, 16)
        sp.dma_start(tok[:], m.dram["x_txt"].rearrange("b t -> (b t)").partition_broadcast(128)).then_inc(landed, 16)
        for t in tiles:
            sp.wait_ge(dve_f.sem, dve_f.at(f"logits{t}"))
            dst = m.dram["h_d"].rearrange("(b t) c -> b (t c)", t=T)[8 * t:8 * t + 8, NTOK * C:].rearrange("b (i n) -> b i n", i=NCH)
            sp.dma_start(dst, lg[t % 2][:].rearrange("p c v -> p (c v)")).then_inc(stored[t % 2], 16)
        for k in range(2):
            sp.wait_ge(stored[k], 16 * KT // 2)
        phase_end(m, sp, ph)
    all_landed = 16 * (len(loads) + 9)

    def tensor(pe):
        for s in (pe_c, pe_r, pe_f):
            s.start(pe)
        S = pe_c
        pe.wait_ge(landed, all_landed)
        pe.wait_ge(dve_c.sem, dve_c.at("xh"))
        for k in range(CP):
            mm = pe.transpose(ps[:, 0, 128 * k:128 * k + 128], xh0[:, k, :], m.ident[:])
        mm.then_inc(S.mark("h0_turned"), 1)
        pe.wait_ge(act_c.sem, act_c.at("h0_copied"))
        for k in range(2):
            mm = pe.matmul(ps[:, 1 + k, :], w["lw1"][:, k * D:(k + 1) * D], hT0[:], start=True, stop=True)
        mm.then_inc(S.mark("mlp1"), 1)
        pe.wait_ge(act_c.sem, act_c.at("gelu1"))
        for k in range(CP):
            for h in range(2):
                mm = pe.matmul(ps[:, 3, 128 * k:128 * k + 128], gl0[:, h, 128 * k:128 * k + 128], w["lw2"][:, h, :], start=h == 0, stop=h == 1)
        mm.then_inc(S.mark("mlp2"), 1)
        pe.wait_ge(dve_c.sem, dve_c.at("local"))
        for k in range(CP):
            mm = pe.transpose(ps[:, 0, 128 * k:128 * k + 128], local[:, k, :], m.ident[:])
        mm.then_inc(S.mark("local_turned"), 1)
        pe.wait_ge(act_c.sem, act_c.at("local_copied"))
        for k in range(CP):
            mm = pe.matmul(ps[:, 1, 128 * k:128 * k + 128], hT0[:, 128 * k:128 * k + 128], w["pool_w"][:], start=True, stop=True)
        mm.then_inc(S.mark("pooled"), 1)
        pe.wait_ge(act_c.sem, act_c.at("pooled_copied"))
        pe.wait_ge(dve_c.sem, dve_c.at("hot1"))
        for half in range(2):
            for k in range(CP):
                mm = pe.matmul(ps[:, 2 + half, :], pooled[:, k, :], hot[:, k, 512 * half:512 * half + 512], start=k == 0, stop=k == CP - 1)
        mm.then_inc(S.mark("summ"), 1)
        pe.wait_ge(act_c.sem, act_c.at("summ_copied"))
        S = pe_r
        with pe.Fori(0, ROUNDS) as i:
            pe.wait_ge(act_r.sem, act_r.before("hm", i))
            pe.sem_inc(m.gate, 1)
            for k, name in ((0, "pre_a"), (1, "pre_b")):
                for half in range(2):
                    mm = pe.matmul(ps[:, 2 * k + half, :], w["msg_w1"][:, k, :], flat(hm)[:, 512 * half:512 * half + 512], start=True, stop=True)
                mm.then_inc(S.mark(name), 1)
            pe.wait_ge(dve_r.sem, dve_r.at("scaled", i))
            pe.sem_inc(m.gate, 1)
            for half in range(2):
                mm = pe.matmul(ps[:, 4 + half, :], w["msg_w2"][:], flat(z[0])[:, 512 * half:512 * half + 512], start=True, stop=True)
            mm.then_inc(S.mark("msg"), 1)
            pe.wait_ge(act_r.sem, act_r.at("agg", i))
            pe.sem_inc(m.gate, 1)
            for half in range(2):
                c = slice(512 * half, 512 * half + 512)
                pe.matmul(ps[:, 6 + half, :], w["upd_w1"][:, 0, :], flat(hm)[:, c], start=True, stop=False)
                mm = pe.matmul(ps[:, 6 + half, :], w["upd_w1"][:, 1, :], agg[:, c], start=False, stop=True)
            mm.then_inc(S.mark("upd1"), 1)
            pe.wait_ge(act_r.sem, act_r.at("u", i))
            pe.sem_inc(m.gate, 1)
            for half in range(2):
                c = slice(512 * half, 512 * half + 512)
                mm = pe.matmul(ps[:, half, :], w["upd_w2"][:], u[:, c], start=True, stop=True)
            mm.then_inc(S.mark("upd2"), 1)
            pe.wait_ge(dve_r.sem, dve_r.at("r", i))
            pe.sem_inc(m.gate, 1)
            for t in tiles:
                mm = pe.transpose(ps[:, 2 + t // 4, t % 4 * 128:t % 4 * 128 + 128], r[:, 128 * t:128 * t + 128], m.ident[:])
            mm.then_inc(S.mark("r_turned"), 1)
            pe.wait_ge(dve_r.sem, dve_r.at("xh", i))
            pe.sem_inc(m.gate, 1)
            for t in tiles:
                mm = pe.transpose(ps[:, 4 + t // 4, t % 4 * 128:t % 4 * 128 + 128], xh[:, t, :], m.ident[:])
            mm.then_inc(S.mark("xh_turned"), 1)
        S = pe_f
        pe.wait_ge(act_r.sem, act_r.at("hm", ROUNDS - 1))
        for t in tiles:
            mm = pe.matmul(ps[:, t // 4, t % 4 * 128:t % 4 * 128 + 128], flat(hm)[:, 128 * t:128 * t + 128], w["bc_w"][:], start=True, stop=True)
        mm.then_inc(S.mark("bc"), 1)
        pe.wait_ge(dve_f.sem, dve_f.at("ltc"))
        for k in range(CP):
            mm = pe.transpose(ps[:, 4, 128 * k:128 * k + 128], xh0[:, k, :], m.ident[:])
        mm.then_inc(S.mark("ltc_turned"), 1)
        pe.wait_ge(dve_f.sem, dve_f.at("bcc"))
        for t in tiles:
            mm = pe.transpose(ps[:, 2 + t // 4, t % 4 * 128:t % 4 * 128 + 128], cent[:, t, :], m.ident[:])
        mm.then_inc(S.mark("bcc_turned"), 1)
        pe.wait_ge(act_f.sem, act_f.at("ltt"))
        pe.wait_ge(dve_f.sem, dve_f.at("hwg"))
        for k in range(CP):
            mm = pe.matmul(ps[:, 5, V * k:V * k + V], ltT[:, 128 * k:128 * k + 128], hwg[:], start=True, stop=True)
        mm.then_inc(S.mark("th"), 1)
        pe.matmul(ps[:, 6, 0:V], fb[:], w["head_w"][:], start=True, stop=True).then_inc(S.mark("lb"), 1)
        pe.wait_ge(act_f.sem, act_f.at("bct"))
        for t in tiles:
            if t >= 2:
                pe.wait_ge(dve_f.sem, dve_f.at(f"pick{t - 2}"))
            pe.matmul(ps[:, t % 2, :], bcT[:, t, :], ltT2[:], start=True, stop=False)
            pe.matmul(ps[:, t % 2, :], ones[:], ltsq[:], start=False, stop=True).then_inc(S.mark(f"var{t}"), 1)
        pe.wait_ge(dve_f.sem, dve_f.at("th1"))
        for t in tiles:
            if t >= 2:
                pe.wait_ge(dve_f.sem, dve_f.at(f"scaled{t - 2}"))
            pe.matmul(ps[:, 2 + t % 2, :], bcT[:, t, :], hwg[:].unsqueeze(1).broadcast_to([D, CH, V]), start=True, stop=False)
            for k in range(CP):
                mm = pe.matmul(ps[:, 2 + t % 2, 128 * k:128 * k + 128], hot[:, k, 128 * t:128 * t + 128], th[:, k].rearrange("p c v -> p (c v)"),
                               start=False, stop=k == CP - 1)
            mm.then_inc(S.mark(f"logits{t}"), 1)
        phase_end(m, pe, ph)

    def scalar(act):
        for s in (act_c, act_r, act_f):
            s.start(act)
        S = act_c
        act.wait_ge(landed, all_landed)
        act.wait_ge(dve_c.sem, dve_c.at("ss"))
        act.activation(st4b[:], st4[:], ACT.Sqrt, bias=eps[:], scale=1.0 / D).then_inc(S.mark("std0"), 1)
        act.wait_ge(pe_c.sem, pe_c.at("h0_turned"))
        act.activation(hT0[:], ps[:, 0, :], ACT.Identity, bias=w["lln_b"][:], scale=w["lln_g"][:]).then_inc(S.mark("h0_copied"), 1)
        act.wait_ge(pe_c.sem, pe_c.at("mlp1"))
        for k in range(2):
            act.activation(gl0[:, k, :], ps[:, 1 + k, :], ACT.Gelu, bias=w["lb1"][:, k:k + 1]).then_inc(S.mark(f"gelu{k}"), 1)
        act.wait_ge(pe_c.sem, pe_c.at("local_turned"))
        act.activation(hT0[:], ps[:, 0, :], ACT.Copy).then_inc(S.mark("local_copied"), 1)
        act.wait_ge(pe_c.sem, pe_c.at("pooled"))
        act.activation(pooled[:].rearrange("p k d -> p (k d)"), ps[:, 1, :], ACT.Copy, scale=1.0 / CH).then_inc(S.mark("pooled_copied"), 1)
        act.wait_ge(pe_c.sem, pe_c.at("summ"))
        act.activation(flat(hm), ps[:, 2:4, :].rearrange("p b n -> p (b n)"), ACT.Identity, bias=w["pool_b"][:]).then_inc(S.mark("summ_copied"), 1)
        S = act_r
        with act.Fori(0, ROUNDS) as i:
            act.wait_ge(pe_r.sem, pe_r.at("pre_a", i))
            act.activation(flat(a), ps[:, 0:2, :].rearrange("p b n -> p (b n)"), ACT.Identity, bias=w["msg_b1"][:]).then_inc(S.mark("a"), 1)
            for d in range(WIN + 1):
                act.wait_ge(dve_r.sem, dve_r.at(f"z{d}", i))
                act.activation(z[d][:, :, d:], z[d][:, :, d:], ACT.Gelu).then_inc(S.mark(f"gelu{d}"), 1)
            act.wait_ge(pe_r.sem, pe_r.at("msg", i))
            act.activation(agg[:], ps[:, 4:6, :].rearrange("p b n -> p (b n)"), ACT.Identity, bias=w["msg_b2"][:]).then_inc(S.mark("agg"), 1)
            act.wait_ge(pe_r.sem, pe_r.at("upd1", i))
            act.activation(u[:], ps[:, 6:8, :].rearrange("p b n -> p (b n)"), ACT.Gelu, bias=w["upd_b1"][:]).then_inc(S.mark("u"), 1)
            act.wait_ge(dve_r.sem, dve_r.at("ss", i))
            act.activation(std[:], ss[:], ACT.Sqrt, bias=eps[:], scale=1.0 / D).then_inc(S.mark("std"), 1)
            act.wait_ge(pe_r.sem, pe_r.at("xh_turned", i))
            act.activation(flat(hm), ps[:, 4:6, :].rearrange("p b n -> p (b n)"), ACT.Identity, bias=w["mln_b"][:], scale=w["mln_g"][:]).then_inc(S.mark("hm"), 1)
        S = act_f
        act.wait_ge(pe_f.sem, pe_f.at("ltc_turned"))
        act.activation(ltT[:], ps[:, 4, :], ACT.Copy).then_inc(S.mark("ltt"), 1)
        act.activation(ltT2[:], ps[:, 4, :], ACT.Copy, scale=2.0).then_inc(S.mark("ltt2"), 1)
        act.activation(ltsq[:], ps[:, 4, :], ACT.Square).then_inc(S.mark("ltsq"), 1)
        act.wait_ge(pe_f.sem, pe_f.at("bcc_turned"))
        act.activation(flat(bcT), ps[:, 2:4, :].rearrange("p b n -> p (b n)"), ACT.Copy).then_inc(S.mark("bct"), 1)
        act.wait_ge(dve_f.sem, dve_f.at("var_all"))
        act.activation(dev[:], var[:], ACT.Sqrt, bias=eps[:], scale=1.0 / D).then_inc(S.mark("std"), 1)
        phase_end(m, act, ph)

    def vector(dve):
        for s in (dve_c, dve_r, dve_f):
            s.start(dve)
        S = dve_c
        wide = lambda v, n=D: cols(v.unsqueeze(2), n)
        dve.memset(eps[:], EPS).then_inc(S.mark("eps"), 1)
        dve.wait_ge(landed, all_landed)
        dve.tensor_tensor(w["h0"][:], w["h0"][:], w["pos"][:], ALU.add).then_inc(S.mark("h0"), 1)
        dve.wait_ge(S.sem, S.at("h0"))
        dve.tensor_reduce(st4[:], w["h0"][:], X, ALU.add).then_inc(S.mark("sum"), 1)
        dve.wait_ge(S.sem, S.at("sum"))
        dve.tensor_scalar(st4b[:], st4[:], 1.0 / D, None, ALU.mult).then_inc(S.mark("mean"), 1)
        dve.wait_ge(S.sem, S.at("mean"))
        dve.tensor_tensor(xh0[:], w["h0"][:], wide(st4b[:]), ALU.subtract).then_inc(S.mark("cent"), 1)
        dve.wait_ge(S.sem, S.at("cent"))
        dve.tensor_tensor(sq0[:], xh0[:], xh0[:], ALU.mult).then_inc(S.mark("sq"), 1)
        dve.wait_ge(S.sem, S.at("sq"))
        dve.tensor_reduce(st4[:], sq0[:], X, ALU.add).then_inc(S.mark("ss"), 1)
        dve.wait_ge(act_c.sem, act_c.at("std0"))
        dve.reciprocal(st4[:], st4b[:]).then_inc(S.mark("recip"), 1)
        dve.wait_ge(S.sem, S.at("recip"))
        dve.tensor_tensor(xh0[:], xh0[:], wide(st4[:]), ALU.mult).then_inc(S.mark("xh"), 1)
        for c2 in range(2):
            rows = slice(64 * c2, 64 * c2 + 64)
            dve.tensor_scalar(hot[rows], tok[rows].rearrange("p (k cp c) -> p c cp k", cp=CP, c=2)[:, c2], w["id_col"][rows], None, ALU.is_equal
                              ).then_inc(S.mark(f"hot{c2}"), 1)
        dve.wait_ge(pe_c.sem, pe_c.at("mlp2"))
        dve.tensor_tensor(local[:].rearrange("p k d -> p (k d)"), ps[:, 3, :], w["h0"][:].rearrange("p k d -> p (k d)"), ALU.add).then_inc(S.mark("local_h"), 1)
        dve.wait_ge(S.sem, S.at("local_h"))
        dve.tensor_tensor(local[:], local[:], w["lb2"][:].unsqueeze(1).broadcast_to([128, CP, D]), ALU.add).then_inc(S.mark("local"), 1)
        S = dve_r
        with dve.Fori(0, ROUNDS) as i:
            dve.wait_ge(pe_r.sem, pe_r.at("pre_b", i))
            dve.tensor_copy(flat(b), ps[:, 2:4, :].rearrange("p b n -> p (b n)")).then_inc(S.mark("b"), 1)
            dve.wait_ge(act_r.sem, act_r.at("a", i))
            dve.wait_ge(S.sem, S.at("b", i))
            for d in range(WIN + 1):
                dve.tensor_tensor(z[d][:, :, d:], a[:, :, d:], b[:, :, 0:NCH - d], ALU.add).then_inc(S.mark(f"z{d}"), 1)
            for d in range(1, WIN + 1):
                dve.wait_ge(act_r.sem, act_r.at(f"gelu{d}", i))
                if d > 1:
                    dve.wait_ge(S.sem, S.at(f"sum{d - 1}", i))
                dve.tensor_tensor(z[0][:, :, d:], z[0][:, :, d:], z[d][:, :, d:], ALU.add).then_inc(S.mark(f"sum{d}"), 1)
            dve.wait_ge(S.sem, S.at(f"sum{WIN}", i))
            dve.tensor_tensor(z[0][:], z[0][:], w["inv_count"][:].unsqueeze(1).broadcast_to([D, NB, NCH]), ALU.mult).then_inc(S.mark("scaled"), 1)
            dve.wait_ge(pe_r.sem, pe_r.at("upd2", i))
            dve.scalar_tensor_tensor(out=r[:], in0=ps[:, 0:2, :].rearrange("p b n -> p (b n)"), scalar=w["upd_b2"][:], in1=flat(hm), op0=ALU.add, op1=ALU.add
                                     ).then_inc(S.mark("r"), 1)
            dve.wait_ge(pe_r.sem, pe_r.at("r_turned", i))
            rows = ps[:, 2:4, :].rearrange("p b (t d) -> p (b t) d", d=D)
            dve.tensor_reduce(ss[:], rows, X, ALU.add).then_inc(S.mark("lsum"), 1)
            dve.wait_ge(S.sem, S.at("lsum", i))
            dve.tensor_scalar(mean[:], ss[:], 1.0 / D, None, ALU.mult).then_inc(S.mark("mean"), 1)
            dve.wait_ge(S.sem, S.at("mean", i))
            dve.tensor_tensor(cent[:], rows, wide(mean[:]), ALU.subtract).then_inc(S.mark("cent"), 1)
            dve.wait_ge(S.sem, S.at("cent", i))
            dve.tensor_tensor(sq[:], cent[:], cent[:], ALU.mult).then_inc(S.mark("sq"), 1)
            dve.wait_ge(S.sem, S.at("sq", i))
            dve.tensor_reduce(ss[:], sq[:], X, ALU.add).then_inc(S.mark("ss"), 1)
            dve.wait_ge(act_r.sem, act_r.at("std", i))
            dve.reciprocal(mean[:], std[:]).then_inc(S.mark("recip"), 1)
            dve.wait_ge(S.sem, S.at("recip", i))
            dve.tensor_tensor(xh[:], cent[:], wide(mean[:]), ALU.mult).then_inc(S.mark("xh"), 1)
        S = dve_f
        dve.memset(ones[:], 1.0).then_inc(S.mark("ones"), 1)
        dve.memset(th[:], 0.0).then_inc(S.mark("th_clear"), 1)
        dve.tensor_copy(fb[:], w["fln_b"][:].broadcast_to([D, 128])).then_inc(S.mark("fb"), 1)
        dve.tensor_scalar(hwg[:], w["head_w"][:], w["fln_g"][:], None, ALU.mult).then_inc(S.mark("hwg"), 1)
        dve.tensor_copy(tokf[:], tokr[:]).then_inc(S.mark("tokf"), 1)
        dve.tensor_reduce(st4[:], local[:], X, ALU.add).then_inc(S.mark("tsum"), 1)
        dve.wait_ge(S.sem, S.at("tsum"))
        dve.tensor_scalar(st4b[:], st4[:], 1.0 / D, None, ALU.mult).then_inc(S.mark("tmean"), 1)
        dve.wait_ge(S.sem, S.at("tmean"))
        dve.tensor_tensor(xh0[:], local[:], wide(st4b[:]), ALU.subtract).then_inc(S.mark("ltc"), 1)
        dve.wait_ge(pe_f.sem, pe_f.at("bc"))
        dve.tensor_tensor(cent[:], ps[:, 0:2, :].rearrange("p b (t d) -> p (b t) d", d=D), w["bc_b"][:].unsqueeze(1).broadcast_to([128, KT, D]), ALU.add).then_inc(S.mark("bc"), 1)
        dve.wait_ge(S.sem, S.at("bc"))
        dve.tensor_reduce(ss[:], cent[:], X, ALU.add).then_inc(S.mark("bsum"), 1)
        dve.wait_ge(S.sem, S.at("bsum"))
        dve.tensor_scalar(mean[:], ss[:], 1.0 / D, None, ALU.mult).then_inc(S.mark("bmean"), 1)
        dve.wait_ge(S.sem, S.at("bmean"))
        dve.tensor_tensor(cent[:], cent[:], wide(mean[:]), ALU.subtract).then_inc(S.mark("bcc"), 1)
        dve.wait_ge(S.sem, S.at("bcc"))
        dve.tensor_tensor(sq[:], cent[:], cent[:], ALU.mult).then_inc(S.mark("bsq"), 1)
        dve.wait_ge(S.sem, S.at("bsq"))
        dve.tensor_reduce(ss[:], sq[:], X, ALU.add).then_inc(S.mark("bss"), 1)
        dve.wait_ge(pe_f.sem, pe_f.at("th"))
        for c2 in range(2):
            rows = slice(64 * c2, 64 * c2 + 64)
            dve.tensor_copy(th[rows, :, c2, :], ps[rows, 5, 0:CP * V].rearrange("p (k v) -> p k v", v=V)).then_inc(S.mark(f"th{c2}"), 1)
        dve.wait_ge(pe_f.sem, pe_f.at("lb"))
        dve.tensor_copy(lb[:], ps[:, 6, 0:V]).then_inc(S.mark("lb"), 1)
        for t in tiles:
            dve.tensor_tensor(hotr[t % 2][:], wide(tokf[:, t, :], V), w["id_row"][:].unsqueeze(1).broadcast_to([128, CH, V]), ALU.is_equal).then_inc(S.mark(f"hotr{t}"), 1)
            dve.wait_ge(pe_f.sem, pe_f.at(f"var{t}"))
            dve.wait_ge(S.sem, S.at(f"hotr{t}"))
            dve.tensor_tensor(pick[t % 2][:], ps[:, t % 2, :].rearrange("p (c v) -> p c v", v=V), hotr[t % 2][:], ALU.mult).then_inc(S.mark(f"pick{t}"), 1)
            dve.wait_ge(S.sem, S.at(f"pick{t}"))
            dve.tensor_reduce(var[:, t, :], pick[t % 2][:], X, ALU.add).then_inc(S.mark(f"var{t}"), 1)
        dve.wait_ge(S.sem, S.at(f"var{KT - 1}"))
        dve.tensor_tensor(var[:], var[:], wide(ss[:], CH), ALU.add).then_inc(S.mark("var_all"), 1)
        dve.wait_ge(act_f.sem, act_f.at("std"))
        dve.reciprocal(rstd[:], dev[:]).then_inc(S.mark("recip"), 1)
        dve.wait_ge(S.sem, S.at("recip"))
        for t in tiles:
            dve.wait_ge(pe_f.sem, pe_f.at(f"logits{t}"))
            if t >= 2:
                dve.wait_ge(stored[t % 2], 16 * (t // 2))
            dve.tensor_tensor(lg[t % 2][:], ps[:, 2 + t % 2, :].rearrange("p (c v) -> p c v", v=V), wide(rstd[:, t, :], V), ALU.mult).then_inc(S.mark(f"scaled{t}"), 1)
            dve.wait_ge(S.sem, S.at(f"scaled{t}"))
            dve.tensor_tensor(lg[t % 2][:], lg[t % 2][:], lb[:].unsqueeze(1).broadcast_to([128, CH, V]), ALU.add).then_inc(S.mark(f"logits{t}"), 1)
        phase_end(m, dve, ph)

    def gpsimd(pool):
        phase_end(m, pool, ph)

    return dict(sync=sync, tensor=tensor, scalar=scalar, vector=vector, gpsimd=gpsimd)


def token_norm(dve, S, i, act_s, pre, src, cent, sq, mean, ss):
    J = NB * T // TM
    wide = lambda v: cols(v[:].unsqueeze(2), C)
    dve.tensor_reduce(ss[:], src[:], X, ALU.add).then_inc(S.mark(f"{pre}_sum"), 1)
    dve.wait_ge(S.sem, S.at(f"{pre}_sum"))
    dve.tensor_scalar(mean[:], ss[:], 1.0 / C, None, ALU.mult).then_inc(S.mark(f"{pre}_mean"), 1)
    dve.wait_ge(S.sem, S.at(f"{pre}_mean"))
    for k in range(4):
        j = slice(J // 4 * k, J // 4 * (k + 1))
        dve.tensor_tensor(cent[:, j], src[:, j], cols(mean[:, j].unsqueeze(2), C), ALU.subtract).then_inc(S.mark(f"{pre}_cent{k}"), 1)
    for k in range(4):
        j = slice(J // 4 * k, J // 4 * (k + 1))
        dve.wait_ge(act_s.sem, act_s.at(f"{pre}_sq{k}"))
        dve.tensor_reduce(ss[:, j], sq[k % 2][:], X, ALU.add).then_inc(S.mark(f"{pre}_ss{k}"), 1)
    dve.wait_ge(act_s.sem, act_s.at(f"{pre}_std"))
    dve.reciprocal(ss[:], mean[:]).then_inc(S.mark(f"{pre}_recip"), 1)
    dve.wait_ge(S.sem, S.at(f"{pre}_recip"))


NORM_DVE = ["sum", "mean"] + [f"cent{k}" for k in range(4)] + [f"ss{k}" for k in range(4)] + ["recip"]
NORM_ACT = [f"sq{k}" for k in range(4)] + ["std"]


def token_norm_squares(act, S, dve_s, pre, cent, sq, mean, ss, eps, ready):
    J = NB * T // TM
    for k in range(4):
        j = slice(J // 4 * k, J // 4 * (k + 1))
        act.wait_ge(dve_s.sem, dve_s.at(ready.format(k=k)))
        if k >= 2:
            act.wait_ge(dve_s.sem, dve_s.at(f"{pre}_ss{k - 2}"))
        act.activation(sq[k % 2][:], cent[:, j], ACT.Square).then_inc(S.mark(f"{pre}_sq{k}"), 1)
    act.wait_ge(dve_s.sem, dve_s.at(f"{pre}_ss3"))
    act.activation(mean[:], ss[:], ACT.Sqrt, bias=eps[0:TM], scale=1.0 / C).then_inc(S.mark(f"{pre}_std"), 1)


def joint_in_phase(nc, m, st, ph):
    J = NB * T // TM
    sb = lambda n, s, d=F32: st.enter_context(nc.sbuf_tensor(n, s, d))
    cent = sb("ji_cent", [TM, J, C])
    sq = [sb(f"ji_sq{k}", [TM, J // 4, C]) for k in range(2)]
    mean, ss, eps = sb("ji_mean", [TM, J]), sb("ji_ss", [TM, J]), sb("ji_eps", [128, 1])
    wv, wvT = sb("ji_wv", [C, C]), sb("ji_wvt", [C, C])
    xh = [sb(f"ji_xh{s}", [TM, GJ, C]) for s in range(2)]
    xT = [sb(f"ji_xt{s}", [C, GT]) for s in range(2)]
    vT = [sb(f"ji_vt{s}", [C, GT]) for s in range(2)]
    ps = m.psum
    landed = m.whole.enter_context(nc.semaphore("ji_landed"))
    stored = [Landed(nc, m.whole, f"ji_stored{s}", 2) for s in range(2)]
    dve_n = Steps(nc, m.whole, "ji_dve_norm", ["eps"] + [f"n_{k}" for k in NORM_DVE] + ["wvt"])
    act_n = Steps(nc, m.whole, "ji_act_norm", [f"n_{k}" for k in NORM_ACT])
    pe_n = Steps(nc, m.whole, "ji_pe_w", ["wvt"])
    pe_s = Steps(nc, m.whole, "ji_pe", [f"{k}{s}" for s in range(2) for k in ("turned", "v")])
    act_s = Steps(nc, m.whole, "ji_act", ["xt0", "xt1"])
    dve_s = Steps(nc, m.whole, "ji_dve", [f"{k}{s}" for s in range(2) for k in ("xh", "vt")])
    P = NG // 2

    def sync(sp):
        for s in range(2):
            stored[s].start(sp)
        sp.dma_start(wv[:], m.dram["attn_Wv"]).then_inc(landed, 16)
        rows = m.dram["h_d"].rearrange("(j p) c -> p j c", p=TM)
        for p0, p1 in ((0, 112), (112, TM)):
            sp.dma_start(m.h[p0:p1], rows[p0:p1]).then_inc(landed, 16)
        with sp.Fori(0, P) as i:
            for s in range(2):
                sp.wait_ge(act_s.sem, act_s.at(f"xt{s}", i))
                sp.sem_inc(m.gate, 1)
                sp.dma_start(m.dram["xt_d"][:, bass.ds(i * 2 * GT + s * GT, GT)], xT[s][:]).then_inc(stored[s].sem, 16)
                sp.wait_ge(dve_s.sem, dve_s.at(f"vt{s}", i))
                sp.sem_inc(m.gate, 1)
                sp.dma_start(m.dram["v_d"][bass.ds(i * 2 * GB + s * GB, GB)].rearrange("b (o s) -> o b s", o=C),
                             vT[s][:].rearrange("o (b s) -> o b s", b=GB)).then_inc(stored[s].sem, 16)
        for s in range(2):
            sp.wait_ge(stored[s].sem, stored[s].at(P - 1))
        phase_end(m, sp, ph)

    def tensor(pe):
        pe_n.start(pe)
        pe_s.start(pe)
        pe.wait_ge(landed, 48)
        pe.transpose(ps[0:C, 0, 0:C], wv[:], m.ident[0:C, 0:C]).then_inc(pe_n.mark("wvt"), 1)
        pe.wait_ge(dve_n.sem, dve_n.at("wvt"))
        with pe.Fori(0, P) as i:
            for s in range(2):
                pe.wait_ge(dve_s.sem, dve_s.at(f"xh{s}", i))
                pe.wait_ge(act_s.sem, act_s.before(f"xt{s}", i))
                pe.sem_inc(m.gate, 1)
                for j in range(GJ):
                    mm = pe.transpose(ps[0:C, 2 * s + j // 4, j % 4 * TM:j % 4 * TM + TM], xh[s][:, j, :], m.ident[0:TM, 0:TM])
                mm.then_inc(pe_s.mark(f"turned{s}"), 1)
                pe.wait_ge(act_s.sem, act_s.at(f"xt{s}", i))
                pe.wait_ge(dve_s.sem, dve_s.before(f"vt{s}", i))
                pe.sem_inc(m.gate, 1)
                for k in range(2):
                    mm = pe.matmul(ps[0:C, 4 + 2 * s + k, 0:GT // 2], wvT[:], xT[s][:, GT // 2 * k:GT // 2 * (k + 1)], start=True, stop=True)
                mm.then_inc(pe_s.mark(f"v{s}"), 1)
        phase_end(m, pe, ph)

    def scalar(act):
        act_n.start(act)
        act_s.start(act)
        token_norm_squares(act, act_n, dve_n, "n", cent, sq, mean, ss, eps, "n_cent{k}")
        with act.Fori(0, P) as i:
            for s in range(2):
                act.wait_ge(pe_s.sem, pe_s.at(f"turned{s}", i))
                act.wait_ge(pe_s.sem, pe_s.before(f"v{s}", i))
                act.wait_ge(stored[s].sem, stored[s].before(i))
                act.activation(xT[s][:, 0:4 * TM], ps[0:C, 2 * s, 0:4 * TM], ACT.Copy)
                act.activation(xT[s][:, 4 * TM:GT], ps[0:C, 2 * s + 1, 0:TM], ACT.Copy).then_inc(act_s.mark(f"xt{s}"), 1)
        phase_end(m, act, ph)

    def vector(dve):
        dve_n.start(dve)
        dve_s.start(dve)
        dve.memset(eps[:], EPS).then_inc(dve_n.mark("eps"), 1)
        dve.wait_ge(landed, 48)
        token_norm(dve, dve_n, 0, act_n, "n", m.h, cent, sq, mean, ss)
        dve.wait_ge(pe_n.sem, pe_n.at("wvt"))
        dve.tensor_copy(wvT[:], ps[0:C, 0, 0:C]).then_inc(dve_n.mark("wvt"), 1)
        with dve.Fori(0, P) as i:
            for s in range(2):
                dve.wait_ge(pe_s.sem, pe_s.before(f"turned{s}", i))
                at = bass.ds(i * 2 * GJ + s * GJ, GJ)
                dve.tensor_tensor(xh[s][:], cent[:, at, :], cols(ss[:, at].unsqueeze(2), C), ALU.mult).then_inc(dve_s.mark(f"xh{s}"), 1)
                dve.wait_ge(pe_s.sem, pe_s.at(f"v{s}", i))
                dve.wait_ge(stored[s].sem, stored[s].before(i))
                dve.tensor_copy(vT[s][:].rearrange("o (k n) -> o k n", k=2), ps[0:C, 4 + 2 * s:6 + 2 * s, 0:GT // 2]).then_inc(dve_s.mark(f"vt{s}"), 1)
        phase_end(m, dve, ph)

    def gpsimd(pool):
        phase_end(m, pool, ph)

    return dict(sync=sync, tensor=tensor, scalar=scalar, vector=vector, gpsimd=gpsimd)


def joint_phase(nc, m, st, ph):
    H, KD, KM = 8, 64, 128
    KT = T - KM
    D1 = KD + 1
    NJ = 8 * T // (2 * TM)
    tiles = ((0, 1), (2, 3), (4,))
    BU = 4
    sb = lambda n, s, d=F32: st.enter_context(nc.sbuf_tensor(n, s, d))
    wq, wk = sb("jo_wq", [KD, 2, 2, 2, C]), sb("jo_wk", [KD, C])
    wqk = sb("jo_wqk", [128, 2, 2 * C])
    xs = [sb(f"jo_x{s}", [128, 2, T]) for s in range(2)]
    v = [sb(f"jo_v{s}", [KM, D1]) for s in range(2)]
    v_tail = [sb(f"jo_v_tail{s}", [BU * KT, BU * D1]) for s in range(2)]
    q = [sb(f"jo_q{s}", [128, T, H // 2]) for s in range(2)]
    mx = [sb(f"jo_max{u}", [TM, BU]) for u in range(2)]
    sc = [sb(f"jo_sc{u}", [TM, BU, T]) for u in range(2)]
    pr = [sb(f"jo_pr{u}", [TM, BU, KM]) for u in range(2)]
    pr_tail = [sb(f"jo_pr_tail{u}", [TM, BU * KT]) for u in range(2)]
    pT = [sb(f"jo_pt{u}", [KM, BU, TM]) for u in range(2)]
    pT_tail = [sb(f"jo_pt_tail{u}", [BU * KT, TM]) for u in range(2)]
    rs = [sb(f"jo_rs{u}", [TM, BU]) for u in range(2)]
    ctx = [sb(f"jo_ctx{s}", [TM, 2 * NJ, KD]) for s in range(2)]
    ps = m.psum
    NP, NU = NB // 2, 6
    TURNED, TAIL, CTX, QUERIES = 4, 5, 6, 7
    wl = m.whole.enter_context(nc.semaphore("jo_weights_landed"))
    xl = [Landed(nc, m.whole, f"jo_x_landed{s}", 2) for s in range(2)]
    vl = [Landed(nc, m.whole, f"jo_v_landed{s}", 1 + BU) for s in range(2)]
    stored = [Landed(nc, m.whole, f"jo_ctx_stored{s}", 2) for s in range(2)]
    S1 = lambda n, steps: Steps(nc, m.whole, n, steps)
    pe_w, act_w, dve_w = S1("jo_pe_w", ["wqk"]), S1("jo_act_w", ["wqk"]), S1("jo_dve_w", ["ready"])
    pe_q = S1("jo_queries", [f"q{s}{k}" for s in range(2) for k in range(2)])
    act_q = S1("jo_queries_copied", [f"q{s}{k}" for s in range(2) for k in range(2)])
    pe_sc = S1("jo_scores", [f"s{n}" for n in range(NU)])
    dve_sc = S1("jo_shifted", [f"{w}{n}" for n in range(NU) for w in ("max", "minus")])
    act_e = S1("jo_exp", [f"e{n}" for n in range(NU)])
    pe_t = S1("jo_turned", [f"t{n}" for n in range(NU)])
    act_t = S1("jo_turned_copied", [f"t{n}" for n in range(NU)])
    pe_v = S1("jo_attended", [f"v{n}" for n in range(NU)])
    dve_v = S1("jo_normed", [f"{w}{n}" for n in range(NU) for w in ("recip", "ctx")])

    def wrapped(n, i):
        return (n, i) if n < NU else (n - NU, i + 1)

    def back(S, fmt, n, i, by):
        return S.at(fmt.format(n - by), i) if n >= by else S.before(fmt.format(n - by + NU), i)

    def blocks(n):
        return 2 * len(tiles[n % 3]), 2 * tiles[n % 3][0]

    def sync(sp):
        for s in range(2):
            xl[s].start(sp)
            vl[s].start(sp)
            stored[s].start(sp)
        for h in range(H):
            sp.dma_start(wq[:, h // 4, h % 2, h // 2 % 2], m.dram["attn_Wq"][h * KD:(h + 1) * KD]).then_inc(wl, 16)
        sp.dma_start(wk[:], m.dram["attn_Wk"]).then_inc(wl, 16)
        for s in range(2):
            sp.dma_start(v_tail[s][:], m.dram["tail_blocks"]).then_inc(wl, 16)
        sp.wait_ge(wl, 16 * 11)
        sp.wait_ge(dve_w.sem, dve_w.at("ready"))

        def load_x(s, i):
            sp.wait_ge(pe_sc.sem, pe_sc.before(f"s{3 * s + 2}", i))
            sp.sem_inc(m.gate, 1)
            for par in range(2):
                sp.dma_start(xs[s][C * par:C * par + C, par], m.dram["xt_d"][:, bass.ds(i * 2 * T + s * T, T)]).then_inc(xl[s].sem, 16)

        def load_v(s, i):
            sp.wait_ge(pe_v.sem, pe_v.before(f"v{3 * s + 2}", i))
            sp.sem_inc(m.gate, 1)
            rows = m.dram["v_d"][bass.ds(i * 2 + s, 1)].rearrange("b (t d) -> t (b d)", d=KD)
            sp.dma_start(v[s][:, 0:KD], rows[0:KM]).then_inc(vl[s].sem, 16)
            for j in range(BU):
                sp.dma_start(v_tail[s][KT * j:KT * (j + 1), D1 * j:D1 * j + KD], rows[KM:T]).then_inc(vl[s].sem, 16)

        def store(s, i, ready):
            sp.wait_ge(dve_v.sem, ready)
            sp.sem_inc(m.gate, 1)
            dst = m.dram["ctx_d"][bass.ds(i * 2 + s, 1)].rearrange("b (p n) -> p (b n)", p=TM)
            src = ctx[s][:].rearrange("p n d -> p (n d)")
            for p0, p1 in ((0, 112), (112, TM)):
                sp.dma_start(dst[p0:p1], src[p0:p1]).then_inc(stored[s].sem, 16)

        for s in range(2):
            load_x(s, 0)
            load_v(s, 0)
        load_x(0, 1)
        with sp.Fori(1, NP - 1) as i:
            load_x(1, i)
            load_v(0, i)
            store(0, i - 1, dve_v.before("ctx2", i))
            load_x(0, i + 1)
            load_v(1, i)
            store(1, i - 1, dve_v.before("ctx5", i))
        load_x(1, NP - 1)
        for s in range(2):
            load_v(s, NP - 1)
            store(s, NP - 2, dve_v.before(f"ctx{3 * s + 2}", NP - 1))
        for s in range(2):
            store(s, NP - 1, dve_v.at(f"ctx{3 * s + 2}", NP - 1))
        for s in range(2):
            sp.wait_ge(stored[s].sem, stored[s].at(NP - 1))
        phase_end(m, sp, ph)

    def tensor(pe):
        for S in (pe_w, pe_q, pe_sc, pe_t, pe_v):
            S.start(pe)
        pe.wait_ge(wl, 16 * 11)
        for k in range(2):
            for par in range(2):
                mm = pe.matmul(ps[:, 0, (2 * k + par) * C:(2 * k + par + 1) * C], wq[:, k, par].rearrange("d f c -> d (f c)"), wk[:], start=True, stop=True)
        mm.then_inc(pe_w.mark("wqk"), 1)
        pe.wait_ge(act_w.sem, act_w.at("wqk"))

        def queries(s, i, k):
            if k == 0:
                pe.wait_ge(xl[s].sem, xl[s].at(i))
            before = act_q.at(f"q{s}0", i) if k else (act_q.at("q01", i) if s else act_q.before("q11", i))
            pe.wait_ge(act_q.sem, before)
            pe.sem_inc(m.gate, 1)
            mm = pe.matmul(ps[:, QUERIES, 0:2 * T], wqk[:, k], xs[s][:].rearrange("p f s -> p (f s)"), start=True, stop=True)
            mm.then_inc(pe_q.mark(f"q{s}{k}"), 1)

        def scores(n, i):
            n, i = wrapped(n, i)
            s, u = n // 3, n % 2
            if n % 3 == 0:
                pe.wait_ge(act_q.sem, act_q.at(f"q{s}1", i))
            pe.wait_ge(dve_sc.sem, back(dve_sc, "minus{}", n, i, 2))
            pe.sem_inc(m.gate, 1)
            rows = q[s][:].rearrange("c s h -> c (s h)")
            for k, j in enumerate(tiles[n % 3]):
                mm = pe.matmul(ps[0:TM, 2 * u + k, 0:2 * T], rows[:, j::NJ], xs[s][:].rearrange("p f s -> p (f s)"), start=True, stop=True)
            mm.then_inc(pe_sc.mark(f"s{n}"), 1)

        def turn(n, i):
            n, i = wrapped(n, i)
            u, (nb, _) = n % 2, blocks(n)
            pe.wait_ge(act_e.sem, act_e.at(f"e{n}", i))
            pe.wait_ge(act_t.sem, back(act_t, "t{}", n, i, 1))
            pe.sem_inc(m.gate, 1)
            for b in range(nb):
                pe.transpose(ps[:, TURNED, b * TM:(b + 1) * TM], pr[u][:, b, :], m.ident[0:TM, 0:TM])
            pe.transpose(ps[0:nb * KT, TAIL, 0:TM], pr_tail[u][:, 0:nb * KT], m.ident[0:TM, 0:TM]).then_inc(pe_t.mark(f"t{n}"), 1)

        def attend(n, i):
            s, u, (nb, _) = n // 3, n % 2, blocks(n)
            if n % 3 == 0:
                pe.wait_ge(vl[s].sem, vl[s].at(i))
            pe.wait_ge(act_t.sem, act_t.at(f"t{n}", i))
            pe.wait_ge(dve_v.sem, back(dve_v, "ctx{}", n, i, 1))
            pe.sem_inc(m.gate, 1)
            pe.matmul(ps[0:TM, CTX, 0:nb * D1], pT_tail[u][0:nb * KT], v_tail[s][0:nb * KT, 0:nb * D1], start=True, stop=False)
            for b in range(nb):
                mm = pe.matmul(ps[0:TM, CTX, b * D1:(b + 1) * D1], pT[u][:, b, :], v[s][:], start=False, stop=b == nb - 1)
            mm.then_inc(pe_v.mark(f"v{n}"), 1)

        def one_pass(i, last=False):
            for n in range(NU):
                s, more = (1, 0) if n == 0 else (0, 1)
                ask = n % 3 == 0 and not (last and more)
                if ask:
                    queries(s, i + more, 0)
                if not (last and n + 2 >= NU):
                    scores(n + 2, i)
                if ask:
                    queries(s, i + more, 1)
                attend(n, i)
                if not (last and n + 1 >= NU):
                    turn(n + 1, i)

        for k in range(2):
            queries(0, 0, k)
        for n in range(2):
            scores(n, 0)
        turn(0, 0)
        with pe.Fori(0, NP - 1) as i:
            one_pass(i)
        one_pass(NP - 1, last=True)
        phase_end(m, pe, ph)

    def scalar(act):
        for S in (act_w, act_q, act_e, act_t):
            S.start(act)
        act.wait_ge(pe_w.sem, pe_w.at("wqk"))
        act.activation(wqk[:].rearrange("c k o -> c (k o)"), ps[:, 0, 0:4 * C], ACT.Copy, scale=H ** -0.5).then_inc(act_w.mark("wqk"), 1)
        act.preload_act_table(ACT.Exp)

        def copy_queries(s, i):
            for k in range(2):
                act.wait_ge(pe_q.sem, pe_q.at(f"q{s}{k}", i))
                if k == 0:
                    act.wait_ge(pe_sc.sem, pe_sc.before(f"s{3 * s + 2}", i))
                act.activation(q[s][:, :, 2 * k:2 * k + 2].rearrange("p s h -> p h s"), ps[:, QUERIES, 0:2 * T].rearrange("p (h s) -> p h s", h=2),
                               ACT.Copy).then_inc(act_q.mark(f"q{s}{k}"), 1)

        def exp(n, i):
            n, i = wrapped(n, i)
            u, (nb, _) = n % 2, blocks(n)
            act.wait_ge(dve_sc.sem, dve_sc.at(f"minus{n}", i))
            act.wait_ge(pe_t.sem, back(pe_t, "t{}", n, i, 2))
            act.activation(pr[u][:, 0:nb], sc[u][:, 0:nb, 0:KM], ACT.Exp)
            act.activation(pr_tail[u][:, 0:nb * KT].rearrange("p (b t) -> p b t", b=nb), sc[u][:, 0:nb, KM:T], ACT.Exp).then_inc(act_e.mark(f"e{n}"), 1)

        def copy_turned(n, i):
            u, (nb, _) = n % 2, blocks(n)
            act.wait_ge(pe_t.sem, pe_t.at(f"t{n}", i))
            act.wait_ge(pe_v.sem, back(pe_v, "v{}", n, i, 2))
            act.activation(pT_tail[u][0:nb * KT], ps[0:nb * KT, TAIL, 0:TM], ACT.Copy)
            act.activation(pT[u][:, 0:nb].rearrange("p n m -> p (n m)"), ps[:, TURNED, 0:nb * TM], ACT.Copy).then_inc(act_t.mark(f"t{n}"), 1)

        def one_pass(i, last=False):
            for n in range(NU):
                copy_turned(n, i)
                if n == 0:
                    copy_queries(1, i)
                elif n == 3 and not last:
                    copy_queries(0, i + 1)
                if not (last and n + 1 >= NU):
                    exp(n + 1, i)

        copy_queries(0, 0)
        exp(0, 0)
        with act.Fori(0, NP - 1) as i:
            one_pass(i)
        one_pass(NP - 1, last=True)
        phase_end(m, act, ph)

    def vector(dve):
        for S in (dve_w, dve_sc, dve_v):
            S.start(dve)
        for s in range(2):
            dve.memset(v[s][:, KD:D1], 1.0)
            clear = dve.memset(xs[s][:], 0.0)
        clear.then_inc(dve_w.mark("ready"), 1)

        def shift(n, i):
            n, i = wrapped(n, i)
            u, (nb, _) = n % 2, blocks(n)
            split = lambda ap: ap.rearrange("p (j r) t -> p j r t", r=2)
            scored = ps[0:TM, 2 * u:2 * u + nb // 2, 0:2 * T].rearrange("p j (r t) -> p j r t", r=2)
            dve.wait_ge(pe_sc.sem, pe_sc.at(f"s{n}", i))
            dve.tensor_reduce(mx[u][:, 0:nb].rearrange("p (j r) -> p j r", r=2), scored, X, ALU.max).then_inc(dve_sc.mark(f"max{n}"), 1)
            dve.wait_ge(dve_sc.sem, dve_sc.at(f"max{n}", i))
            dve.wait_ge(act_e.sem, back(act_e, "e{}", n, i, 2))
            dve.tensor_tensor(split(sc[u][:, 0:nb]), scored, split(cols(mx[u][:, 0:nb].unsqueeze(2), T)), ALU.subtract).then_inc(dve_sc.mark(f"minus{n}"), 1)

        def normalise(n, i):
            s, u, (nb, first) = n // 3, n % 2, blocks(n)
            o = ps[0:TM, CTX, 0:nb * D1].rearrange("p (b d) -> p b d", b=nb)
            dve.wait_ge(pe_v.sem, pe_v.at(f"v{n}", i))
            dve.reciprocal(rs[u][:, 0:nb], o[:, :, KD]).then_inc(dve_v.mark(f"recip{n}"), 1)
            dve.wait_ge(dve_v.sem, dve_v.at(f"recip{n}", i))
            if n % 3 == 0:
                dve.wait_ge(stored[s].sem, stored[s].before(i))
            dve.tensor_tensor(ctx[s][:, first:first + nb, :], o[:, :, 0:KD], cols(rs[u][:, 0:nb].unsqueeze(2), KD), ALU.mult).then_inc(dve_v.mark(f"ctx{n}"), 1)

        def one_pass(i, last=False):
            for n in range(NU):
                if not (last and n + 2 >= NU):
                    shift(n + 2, i)
                normalise(n, i)

        for n in range(2):
            shift(n, 0)
        with dve.Fori(0, NP - 1) as i:
            one_pass(i)
        one_pass(NP - 1, last=True)
        phase_end(m, dve, ph)

    def gpsimd(pool):
        phase_end(m, pool, ph)

    return dict(sync=sync, tensor=tensor, scalar=scalar, vector=vector, gpsimd=gpsimd)


def joint_out_phase(nc, m, st, ph):
    J, KT = NB * T // TM, 4
    sb = lambda n, s, d=F32: st.enter_context(nc.sbuf_tensor(n, s, d))
    wo, woT = sb("po_wo", [C, 128, KT]), sb("po_wot", [128, KT, C])
    cx = [sb(f"po_cx{s}", [128, GB, KT, T]) for s in range(2)]
    oT = [sb(f"po_ot{s}", [C, GT]) for s in range(2)]
    sq = [sb(f"po_sq{k}", [TM, J // 4, C]) for k in range(2)]
    mean, ss, eps, eps_rms = sb("po_mean", [TM, J]), sb("po_ss", [TM, J]), sb("po_eps", [128, 1]), sb("po_eps_rms", [128, 1])
    zt = [sb(f"po_z{s}", [TM, GJ, C]) for s in range(2)]
    zT = [sb(f"po_zt{s}", [C, GT]) for s in range(2)]
    ps = m.psum
    P = NG // 2
    S1 = lambda n, steps: Steps(nc, m.whole, n, steps)
    wl = m.whole.enter_context(nc.semaphore("po_weights_landed"))
    cl = [Landed(nc, m.whole, f"po_ctx_landed{s}", GB) for s in range(2)]
    stored = [Landed(nc, m.whole, f"po_z_stored{s}", 1) for s in range(2)]
    pe_w, dve_w = S1("po_pe_w", ["wot"]), S1("po_dve_w", ["eps", "wot"])
    pe_s = S1("po_pe", [f"{k}{s}" for s in range(2) for k in ("out", "turned")])
    act_s = S1("po_act", ["ot0", "ot1"])
    dve_s = S1("po_dve", ["h0", "h1"])
    dve_n = S1("po_dve_norm", [f"n_{k}" for k in NORM_DVE] + [f"y{k}" for k in range(4)] + [f"r_ss{k}" for k in range(4)] + ["r_recip"])
    act_n = S1("po_act_norm", [f"n_{k}" for k in NORM_ACT] + [f"r_{k}" for k in NORM_ACT])
    pe_z, act_z, dve_z = S1("po_pe_z", ["z0", "z1"]), S1("po_act_z", ["z0", "z1"]), S1("po_dve_z", ["z0", "z1"])

    def sync(sp):
        for s in range(2):
            cl[s].start(sp)
            stored[s].start(sp)
        sp.dma_start(wo[:], m.dram["attn_Wo"].rearrange("o (p k) -> o p k", k=KT)).then_inc(wl, 16)
        with sp.Fori(0, P) as i:
            for s in range(2):
                sp.wait_ge(pe_s.sem, pe_s.before(f"out{s}", i))
                sp.sem_inc(m.gate, 1)
                for b in range(GB):
                    sp.dma_start(cx[s][:, b].rearrange("p k t -> p (k t)"),
                                 m.dram["ctx_d"][bass.ds(i * 2 * GB + (s * GB + b), 1)].rearrange("b (p n) -> p (b n)", p=128)).then_inc(cl[s].sem, 16)
        with sp.Fori(0, P) as i:
            for s in range(2):
                sp.wait_ge(act_z.sem, act_z.at(f"z{s}", i))
                sp.sem_inc(m.gate, 1)
                sp.dma_start(m.dram["zt_d"][:, bass.ds(i * 2 * GT + s * GT, GT)], zT[s][:]).then_inc(stored[s].sem, 16)
        for s in range(2):
            sp.wait_ge(stored[s].sem, stored[s].at(P - 1))
        phase_end(m, sp, ph)

    def tensor(pe):
        for S in (pe_w, pe_s, pe_z):
            S.start(pe)
        pe.wait_ge(wl, 16)
        for k in range(KT):
            mm = pe.transpose(ps[:, 0, k * C:(k + 1) * C], wo[:, :, k], m.ident[0:C, 0:C])
        mm.then_inc(pe_w.mark("wot"), 1)
        pe.wait_ge(dve_w.sem, dve_w.at("wot"))
        with pe.Fori(0, P) as i:
            for s in range(2):
                pe.wait_ge(cl[s].sem, cl[s].at(i))
                pe.wait_ge(act_s.sem, act_s.before(f"ot{s}", i))
                pe.sem_inc(m.gate, 1)
                for half in range(2):
                    for k in range(KT):
                        mm = pe.matmul(ps[0:C, 2 * s + half, 0:2 * T], woT[:, k, :], cx[s][:, 2 * half:2 * half + 2, k, :], start=k == 0, stop=k == KT - 1)
                mm.then_inc(pe_s.mark(f"out{s}"), 1)
                pe.wait_ge(act_s.sem, act_s.at(f"ot{s}", i))
                pe.wait_ge(dve_s.sem, dve_s.before(f"h{s}", i))
                pe.sem_inc(m.gate, 1)
                for j in range(GJ):
                    mm = pe.transpose(ps[0:TM, 4 + s, j * C:(j + 1) * C], oT[s][:, j * TM:(j + 1) * TM], m.ident[0:C, 0:C])
                mm.then_inc(pe_s.mark(f"turned{s}"), 1)
        turn_groups(m, pe, P, pe_z, dve_z, act_z, zt, C)
        phase_end(m, pe, ph)

    def scalar(act):
        for S in (act_s, act_n, act_z):
            S.start(act)
        with act.Fori(0, P) as i:
            for s in range(2):
                act.wait_ge(pe_s.sem, pe_s.at(f"out{s}", i))
                act.wait_ge(pe_s.sem, pe_s.before(f"turned{s}", i))
                act.activation(oT[s][:].rearrange("c (h n) -> c h n", h=2), ps[0:C, 2 * s:2 * s + 2, 0:2 * T], ACT.Copy).then_inc(act_s.mark(f"ot{s}"), 1)
        token_norm_squares(act, act_n, dve_n, "n", m.y, sq, mean, ss, eps, "n_cent{k}")
        token_norm_squares(act, act_n, dve_n, "r", m.y, sq, mean, ss, eps_rms, "y{k}")
        with act.Fori(0, P) as i:
            for s in range(2):
                act.wait_ge(pe_z.sem, pe_z.at(f"z{s}", i))
                act.wait_ge(stored[s].sem, stored[s].before(i))
                act.activation(zT[s][:, 0:4 * TM], ps[0:C, 2 * s, 0:4 * TM], ACT.Copy)
                act.activation(zT[s][:, 4 * TM:GT], ps[0:C, 2 * s + 1, 0:TM], ACT.Copy).then_inc(act_z.mark(f"z{s}"), 1)
        phase_end(m, act, ph)

    def vector(dve):
        for S in (dve_w, dve_s, dve_n, dve_z):
            S.start(dve)
        dve.memset(eps[:], EPS)
        dve.memset(eps_rms[:], 1e-6).then_inc(dve_w.mark("eps"), 1)
        dve.wait_ge(pe_w.sem, pe_w.at("wot"))
        dve.tensor_copy(woT[:], ps[:, 0, 0:KT * C].rearrange("p (k o) -> p k o", k=KT)).then_inc(dve_w.mark("wot"), 1)
        with dve.Fori(0, P) as i:
            for s in range(2):
                at = bass.ds(i * 2 * GJ + s * GJ, GJ)
                dve.wait_ge(pe_s.sem, pe_s.at(f"turned{s}", i))
                dve.tensor_tensor(m.h[:, at, :], ps[0:TM, 4 + s, 0:GJ * C].rearrange("p (j c) -> p j c", c=C), m.h[:, at, :], ALU.add).then_inc(dve_s.mark(f"h{s}"), 1)
        dve.wait_ge(dve_s.sem, dve_s.at("h1", P - 1))
        token_norm(dve, dve_n, 0, act_n, "n", m.h, m.y, sq, mean, ss)
        for k in range(4):
            j = slice(J // 4 * k, J // 4 * (k + 1))
            dve.tensor_tensor(m.y[:, j], m.y[:, j], cols(ss[:, j].unsqueeze(2), C), ALU.mult).then_inc(dve_n.mark(f"y{k}"), 1)
        root_mean_square(dve, dve_n, act_n, sq, mean, ss, "y3")
        scale_groups(dve, P, dve_z, pe_z, zt, m.y, ss)
        phase_end(m, dve, ph)

    def gpsimd(pool):
        phase_end(m, pool, ph)

    return dict(sync=sync, tensor=tensor, scalar=scalar, vector=vector, gpsimd=gpsimd)


def root_mean_square(dve, S, act_s, sq, mean, ss, last_use):
    J = NB * T // TM
    dve.wait_ge(S.sem, S.at(last_use))
    for k in range(4):
        j = slice(J // 4 * k, J // 4 * (k + 1))
        dve.wait_ge(act_s.sem, act_s.at(f"r_sq{k}"))
        dve.tensor_reduce(ss[:, j], sq[k % 2][:], X, ALU.add).then_inc(S.mark(f"r_ss{k}"), 1)
    dve.wait_ge(act_s.sem, act_s.at("r_std"))
    dve.reciprocal(ss[:], mean[:]).then_inc(S.mark("r_recip"), 1)
    dve.wait_ge(S.sem, S.at("r_recip"))


def scale_groups(dve, passes, S, pe_s, dst, src, factor):
    with dve.Fori(0, passes) as i:
        for s in range(2):
            dve.wait_ge(pe_s.sem, pe_s.before(f"z{s}", i))
            at = bass.ds(i * 2 * GJ + s * GJ, GJ)
            dve.tensor_tensor(dst[s][:], src[:, at, :], cols(factor[:, at].unsqueeze(2), C), ALU.mult).then_inc(S.mark(f"z{s}"), 1)


def turn_groups(m, pe, passes, S, dve_s, act_s, src, rows):
    with pe.Fori(0, passes) as i:
        for s in range(2):
            pe.wait_ge(dve_s.sem, dve_s.at(f"z{s}", i))
            pe.wait_ge(act_s.sem, act_s.before(f"z{s}", i))
            pe.sem_inc(m.gate, 1)
            for j in range(GJ):
                mm = pe.transpose(m.psum[0:rows, 2 * s + j // 4, j % 4 * TM:j % 4 * TM + TM], src[s][:, j, :], m.ident[0:TM, 0:TM])
            mm.then_inc(S.mark(f"z{s}"), 1)


def causal_phase(nc, m, st, ph):
    H, HD, KV, R, KM = 4, 16, 2, 32, 128
    KT, NJ, D1 = T - KM, H * T // TM, KV * HD + 1
    sb = lambda n, s, d=F32: st.enter_context(nc.sbuf_tensor(n, s, d))
    w4, wT = sb("ca_w4", [128, 4, C]), sb("ca_wt", [C, 4, 128])
    wv, wvT = sb("ca_wv", [KV * HD, C]), sb("ca_wvt", [C, KV * HD])
    l1 = sb("ca_ln1", [C, 1])
    cos, sin = sb("ca_cos", [128, 2 * T]), sb("ca_sin", [128, 2 * T])
    mask32, mask = sb("ca_mask32", [TM, NJ * T]), sb("ca_mask", [TM, NJ * T], BF16)
    ident = sb("ca_ident", [TM, TM], BF16)
    pick, own = sb("ca_pick", [TM, NJ, KV]), sb("ca_own", [NJ * KT, NJ])
    z = [sb(f"ca_z{k}", [C, T]) for k in range(4)]
    z_tail = [sb(f"ca_z_tail{k}", [C, NJ, KT]) for k in range(4)]
    v = [sb(f"ca_v{k}", [KM, D1]) for k in range(4)]
    v_tail = [sb(f"ca_v_tail{k}", [NJ * KT, NJ, D1]) for k in range(4)]
    y = [sb(f"ca_y{k}", [TM, NJ, HD]) for k in range(4)]
    t1, t2 = ([sb(f"ca_{n}{s}", [128, 2 * T]) for s in range(2)] for n in ("t1", "t2"))
    qz = [sb(f"ca_q{s}", [128, T, H]) for s in range(2)]
    kk = [sb(f"ca_k{s}", [128, T]) for s in range(2)]
    sc = [sb(f"ca_sc{s}", [TM, NJ, T]) for s in range(2)]
    pr = [sb(f"ca_pr{s}", [TM, NJ, KM]) for s in range(2)]
    pr_tail = [sb(f"ca_pr_tail{s}", [TM, NJ, KT]) for s in range(2)]
    mx = [sb(f"ca_mx{s}", [TM, NJ]) for s in range(2)]
    pT = [sb(f"ca_pt{s}", [KM, NJ, TM]) for s in range(2)]
    pT_tail = [sb(f"ca_pt_tail{s}", [NJ * KT, TM]) for s in range(2)]
    rs = [sb(f"ca_rs{s}", [TM, NJ]) for s in range(2)]
    picked = [sb(f"ca_picked{s}", [TM, NJ, KV]) for s in range(2)]
    both = [sb(f"ca_both{s}", [TM, NJ, KV, HD]) for s in range(2)]
    ps = m.psum
    NU = 4
    NP = NB // NU
    HALVES = ((0, 0, 3), (1, 3, NJ))
    COS, SIN, OUT, VC = 6, 7, 2 * T, 2 * T
    S1 = lambda n, steps: Steps(nc, m.whole, n, steps)
    each = lambda *names: [f"{w}{n}" for n in range(NU) for w in names]
    wl = m.whole.enter_context(nc.semaphore("ca_weights_landed"))
    zl = [Landed(nc, m.whole, f"ca_z_landed{n}", 2) for n in range(NU)]
    stored = [Landed(nc, m.whole, f"ca_y_stored{n}", 2) for n in range(NU)]
    dve_w, pe_w, act_w = S1("ca_dve_w", ["ones", "clear", "mask"]), S1("ca_pe_w", ["turned"]), S1("ca_act_w", ["wt", "wvt"])
    pe_q, pe_sc, pe_t, pe_v = (S1(f"ca_pe_{n}", each(x)) for n, x in (("qkv", "qkv"), ("scores", "s"), ("turned", "t"), ("attended", "o")))
    dve_r = S1("ca_dve_rope", each("cos", "sin", "v", "v_tail"))
    pool_r, pool_y = S1("ca_pool_rope", each(*[f"q{h}_" for h in range(H)], "k")), S1("ca_pool_y", each("y"))
    dve_sc = S1("ca_dve_scores", each("max0_", "max1_", "minus0_", "minus1_"))
    dve_o = S1("ca_dve_out", each("recip", "picked", "both"))
    act_e, act_t = S1("ca_act_exp", each("e")), S1("ca_act_turned", each("t"))

    def wrapped(n, i):
        return (n, i) if n < NU else (n - NU, i + 1)

    def back(S, name, n, i, by):
        return S.at(f"{name}{n - by}", i) if n >= by else S.before(f"{name}{n - by + NU}", i)

    def sync(sp):
        for n in range(NU):
            zl[n].start(sp)
            stored[n].start(sp)
        for dst, src in ((l1[:], m.dram["ffn_ln1_w"].rearrange("(c o) -> c o", o=1)), (wv[:], m.dram["ffn_wv"]), (cos[:], m.dram["rope_cos"]),
                         (sin[:], m.dram["rope_sin"]), (mask32[:], m.dram["causal_mask"]), (own[:], m.dram["own_block"]),
                         (pick[:].rearrange("p j k -> p (j k)"), m.dram["pick_value_head"])):
            sp.dma_start(dst, src).then_inc(wl, 16)
        sp.wait_ge(dve_w.sem, dve_w.at("clear"))
        for h in range(H):
            for k, src, r0 in ((0, m.dram["ffn_wq"], HD * h), (2, m.dram["ffn_wk"], HD * (h // 2))):
                sp.dma_start(w4[R * h:R * h + HD, k, :], src[r0:r0 + HD]).then_inc(wl, 16)
                sp.dma_start(w4[R * h:R * h + HD // 2, k + 1, :], src[r0 + HD // 2:r0 + HD]).then_inc(wl, 16)
                sp.dma_start(w4[R * h + HD // 2:R * h + HD, k + 1, :], src[r0:r0 + HD // 2]).then_inc(wl, 16)

        def load(n, i):
            sp.wait_ge(pe_q.sem, pe_q.before(f"qkv{n}", i))
            sp.sem_inc(m.gate, 1)
            t0 = i * NU * T + n * T
            sp.dma_start(z[n][:], m.dram["zt_d"][:, bass.ds(t0, T)]).then_inc(zl[n].sem, 16)
            sp.dma_start(z_tail[n][:], m.dram["zt_d"][:, bass.ds(t0 + KM, KT)].unsqueeze(1).broadcast_to([C, NJ, KT])).then_inc(zl[n].sem, 16)

        def store(n, i, ready):
            sp.wait_ge(pool_y.sem, ready)
            sp.sem_inc(m.gate, 1)
            dst = m.dram["y_d"][bass.ds(i * NU + n, 1)].rearrange("b (p n) -> p (b n)", p=TM)
            src = y[n][:].rearrange("p j d -> p (j d)")
            for p0, p1 in ((0, 112), (112, TM)):
                sp.dma_start(dst[p0:p1], src[p0:p1]).then_inc(stored[n].sem, 16)

        for n in range(NU):
            load(n, 0)
        with sp.Fori(1, NP) as i:
            for n in range(NU):
                load(n, i)
                store(n, i - 1, pool_y.before(f"y{n}", i))
        for n in range(NU):
            store(n, NP - 1, pool_y.at(f"y{n}", NP - 1))
        for n in range(NU):
            sp.wait_ge(stored[n].sem, stored[n].at(NP - 1))
        phase_end(m, sp, ph)

    def tensor(pe):
        for S in (pe_w, pe_q, pe_sc, pe_t, pe_v):
            S.start(pe)
        pe.wait_ge(wl, 16 * 31)
        for k in range(4):
            pe.transpose(ps[0:C, 0, 128 * k:128 * k + 128], w4[:, k, :], m.ident[:])
        pe.transpose(ps[0:C, 1, 0:KV * HD], wv[:], m.ident[0:KV * HD, 0:KV * HD]).then_inc(pe_w.mark("turned"), 1)
        pe.wait_ge(act_w.sem, act_w.at("wvt"))
        pe.wait_ge(dve_w.sem, dve_w.at("mask"))

        def project(n, i):
            n, i = wrapped(n, i)
            pe.wait_ge(zl[n].sem, zl[n].at(i))
            pe.wait_ge(dve_r.sem, back(dve_r, "v_tail", n, i, 1))
            pe.wait_ge(dve_o.sem, dve_o.before(f"both{n}", i))
            pe.sem_inc(m.gate, 1)
            for k in range(4):
                pe.matmul(ps[:, COS + k % 2, k // 2 * T:(k // 2 + 1) * T], wT[:, k, :], z[n][:], start=True, stop=True)
            pe.matmul(ps[:, SIN, VC:VC + KV * HD], z[n][:, 0:KM], wvT[:], start=True, stop=True)
            pe.matmul(ps[0:NJ * KT, SIN, VC + KV * HD:VC + 2 * KV * HD], z_tail[n][:].rearrange("c j t -> c (j t)"), wvT[:],
                      start=True, stop=True).then_inc(pe_q.mark(f"qkv{n}"), 1)

        def scores(n, i):
            n, i = wrapped(n, i)
            s = n % 2
            pe.wait_ge(pool_r.sem, pool_r.at(f"k{n}", i))
            pe.wait_ge(dve_sc.sem, back(dve_sc, "minus1_", n, i, 2))
            pe.sem_inc(m.gate, 1)
            rows = qz[s][:].rearrange("c t h -> c (t h)")
            for k, a, b in HALVES:
                pe.matmul(ps[0:TM, 2 * s + k, 0:(b - a) * T], ident[:], mask[:, a * T:b * T], start=True, stop=False)
                for j in range(a, b):
                    mm = pe.matmul(ps[0:TM, 2 * s + k, (j - a) * T:(j - a + 1) * T], rows[:, j::NJ], kk[s][:], start=False, stop=j == b - 1)
            mm.then_inc(pe_sc.mark(f"s{n}"), 1)

        def turn(n, i):
            n, i = wrapped(n, i)
            s = n % 2
            pe.wait_ge(act_e.sem, act_e.at(f"e{n}", i))
            pe.wait_ge(act_t.sem, back(act_t, "t", n, i, 1))
            pe.sem_inc(m.gate, 1)
            for j in range(NJ):
                pe.transpose(ps[:, 4 + j // 4, j % 4 * TM:j % 4 * TM + TM], pr[s][:, j, :], m.ident[0:TM, 0:TM])
            pe.transpose(ps[0:NJ * KT, 5, TM:2 * TM], pr_tail[s][:].rearrange("p j t -> p (j t)"), m.ident[0:TM, 0:TM]).then_inc(pe_t.mark(f"t{n}"), 1)

        def attend(n, i, projected):
            s = n % 2
            pe.wait_ge(act_t.sem, act_t.at(f"t{n}", i))
            if projected:
                n3, i3 = wrapped(n + 3, i)
                pe.wait_ge(dve_r.sem, dve_r.at(f"v_tail{n3}", i3))
            else:
                pe.wait_ge(dve_o.sem, back(dve_o, "both", n, i, 1))
            pe.sem_inc(m.gate, 1)
            o = ps[0:TM, COS, OUT:OUT + NJ * D1]
            pe.matmul(o, pT_tail[s][:], v_tail[n][:].rearrange("k j d -> k (j d)"), start=True, stop=False)
            for j in range(NJ):
                mm = pe.matmul(o[:, j * D1:(j + 1) * D1], pT[s][:, j, :], v[n][:], start=False, stop=j == NJ - 1)
            mm.then_inc(pe_v.mark(f"o{n}"), 1)

        def one_pass(i, end=False):
            for n in range(NU):
                projected = not (end and n + 3 >= NU)
                if projected:
                    project(n + 3, i)
                if not (end and n + 2 >= NU):
                    scores(n + 2, i)
                attend(n, i, projected)
                if not (end and n + 1 >= NU):
                    turn(n + 1, i)

        for n in range(3):
            project(n, 0)
        for n in range(2):
            scores(n, 0)
        turn(0, 0)
        with pe.Fori(0, NP - 1) as i:
            one_pass(i)
        one_pass(NP - 1, end=True)
        phase_end(m, pe, ph)

    def scalar(act):
        for S in (act_w, act_e, act_t):
            S.start(act)
        act.wait_ge(wl, 16 * 31)
        act.wait_ge(pe_w.sem, pe_w.at("turned"))
        act.activation(wT[:].rearrange("c k n -> c (k n)"), ps[0:C, 0, :], ACT.Copy, scale=l1[:]).then_inc(act_w.mark("wt"), 1)
        act.activation(wvT[:], ps[0:C, 1, 0:KV * HD], ACT.Copy, scale=l1[:]).then_inc(act_w.mark("wvt"), 1)
        act.preload_act_table(ACT.Exp)

        def exp(n, i):
            n, i = wrapped(n, i)
            s = n % 2
            act.wait_ge(dve_sc.sem, dve_sc.at(f"minus1_{n}", i))
            act.wait_ge(pe_t.sem, back(pe_t, "t", n, i, 2))
            act.activation(pr[s][:], sc[s][:, :, 0:KM], ACT.Exp)
            act.activation(pr_tail[s][:], sc[s][:, :, KM:T], ACT.Exp).then_inc(act_e.mark(f"e{n}"), 1)

        def copy_turned(n, i):
            s = n % 2
            act.wait_ge(pe_t.sem, pe_t.at(f"t{n}", i))
            act.wait_ge(pe_v.sem, back(pe_v, "o", n, i, 2))
            act.activation(pT[s][:, 0:4].rearrange("k j p -> k (j p)"), ps[:, 4, 0:4 * TM], ACT.Copy)
            act.activation(pT[s][:, 4], ps[:, 5, 0:TM], ACT.Copy)
            act.activation(pT_tail[s][:], ps[0:NJ * KT, 5, TM:2 * TM], ACT.Copy).then_inc(act_t.mark(f"t{n}"), 1)

        def one_pass(i, end=False):
            for n in range(NU):
                copy_turned(n, i)
                if not (end and n + 1 >= NU):
                    exp(n + 1, i)

        exp(0, 0)
        with act.Fori(0, NP - 1) as i:
            one_pass(i)
        one_pass(NP - 1, end=True)
        phase_end(m, act, ph)

    def vector(dve):
        for S in (dve_w, dve_r, dve_sc, dve_o):
            S.start(dve)
        for s in range(2):
            dve.memset(qz[s][:], 0.0)
        for n in range(NU):
            ins = dve.memset(v[n][:, D1 - 1:D1], 1.0)
        ins.then_inc(dve_w.mark("ones"), 1)
        dve.memset(w4[:], 0.0).then_inc(dve_w.mark("clear"), 1)
        dve.wait_ge(wl, 16 * 31)
        for n in range(NU):
            dve.tensor_copy(v_tail[n][:, :, D1 - 1], own[:])
        dve.tensor_copy(ident[:], m.ident[0:TM, 0:TM])
        dve.tensor_copy(mask[:], mask32[:]).then_inc(dve_w.mark("mask"), 1)
        dve.wait_ge(dve_w.sem, dve_w.at("mask"))

        def rotate(n, i):
            n, i = wrapped(n, i)
            s = n % 2
            dve.wait_ge(pe_q.sem, pe_q.at(f"qkv{n}", i))
            dve.wait_ge(pool_r.sem, back(pool_r, "k", n, i, 2))
            dve.tensor_tensor(t1[s][:], ps[:, COS, 0:2 * T], cos[:], ALU.mult).then_inc(dve_r.mark(f"cos{n}"), 1)
            dve.tensor_tensor(t2[s][:], ps[:, SIN, 0:2 * T], sin[:], ALU.mult).then_inc(dve_r.mark(f"sin{n}"), 1)
            dve.wait_ge(pe_v.sem, pe_v.before(f"o{n}", i))
            dve.tensor_copy(v[n][:, 0:KV * HD], ps[:, SIN, VC:VC + KV * HD]).then_inc(dve_r.mark(f"v{n}"), 1)
            dve.tensor_tensor(v_tail[n][:, :, 0:KV * HD], ps[0:NJ * KT, SIN, VC + KV * HD:VC + 2 * KV * HD].unsqueeze(1).broadcast_to([NJ * KT, NJ, KV * HD]),
                              cols(own[:].unsqueeze(2), KV * HD), ALU.mult).then_inc(dve_r.mark(f"v_tail{n}"), 1)

        def shift(n, i):
            n, i = wrapped(n, i)
            s = n % 2
            scored = lambda k, a, b: ps[0:TM, 2 * s + k, 0:(b - a) * T].rearrange("p (j t) -> p j t", t=T)
            dve.wait_ge(pe_sc.sem, pe_sc.at(f"s{n}", i))
            for k, a, b in HALVES:
                dve.tensor_reduce(mx[s][:, a:b], scored(k, a, b), X, ALU.max).then_inc(dve_sc.mark(f"max{k}_{n}"), 1)
            dve.wait_ge(act_e.sem, back(act_e, "e", n, i, 2))
            for k, a, b in HALVES:
                dve.wait_ge(dve_sc.sem, dve_sc.at(f"max{k}_{n}", i))
                dve.tensor_tensor(sc[s][:, a:b], scored(k, a, b), cols(mx[s][:, a:b].unsqueeze(2), T), ALU.subtract).then_inc(dve_sc.mark(f"minus{k}_{n}"), 1)

        def normalise(n, i):
            s = n % 2
            o = ps[0:TM, COS, OUT:OUT + NJ * D1].rearrange("p (j d) -> p j d", j=NJ)
            dve.wait_ge(pe_v.sem, pe_v.at(f"o{n}", i))
            dve.reciprocal(rs[s][:], o[:, :, D1 - 1]).then_inc(dve_o.mark(f"recip{n}"), 1)
            dve.wait_ge(dve_o.sem, dve_o.at(f"recip{n}", i))
            dve.tensor_tensor(picked[s][:], pick[:], cols(rs[s][:].unsqueeze(2), KV), ALU.mult).then_inc(dve_o.mark(f"picked{n}"), 1)
            dve.wait_ge(dve_o.sem, dve_o.at(f"picked{n}", i))
            dve.wait_ge(pool_y.sem, back(pool_y, "y", n, i, 2))
            dve.tensor_tensor(both[s][:], o[:, :, 0:KV * HD].rearrange("p j (k d) -> p j k d", k=KV), cols(picked[s][:].unsqueeze(3), HD),
                              ALU.mult).then_inc(dve_o.mark(f"both{n}"), 1)

        def one_pass(i, end=False):
            for n in range(NU):
                if not (end and n + 3 >= NU):
                    rotate(n + 3, i)
                if not (end and n + 2 >= NU):
                    shift(n + 2, i)
                normalise(n, i)

        for n in range(3):
            rotate(n, 0)
        for n in range(2):
            shift(n, 0)
        with dve.Fori(0, NP - 1) as i:
            one_pass(i)
        one_pass(NP - 1, end=True)
        phase_end(m, dve, ph)

    def gpsimd(pool):
        pool_r.start(pool)
        pool_y.start(pool)
        pool.wait_ge(dve_w.sem, dve_w.at("ones"))

        def rotate(n, i):
            n, i = wrapped(n, i)
            s = n % 2
            pool.wait_ge(dve_r.sem, dve_r.at(f"sin{n}", i))
            pool.wait_ge(pe_sc.sem, back(pe_sc, "s", n, i, 2))
            pool.wait_ge(pool_r.sem, back(pool_r, "k", n, i, 1))
            pool.wait_ge(pool_y.sem, pool_y.before(f"y{n}", i))
            pool.sem_inc(m.gate, 1)
            for h in range(H):
                r = slice(R * h, R * h + R)
                pool.tensor_tensor(qz[s][r, :, h], t1[s][r, 0:T], t2[s][r, 0:T], ALU.add).then_inc(pool_r.mark(f"q{h}_{n}"), 1)
            pool.wait_ge(pool_r.sem, pool_r.at(f"q{H - 1}_{n}", i))
            pool.tensor_tensor(kk[s][:], t1[s][:, T:2 * T], t2[s][:, T:2 * T], ALU.add).then_inc(pool_r.mark(f"k{n}"), 1)

        def pick_sum(n, i, rotated):
            if rotated:
                n3, i3 = wrapped(n + 3, i)
                pool.wait_ge(pool_r.sem, pool_r.at(f"k{n3}", i3))
            pool.wait_ge(dve_o.sem, dve_o.at(f"both{n}", i))
            pool.wait_ge(stored[n].sem, stored[n].before(i))
            pool.sem_inc(m.gate, 1)
            pool.tensor_tensor(y[n][:], both[n % 2][:, :, 0], both[n % 2][:, :, 1], ALU.add).then_inc(pool_y.mark(f"y{n}"), 1)

        def one_pass(i, end=False):
            for n in range(NU):
                rotated = not (end and n + 3 >= NU)
                if rotated:
                    rotate(n + 3, i)
                pick_sum(n, i, rotated)

        for n in range(3):
            rotate(n, 0)
        with pool.Fori(0, NP - 1) as i:
            one_pass(i)
        one_pass(NP - 1, end=True)
        phase_end(m, pool, ph)

    return dict(sync=sync, tensor=tensor, scalar=scalar, vector=vector, gpsimd=gpsimd)


def causal_out_phase(nc, m, st, ph):
    J, NE = NB * T // TM, 8
    sb = lambda n, s, d=F32: st.enter_context(nc.sbuf_tensor(n, s, d))
    wo, woT = sb("fo_wo", [C, C]), sb("fo_wot", [C, C])
    rw, rT, l2 = sb("fo_router", [NE, C]), sb("fo_router_t", [C, NE]), sb("fo_ln2", [C, 1])
    yr = [sb(f"fo_y{s}", [TM, GJ, C]) for s in range(2)]
    yt = [sb(f"fo_yt{s}", [C, GT]) for s in range(2)]
    sq = [sb(f"fo_sq{k}", [TM, J // 4, C]) for k in range(2)]
    mean, ss, eps_rms = sb("fo_mean", [TM, J]), sb("fo_ss", [TM, J]), sb("fo_eps_rms", [128, 1])
    zt = [sb(f"fo_z{s}", [TM, GJ, C]) for s in range(2)]
    zT = [sb(f"fo_zt{s}", [C, GT]) for s in range(2)]
    lg, pr, eq, one1, one2 = (sb(f"fo_{n}", [TM, J, NE]) for n in ("logits", "probs", "eq", "one1", "one2"))
    desc = sb("fo_desc", [TM, NE])
    mx, rs, p2, ws = (sb(f"fo_{n}", [TM, J]) for n in ("mx", "rs", "p2", "ws"))
    ps = m.psum
    P = NG // 2
    S1 = lambda n, steps: Steps(nc, m.whole, n, steps)
    wl = m.whole.enter_context(nc.semaphore("fo_weights_landed"))
    yl = [Landed(nc, m.whole, f"fo_y_landed{s}", 2) for s in range(2)]
    stored = [Landed(nc, m.whole, f"fo_z_stored{s}", 1) for s in range(2)]
    pe_w, act_w, dve_w = S1("fo_pe_w", ["wot", "rt"]), S1("fo_act_w", ["wot", "rt"]), S1("fo_dve_w", ["eps"])
    pe_y, act_y = S1("fo_pe_y", ["y0", "y1"]), S1("fo_act_y", ["y0", "y1"])
    pe_s, dve_s = S1("fo_pe", ["o0", "o1"]), S1("fo_dve", ["y0", "y1"])
    dve_n = S1("fo_dve_norm", [f"r_ss{k}" for k in range(4)] + ["r_recip", "h"])
    act_n = S1("fo_act_norm", [f"r_{k}" for k in NORM_ACT])
    pe_z, act_z, dve_z = S1("fo_pe_z", ["z0", "z1"]), S1("fo_act_z", ["z0", "z1"]), S1("fo_dve_z", ["z0", "z1"])
    pe_l, dve_l = S1("fo_pe_logits", ["l0", "l1"]), S1("fo_dve_logits", ["l0", "l1"])
    dve_g = S1("fo_dve_gates", ["max", "minus", "sum", "recip", "probs", "p1", "eq1", "cand1", "best1", "one1", "rest", "p2",
                                "eq2", "cand2", "best2", "one2", "wsum", "wrecip", "both", "picked", "gates"])
    act_g = S1("fo_act_gates", ["exp"])

    def sync(sp):
        for s in range(2):
            yl[s].start(sp)
            stored[s].start(sp)
        sp.dma_start(wo[:], m.dram["ffn_wo"]).then_inc(wl, 16)
        sp.dma_start(rw[:], m.dram["ffn_router_w"]).then_inc(wl, 16)
        sp.dma_start(l2[:], m.dram["ffn_ln2_w"].rearrange("(c o) -> c o", o=1)).then_inc(wl, 16)
        sp.dma_start(desc[:], m.dram["descending"].partition_broadcast(TM)).then_inc(wl, 16)
        with sp.Fori(0, P) as i:
            for s in range(2):
                sp.wait_ge(pe_y.sem, pe_y.before(f"y{s}", i))
                sp.sem_inc(m.gate, 1)
                rows = m.dram["y_d"].rearrange("b (t c) -> (b t) c", c=C)[bass.ds(i * 2 * GT + s * GT, GT)].rearrange("(j p) c -> p j c", p=TM)
                for p0, p1 in ((0, 112), (112, TM)):
                    sp.dma_start(yr[s][p0:p1], rows[p0:p1]).then_inc(yl[s].sem, 16)
        with sp.Fori(0, P) as i:
            for s in range(2):
                sp.wait_ge(act_z.sem, act_z.at(f"z{s}", i))
                sp.sem_inc(m.gate, 1)
                sp.dma_start(m.dram["zt_d"][:, bass.ds(i * 2 * GT + s * GT, GT)], zT[s][:]).then_inc(stored[s].sem, 16)
        for s in range(2):
            sp.wait_ge(stored[s].sem, stored[s].at(P - 1))
        phase_end(m, sp, ph)

    def tensor(pe):
        for S in (pe_w, pe_y, pe_s, pe_z, pe_l):
            S.start(pe)
        pe.wait_ge(wl, 64)
        pe.transpose(ps[0:C, 0, 0:C], wo[:], m.ident[0:C, 0:C]).then_inc(pe_w.mark("wot"), 1)
        pe.transpose(ps[0:C, 1, 0:NE], rw[:], m.ident[0:NE, 0:NE]).then_inc(pe_w.mark("rt"), 1)
        pe.wait_ge(act_w.sem, act_w.at("rt"))
        with pe.Fori(0, P) as i:
            for s in range(2):
                pe.wait_ge(yl[s].sem, yl[s].at(i))
                pe.wait_ge(act_y.sem, act_y.before(f"y{s}", i))
                pe.sem_inc(m.gate, 1)
                for j in range(GJ):
                    mm = pe.transpose(ps[0:C, 2 + 2 * s + j // 4, j % 4 * TM:j % 4 * TM + TM], yr[s][:, j, :], m.ident[0:TM, 0:TM])
                mm.then_inc(pe_y.mark(f"y{s}"), 1)
            for s in range(2):
                pe.wait_ge(act_y.sem, act_y.at(f"y{s}", i))
                pe.wait_ge(dve_s.sem, dve_s.before(f"y{s}", i))
                pe.sem_inc(m.gate, 1)
                for j in range(GJ):
                    mm = pe.matmul(ps[0:TM, s, j * C:(j + 1) * C], yt[s][:, j * TM:(j + 1) * TM], woT[:], start=True, stop=True)
                mm.then_inc(pe_s.mark(f"o{s}"), 1)
        with pe.Fori(0, P) as i:
            for s in range(2):
                pe.wait_ge(dve_z.sem, dve_z.at(f"z{s}", i))
                pe.wait_ge(act_z.sem, act_z.before(f"z{s}", i))
                pe.sem_inc(m.gate, 1)
                for j in range(GJ):
                    mm = pe.transpose(ps[0:C, 2 * s + j // 4, j % 4 * TM:j % 4 * TM + TM], zt[s][:, j, :], m.ident[0:TM, 0:TM])
                mm.then_inc(pe_z.mark(f"z{s}"), 1)
                pe.wait_ge(act_z.sem, act_z.at(f"z{s}", i))
                pe.wait_ge(dve_l.sem, dve_l.before(f"l{s}", i))
                pe.sem_inc(m.gate, 1)
                for j in range(GJ):
                    mm = pe.matmul(ps[0:TM, 4 + s, j * NE:(j + 1) * NE], zT[s][:, j * TM:(j + 1) * TM], rT[:], start=True, stop=True)
                mm.then_inc(pe_l.mark(f"l{s}"), 1)
        phase_end(m, pe, ph)

    def scalar(act):
        for S in (act_w, act_y, act_n, act_z, act_g):
            S.start(act)
        act.wait_ge(wl, 64)
        act.wait_ge(pe_w.sem, pe_w.at("rt"))
        act.activation(woT[:], ps[0:C, 0, 0:C], ACT.Copy).then_inc(act_w.mark("wot"), 1)
        act.activation(rT[:], ps[0:C, 1, 0:NE], ACT.Copy, scale=l2[:]).then_inc(act_w.mark("rt"), 1)
        with act.Fori(0, P) as i:
            for s in range(2):
                act.wait_ge(pe_y.sem, pe_y.at(f"y{s}", i))
                act.wait_ge(pe_s.sem, pe_s.before(f"o{s}", i))
                act.activation(yt[s][:, 0:4 * TM], ps[0:C, 2 + 2 * s, 0:4 * TM], ACT.Copy)
                act.activation(yt[s][:, 4 * TM:GT], ps[0:C, 3 + 2 * s, 0:TM], ACT.Copy).then_inc(act_y.mark(f"y{s}"), 1)
        act.wait_ge(dve_s.sem, dve_s.at("y1", P - 1))
        for k in range(4):
            j = slice(J // 4 * k, J // 4 * (k + 1))
            if k >= 2:
                act.wait_ge(dve_n.sem, dve_n.at(f"r_ss{k - 2}"))
            act.activation(sq[k % 2][:], m.y[:, j], ACT.Square).then_inc(act_n.mark(f"r_sq{k}"), 1)
        act.wait_ge(dve_n.sem, dve_n.at("r_ss3"))
        act.activation(mean[:], ss[:], ACT.Sqrt, bias=eps_rms[0:TM], scale=1.0 / C).then_inc(act_n.mark("r_std"), 1)
        with act.Fori(0, P) as i:
            for s in range(2):
                act.wait_ge(pe_z.sem, pe_z.at(f"z{s}", i))
                act.wait_ge(stored[s].sem, stored[s].before(i))
                act.wait_ge(pe_l.sem, pe_l.before(f"l{s}", i))
                act.activation(zT[s][:, 0:4 * TM], ps[0:C, 2 * s, 0:4 * TM], ACT.Copy)
                act.activation(zT[s][:, 4 * TM:GT], ps[0:C, 2 * s + 1, 0:TM], ACT.Copy).then_inc(act_z.mark(f"z{s}"), 1)
        act.wait_ge(dve_g.sem, dve_g.at("minus"))
        act.activation(pr[:], lg[:], ACT.Exp).then_inc(act_g.mark("exp"), 1)
        phase_end(m, act, ph)

    def vector(dve):
        for S in (dve_w, dve_s, dve_n, dve_z, dve_l, dve_g):
            S.start(dve)
        dve.memset(eps_rms[:], 1e-6).then_inc(dve_w.mark("eps"), 1)
        with dve.Fori(0, P) as i:
            for s in range(2):
                at = bass.ds(i * 2 * GJ + s * GJ, GJ)
                dve.wait_ge(pe_s.sem, pe_s.at(f"o{s}", i))
                dve.tensor_tensor(m.y[:, at, :], ps[0:TM, s, 0:GJ * C].rearrange("p (j c) -> p j c", c=C), m.y[:, at, :], ALU.add).then_inc(dve_s.mark(f"y{s}"), 1)
        dve.wait_ge(dve_s.sem, dve_s.at("y1", P - 1))
        for k in range(4):
            j = slice(J // 4 * k, J // 4 * (k + 1))
            dve.wait_ge(act_n.sem, act_n.at(f"r_sq{k}"))
            dve.tensor_reduce(ss[:, j], sq[k % 2][:], X, ALU.add).then_inc(dve_n.mark(f"r_ss{k}"), 1)
        dve.wait_ge(act_n.sem, act_n.at("r_std"))
        dve.reciprocal(ss[:], mean[:]).then_inc(dve_n.mark("r_recip"), 1)
        dve.tensor_tensor(m.h[:], m.h[:], m.y[:], ALU.add).then_inc(dve_n.mark("h"), 1)
        dve.wait_ge(dve_n.sem, dve_n.at("h"))
        with dve.Fori(0, P) as i:
            for s in range(2):
                at = bass.ds(i * 2 * GJ + s * GJ, GJ)
                dve.wait_ge(pe_z.sem, pe_z.before(f"z{s}", i))
                dve.tensor_tensor(zt[s][:], m.y[:, at, :], cols(ss[:, at].unsqueeze(2), C), ALU.mult).then_inc(dve_z.mark(f"z{s}"), 1)
                dve.wait_ge(pe_l.sem, pe_l.at(f"l{s}", i))
                dve.tensor_scalar(lg[:, at, :], ps[0:TM, 4 + s, 0:GJ * NE].rearrange("p (j e) -> p j e", e=NE), 1.0, None, ALU.mult).then_inc(dve_l.mark(f"l{s}"), 1)
        S = dve_g
        wide = lambda v: cols(v[:].unsqueeze(2), NE)
        place = desc[:].unsqueeze(1).broadcast_to([TM, J, NE])
        dve.wait_ge(wl, 64)
        dve.wait_ge(dve_l.sem, dve_l.at("l1", P - 1))
        dve.tensor_reduce(mx[:], lg[:], X, ALU.max).then_inc(S.mark("max"), 1)
        dve.wait_ge(S.sem, S.at("max"))
        dve.tensor_tensor(lg[:], lg[:], wide(mx), ALU.subtract).then_inc(S.mark("minus"), 1)
        dve.wait_ge(act_g.sem, act_g.at("exp"))
        dve.tensor_reduce(rs[:], pr[:], X, ALU.add).then_inc(S.mark("sum"), 1)
        dve.wait_ge(S.sem, S.at("sum"))
        dve.reciprocal(mx[:], rs[:]).then_inc(S.mark("recip"), 1)
        dve.wait_ge(S.sem, S.at("recip"))
        dve.tensor_tensor(pr[:], pr[:], wide(mx), ALU.mult).then_inc(S.mark("probs"), 1)
        dve.wait_ge(S.sem, S.at("probs"))
        dve.tensor_reduce(mx[:], pr[:], X, ALU.max).then_inc(S.mark("p1"), 1)
        dve.wait_ge(S.sem, S.at("p1"))
        dve.tensor_tensor(eq[:], pr[:], wide(mx), ALU.is_equal).then_inc(S.mark("eq1"), 1)
        dve.wait_ge(S.sem, S.at("eq1"))
        dve.tensor_tensor(eq[:], eq[:], place, ALU.mult).then_inc(S.mark("cand1"), 1)
        dve.wait_ge(S.sem, S.at("cand1"))
        dve.tensor_reduce(rs[:], eq[:], X, ALU.max).then_inc(S.mark("best1"), 1)
        dve.wait_ge(S.sem, S.at("best1"))
        dve.tensor_tensor(one1[:], place, wide(rs), ALU.is_equal).then_inc(S.mark("one1"), 1)
        dve.wait_ge(S.sem, S.at("one1"))
        dve.scalar_tensor_tensor(out=lg[:], in0=one1[:], scalar=-2.0, in1=pr[:], op0=ALU.mult, op1=ALU.add).then_inc(S.mark("rest"), 1)
        dve.wait_ge(S.sem, S.at("rest"))
        dve.tensor_reduce(p2[:], lg[:], X, ALU.max).then_inc(S.mark("p2"), 1)
        dve.wait_ge(S.sem, S.at("p2"))
        dve.tensor_tensor(eq[:], lg[:], wide(p2), ALU.is_equal).then_inc(S.mark("eq2"), 1)
        dve.wait_ge(S.sem, S.at("eq2"))
        dve.tensor_tensor(eq[:], eq[:], place, ALU.mult).then_inc(S.mark("cand2"), 1)
        dve.wait_ge(S.sem, S.at("cand2"))
        dve.tensor_reduce(rs[:], eq[:], X, ALU.max).then_inc(S.mark("best2"), 1)
        dve.wait_ge(S.sem, S.at("best2"))
        dve.tensor_tensor(one2[:], place, wide(rs), ALU.is_equal).then_inc(S.mark("one2"), 1)
        dve.scalar_tensor_tensor(out=ws[:], in0=mx[:], scalar=1e-9, in1=p2[:], op0=ALU.add, op1=ALU.add).then_inc(S.mark("wsum"), 1)
        dve.wait_ge(S.sem, S.at("wsum"))
        dve.reciprocal(rs[:], ws[:]).then_inc(S.mark("wrecip"), 1)
        dve.wait_ge(S.sem, S.at("wrecip"))
        dve.tensor_tensor(one1[:], one1[:], one2[:], ALU.add).then_inc(S.mark("both"), 1)
        dve.wait_ge(S.sem, S.at("both"))
        dve.tensor_tensor(one1[:], one1[:], pr[:], ALU.mult).then_inc(S.mark("picked"), 1)
        dve.wait_ge(S.sem, S.at("picked"))
        dve.tensor_tensor(m.gates[:], one1[:], wide(rs), ALU.mult).then_inc(S.mark("gates"), 1)
        phase_end(m, dve, ph)

    def gpsimd(pool):
        phase_end(m, pool, ph)

    return dict(sync=sync, tensor=tensor, scalar=scalar, vector=vector, gpsimd=gpsimd)


def experts_phase(nc, m, st, ph):
    NE, HID, KH, N = 8, 170, 85, 2 * TM
    J = NB * T // TM
    R = 3
    P = J // 2 // R
    assert J // 2 == R * P + 1
    NU = R * NE
    GT5 = J * NE // 128
    sb = lambda n, s, d=F32: st.enter_context(nc.sbuf_tensor(n, s, d))
    w13, w2 = sb("ex_w13", [KH, NE, 2, 2, 2, C]), sb("ex_w2", [C, NE, HID])
    rest = sb("ex_w_rest", [2 * C, NE, 4, KH])
    w_hi, w_mid, w_low = (sb(f"ex_w_{n}", [2 * C, NE, 4, KH], BF16) for n in ("hi", "mid", "low_hi"))
    w2T = sb("ex_w2t", [KH, NE, 2, C])
    l2 = sb("ex_ln2", [2 * C, 1])
    gT = sb("ex_gates_turned", [128, GT5, TM])
    z = [sb(f"ex_z{s}", [2 * C, N]) for s in range(R)]
    z_hi, z_rest = sb("ex_z_hi", [2 * C, N], BF16), sb("ex_z_rest", [2 * C, N])
    z_him, z_hil = ([sb(f"ex_z_{n}{s}", [2 * C, N], BF16) for s in range(R)] for n in ("hi_mid", "hi_low"))
    gate_rows = [sb(f"ex_gate_rows{s}", [KH, 2, NE, TM]) for s in range(R)]
    silu = [sb(f"ex_silu{k}", [KH, 2 * N]) for k in range(3)]
    gated = [sb(f"ex_gated{k}", [KH, 2, N]) for k in range(3)]
    hid = [sb(f"ex_hid{k}", [KH, 2, N]) for k in range(3)]
    outT = [sb(f"ex_out_t{s}", [C, N]) for s in range(R)]
    turned = [sb(f"ex_turned{s}", [TM, 2, C]) for s in range(R)]
    res = [sb(f"ex_out{s}", [TM, 2, C]) for s in range(R)]
    ps = m.psum
    OUT, TURNED = 6, 7
    S1 = lambda n, steps: Steps(nc, m.whole, n, steps)
    wl = m.whole.enter_context(nc.semaphore("ex_weights_landed"))
    gates_stored = m.whole.enter_context(nc.semaphore("ex_gates_stored"))
    zl = [Landed(nc, m.whole, f"ex_z_landed{s}", 3) for s in range(R)]
    stored = [Landed(nc, m.whole, f"ex_stored{s}", 2) for s in range(R)]
    pe_w, act_w = S1("ex_pe_w", ["gates"] + [f"w{e}" for e in range(NE)]), S1("ex_act_w", ["gates"] + [f"w{e}" for e in range(NE)])
    pe_u = S1("ex_pe_up", [f"{g}{n}" for n in range(NU) for g in ("silu", "up")])
    pe_d = S1("ex_pe_down", [f"d{n}" for n in range(NU)])
    pe_t = S1("ex_pe_turned", [f"t{s}" for s in range(R)])
    act_s = S1("ex_act_silu", [f"s{n}" for n in range(NU)])
    act_o = S1("ex_act_out", [f"o{s}" for s in range(R)])
    act_t = S1("ex_act_turned", [f"t{s}" for s in range(R)])
    dve_w = S1("ex_dve_w", ["hi", "rest", "mid", "rest2", "low", "low_hi"])
    dve_g = S1("ex_dve_gated", [f"g{n}" for n in range(NU)])
    parts = ["hi", "rest", "mid", "rest2", "low", "hi_mid", "hi_low"]
    pool_z = S1("ex_pool_parts", [f"{n}{s}" for s in range(R) for n in parts])
    dve_h = S1("ex_dve_hidden", [f"h{n}" for n in range(NU)])
    pool_o = S1("ex_pool_out", [f"o{s}" for s in range(R)])

    def wrapped(n, i):
        return (n, i) if n < NU else (n - NU, i + 1)

    def back(S, k, n, i, by):
        return S.at(f"{k}{n - by}", i) if n >= by else S.before(f"{k}{n - by + NU}", i)

    def sync(sp):
        for s in range(R):
            zl[s].start(sp)
            stored[s].start(sp)
        for k, w in enumerate(("ffn_w1", "ffn_w3")):
            for t in range(2):
                for twice in range(2):
                    sp.dma_start(w13[:, :, k, t, twice], m.dram[w][:, t * KH:(t + 1) * KH].rearrange("e k c -> k e c")).then_inc(wl, 16)
        sp.dma_start(w2[:], m.dram["ffn_w2"].rearrange("e c k -> c e k")).then_inc(wl, 16)
        for k in range(2):
            sp.dma_start(l2[C * k:C * k + C], m.dram["ffn_ln2_w"].rearrange("(c o) -> c o", o=1)).then_inc(wl, 16)
        sp.wait_ge(act_w.sem, act_w.at("gates"))
        sp.dma_start(m.dram["gates_d"].rearrange("(b q) p -> q b p", q=128), gT[:]).then_inc(gates_stored, 16)
        sp.wait_ge(gates_stored, 16)

        def load(s, i):
            sp.wait_ge(pool_z.sem, pool_z.before(f"hi_low{s}", i))
            sp.sem_inc(m.gate, 1)
            sp.wait_ge(dve_g.sem, dve_g.before(f"g{s * NE + NE - 1}", i))
            sp.sem_inc(m.gate, 1)
            for k in range(2):
                sp.dma_start(z[s][C * k:C * k + C], m.dram["zt_d"][:, bass.ds(i * R * N + s * N, N)]).then_inc(zl[s].sem, 16)
            rows = m.dram["gates_d"][bass.ds(i * R * 2 * NE + s * 2 * NE, 2 * NE)].rearrange("(o r) p -> o (r p)", o=1)
            sp.dma_start(gate_rows[s][:].rearrange("c j e p -> c (j e p)"), rows.broadcast_to([KH, 2 * NE * TM])).then_inc(zl[s].sem, 16)

        def store(s, i, ready):
            sp.wait_ge(pool_o.sem, ready)
            sp.sem_inc(m.gate, 1)
            dst = m.out.rearrange("b t c -> (b t) c")[bass.ds(i * R * N + s * N, N)].rearrange("(j p) c -> p j c", p=TM)
            for p0, p1 in ((0, 112), (112, TM)):
                sp.dma_start(dst[p0:p1], res[s][p0:p1]).then_inc(stored[s].sem, 16)

        for s in range(R):
            load(s, 0)
        with sp.Fori(1, P) as i:
            for s in range(R):
                load(s, i)
                store(s, i - 1, pool_o.before(f"o{s}", i))
        load(0, P)
        for s in range(R):
            store(s, P - 1, pool_o.at(f"o{s}", P - 1))
        store(0, P, pool_o.at("o0", P))
        sp.wait_ge(stored[0].sem, stored[0].at(P))
        for s in range(1, R):
            sp.wait_ge(stored[s].sem, stored[s].at(P - 1))
        phase_end(m, sp, ph)

    def tensor(pe):
        for S in (pe_w, pe_u, pe_d, pe_t):
            S.start(pe)
        for b in range(GT5):
            mm = pe.transpose(ps[:, 4 + b // 4, b % 4 * TM:b % 4 * TM + TM], m.gates[:, 16 * b:16 * b + 16, :].rearrange("p j e -> p (j e)"), m.ident[0:TM, 0:TM])
        mm.then_inc(pe_w.mark("gates"), 1)
        pe.wait_ge(wl, 16 * 11)
        for e in range(NE):
            if e >= 2:
                pe.wait_ge(act_w.sem, act_w.at(f"w{e - 2}"))
            b = 2 * (e % 2)
            for t in range(2):
                for k in range(2):
                    pe.transpose(ps[:, b, (2 * k + t) * KH:(2 * k + t + 1) * KH], w13[:, e, k, t].rearrange("k w c -> k (w c)"), m.ident[0:KH, 0:KH])
                mm = pe.transpose(ps[0:KH, b + 1, t * C:(t + 1) * C], w2[:, e, t * KH:(t + 1) * KH], m.ident[0:C, 0:C])
            mm.then_inc(pe_w.mark(f"w{e}"), 1)
        pe.wait_ge(act_w.sem, act_w.at(f"w{NE - 1}"))
        pe.wait_ge(dve_w.sem, dve_w.at("low_hi"))

        def up(n, i):
            n, i = wrapped(n, i)
            s, e = divmod(n, NE)
            if e == 0:
                pe.wait_ge(pool_z.sem, pool_z.at(f"hi_low{s}", i))
            pe.wait_ge(dve_h.sem, back(dve_h, "h", n, i, 3))
            pe.sem_inc(m.gate, 1)
            b = 2 * (n % 3)
            for k, name in enumerate(("silu", "up")):
                for t in range(2):
                    for w, x in ((w_hi, z_him), (w_mid, z_him), (w_low, z_hil)):
                        mm = pe.matmul(ps[0:KH, b + k, t * N:(t + 1) * N], w[:, e, 2 * k + t, :], x[s][:], start=w is w_hi, stop=w is w_low)
                mm.then_inc(pe_u.mark(f"{name}{n}"), 1)

        def down(n, i):
            s, e = divmod(n, NE)
            pe.wait_ge(dve_h.sem, dve_h.at(f"h{n}", i))
            if e == 0:
                pe.wait_ge(act_o.sem, act_o.at(f"o{s - 1}", i) if s else act_o.before(f"o{R - 1}", i))
            pe.sem_inc(m.gate, 1)
            for t in range(2):
                mm = pe.matmul(ps[0:C, OUT, 0:N], w2T[:, e, t, :], hid[n % 3][:, t], start=e == 0 and t == 0, stop=e == NE - 1 and t == 1)
            mm.then_inc(pe_d.mark(f"d{n}"), 1)

        def turn(s, i):
            pe.wait_ge(act_o.sem, act_o.at(f"o{s}", i))
            pe.wait_ge(act_t.sem, act_t.at(f"t{s - 1}", i) if s else act_t.before(f"t{R - 1}", i))
            pe.sem_inc(m.gate, 1)
            for j in range(2):
                mm = pe.transpose(ps[0:TM, TURNED, j * C:(j + 1) * C], outT[s][:, j * TM:(j + 1) * TM], m.ident[0:C, 0:C])
            mm.then_inc(pe_t.mark(f"t{s}"), 1)

        def one_pass(i, units=NU, end=False):
            for n in range(units):
                if n % NE and not (end and n + 2 >= units):
                    up(n + 2, i)
                down(n, i)
                if n % NE == NE - 1:
                    if not end:
                        up(n + 3, i)
                    turn(n // NE, i)

        for n in range(3):
            up(n, 0)
        with pe.Fori(0, P) as i:
            one_pass(i)
        one_pass(P, NE, end=True)
        phase_end(m, pe, ph)

    def scalar(act):
        for S in (act_w, act_s, act_o, act_t):
            S.start(act)
        act.wait_ge(pe_w.sem, pe_w.at("gates"))
        act.activation(gT[:, 0:4], ps[:, 4, 0:4 * TM].rearrange("q (b p) -> q b p", b=4), ACT.Copy)
        act.activation(gT[:, 4], ps[:, 5, 0:TM], ACT.Copy).then_inc(act_w.mark("gates"), 1)
        act.wait_ge(wl, 16 * 11)
        for e in range(NE):
            b = 2 * (e % 2)
            act.wait_ge(pe_w.sem, pe_w.at(f"w{e}"))
            act.activation(rest[:, e], ps[:, b, 0:4 * KH].rearrange("c (t k) -> c t k", t=4), ACT.Copy, scale=l2[:])
            act.activation(w2T[:, e], ps[0:KH, b + 1, 0:2 * C].rearrange("c (t k) -> c t k", t=2), ACT.Copy).then_inc(act_w.mark(f"w{e}"), 1)
        act.preload_act_table(ACT.Silu)

        def silu_of(n, i):
            n, i = wrapped(n, i)
            act.wait_ge(pe_u.sem, pe_u.at(f"silu{n}", i))
            act.wait_ge(dve_h.sem, back(dve_h, "h", n, i, 3))
            act.activation(silu[n % 3][:], ps[0:KH, 2 * (n % 3), 0:2 * N], ACT.Silu).then_inc(act_s.mark(f"s{n}"), 1)

        def one_pass(i, units=NU, end=False):
            for n in range(units):
                if n % NE and not (end and n + 2 >= units):
                    silu_of(n + 2, i)
                if n % NE == NE - 1:
                    s = n // NE
                    act.wait_ge(pe_d.sem, pe_d.at(f"d{n}", i))
                    act.wait_ge(pe_t.sem, pe_t.before(f"t{s}", i))
                    act.activation(outT[s][:], ps[0:C, OUT, 0:N], ACT.Copy).then_inc(act_o.mark(f"o{s}"), 1)
                    if not end:
                        silu_of(n + 3, i)
                    act.wait_ge(pe_t.sem, pe_t.at(f"t{s}", i))
                    act.wait_ge(pool_o.sem, pool_o.before(f"o{s}", i))
                    act.activation(turned[s][:], ps[0:TM, TURNED, 0:2 * C].rearrange("p (j c) -> p j c", j=2), ACT.Copy).then_inc(act_t.mark(f"t{s}"), 1)

        for n in range(3):
            silu_of(n, 0)
        with act.Fori(0, P) as i:
            one_pass(i)
        one_pass(P, NE, end=True)
        phase_end(m, act, ph)

    def vector(dve):
        for S in (dve_w, dve_g, dve_h):
            S.start(dve)
        dve.wait_ge(act_w.sem, act_w.at(f"w{NE - 1}"))
        dve.tensor_copy(w_hi[:], rest[:]).then_inc(dve_w.mark("hi"), 1)
        dve.wait_ge(dve_w.sem, dve_w.at("hi"))
        dve.tensor_tensor(rest[:], rest[:], w_hi[:], ALU.subtract).then_inc(dve_w.mark("rest"), 1)
        dve.wait_ge(dve_w.sem, dve_w.at("rest"))
        dve.tensor_copy(w_mid[:], rest[:]).then_inc(dve_w.mark("mid"), 1)
        dve.wait_ge(dve_w.sem, dve_w.at("mid"))
        dve.tensor_tensor(rest[:], rest[:], w_mid[:], ALU.subtract).then_inc(dve_w.mark("rest2"), 1)
        dve.wait_ge(dve_w.sem, dve_w.at("rest2"))
        dve.tensor_copy(w_low[0:C], rest[0:C]).then_inc(dve_w.mark("low"), 1)
        dve.tensor_copy(w_low[C:2 * C], w_hi[C:2 * C]).then_inc(dve_w.mark("low_hi"), 1)

        def hidden(n, i):
            s, e = divmod(n, NE)
            if e == 0:
                dve.wait_ge(zl[s].sem, zl[s].at(i))
            dve.wait_ge(act_s.sem, act_s.at(f"s{n}", i))
            dve.tensor_tensor(gated[n % 3][:].rearrange("k t (j p) -> k t j p", j=2), silu[n % 3][:].rearrange("k (t j p) -> k t j p", t=2, j=2),
                              gate_rows[s][:, :, e].unsqueeze(1).broadcast_to([KH, 2, 2, TM]), ALU.mult).then_inc(dve_g.mark(f"g{n}"), 1)
            dve.wait_ge(dve_g.sem, dve_g.at(f"g{n}", i))
            dve.wait_ge(pe_u.sem, pe_u.at(f"up{n}", i))
            dve.wait_ge(pe_d.sem, back(pe_d, "d", n, i, 3))
            dve.tensor_tensor(hid[n % 3][:].rearrange("k t n -> k (t n)"), ps[0:KH, 2 * (n % 3) + 1, 0:2 * N], gated[n % 3][:].rearrange("k t n -> k (t n)"), ALU.mult).then_inc(dve_h.mark(f"h{n}"), 1)

        def one_pass(i, units=NU, end=False):
            for n in range(units):
                hidden(n, i)

        with dve.Fori(0, P) as i:
            one_pass(i)
        one_pass(P, NE, end=True)
        phase_end(m, dve, ph)

    def gpsimd(pool):
        pool_o.start(pool)
        pool_z.start(pool)

        def split(s, i):
            top, low = slice(0, C), slice(C, 2 * C)
            step = lambda n: pool_z.at(f"{n}{s}", i)
            pool.wait_ge(zl[s].sem, zl[s].at(i))
            pool.wait_ge(pe_u.sem, pe_u.before(f"up{s * NE + NE - 1}", i))
            pool.sem_inc(m.gate, 1)
            pool.tensor_copy(z_hi[:], z[s][:]).then_inc(pool_z.mark(f"hi{s}"), 1)
            pool.wait_ge(pool_z.sem, step("hi"))
            pool.sem_inc(m.gate, 1)
            pool.tensor_tensor(z_rest[:], z[s][:], z_hi[:], ALU.subtract).then_inc(pool_z.mark(f"rest{s}"), 1)
            pool.wait_ge(pool_z.sem, step("rest"))
            pool.sem_inc(m.gate, 1)
            pool.tensor_copy(z_him[s][low], z_rest[low]).then_inc(pool_z.mark(f"mid{s}"), 1)
            pool.wait_ge(pool_z.sem, step("mid"))
            pool.sem_inc(m.gate, 1)
            pool.tensor_tensor(z_rest[low], z_rest[low], z_him[s][low], ALU.subtract).then_inc(pool_z.mark(f"rest2{s}"), 1)
            pool.wait_ge(pool_z.sem, step("rest2"))
            pool.sem_inc(m.gate, 1)
            pool.tensor_copy(z_hil[s][low], z_rest[low]).then_inc(pool_z.mark(f"low{s}"), 1)
            pool.tensor_copy(z_him[s][top], z_hi[top]).then_inc(pool_z.mark(f"hi_mid{s}"), 1)
            pool.tensor_copy(z_hil[s][top], z_hi[top]).then_inc(pool_z.mark(f"hi_low{s}"), 1)
            pool.wait_ge(pool_z.sem, step("hi_low"))
            pool.sem_inc(m.gate, 1)

        def finish(s, i):
            pool.wait_ge(act_t.sem, act_t.at(f"t{s}", i))
            pool.wait_ge(stored[s].sem, stored[s].before(i))
            pool.sem_inc(m.gate, 1)
            pool.tensor_tensor(res[s][:], turned[s][:], m.h[:, bass.ds(i * 2 * R + 2 * s, 2), :], ALU.add).then_inc(pool_o.mark(f"o{s}"), 1)

        for s in range(R):
            split(s, 0)
        with pool.Fori(0, P - 1) as i:
            for s in range(R):
                finish(s, i)
                split(s, i + 1)
        for s in range(R):
            finish(s, P - 1)
            if s == 0:
                split(0, P)
        finish(0, P)
        phase_end(m, pool, ph)

    return dict(sync=sync, tensor=tensor, scalar=scalar, vector=vector, gpsimd=gpsimd)


PHASES = [patch_phase, vit_phase, text_phase, joint_in_phase, joint_phase, joint_out_phase, causal_phase, causal_out_phase, experts_phase]
DEBUG = False





def program(nc, dram, scratch, out):
    with ExitStack() as whole:
        m = Shared({**dram, **scratch})
        m.out = out
        m.whole = whole
        m.psum = whole.enter_context(nc.psum_tensor("banks", [128, 8, BANK], F32))
        m.ident = whole.enter_context(nc.sbuf_tensor("ident", [128, 128], F32))
        m.phase_done = whole.enter_context(nc.semaphore("phase_done"))
        m.gate = whole.enter_context(nc.semaphore("gate"))
        m.ident_landed = whole.enter_context(nc.semaphore("ident_landed"))
        m.vit_x = whole.enter_context(nc.sbuf_tensor("vit_x", [128, 16, C], F32))
        m.pos_tile = whole.enter_context(nc.sbuf_tensor("pos_tile", [128, C], F32))
        m.h = whole.enter_context(nc.sbuf_tensor("h", [TM, NB * T // TM, C], F32))
        m.y = whole.enter_context(nc.sbuf_tensor("y", [TM, NB * T // TM, C], F32))
        m.gates = whole.enter_context(nc.sbuf_tensor("gates", [TM, NB * T // TM, 8], F32))
        phases = []
        for ph, build in enumerate(PHASES):
            with ExitStack() as st:
                phases.append(build(nc, m, st, ph))
        block = whole.enter_context(nc.Block())

        @block.sync
        def _(sp):
            sp.dma_start(m.ident[:], m.dram["identity"]).then_inc(m.ident_landed, 16)
            for p in phases:
                p["sync"](sp)

        @block.tensor
        def _(pe):
            pe.wait_ge(m.ident_landed, 16)
            for p in phases:
                p["tensor"](pe)

        @block.scalar
        def _(act):
            for p in phases:
                p["scalar"](act)

        @block.vector
        def _(dve):
            for p in phases:
                p["vector"](dve)

        @block.gpsimd
        def _(pool):
            for p in phases:
                p["gpsimd"](pool)


def _constants(np):
    f = np.float32
    freqs = np.outer(np.arange(T, dtype=f), 1.0 / 10000.0 ** (np.arange(0, 16, 2, dtype=f) / 16)).astype(f)
    sign = np.repeat(np.array([-1, 1], f), 8)[:, None]
    cos, sin = np.cos(np.tile(freqs, 2)).T, sign * np.sin(np.tile(freqs, 2)).T
    table = lambda t: np.tile(np.concatenate([np.concatenate([0.25 * t, t], 1), np.zeros((16, 2 * T), f)]), (4, 1)).astype(f)
    row = 5 * np.arange(TM)[:, None] + np.arange(5)
    mask = np.where(np.arange(T) <= (row // 4)[:, :, None], 0, MASKED).astype(f).reshape(TM, 5 * T)
    pick = (row[:, :, None] % 4 // 2 == np.arange(2)).astype(f).reshape(TM, 10)
    tail = np.kron(np.eye(4, dtype=f), np.concatenate([np.zeros((17, 64), f), np.ones((17, 1), f)], 1))
    return {
        "tail_blocks": tail,
        "rope_cos": table(cos),
        "rope_sin": table(sin),
        "causal_mask": mask,
        "pick_value_head": pick,
        "own_block": np.kron(np.eye(5, dtype=f), np.ones((17, 1), f)),
        "descending": np.arange(8, 0, -1).astype(f),
        "identity": np.eye(128, dtype=f),
        "inv_count": (1 / np.minimum(np.arange(16) + 1, 5)).astype(f),
        "id_col": (np.arange(128) % 64).astype(f)[:, None],
        "id_row": np.arange(64).astype(f),
    }


_SCRATCH = {"h_d": (NB * T, C), "xt_d": (C, NB * T), "v_d": (NB, T * C), "ctx_d": (NB, T * 8 * C),
            "zt_d": (C, NB * T), "y_d": (NB, T * C), "gates_d": (NB * T // TM * 8, TM)}


def kernel(**inputs):
    import numpy as _np
    import concourse.bacc as _bacc
    from concourse import mybir as _mybir
    from concourse.bass_utils import run_bass_kernel_spmd as _run

    nc = _bacc.Bacc("TRN2", target_bir_lowering=False, num_devices=1)
    arrays, dram = {}, {}
    for name, a in {**inputs, **_constants(_np)}.items():
        a = _np.ascontiguousarray(a)
        arrays[f"in_{name}"] = a
        dram[name.removeprefix("L0_")] = nc.dram_tensor(f"in_{name}", a.shape, _mybir.dt.from_np(a.dtype), kind="ExternalInput").ap()
    scratch = {n: nc.dram_tensor(n, s, _mybir.dt.float32, kind="ExternalOutput" if DEBUG else "Internal").ap() for n, s in _SCRATCH.items()}
    out = nc.dram_tensor("fused_out", (NB, T, C), _mybir.dt.float32, kind="ExternalOutput").ap()
    program(nc, dram, scratch, out)
    r = _run(nc, [arrays], core_ids=[0])
    return r.results[0]["fused_out"]
```

```python
from contextlib import ExitStack

import concourse.bass as bass
from concourse import mybir

F32 = mybir.dt.float32
BF16 = mybir.dt.bfloat16
I32 = mybir.dt.int32
ALU = mybir.AluOpType
ACT = mybir.ActivationFunctionType
X = mybir.AxisListType.X

NB = 64
C = 64
NTOK = 17
T = 145
TOKENS = NB * T
TM = 116
GB = 4
GT = GB * T
GJ = GT // TM
NG = NB // GB
EPS = 1e-5
MASKED = -1e30
BANK = 512


class Steps:

    def __init__(self, nc, stack, name, steps):
        self.sem = stack.enter_context(nc.semaphore(name))
        self.steps = steps
        self.n = len(steps)
        self.next = 0

    def start(self, eng):
        eng.sem_inc(self.sem, self.n)

    def mark(self, step):
        assert self.steps[self.next % self.n] == step, (step, self.steps[self.next % self.n])
        self.next += 1
        return self.sem

    def at(self, step, i=0):
        return i * self.n + (self.n + self.steps.index(step) + 1)

    def before(self, step, i=0):
        return i * self.n + (self.steps.index(step) + 1)


class Landed:

    def __init__(self, nc, stack, name, k):
        self.sem = stack.enter_context(nc.semaphore(name))
        self.k = 16 * k

    def start(self, eng):
        eng.sem_inc(self.sem, self.k)

    def at(self, i=0):
        return i * self.k + 2 * self.k

    def before(self, i=0):
        return i * self.k + self.k


class Shared:

    def __init__(self, dram):
        self.dram = dram


def cols(ap, n):
    return ap.broadcast_to(list(ap.shape[:-1]) + [n])


def skewed(eng, passes, ahead, behind):
    ahead(0, 0)

    def one_pass(i, end=False):
        ahead(1, i)
        behind(0, i)
        if not end:
            ahead(0, i + 1)
        behind(1, i)

    with eng.Fori(0, passes - 1) as i:
        one_pass(i)
    one_pass(passes - 1, end=True)


def phase_end(m, eng, phase):
    eng.drain().then_inc(m.phase_done, 1)
    eng.wait_ge(m.phase_done, 5 * (phase + 1))
    eng.sem_inc(m.gate, 1)


def patch_phase(nc, m, st, ph):
    IMG, P, GRID, DIM = 128, 32, 4, 64
    CH = 3
    K = CH * P
    B8 = 8
    NI = NB // B8
    NP = B8 * GRID * GRID
    PD = CH * P * P
    sb = lambda n, s, d=F32: st.enter_context(nc.sbuf_tensor(n, s, d))
    img = [sb(f"img{s}", [K, B8, GRID, IMG]) for s in range(2)]
    sq = [sb(f"img_sq{s}", [K, NP // 4, 4 * P]) for s in range(2)]
    sqsum = [sb(f"sqsum{s}", [K, NP]) for s in range(2)]
    proj = [sb(f"proj{s}", [DIM + 1, NP]) for s in range(2)]
    w = sb("w_patch", [K, P, DIM])
    wg = sb("w_patch_gained", [K, P, DIM + 1])
    wb = sb("w_patch_biased", [K, P, DIM])
    gain, shift = sb("patch_gain", [K, P]), sb("patch_shift", [K, P])
    wsum, wbsum = sb("w_gained_sum", [K, DIM]), sb("w_biased_sum", [K, DIM])
    ones = sb("ones_patch", [K, 128])
    colsum, bias = sb("colsum", [128, DIM]), sb("bias_p", [128, DIM])
    bp = sb("b_patch_rows", [128, DIM])
    g2, b2 = sb("ln_p2_g_rows", [128, DIM]), sb("ln_p2_b_rows", [128, DIM])
    pos = sb("pos_rows", [128, DIM])
    cls = sb("cls_rows", [128, DIM])
    raw = sb("raw_tokens", [128, NI, DIM + 2])
    y, t = sb("patch_y", [128, NI, DIM]), sb("patch_t", [128, NI, DIM])
    mean, var, tmp = sb("p_mean", [128, NI]), sb("p_var", [128, NI]), sb("p_tmp", [128, NI])
    eps = sb("p_eps", [128, 1])
    ps = m.psum
    sem = lambda n: m.whole.enter_context(nc.semaphore(n))
    consts = sem("patch_consts_landed")
    placed = sem("patch_tokens_placed")
    imgs = [Landed(nc, m.whole, f"img_landed{s}", CH * GRID) for s in range(2)]
    pe_s = Steps(nc, m.whole, "patch_pe", [f"{k}{s}" for s in range(2) for k in ("projected", "squares", "turned")])
    act_s = Steps(nc, m.whole, "patch_act", [f"{k}{s}" for s in range(2) for k in ("squared", "proj_copied")])
    dve_s = Steps(nc, m.whole, "patch_dve", [f"{k}{s}" for s in range(2) for k in ("sq_reduced", "raw_copied", "sumsq_copied")])
    pe_w = Steps(nc, m.whole, "patch_pe_w", ["sums"])
    dve_w = Steps(nc, m.whole, "patch_dve_w", ["ones", "gained", "ones_col", "biased", "wsum", "wbsum", "colsum", "bias", "eps", "x_clear"])
    fin = ["mean", "msq", "ex2", "var", "recip", "mu_w", "minus", "scaled", "biased", "sum", "mean2", "cent",
           "sq2", "ss2", "recip2", "norm2", "gain2", "shift2", "pos_added"]
    dve_f = Steps(nc, m.whole, "patch_dve_f", fin)
    act_f = Steps(nc, m.whole, "patch_act_f", ["std", "std2"])

    def sync(sp):
        sp.dma_start(w[:], m.dram["tok_W_patch"].rearrange("(p x) o -> p x o", x=P)).then_inc(consts, 16)
        sp.dma_start(gain[:], m.dram["tok_ln_p1_g"].rearrange("(p x) -> p x", x=P)).then_inc(consts, 16)
        sp.dma_start(shift[:], m.dram["tok_ln_p1_b"].rearrange("(p x) -> p x", x=P)).then_inc(consts, 16)
        sp.dma_start(bp[:], m.dram["tok_b_patch"].partition_broadcast(128)).then_inc(consts, 16)
        sp.dma_start(g2[:], m.dram["tok_ln_p2_g"].partition_broadcast(128)).then_inc(consts, 16)
        sp.dma_start(b2[:], m.dram["tok_ln_p2_b"].partition_broadcast(128)).then_inc(consts, 16)
        for s in range(2):
            imgs[s].start(sp)
        with sp.Fori(0, NI // 2) as i:
            for s in range(2):
                sp.wait_ge(pe_s.sem, pe_s.before(f"projected{s}", i))
                sp.sem_inc(m.gate, 1)
                sp.wait_ge(act_s.sem, act_s.before(f"squared{s}", i))
                sp.sem_inc(m.gate, 1)
                for c in range(CH):
                    for g in range(GRID):
                        sp.dma_start(img[s][c * P:(c + 1) * P, :, g, :],
                                     m.dram["x"][bass.ds(i * 2 * B8 + s * B8, B8), c, g * P:(g + 1) * P].rearrange("b r w -> r b w")
                                     ).then_inc(imgs[s].sem, 16)
        sp.wait_ge(dve_w.sem, dve_w.at("x_clear"))
        for j in range(4):
            sp.dma_start(m.pos_tile[32 * j:32 * j + NTOK], m.dram["tok_pos"][0]).then_inc(consts, 16)
            sp.dma_start(m.vit_x[32 * j:32 * j + 1], m.dram["tok_cls"][0, 0:1].unsqueeze(1).broadcast_to([1, 16, DIM])).then_inc(placed, 16)
        sp.wait_ge(dve_f.sem, dve_f.at("shift2"))
        for j in range(4):
            for half in range(2):
                p0 = (4 * half + j) * 16
                sp.dma_start(m.vit_x[32 * j + 1:32 * j + NTOK, half::2, :], y[p0:p0 + 16]).then_inc(placed, 16)
        sp.wait_ge(placed, 16 * 12)
        phase_end(m, sp, ph)

    def tensor(pe):
        pe_w.start(pe)
        pe_s.start(pe)
        pe.wait_ge(dve_w.sem, dve_w.at("wbsum"))
        pe.matmul(ps[:, 0, 0:DIM], ones[:], wsum[:], start=True, stop=True)
        pe.matmul(ps[:, 1, 0:DIM], ones[:], wbsum[:], start=True, stop=True).then_inc(pe_w.mark("sums"), 1)
        with pe.Fori(0, NI // 2) as i:
            for s in range(2):
                pe.wait_ge(imgs[s].sem, imgs[s].at(i))
                pe.wait_ge(act_s.sem, act_s.before(f"proj_copied{s}", i))
                pe.sem_inc(m.gate, 1)
                for px in range(P):
                    mm = pe.matmul(ps[0:DIM + 1, 2 + s, 0:NP], wg[:, px, :],
                                   img[s][:].rearrange("k b g (h x) -> k (b g h) x", x=P)[:, :, px],
                                   start=px == 0, stop=px == P - 1)
                mm.then_inc(pe_s.mark(f"projected{s}"), 1)
                pe.wait_ge(dve_s.sem, dve_s.at(f"sq_reduced{s}", i))
                pe.wait_ge(dve_s.sem, dve_s.before(f"sumsq_copied{s}", i))
                pe.sem_inc(m.gate, 1)
                pe.matmul(ps[:, 4 + s, 0:1], sqsum[s][:], ones[:, 0:1], start=True, stop=True).then_inc(pe_s.mark(f"squares{s}"), 1)
                pe.wait_ge(act_s.sem, act_s.at(f"proj_copied{s}", i))
                pe.sem_inc(m.gate, 1)
                pe.transpose(ps[:, 6 + s, 0:DIM + 1], proj[s][:], m.ident[0:DIM + 1, 0:DIM + 1]).then_inc(pe_s.mark(f"turned{s}"), 1)
        phase_end(m, pe, ph)

    def scalar(act):
        act_s.start(act)
        act_f.start(act)
        with act.Fori(0, NI // 2) as i:
            for s in range(2):
                act.wait_ge(imgs[s].sem, imgs[s].at(i))
                act.wait_ge(dve_s.sem, dve_s.before(f"sq_reduced{s}", i))
                act.activation(sq[s][:].rearrange("k n (g p) -> k (n g p)", g=4), img[s][:].rearrange("k b g w -> k (b g w)"),
                               ACT.Square).then_inc(act_s.mark(f"squared{s}"), 1)
                act.wait_ge(pe_s.sem, pe_s.at(f"projected{s}", i))
                act.wait_ge(pe_s.sem, pe_s.before(f"turned{s}", i))
                act.activation(proj[s][:], ps[0:DIM + 1, 2 + s, 0:NP], ACT.Copy).then_inc(act_s.mark(f"proj_copied{s}"), 1)
        act.wait_ge(dve_w.sem, dve_w.at("eps"))
        act.wait_ge(dve_f.sem, dve_f.at("var"))
        act.activation(tmp[:], var[:], ACT.Sqrt, bias=eps[:]).then_inc(act_f.mark("std"), 1)
        act.wait_ge(dve_f.sem, dve_f.at("ss2"))
        act.activation(tmp[:], var[:], ACT.Sqrt, bias=eps[:], scale=1.0 / DIM).then_inc(act_f.mark("std2"), 1)
        phase_end(m, act, ph)

    def vector(dve):
        dve_w.start(dve)
        dve_s.start(dve)
        dve_f.start(dve)
        dve.memset(ones[:], 1.0).then_inc(dve_w.mark("ones"), 1)
        dve.wait_ge(consts, 16 * 6)
        dve.tensor_tensor(wg[:, :, 0:DIM], w[:], cols(gain[:].unsqueeze(2), DIM), ALU.mult).then_inc(dve_w.mark("gained"), 1)
        dve.memset(wg[:, :, DIM:DIM + 1], 1.0).then_inc(dve_w.mark("ones_col"), 1)
        dve.tensor_tensor(wb[:], w[:], cols(shift[:].unsqueeze(2), DIM), ALU.mult).then_inc(dve_w.mark("biased"), 1)
        dve.wait_ge(dve_w.sem, dve_w.at("biased"))
        dve.tensor_reduce(wsum[:], wg[:, :, 0:DIM].rearrange("k x o -> k o x"), X, ALU.add).then_inc(dve_w.mark("wsum"), 1)
        dve.tensor_reduce(wbsum[:], wb[:].rearrange("k x o -> k o x"), X, ALU.add).then_inc(dve_w.mark("wbsum"), 1)
        dve.wait_ge(pe_w.sem, pe_w.at("sums"))
        dve.tensor_copy(colsum[:], ps[:, 0, 0:DIM]).then_inc(dve_w.mark("colsum"), 1)
        dve.tensor_tensor(bias[:], ps[:, 1, 0:DIM], bp[:], ALU.add).then_inc(dve_w.mark("bias"), 1)
        dve.memset(eps[:], EPS).then_inc(dve_w.mark("eps"), 1)
        dve.memset(m.pos_tile[:], 0.0)
        dve.memset(m.vit_x[:], 0.0).then_inc(dve_w.mark("x_clear"), 1)
        with dve.Fori(0, NI // 2) as i:
            for s in range(2):
                dve.wait_ge(act_s.sem, act_s.at(f"squared{s}", i))
                dve.wait_ge(pe_s.sem, pe_s.before(f"squares{s}", i))
                dve.tensor_reduce(sqsum[s][:], sq[s][:].rearrange("k n (g p) -> k (n g) p", g=4), X, ALU.add
                                  ).then_inc(dve_s.mark(f"sq_reduced{s}"), 1)
                dve.wait_ge(pe_s.sem, pe_s.at(f"turned{s}", i))
                dve.tensor_scalar(raw[:, bass.ds(2 * i + s, 1), 0:DIM + 1], ps[:, 6 + s, 0:DIM + 1].unsqueeze(1), 1.0, None, ALU.mult
                                  ).then_inc(dve_s.mark(f"raw_copied{s}"), 1)
                dve.tensor_scalar(raw[:, bass.ds(2 * i + s, 1), DIM + 1:DIM + 2], ps[:, 4 + s, 0:1].unsqueeze(1), 1.0, None, ALU.mult
                                  ).then_inc(dve_s.mark(f"sumsq_copied{s}"), 1)
        dve.wait_ge(dve_s.sem, dve_s.at("sumsq_copied1", NI // 2 - 1))
        F = dve_f
        dve.tensor_scalar(mean[:], raw[:, :, DIM], 1.0 / PD, None, ALU.mult).then_inc(F.mark("mean"), 1)
        dve.wait_ge(F.sem, F.at("mean"))
        dve.tensor_tensor(tmp[:], mean[:], mean[:], ALU.mult).then_inc(F.mark("msq"), 1)
        dve.tensor_scalar(var[:], raw[:, :, DIM + 1], 1.0 / PD, None, ALU.mult).then_inc(F.mark("ex2"), 1)
        dve.wait_ge(F.sem, F.at("ex2"))
        dve.tensor_tensor(var[:], var[:], tmp[:], ALU.subtract).then_inc(F.mark("var"), 1)
        dve.wait_ge(act_f.sem, act_f.at("std"))
        dve.reciprocal(var[:], tmp[:]).then_inc(F.mark("recip"), 1)
        dve.tensor_tensor(t[:], colsum[:].unsqueeze(1).broadcast_to([128, NI, DIM]), cols(mean[:].unsqueeze(2), DIM), ALU.mult).then_inc(F.mark("mu_w"), 1)
        dve.wait_ge(F.sem, F.at("mu_w"))
        dve.tensor_tensor(y[:], raw[:, :, 0:DIM], t[:], ALU.subtract).then_inc(F.mark("minus"), 1)
        dve.wait_ge(F.sem, F.at("minus"))
        dve.tensor_tensor(y[:], y[:], cols(var[:].unsqueeze(2), DIM), ALU.mult).then_inc(F.mark("scaled"), 1)
        dve.wait_ge(F.sem, F.at("scaled"))
        dve.tensor_tensor(y[:], y[:], bias[:].unsqueeze(1).broadcast_to([128, NI, DIM]), ALU.add).then_inc(F.mark("biased"), 1)
        dve.wait_ge(F.sem, F.at("biased"))
        dve.tensor_reduce(mean[:], y[:], X, ALU.add).then_inc(F.mark("sum"), 1)
        dve.wait_ge(F.sem, F.at("sum"))
        dve.tensor_scalar(mean[:], mean[:], 1.0 / DIM, None, ALU.mult).then_inc(F.mark("mean2"), 1)
        dve.wait_ge(F.sem, F.at("mean2"))
        dve.tensor_tensor(y[:], y[:], cols(mean[:].unsqueeze(2), DIM), ALU.subtract).then_inc(F.mark("cent"), 1)
        dve.wait_ge(F.sem, F.at("cent"))
        dve.tensor_tensor(t[:], y[:], y[:], ALU.mult).then_inc(F.mark("sq2"), 1)
        dve.wait_ge(F.sem, F.at("sq2"))
        dve.tensor_reduce(var[:], t[:], X, ALU.add).then_inc(F.mark("ss2"), 1)
        dve.wait_ge(act_f.sem, act_f.at("std2"))
        dve.reciprocal(mean[:], tmp[:]).then_inc(F.mark("recip2"), 1)
        dve.wait_ge(F.sem, F.at("recip2"))
        dve.tensor_tensor(y[:], y[:], cols(mean[:].unsqueeze(2), DIM), ALU.mult).then_inc(F.mark("norm2"), 1)
        dve.wait_ge(F.sem, F.at("norm2"))
        dve.tensor_tensor(y[:], y[:], g2[:].unsqueeze(1).broadcast_to([128, NI, DIM]), ALU.mult).then_inc(F.mark("gain2"), 1)
        dve.wait_ge(F.sem, F.at("gain2"))
        dve.tensor_tensor(y[:], y[:], b2[:].unsqueeze(1).broadcast_to([128, NI, DIM]), ALU.add).then_inc(F.mark("shift2"), 1)
        dve.wait_ge(placed, 16 * 12)
        dve.wait_ge(consts, 16 * 10)
        dve.tensor_tensor(m.vit_x[:], m.vit_x[:], m.pos_tile[:].unsqueeze(1).broadcast_to([128, 16, DIM]), ALU.add).then_inc(F.mark("pos_added"), 1)
        phase_end(m, dve, ph)

    def gpsimd(pool):
        phase_end(m, pool, ph)

    return dict(sync=sync, tensor=tensor, scalar=scalar, vector=vector, gpsimd=gpsimd)


def vit_phase(nc, m, st, ph):
    G, R, H, DH, MLP, DEPTH = 8, 32, 4, 64, 128, 4
    F2 = range(2)
    sb = lambda n, s, d=F32: st.enter_context(nc.sbuf_tensor(n, s, d))
    wqkv, wo, w1, w2 = sb("wqkv", [C, 3 * H * DH]), sb("wo_h", [DH, H, C]), sb("w1_v", [C, MLP]), sb("w2_v", [MLP, C])
    ag, ab = (sb(n, [2 * C, 1]) for n in ("attn_g", "attn_b"))
    fg, fb = (sb(n, [C, 1]) for n in ("ff_g", "ff_b"))
    b1 = sb("b1_col", [MLP, 1])
    bo, b2 = sb("bo_rows", [128, C]), sb("b2_rows", [128, C])
    lfg, lfb = sb("ln_f_g_rows", [128, C]), sb("ln_f_b_rows", [128, C])
    wT = sb("wqkv_t", [DH, 3 * H, C])
    wqk = sb("wq_wk", [C, H, C])
    wvo = sb("wv_wo", [2 * C, H // 2, C])
    two = lambda n, shape: [sb(f"{n}{f}", shape) for f in F2]
    cent, sq, xh = two("v_cent", [128, G, C]), two("v_sq", [128, G, C]), two("v_xh", [128, G, 2, C])
    mean, ss, rstd = two("v_mean", [128, G]), two("v_ss", [128, G]), two("v_rstd", [128, G])
    eps = sb("v_eps", [128, 1])
    hT = two("v_ht", [2 * C, 2, G * 4, R])
    tT = two("v_tt", [2 * C, H // 2, G * 4, R])
    sc, ex = two("v_scores", [128, G * H, NTOK]), two("v_exp", [128, G * H, NTOK])
    mx, rs = two("v_max", [128, G * H]), two("v_rs", [128, G * H])
    pr = two("v_probs", [128, G * H, R])
    prT = two("v_probs_t", [128, G * H, R])
    pd = two("v_probs_diag", [128, G * H, 4, NTOK])
    mixed = two("v_mixed", [2 * C, H // 2, G, 4, R])
    gl = two("v_gelu", [MLP, G * 4, R])
    ps = m.psum
    X4 = [m.vit_x[:, G * f:G * (f + 1)] for f in F2]
    fin_landed = m.whole.enter_context(nc.semaphore("vit_final_landed"))
    stored = m.whole.enter_context(nc.semaphore("vit_stored"))
    NW = 13
    wts = Landed(nc, m.whole, "vit_weights_landed", NW)
    fq = [f"{f}{q}" for q in F2 for f in F2]
    both = lambda *names: [f"{n}{f}" for n in names for f in F2]
    pe_s = Steps(nc, m.whole, "vit_pe", ["w_turned", "combined"] + both("h_turned") + both("t_proj")
                 + [f"scores{x}" for x in fq] + [f"mixed{f}{q}" for q in F2 for f in F2] + both("attended", "f_turned", "mlp1", "mlp2"))
    act_s = Steps(nc, m.whole, "vit_act", ["w_copied", "wqk_copied", "wvo_copied"] + both("ha") + ["t0"]
                  + [f"sc{x}{j}" for x in fq for j in (0, 1)] + both("exp") + [f"u{f}{q}" for q in F2 for f in F2] + both("std_f", "hf", "gelu"))
    act_a = Steps(nc, m.whole, "vit_act_a", both("std"))
    ln = lambda f: [f"ln{f}_{n}" for n in ("sum", "mean", "cent", "sq", "ss", "recip", "xh")]
    dve_a = Steps(nc, m.whole, "vit_dve_a", ln(0) + ln(1))
    dve_s = Steps(nc, m.whole, "vit_dve", ["t1"] + [f"sc{x}{j}" for x in fq for j in (2, 3)]
                  + [f"{n}{f}" for f in F2 for n in ("max", "minus")]
                  + [f"{n}{f}" for f in F2 for n in ("rsum", "rrecip", "probs", "probs_t", "diag0_", "diag1_")]
                  + [n for f in F2 for n in [f"x_attn{f}", f"x_bo{f}"] + ln(f)] + [f"{n}{f}" for f in F2 for n in ("x_mlp", "x_b2_")])
    pool_s = Steps(nc, m.whole, "vit_pool", ["diag2_0", "diag3_0", "diag2_1", "diag3_1"])
    dve_f = Steps(nc, m.whole, "vit_dve_ends", ["clear", "gain0", "shift0", "gain1", "shift1"])

    def sync(sp):
        sp.dma_start(lfg[:], m.dram["tok_ln_f_g"].partition_broadcast(128)).then_inc(fin_landed, 16)
        sp.dma_start(lfb[:], m.dram["tok_ln_f_b"].partition_broadcast(128)).then_inc(fin_landed, 16)
        wts.start(sp)
        with sp.Fori(0, DEPTH) as i:
            sp.wait_ge(dve_s.sem, dve_s.before("x_b2_1", i))
            sp.sem_inc(m.gate, 1)
            at = bass.ds(i, 1)
            sp.dma_start(wqkv[:], m.dram["tok_Wqkv"][at].rearrange("l c n -> c (l n)")).then_inc(wts.sem, 16)
            sp.dma_start(wo[:], m.dram["tok_Wo"][at].rearrange("l (h d) o -> d (l h) o", h=H)).then_inc(wts.sem, 16)
            sp.dma_start(w1[:], m.dram["tok_W1"][at].rearrange("l c n -> c (l n)")).then_inc(wts.sem, 16)
            sp.dma_start(w2[:], m.dram["tok_W2"][at].rearrange("l c n -> c (l n)")).then_inc(wts.sem, 16)
            for dst, src in ((ag[0:C], m.dram["tok_attn_ln_g"]), (ag[C:2 * C], m.dram["tok_attn_ln_g"]), (ab[0:C], m.dram["tok_attn_ln_b"]),
                             (ab[C:2 * C], m.dram["tok_attn_ln_b"]), (fg[:], m.dram["tok_ff_ln_g"]), (fb[:], m.dram["tok_ff_ln_b"]), (b1[:], m.dram["tok_b1"])):
                sp.dma_start(dst, src[at].rearrange("l c -> c l")).then_inc(wts.sem, 16)
            for dst, src in ((bo, m.dram["tok_bo"]), (b2, m.dram["tok_b2"])):
                sp.dma_start(dst[:], src[at].rearrange("l c -> (l c)").partition_broadcast(128)).then_inc(wts.sem, 16)
        sp.wait_ge(dve_f.sem, dve_f.at("shift1"))
        for f in F2:
            for j in range(4):
                sp.dma_start(m.dram["h_d"].rearrange("(g j t) c -> j t g c", j=4, t=T)[j, 0:NTOK, G * f:G * (f + 1)],
                             xh[f][32 * j:32 * j + NTOK, :, 0]).then_inc(stored, 16)
        sp.wait_ge(stored, 16 * 8)
        phase_end(m, sp, ph)

    def tensor(pe):
        pe_s.start(pe)

        def turn(f, step, copies):
            for g in range(G):
                mm = pe.transpose(ps[0:copies * C, 4 * f + 2 + g // 4, g % 4 * 128:(g % 4 + 1) * 128], xh[f][:, g, 0:copies].rearrange("p r c -> p (r c)"), m.ident[:])
            mm.then_inc(pe_s.mark(f"{step}{f}"), 1)

        with pe.Fori(0, DEPTH) as i:
            pe.wait_ge(wts.sem, wts.at(i))
            pe.wait_ge(dve_s.sem, dve_s.before("x_mlp0", i))
            pe.wait_ge(act_s.sem, act_s.before("gelu0", i))
            pe.sem_inc(m.gate, 1)
            for k in range(3 * H):
                mm = pe.transpose(ps[0:DH, k // 8, k % 8 * C:(k % 8 + 1) * C], wqkv[:, k * DH:(k + 1) * DH], m.ident[0:C, 0:C])
            mm.then_inc(pe_s.mark("w_turned"), 1)
            pe.wait_ge(act_s.sem, act_s.at("w_copied", i))
            pe.sem_inc(m.gate, 1)
            for h in range(H):
                pe.matmul(ps[0:C, 0, h * C:(h + 1) * C], wT[:, h, :], wT[:, H + h, :], start=True, stop=True)
                mm = pe.matmul(ps[:, 1, h * C:(h + 1) * C], wT[:, 2 * H + h // 2 * 2:2 * H + h // 2 * 2 + 2, :].rearrange("d h c -> d (h c)"), wo[:, h, :],
                               start=True, stop=True)
            mm.then_inc(pe_s.mark("combined"), 1)
            for f in F2:
                pe.wait_ge(dve_a.sem, dve_a.at(f"ln{f}_xh", i))
                pe.sem_inc(m.gate, 1)
                turn(f, "h_turned", 2)
            for f in F2:
                pe.wait_ge(act_s.sem, act_s.at("wvo_copied", i))
                pe.wait_ge(act_s.sem, act_s.at(f"ha{f}", i))
                pe.sem_inc(m.gate, 1)
                for q in F2:
                    for k in F2:
                        mm = pe.matmul(ps[:, 4 * f + 2 * q + k, 0:16 * NTOK], wqk[:, 2 * k:2 * k + 2, :].rearrange("c h o -> c (h o)"),
                                       hT[f][0:C, 0, 16 * q:16 * q + 16, 0:NTOK], start=True, stop=True)
                mm.then_inc(pe_s.mark(f"t_proj{f}"), 1)
            for q in F2:
                for f in F2:
                    if q:
                        pe.wait_ge(act_s.sem, act_s.at(f"sc{f}01", i))
                        pe.wait_ge(dve_s.sem, dve_s.at(f"sc{f}03", i))
                    elif f == 0:
                        pe.wait_ge(act_s.sem, act_s.at("t0", i))
                    else:
                        pe.wait_ge(dve_s.sem, dve_s.at("t1", i))
                    pe.sem_inc(m.gate, 1)
                    for k in range(4):
                        g = 4 * q + k
                        for h2 in range(H // 2):
                            mm = pe.matmul(ps[:, 4 * f + k, h2 * 136:(h2 + 1) * 136], tT[f][:, h2, 4 * g:4 * g + 4, :].rearrange("c b r -> c (b r)"),
                                           hT[f][:, :, 4 * g:4 * g + 4, 0:NTOK], start=True, stop=True)
                    mm.then_inc(pe_s.mark(f"scores{f}{q}"), 1)
            for q in F2:
                for f in F2:
                    if q:
                        pe.wait_ge(act_s.sem, act_s.at(f"u{f}0", i))
                    else:
                        pe.wait_ge(dve_s.sem, dve_s.at(f"diag1_{f}", i))
                        pe.wait_ge(pool_s.sem, pool_s.at(f"diag3_{f}", i))
                    pe.sem_inc(m.gate, 1)
                    for k in range(4):
                        g = 4 * q + k
                        mm = pe.matmul(ps[:, 4 * f + k, 0:H * 4 * NTOK], xh[f][:, g].rearrange("p r c -> p (r c)"),
                                       pd[f][:, g * H:(g + 1) * H].rearrange("p h j r -> p (h j r)"), start=True, stop=True)
                    mm.then_inc(pe_s.mark(f"mixed{f}{q}"), 1)
            for f in F2:
                pe.wait_ge(act_s.sem, act_s.at(f"u{f}1", i))
                pe.sem_inc(m.gate, 1)
                for g in range(G):
                    for k in F2:
                        mm = pe.matmul(ps[:, 4 * f, g * C:(g + 1) * C], mixed[f][:, k, g].rearrange("c j r -> c (j r)"), wvo[:, k, :], start=k == 0, stop=k == 1)
                mm.then_inc(pe_s.mark(f"attended{f}"), 1)
            for f in F2:
                pe.wait_ge(dve_s.sem, dve_s.at(f"ln{f}_xh", i))
                pe.sem_inc(m.gate, 1)
                turn(f, "f_turned", 1)
            for f in F2:
                pe.wait_ge(act_s.sem, act_s.at(f"hf{f}", i))
                pe.sem_inc(m.gate, 1)
                for q in F2:
                    mm = pe.matmul(ps[:, 4 * f + q, 0:16 * NTOK], w1[:], hT[f][0:C, 0, 16 * q:16 * q + 16, 0:NTOK], start=True, stop=True)
                mm.then_inc(pe_s.mark(f"mlp1{f}"), 1)
            for f in F2:
                pe.wait_ge(act_s.sem, act_s.at(f"gelu{f}", i))
                pe.sem_inc(m.gate, 1)
                for g in range(G):
                    mm = pe.matmul(ps[:, 4 * f + 2, g * C:(g + 1) * C], gl[f][:, 4 * g:4 * g + 4, :].rearrange("c b r -> c (b r)"), w2[:], start=True, stop=True)
                mm.then_inc(pe_s.mark(f"mlp2{f}"), 1)
        phase_end(m, pe, ph)

    def scalar(act):
        act_s.start(act)
        act_a.start(act)
        act.wait_ge(dve_f.sem, dve_f.at("clear"))

        def deviations(i):
            for f in F2:
                act.wait_ge(dve_a.sem, dve_a.at(f"ln{f}_ss", i))
                act.activation(rstd[f][:], ss[f][:], ACT.Sqrt, bias=eps[:], scale=1.0 / C).then_inc(act_a.mark(f"std{f}"), 1)

        def copy_turned(f, gain, shift, block):
            rows = slice(C * block, C * block + C)
            for q in F2:
                done = act.activation(hT[f][rows, block, 16 * q:16 * q + 16, 0:NTOK], ps[rows, 4 * f + 2 + q, :].rearrange("c (b r) -> c b r", r=R)[:, :, 0:NTOK],
                                      ACT.Identity, bias=shift[rows], scale=gain[rows])
            return done

        deviations(0)
        with act.Fori(0, DEPTH) as i:
            act.wait_ge(wts.sem, wts.at(i))
            act.wait_ge(pe_s.sem, pe_s.at("w_turned", i))
            act.activation(wT[:, 0:8, :], ps[0:DH, 0, :].rearrange("c (k o) -> c k o", o=C), ACT.Copy)
            act.activation(wT[:, 8:12, :], ps[0:DH, 1, 0:256].rearrange("c (k o) -> c k o", o=C), ACT.Copy).then_inc(act_s.mark("w_copied"), 1)
            act.wait_ge(pe_s.sem, pe_s.at("combined", i))
            act.activation(wqk[:].rearrange("c h o -> c (h o)"), ps[0:C, 0, 0:H * C], ACT.Copy, scale=DH ** -0.5).then_inc(act_s.mark("wqk_copied"), 1)
            for k in F2:
                rows = slice(C * k, C * k + C)
                kept = act.activation(wvo[rows], ps[rows, 1, 0:H * C].rearrange("c (p h o) -> c p h o", p=H // 2, h=2)[:, :, k], ACT.Copy)
            kept.then_inc(act_s.mark("wvo_copied"), 1)
            for f in F2:
                act.wait_ge(pe_s.sem, pe_s.at(f"h_turned{f}", i))
                copy_turned(f, ag, ab, 0)
                copy_turned(f, ag, ab, 1).then_inc(act_s.mark(f"ha{f}"), 1)
            act.wait_ge(pe_s.sem, pe_s.at("t_proj0", i))
            for q in F2:
                copied = act.activation(tT[0][:, :, 16 * q:16 * q + 16, 0:NTOK], ps[:, 2 * q:2 * q + 2, 0:16 * NTOK].rearrange("c h (b r) -> c h b r", b=16), ACT.Copy)
            copied.then_inc(act_s.mark("t0"), 1)
            for q in F2:
                for f in F2:
                    act.wait_ge(pe_s.sem, pe_s.at(f"scores{f}{q}", i))
                    for j in range(2):
                        act.activation(sc[f][32 * j:32 * j + 32, 16 * q:16 * q + 16, :].rearrange("p (g h) n -> p g h n", g=4),
                                       ps[32 * j:32 * j + 32, 4 * f:4 * f + 4, 0:4 * 68].rearrange("p g (h n) -> p g h n", h=4)[:, :, :, NTOK * j:NTOK * j + NTOK],
                                       ACT.Copy).then_inc(act_s.mark(f"sc{f}{q}{j}"), 1)
            for f in F2:
                act.wait_ge(dve_s.sem, dve_s.at(f"minus{f}", i))
                act.activation(ex[f][:], sc[f][:], ACT.Exp).then_inc(act_s.mark(f"exp{f}"), 1)
            for q in F2:
                for f in F2:
                    act.wait_ge(pe_s.sem, pe_s.at(f"mixed{f}{q}", i))
                    for k in F2:
                        rows = slice(C * k, C * k + C)
                        for p in F2:
                            h = 2 * p + k
                            u = act.activation(mixed[f][rows, p, 4 * q:4 * q + 4, :, 0:NTOK],
                                               ps[rows, 4 * f:4 * f + 4, h * 4 * NTOK:(h + 1) * 4 * NTOK].rearrange("c g (j r) -> c g j r", j=4),
                                               ACT.Identity, bias=ab[rows], scale=ag[rows])
                    u.then_inc(act_s.mark(f"u{f}{q}"), 1)
            for f in F2:
                act.wait_ge(dve_s.sem, dve_s.at(f"ln{f}_ss", i))
                act.activation(rstd[f][:], ss[f][:], ACT.Sqrt, bias=eps[:], scale=1.0 / C).then_inc(act_s.mark(f"std_f{f}"), 1)
            for f in F2:
                act.wait_ge(pe_s.sem, pe_s.at(f"f_turned{f}", i))
                copy_turned(f, fg, fb, 0).then_inc(act_s.mark(f"hf{f}"), 1)
            for f in F2:
                act.wait_ge(pe_s.sem, pe_s.at(f"mlp1{f}", i))
                act.activation(gl[f][:, :, 0:NTOK].rearrange("p (q b) r -> p q b r", q=2), ps[:, 4 * f:4 * f + 2, 0:16 * NTOK].rearrange("p q (b r) -> p q b r", b=16),
                               ACT.Gelu, bias=b1[:]).then_inc(act_s.mark(f"gelu{f}"), 1)
            deviations(i + 1)
        phase_end(m, act, ph)

    def norm(dve, S, f, i, std_sem, std_at, copies):
        k = f"ln{f}"
        wide = lambda v: cols(v[:].unsqueeze(2), C)
        dve.tensor_reduce(mean[f][:], X4[f], X, ALU.add).then_inc(S.mark(f"{k}_sum"), 1)
        dve.wait_ge(S.sem, S.at(f"{k}_sum", i))
        dve.tensor_scalar(mean[f][:], mean[f][:], 1.0 / C, None, ALU.mult).then_inc(S.mark(f"{k}_mean"), 1)
        dve.wait_ge(S.sem, S.at(f"{k}_mean", i))
        dve.tensor_tensor(cent[f][:], X4[f], wide(mean[f]), ALU.subtract).then_inc(S.mark(f"{k}_cent"), 1)
        dve.wait_ge(S.sem, S.at(f"{k}_cent", i))
        dve.tensor_tensor(sq[f][:], cent[f][:], cent[f][:], ALU.mult).then_inc(S.mark(f"{k}_sq"), 1)
        dve.wait_ge(S.sem, S.at(f"{k}_sq", i))
        dve.tensor_reduce(ss[f][:], sq[f][:], X, ALU.add).then_inc(S.mark(f"{k}_ss"), 1)
        dve.wait_ge(std_sem, std_at)
        dve.reciprocal(mean[f][:], rstd[f][:]).then_inc(S.mark(f"{k}_recip"), 1)
        dve.wait_ge(S.sem, S.at(f"{k}_recip", i))
        shape = [128, G, copies, C]
        dve.tensor_tensor(xh[f][:, :, 0:copies], cent[f][:].unsqueeze(2).broadcast_to(shape), mean[f][:].unsqueeze(2).unsqueeze(3).broadcast_to(shape), ALU.mult).then_inc(S.mark(f"{k}_xh"), 1)

    def vector(dve):
        for S in (dve_a, dve_s, dve_f):
            S.start(dve)
        dve.memset(eps[:], EPS)
        for f in F2:
            for z in (hT, tT, pr, pd, mixed, gl):
                ins = dve.memset(z[f][:], 0.0)
        ins.then_inc(dve_f.mark("clear"), 1)
        dve.wait_ge(dve_f.sem, dve_f.at("clear"))
        S = dve_s

        def add_rows(step, rows, f, bank, i):
            flat = X4[f].rearrange("p g c -> p (g c)")
            dve.tensor_tensor(flat, ps[:, bank, :], flat, ALU.add).then_inc(S.mark(f"{step[0]}{f}"), 1)
            dve.wait_ge(S.sem, S.at(f"{step[0]}{f}", i))
            dve.tensor_tensor(X4[f], X4[f], rows[:].unsqueeze(1).broadcast_to([128, G, C]), ALU.add).then_inc(S.mark(f"{step[1]}{f}"), 1)
            dve.wait_ge(S.sem, S.at(f"{step[1]}{f}", i))

        for f in F2:
            norm(dve, dve_a, f, 0, act_a.sem, act_a.at(f"std{f}"), 2)
        with dve.Fori(0, DEPTH) as i:
            dve.wait_ge(pe_s.sem, pe_s.at("t_proj1", i))
            for q in F2:
                copied = dve.tensor_copy(tT[1][:, :, 16 * q:16 * q + 16, 0:NTOK], ps[:, 4 + 2 * q:6 + 2 * q, 0:16 * NTOK].rearrange("c h (b r) -> c h b r", b=16))
            copied.then_inc(S.mark("t1"), 1)
            for q in F2:
                for f in F2:
                    dve.wait_ge(pe_s.sem, pe_s.at(f"scores{f}{q}", i))
                    for j in (2, 3):
                        dve.tensor_copy(sc[f][32 * j:32 * j + 32, 16 * q:16 * q + 16, :].rearrange("p (g h) n -> p g h n", g=4),
                                        ps[32 * j:32 * j + 32, 4 * f:4 * f + 4, 0:4 * 68].rearrange("p g (h n) -> p g h n", h=4)[:, :, :, NTOK * j:NTOK * j + NTOK]
                                        ).then_inc(S.mark(f"sc{f}{q}{j}"), 1)
            for f in F2:
                dve.wait_ge(act_s.sem, act_s.at(f"sc{f}11", i))
                dve.wait_ge(S.sem, S.at(f"sc{f}13", i))
                dve.tensor_reduce(mx[f][:], sc[f][:], X, ALU.max).then_inc(S.mark(f"max{f}"), 1)
                dve.wait_ge(S.sem, S.at(f"max{f}", i))
                dve.tensor_tensor(sc[f][:], sc[f][:], cols(mx[f][:].unsqueeze(2), NTOK), ALU.subtract).then_inc(S.mark(f"minus{f}"), 1)
            for f in F2:
                dve.wait_ge(act_s.sem, act_s.at(f"exp{f}", i))
                dve.tensor_reduce(rs[f][:], ex[f][:], X, ALU.add).then_inc(S.mark(f"rsum{f}"), 1)
                dve.wait_ge(S.sem, S.at(f"rsum{f}", i))
                dve.reciprocal(mx[f][:], rs[f][:]).then_inc(S.mark(f"rrecip{f}"), 1)
                dve.wait_ge(S.sem, S.at(f"rrecip{f}", i))
                dve.tensor_tensor(pr[f][:, :, 0:NTOK], ex[f][:], cols(mx[f][:].unsqueeze(2), NTOK), ALU.mult).then_inc(S.mark(f"probs{f}"), 1)
                dve.wait_ge(S.sem, S.at(f"probs{f}", i))
                dve.wait_ge(pool_s.sem, pool_s.before(f"diag3_{f}", i))
                dve.transpose(prT[f][:].rearrange("p k r -> p (k r)"), pr[f][:].rearrange("p k r -> p (k r)")).then_inc(S.mark(f"probs_t{f}"), 1)
                dve.wait_ge(S.sem, S.at(f"probs_t{f}", i))
                for j in range(2):
                    dve.tensor_copy(pd[f][32 * j:32 * j + 32, :, j], prT[f][32 * j:32 * j + 32, :, 0:NTOK]).then_inc(S.mark(f"diag{j}_{f}"), 1)
            dve.wait_ge(wts.sem, wts.at(i))
            for f in F2:
                dve.wait_ge(pe_s.sem, pe_s.at(f"attended{f}", i))
                add_rows(("x_attn", "x_bo"), bo, f, 4 * f, i)
                norm(dve, S, f, i, act_s.sem, act_s.at(f"std_f{f}", i), 1)
            for f in F2:
                dve.wait_ge(pe_s.sem, pe_s.at(f"mlp2{f}", i))
                add_rows(("x_mlp", "x_b2_"), b2, f, 4 * f + 2, i)
                norm(dve, dve_a, f, i + 1, act_a.sem, act_a.at(f"std{f}", i + 1), 2)
        dve.wait_ge(fin_landed, 32)
        dve.wait_ge(dve_a.sem, dve_a.at("ln1_xh", DEPTH))
        for f in F2:
            dve.tensor_tensor(xh[f][:, :, 0], xh[f][:, :, 0], lfg[:].unsqueeze(1).broadcast_to([128, G, C]), ALU.mult).then_inc(dve_f.mark(f"gain{f}"), 1)
            dve.wait_ge(dve_f.sem, dve_f.at(f"gain{f}"))
            dve.tensor_tensor(xh[f][:, :, 0], xh[f][:, :, 0], lfb[:].unsqueeze(1).broadcast_to([128, G, C]), ALU.add).then_inc(dve_f.mark(f"shift{f}"), 1)
        phase_end(m, dve, ph)

    def gpsimd(pool):
        pool_s.start(pool)
        with pool.Fori(0, DEPTH) as i:
            for f in F2:
                pool.wait_ge(dve_s.sem, dve_s.at(f"probs_t{f}", i))
                pool.sem_inc(m.gate, 1)
                for j in (2, 3):
                    pool.tensor_copy(pd[f][32 * j:32 * j + 32, :, j], prT[f][32 * j:32 * j + 32, :, 0:NTOK]).then_inc(pool_s.mark(f"diag{j}_{f}"), 1)
        phase_end(m, pool, ph)

    return dict(sync=sync, tensor=tensor, scalar=scalar, vector=vector, gpsimd=gpsimd)


def text_phase(nc, m, st, ph):
    D, V, CH, NCH, WIN, HID, ROUNDS = 128, 64, 8, 16, 4, 256, 3
    CP = CH // 2
    K = NB * NCH
    KT = K // 128
    sb = lambda n, s, d=F32: st.enter_context(nc.sbuf_tensor(n, s, d))
    w = {n: sb(f"x_{n}", s) for n, s in {
        "h0": [128, CP, D], "pos": [128, CP, D], "lln_g": [D, 1], "lln_b": [D, 1], "lw1": [D, HID], "lb1": [D, 2], "lw2": [D, 2, D],
        "lb2": [128, D], "pool_w": [D, D], "pool_b": [D, 1], "msg_w1": [D, 2, D], "msg_b1": [D, 1], "msg_w2": [D, D], "msg_b2": [D, 1],
        "upd_w1": [D, 2, D], "upd_b1": [D, 1], "upd_w2": [D, D], "upd_b2": [D, 1], "mln_g": [D, 1], "mln_b": [D, 1],
        "bc_w": [D, D], "bc_b": [128, D], "fln_g": [D, 1], "fln_b": [D, 1], "head_w": [D, V], "inv_count": [128, NCH],
        "id_col": [128, 1], "id_row": [128, V]}.items()}
    tok = sb("x_tok", [128, K * CH], I32)
    tokr, tokf = sb("x_tok_rows", [128, KT, CH], I32), sb("x_tok_rows_f", [128, KT, CH])
    hot = sb("x_hot", [128, CP, K])
    local, xh0, sq0 = sb("x_local", [128, CP, D]), sb("x_xh0", [128, CP, D]), sb("x_sq0", [128, CP, D])
    st4, st4b, eps = sb("x_st4", [128, CP]), sb("x_st4b", [128, CP]), sb("x_eps", [128, 1])
    hT0, gl0 = sb("x_ht0", [D, CP * 128]), sb("x_gl0", [D, 2, CP * 128])
    pooled = sb("x_pooled", [128, CP, D])
    hm = sb("x_hm", [D, NB, NCH])
    a, b = sb("x_a", [D, NB, NCH]), sb("x_b", [D, NB, NCH])
    z = [sb(f"x_z{d}", [D, NB, NCH]) for d in range(WIN + 1)]
    agg, u = sb("x_agg", [D, K]), sb("x_u", [D, K])
    r, cent, sq, xh = sb("x_r", [D, K]), sb("x_cent", [128, KT, D]), sb("x_sq", [128, KT, D]), sb("x_xh", [128, KT, D])
    mean, ss, std = sb("x_mean", [128, KT]), sb("x_ss", [128, KT]), sb("x_std", [128, KT])
    ltT, ltT2, ltsq = sb("x_ltt", [D, CP * 128]), sb("x_ltt2", [D, CP * 128]), sb("x_ltsq", [D, CP * 128])
    bcT = sb("x_bct", [D, KT, 128])
    hwg = sb("x_hwg", [D, V])
    th = sb("x_th", [128, CP, 2, V])
    ones, fb = sb("x_ones", [D, 128]), sb("x_fb", [D, 128])
    lb = sb("x_lb", [128, V])
    hotr = [sb(f"x_hotr{k}", [128, CH, V]) for k in range(2)]
    pick = [sb(f"x_pick{k}", [128, CH, V]) for k in range(2)]
    var, dev, rstd = sb("x_var", [128, KT, CH]), sb("x_dev", [128, KT, CH]), sb("x_rstd", [128, KT, CH])
    lg = [sb(f"x_lg{k}", [128, CH, V]) for k in range(2)]
    ps = m.psum
    flat = lambda t: t[:].rearrange("d n c -> d (n c)")
    landed = m.whole.enter_context(nc.semaphore("text_landed"))
    stored = [m.whole.enter_context(nc.semaphore(f"text_stored{k}")) for k in range(2)]
    nload = 0

    tiles = range(KT)
    pe_c = Steps(nc, m.whole, "text_pe_setup", ["h0_turned", "mlp1", "mlp2", "local_turned", "pooled", "summ"])
    act_c = Steps(nc, m.whole, "text_act_setup", ["std0", "h0_copied", "gelu0", "gelu1", "local_copied", "pooled_copied", "summ_copied"])
    ln0 = ["sum", "mean", "cent", "sq", "ss", "recip", "xh"]
    dve_c = Steps(nc, m.whole, "text_dve_setup", ["eps", "h0"] + ln0 + ["hot0", "hot1", "local_h", "local"])
    pe_r = Steps(nc, m.whole, "text_pe_round", ["pre_a", "pre_b", "msg", "upd1", "upd2", "r_turned", "xh_turned"])
    act_r = Steps(nc, m.whole, "text_act_round", ["a"] + [f"gelu{d}" for d in range(WIN + 1)] + ["agg", "u", "std", "hm"])
    dve_r = Steps(nc, m.whole, "text_dve_round", ["b"] + [f"z{d}" for d in range(WIN + 1)] + [f"sum{d}" for d in range(1, WIN + 1)]
                  + ["scaled", "r"] + ["lsum", "mean", "cent", "sq", "ss", "recip", "xh"])
    pe_f = Steps(nc, m.whole, "text_pe_final", ["bc", "ltc_turned", "bcc_turned", "th", "lb"] + [f"var{t}" for t in tiles] + [f"logits{t}" for t in tiles])
    act_f = Steps(nc, m.whole, "text_act_final", ["ltt", "ltt2", "ltsq", "bct", "std"])
    dve_f = Steps(nc, m.whole, "text_dve_final", ["ones", "th_clear", "fb", "hwg", "tokf", "tsum", "tmean", "ltc", "bc", "bsum", "bmean", "bcc", "bsq", "bss", "th0", "th1", "lb"]
                  + [f"{n}{t}" for t in tiles for n in ("hotr", "pick", "var")] + ["var_all", "recip"]
                  + [f"{n}{t}" for t in tiles for n in ("scaled", "logits")])

    loads = []
    for c2 in range(2):
        rows = slice(64 * c2, 64 * c2 + 64)
        loads.append((w["h0"][rows], m.dram["txt_emb"].unsqueeze(1).broadcast_to([V, CP, D])))
        loads.append((w["pos"][rows], m.dram["txt_pos"].rearrange("(cp c2) d -> c2 cp d", c2=2)[c2].partition_broadcast(64)))
    col = lambda ap: ap.rearrange("(c o) -> c o", o=1)
    for n in ("lln_g", "lln_b", "pool_b", "msg_b1", "msg_b2", "upd_b1", "upd_b2", "mln_g", "mln_b", "fln_g", "fln_b"):
        loads.append((w[n][:], col(m.dram[f"txt_{n}"])))
    for n in ("lw1", "pool_w", "msg_w2", "upd_w2", "bc_w", "head_w"):
        loads.append((w[n][:], m.dram[f"txt_{n}"]))
    for n in ("msg_w1", "upd_w1", "lw2"):
        loads.append((w[n][:], m.dram[f"txt_{n}"].rearrange("(k c) o -> c k o", k=2)))
    for k in range(2):
        loads.append((w["lb1"][:, k:k + 1], col(m.dram["txt_lb1"][D * k:D * k + D])))
    for n, src in (("lb2", m.dram["txt_lb2"]), ("bc_b", m.dram["txt_bc_b"]), ("inv_count", m.dram["inv_count"]), ("id_row", m.dram["id_row"])):
        loads.append((w[n][:], src.partition_broadcast(128)))
    loads.append((w["id_col"][:], m.dram["id_col"]))

    def sync(sp):
        for dst, src in loads:
            sp.dma_start(dst, src).then_inc(landed, 16)
        for b8 in range(8):
            sp.dma_start(tokr[16 * b8:16 * b8 + 16], m.dram["x_txt"].rearrange("(t b) (i c) -> b i t c", b=8, c=CH)[b8]).then_inc(landed, 16)
        sp.dma_start(tok[:], m.dram["x_txt"].rearrange("b t -> (b t)").partition_broadcast(128)).then_inc(landed, 16)
        for t in tiles:
            sp.wait_ge(dve_f.sem, dve_f.at(f"logits{t}"))
            dst = m.dram["h_d"].rearrange("(b t) c -> b (t c)", t=T)[8 * t:8 * t + 8, NTOK * C:].rearrange("b (i n) -> b i n", i=NCH)
            sp.dma_start(dst, lg[t % 2][:].rearrange("p c v -> p (c v)")).then_inc(stored[t % 2], 16)
        for k in range(2):
            sp.wait_ge(stored[k], 16 * KT // 2)
        phase_end(m, sp, ph)
    all_landed = 16 * (len(loads) + 9)

    def tensor(pe):
        for s in (pe_c, pe_r, pe_f):
            s.start(pe)
        S = pe_c
        pe.wait_ge(landed, all_landed)
        pe.wait_ge(dve_c.sem, dve_c.at("xh"))
        for k in range(CP):
            mm = pe.transpose(ps[:, 0, 128 * k:128 * k + 128], xh0[:, k, :], m.ident[:])
        mm.then_inc(S.mark("h0_turned"), 1)
        pe.wait_ge(act_c.sem, act_c.at("h0_copied"))
        for k in range(2):
            mm = pe.matmul(ps[:, 1 + k, :], w["lw1"][:, k * D:(k + 1) * D], hT0[:], start=True, stop=True)
        mm.then_inc(S.mark("mlp1"), 1)
        pe.wait_ge(act_c.sem, act_c.at("gelu1"))
        for k in range(CP):
            for h in range(2):
                mm = pe.matmul(ps[:, 3, 128 * k:128 * k + 128], gl0[:, h, 128 * k:128 * k + 128], w["lw2"][:, h, :], start=h == 0, stop=h == 1)
        mm.then_inc(S.mark("mlp2"), 1)
        pe.wait_ge(dve_c.sem, dve_c.at("local"))
        for k in range(CP):
            mm = pe.transpose(ps[:, 0, 128 * k:128 * k + 128], local[:, k, :], m.ident[:])
        mm.then_inc(S.mark("local_turned"), 1)
        pe.wait_ge(act_c.sem, act_c.at("local_copied"))
        for k in range(CP):
            mm = pe.matmul(ps[:, 1, 128 * k:128 * k + 128], hT0[:, 128 * k:128 * k + 128], w["pool_w"][:], start=True, stop=True)
        mm.then_inc(S.mark("pooled"), 1)
        pe.wait_ge(act_c.sem, act_c.at("pooled_copied"))
        pe.wait_ge(dve_c.sem, dve_c.at("hot1"))
        for half in range(2):
            for k in range(CP):
                mm = pe.matmul(ps[:, 2 + half, :], pooled[:, k, :], hot[:, k, 512 * half:512 * half + 512], start=k == 0, stop=k == CP - 1)
        mm.then_inc(S.mark("summ"), 1)
        pe.wait_ge(act_c.sem, act_c.at("summ_copied"))
        S = pe_r
        with pe.Fori(0, ROUNDS) as i:
            pe.wait_ge(act_r.sem, act_r.before("hm", i))
            pe.sem_inc(m.gate, 1)
            for k, name in ((0, "pre_a"), (1, "pre_b")):
                for half in range(2):
                    mm = pe.matmul(ps[:, 2 * k + half, :], w["msg_w1"][:, k, :], flat(hm)[:, 512 * half:512 * half + 512], start=True, stop=True)
                mm.then_inc(S.mark(name), 1)
            pe.wait_ge(dve_r.sem, dve_r.at("scaled", i))
            pe.sem_inc(m.gate, 1)
            for half in range(2):
                mm = pe.matmul(ps[:, 4 + half, :], w["msg_w2"][:], flat(z[0])[:, 512 * half:512 * half + 512], start=True, stop=True)
            mm.then_inc(S.mark("msg"), 1)
            pe.wait_ge(act_r.sem, act_r.at("agg", i))
            pe.sem_inc(m.gate, 1)
            for half in range(2):
                c = slice(512 * half, 512 * half + 512)
                pe.matmul(ps[:, 6 + half, :], w["upd_w1"][:, 0, :], flat(hm)[:, c], start=True, stop=False)
                mm = pe.matmul(ps[:, 6 + half, :], w["upd_w1"][:, 1, :], agg[:, c], start=False, stop=True)
            mm.then_inc(S.mark("upd1"), 1)
            pe.wait_ge(act_r.sem, act_r.at("u", i))
            pe.sem_inc(m.gate, 1)
            for half in range(2):
                c = slice(512 * half, 512 * half + 512)
                mm = pe.matmul(ps[:, half, :], w["upd_w2"][:], u[:, c], start=True, stop=True)
            mm.then_inc(S.mark("upd2"), 1)
            pe.wait_ge(dve_r.sem, dve_r.at("r", i))
            pe.sem_inc(m.gate, 1)
            for t in tiles:
                mm = pe.transpose(ps[:, 2 + t // 4, t % 4 * 128:t % 4 * 128 + 128], r[:, 128 * t:128 * t + 128], m.ident[:])
            mm.then_inc(S.mark("r_turned"), 1)
            pe.wait_ge(dve_r.sem, dve_r.at("xh", i))
            pe.sem_inc(m.gate, 1)
            for t in tiles:
                mm = pe.transpose(ps[:, 4 + t // 4, t % 4 * 128:t % 4 * 128 + 128], xh[:, t, :], m.ident[:])
            mm.then_inc(S.mark("xh_turned"), 1)
        S = pe_f
        pe.wait_ge(act_r.sem, act_r.at("hm", ROUNDS - 1))
        for t in tiles:
            mm = pe.matmul(ps[:, t // 4, t % 4 * 128:t % 4 * 128 + 128], flat(hm)[:, 128 * t:128 * t + 128], w["bc_w"][:], start=True, stop=True)
        mm.then_inc(S.mark("bc"), 1)
        pe.wait_ge(dve_f.sem, dve_f.at("ltc"))
        for k in range(CP):
            mm = pe.transpose(ps[:, 4, 128 * k:128 * k + 128], xh0[:, k, :], m.ident[:])
        mm.then_inc(S.mark("ltc_turned"), 1)
        pe.wait_ge(dve_f.sem, dve_f.at("bcc"))
        for t in tiles:
            mm = pe.transpose(ps[:, 2 + t // 4, t % 4 * 128:t % 4 * 128 + 128], cent[:, t, :], m.ident[:])
        mm.then_inc(S.mark("bcc_turned"), 1)
        pe.wait_ge(act_f.sem, act_f.at("ltt"))
        pe.wait_ge(dve_f.sem, dve_f.at("hwg"))
        for k in range(CP):
            mm = pe.matmul(ps[:, 5, V * k:V * k + V], ltT[:, 128 * k:128 * k + 128], hwg[:], start=True, stop=True)
        mm.then_inc(S.mark("th"), 1)
        pe.matmul(ps[:, 6, 0:V], fb[:], w["head_w"][:], start=True, stop=True).then_inc(S.mark("lb"), 1)
        pe.wait_ge(act_f.sem, act_f.at("bct"))
        for t in tiles:
            if t >= 2:
                pe.wait_ge(dve_f.sem, dve_f.at(f"pick{t - 2}"))
            pe.matmul(ps[:, t % 2, :], bcT[:, t, :], ltT2[:], start=True, stop=False)
            pe.matmul(ps[:, t % 2, :], ones[:], ltsq[:], start=False, stop=True).then_inc(S.mark(f"var{t}"), 1)
        pe.wait_ge(dve_f.sem, dve_f.at("th1"))
        for t in tiles:
            if t >= 2:
                pe.wait_ge(dve_f.sem, dve_f.at(f"scaled{t - 2}"))
            pe.matmul(ps[:, 2 + t % 2, :], bcT[:, t, :], hwg[:].unsqueeze(1).broadcast_to([D, CH, V]), start=True, stop=False)
            for k in range(CP):
                mm = pe.matmul(ps[:, 2 + t % 2, 128 * k:128 * k + 128], hot[:, k, 128 * t:128 * t + 128], th[:, k].rearrange("p c v -> p (c v)"),
                               start=False, stop=k == CP - 1)
            mm.then_inc(S.mark(f"logits{t}"), 1)
        phase_end(m, pe, ph)

    def scalar(act):
        for s in (act_c, act_r, act_f):
            s.start(act)
        S = act_c
        act.wait_ge(landed, all_landed)
        act.wait_ge(dve_c.sem, dve_c.at("ss"))
        act.activation(st4b[:], st4[:], ACT.Sqrt, bias=eps[:], scale=1.0 / D).then_inc(S.mark("std0"), 1)
        act.wait_ge(pe_c.sem, pe_c.at("h0_turned"))
        act.activation(hT0[:], ps[:, 0, :], ACT.Identity, bias=w["lln_b"][:], scale=w["lln_g"][:]).then_inc(S.mark("h0_copied"), 1)
        act.wait_ge(pe_c.sem, pe_c.at("mlp1"))
        for k in range(2):
            act.activation(gl0[:, k, :], ps[:, 1 + k, :], ACT.Gelu, bias=w["lb1"][:, k:k + 1]).then_inc(S.mark(f"gelu{k}"), 1)
        act.wait_ge(pe_c.sem, pe_c.at("local_turned"))
        act.activation(hT0[:], ps[:, 0, :], ACT.Copy).then_inc(S.mark("local_copied"), 1)
        act.wait_ge(pe_c.sem, pe_c.at("pooled"))
        act.activation(pooled[:].rearrange("p k d -> p (k d)"), ps[:, 1, :], ACT.Copy, scale=1.0 / CH).then_inc(S.mark("pooled_copied"), 1)
        act.wait_ge(pe_c.sem, pe_c.at("summ"))
        act.activation(flat(hm), ps[:, 2:4, :].rearrange("p b n -> p (b n)"), ACT.Identity, bias=w["pool_b"][:]).then_inc(S.mark("summ_copied"), 1)
        S = act_r
        with act.Fori(0, ROUNDS) as i:
            act.wait_ge(pe_r.sem, pe_r.at("pre_a", i))
            act.activation(flat(a), ps[:, 0:2, :].rearrange("p b n -> p (b n)"), ACT.Identity, bias=w["msg_b1"][:]).then_inc(S.mark("a"), 1)
            for d in range(WIN + 1):
                act.wait_ge(dve_r.sem, dve_r.at(f"z{d}", i))
                act.activation(z[d][:, :, d:], z[d][:, :, d:], ACT.Gelu).then_inc(S.mark(f"gelu{d}"), 1)
            act.wait_ge(pe_r.sem, pe_r.at("msg", i))
            act.activation(agg[:], ps[:, 4:6, :].rearrange("p b n -> p (b n)"), ACT.Identity, bias=w["msg_b2"][:]).then_inc(S.mark("agg"), 1)
            act.wait_ge(pe_r.sem, pe_r.at("upd1", i))
            act.activation(u[:], ps[:, 6:8, :].rearrange("p b n -> p (b n)"), ACT.Gelu, bias=w["upd_b1"][:]).then_inc(S.mark("u"), 1)
            act.wait_ge(dve_r.sem, dve_r.at("ss", i))
            act.activation(std[:], ss[:], ACT.Sqrt, bias=eps[:], scale=1.0 / D).then_inc(S.mark("std"), 1)
            act.wait_ge(pe_r.sem, pe_r.at("xh_turned", i))
            act.activation(flat(hm), ps[:, 4:6, :].rearrange("p b n -> p (b n)"), ACT.Identity, bias=w["mln_b"][:], scale=w["mln_g"][:]).then_inc(S.mark("hm"), 1)
        S = act_f
        act.wait_ge(pe_f.sem, pe_f.at("ltc_turned"))
        act.activation(ltT[:], ps[:, 4, :], ACT.Copy).then_inc(S.mark("ltt"), 1)
        act.activation(ltT2[:], ps[:, 4, :], ACT.Copy, scale=2.0).then_inc(S.mark("ltt2"), 1)
        act.activation(ltsq[:], ps[:, 4, :], ACT.Square).then_inc(S.mark("ltsq"), 1)
        act.wait_ge(pe_f.sem, pe_f.at("bcc_turned"))
        act.activation(flat(bcT), ps[:, 2:4, :].rearrange("p b n -> p (b n)"), ACT.Copy).then_inc(S.mark("bct"), 1)
        act.wait_ge(dve_f.sem, dve_f.at("var_all"))
        act.activation(dev[:], var[:], ACT.Sqrt, bias=eps[:], scale=1.0 / D).then_inc(S.mark("std"), 1)
        phase_end(m, act, ph)

    def vector(dve):
        for s in (dve_c, dve_r, dve_f):
            s.start(dve)
        S = dve_c
        wide = lambda v, n=D: cols(v.unsqueeze(2), n)
        dve.memset(eps[:], EPS).then_inc(S.mark("eps"), 1)
        dve.wait_ge(landed, all_landed)
        dve.tensor_tensor(w["h0"][:], w["h0"][:], w["pos"][:], ALU.add).then_inc(S.mark("h0"), 1)
        dve.wait_ge(S.sem, S.at("h0"))
        dve.tensor_reduce(st4[:], w["h0"][:], X, ALU.add).then_inc(S.mark("sum"), 1)
        dve.wait_ge(S.sem, S.at("sum"))
        dve.tensor_scalar(st4b[:], st4[:], 1.0 / D, None, ALU.mult).then_inc(S.mark("mean"), 1)
        dve.wait_ge(S.sem, S.at("mean"))
        dve.tensor_tensor(xh0[:], w["h0"][:], wide(st4b[:]), ALU.subtract).then_inc(S.mark("cent"), 1)
        dve.wait_ge(S.sem, S.at("cent"))
        dve.tensor_tensor(sq0[:], xh0[:], xh0[:], ALU.mult).then_inc(S.mark("sq"), 1)
        dve.wait_ge(S.sem, S.at("sq"))
        dve.tensor_reduce(st4[:], sq0[:], X, ALU.add).then_inc(S.mark("ss"), 1)
        dve.wait_ge(act_c.sem, act_c.at("std0"))
        dve.reciprocal(st4[:], st4b[:]).then_inc(S.mark("recip"), 1)
        dve.wait_ge(S.sem, S.at("recip"))
        dve.tensor_tensor(xh0[:], xh0[:], wide(st4[:]), ALU.mult).then_inc(S.mark("xh"), 1)
        for c2 in range(2):
            rows = slice(64 * c2, 64 * c2 + 64)
            dve.tensor_scalar(hot[rows], tok[rows].rearrange("p (k cp c) -> p c cp k", cp=CP, c=2)[:, c2], w["id_col"][rows], None, ALU.is_equal
                              ).then_inc(S.mark(f"hot{c2}"), 1)
        dve.wait_ge(pe_c.sem, pe_c.at("mlp2"))
        dve.tensor_tensor(local[:].rearrange("p k d -> p (k d)"), ps[:, 3, :], w["h0"][:].rearrange("p k d -> p (k d)"), ALU.add).then_inc(S.mark("local_h"), 1)
        dve.wait_ge(S.sem, S.at("local_h"))
        dve.tensor_tensor(local[:], local[:], w["lb2"][:].unsqueeze(1).broadcast_to([128, CP, D]), ALU.add).then_inc(S.mark("local"), 1)
        S = dve_r
        with dve.Fori(0, ROUNDS) as i:
            dve.wait_ge(pe_r.sem, pe_r.at("pre_b", i))
            dve.tensor_copy(flat(b), ps[:, 2:4, :].rearrange("p b n -> p (b n)")).then_inc(S.mark("b"), 1)
            dve.wait_ge(act_r.sem, act_r.at("a", i))
            dve.wait_ge(S.sem, S.at("b", i))
            for d in range(WIN + 1):
                dve.tensor_tensor(z[d][:, :, d:], a[:, :, d:], b[:, :, 0:NCH - d], ALU.add).then_inc(S.mark(f"z{d}"), 1)
            for d in range(1, WIN + 1):
                dve.wait_ge(act_r.sem, act_r.at(f"gelu{d}", i))
                if d > 1:
                    dve.wait_ge(S.sem, S.at(f"sum{d - 1}", i))
                dve.tensor_tensor(z[0][:, :, d:], z[0][:, :, d:], z[d][:, :, d:], ALU.add).then_inc(S.mark(f"sum{d}"), 1)
            dve.wait_ge(S.sem, S.at(f"sum{WIN}", i))
            dve.tensor_tensor(z[0][:], z[0][:], w["inv_count"][:].unsqueeze(1).broadcast_to([D, NB, NCH]), ALU.mult).then_inc(S.mark("scaled"), 1)
            dve.wait_ge(pe_r.sem, pe_r.at("upd2", i))
            dve.scalar_tensor_tensor(out=r[:], in0=ps[:, 0:2, :].rearrange("p b n -> p (b n)"), scalar=w["upd_b2"][:], in1=flat(hm), op0=ALU.add, op1=ALU.add
                                     ).then_inc(S.mark("r"), 1)
            dve.wait_ge(pe_r.sem, pe_r.at("r_turned", i))
            rows = ps[:, 2:4, :].rearrange("p b (t d) -> p (b t) d", d=D)
            dve.tensor_reduce(ss[:], rows, X, ALU.add).then_inc(S.mark("lsum"), 1)
            dve.wait_ge(S.sem, S.at("lsum", i))
            dve.tensor_scalar(mean[:], ss[:], 1.0 / D, None, ALU.mult).then_inc(S.mark("mean"), 1)
            dve.wait_ge(S.sem, S.at("mean", i))
            dve.tensor_tensor(cent[:], rows, wide(mean[:]), ALU.subtract).then_inc(S.mark("cent"), 1)
            dve.wait_ge(S.sem, S.at("cent", i))
            dve.tensor_tensor(sq[:], cent[:], cent[:], ALU.mult).then_inc(S.mark("sq"), 1)
            dve.wait_ge(S.sem, S.at("sq", i))
            dve.tensor_reduce(ss[:], sq[:], X, ALU.add).then_inc(S.mark("ss"), 1)
            dve.wait_ge(act_r.sem, act_r.at("std", i))
            dve.reciprocal(mean[:], std[:]).then_inc(S.mark("recip"), 1)
            dve.wait_ge(S.sem, S.at("recip", i))
            dve.tensor_tensor(xh[:], cent[:], wide(mean[:]), ALU.mult).then_inc(S.mark("xh"), 1)
        S = dve_f
        dve.memset(ones[:], 1.0).then_inc(S.mark("ones"), 1)
        dve.memset(th[:], 0.0).then_inc(S.mark("th_clear"), 1)
        dve.tensor_copy(fb[:], w["fln_b"][:].broadcast_to([D, 128])).then_inc(S.mark("fb"), 1)
        dve.tensor_scalar(hwg[:], w["head_w"][:], w["fln_g"][:], None, ALU.mult).then_inc(S.mark("hwg"), 1)
        dve.tensor_copy(tokf[:], tokr[:]).then_inc(S.mark("tokf"), 1)
        dve.tensor_reduce(st4[:], local[:], X, ALU.add).then_inc(S.mark("tsum"), 1)
        dve.wait_ge(S.sem, S.at("tsum"))
        dve.tensor_scalar(st4b[:], st4[:], 1.0 / D, None, ALU.mult).then_inc(S.mark("tmean"), 1)
        dve.wait_ge(S.sem, S.at("tmean"))
        dve.tensor_tensor(xh0[:], local[:], wide(st4b[:]), ALU.subtract).then_inc(S.mark("ltc"), 1)
        dve.wait_ge(pe_f.sem, pe_f.at("bc"))
        dve.tensor_tensor(cent[:], ps[:, 0:2, :].rearrange("p b (t d) -> p (b t) d", d=D), w["bc_b"][:].unsqueeze(1).broadcast_to([128, KT, D]), ALU.add).then_inc(S.mark("bc"), 1)
        dve.wait_ge(S.sem, S.at("bc"))
        dve.tensor_reduce(ss[:], cent[:], X, ALU.add).then_inc(S.mark("bsum"), 1)
        dve.wait_ge(S.sem, S.at("bsum"))
        dve.tensor_scalar(mean[:], ss[:], 1.0 / D, None, ALU.mult).then_inc(S.mark("bmean"), 1)
        dve.wait_ge(S.sem, S.at("bmean"))
        dve.tensor_tensor(cent[:], cent[:], wide(mean[:]), ALU.subtract).then_inc(S.mark("bcc"), 1)
        dve.wait_ge(S.sem, S.at("bcc"))
        dve.tensor_tensor(sq[:], cent[:], cent[:], ALU.mult).then_inc(S.mark("bsq"), 1)
        dve.wait_ge(S.sem, S.at("bsq"))
        dve.tensor_reduce(ss[:], sq[:], X, ALU.add).then_inc(S.mark("bss"), 1)
        dve.wait_ge(pe_f.sem, pe_f.at("th"))
        for c2 in range(2):
            rows = slice(64 * c2, 64 * c2 + 64)
            dve.tensor_copy(th[rows, :, c2, :], ps[rows, 5, 0:CP * V].rearrange("p (k v) -> p k v", v=V)).then_inc(S.mark(f"th{c2}"), 1)
        dve.wait_ge(pe_f.sem, pe_f.at("lb"))
        dve.tensor_copy(lb[:], ps[:, 6, 0:V]).then_inc(S.mark("lb"), 1)
        for t in tiles:
            dve.tensor_tensor(hotr[t % 2][:], wide(tokf[:, t, :], V), w["id_row"][:].unsqueeze(1).broadcast_to([128, CH, V]), ALU.is_equal).then_inc(S.mark(f"hotr{t}"), 1)
            dve.wait_ge(pe_f.sem, pe_f.at(f"var{t}"))
            dve.wait_ge(S.sem, S.at(f"hotr{t}"))
            dve.tensor_tensor(pick[t % 2][:], ps[:, t % 2, :].rearrange("p (c v) -> p c v", v=V), hotr[t % 2][:], ALU.mult).then_inc(S.mark(f"pick{t}"), 1)
            dve.wait_ge(S.sem, S.at(f"pick{t}"))
            dve.tensor_reduce(var[:, t, :], pick[t % 2][:], X, ALU.add).then_inc(S.mark(f"var{t}"), 1)
        dve.wait_ge(S.sem, S.at(f"var{KT - 1}"))
        dve.tensor_tensor(var[:], var[:], wide(ss[:], CH), ALU.add).then_inc(S.mark("var_all"), 1)
        dve.wait_ge(act_f.sem, act_f.at("std"))
        dve.reciprocal(rstd[:], dev[:]).then_inc(S.mark("recip"), 1)
        dve.wait_ge(S.sem, S.at("recip"))
        for t in tiles:
            dve.wait_ge(pe_f.sem, pe_f.at(f"logits{t}"))
            if t >= 2:
                dve.wait_ge(stored[t % 2], 16 * (t // 2))
            dve.tensor_tensor(lg[t % 2][:], ps[:, 2 + t % 2, :].rearrange("p (c v) -> p c v", v=V), wide(rstd[:, t, :], V), ALU.mult).then_inc(S.mark(f"scaled{t}"), 1)
            dve.wait_ge(S.sem, S.at(f"scaled{t}"))
            dve.tensor_tensor(lg[t % 2][:], lg[t % 2][:], lb[:].unsqueeze(1).broadcast_to([128, CH, V]), ALU.add).then_inc(S.mark(f"logits{t}"), 1)
        phase_end(m, dve, ph)

    def gpsimd(pool):
        phase_end(m, pool, ph)

    return dict(sync=sync, tensor=tensor, scalar=scalar, vector=vector, gpsimd=gpsimd)


def token_norm(dve, S, act_s, pre, src, cent, sq, mean, ss, landed=None):
    J = NB * T // TM
    quarters = [slice(J // 4 * k, J // 4 * (k + 1)) for k in range(4)]
    for k, j in enumerate(quarters):
        if landed:
            dve.wait_ge(landed[k], 32)
        dve.tensor_reduce(ss[:, j], src[:, j], X, ALU.add).then_inc(S.mark(f"{pre}_sum{k}"), 1)
        dve.wait_ge(S.sem, S.at(f"{pre}_sum{k}"))
        dve.tensor_scalar(mean[:, j], ss[:, j], 1.0 / C, None, ALU.mult).then_inc(S.mark(f"{pre}_mean{k}"), 1)
        dve.wait_ge(S.sem, S.at(f"{pre}_mean{k}"))
        dve.tensor_tensor(cent[:, j], src[:, j], cols(mean[:, j].unsqueeze(2), C), ALU.subtract).then_inc(S.mark(f"{pre}_cent{k}"), 1)
        if k:
            squares_sum(dve, S, act_s, pre, k - 1, sq, ss)
    squares_sum(dve, S, act_s, pre, 3, sq, ss)
    dve.wait_ge(act_s.sem, act_s.at(f"{pre}_std"))
    dve.reciprocal(ss[:], mean[:]).then_inc(S.mark(f"{pre}_recip"), 1)
    dve.wait_ge(S.sem, S.at(f"{pre}_recip"))


def squares_sum(dve, S, act_s, pre, k, sq, ss):
    J = NB * T // TM
    dve.wait_ge(act_s.sem, act_s.at(f"{pre}_sq{k}"))
    dve.tensor_reduce(ss[:, J // 4 * k:J // 4 * (k + 1)], sq[k % 2][:], X, ALU.add).then_inc(S.mark(f"{pre}_ss{k}"), 1)


NORM_DVE = [n for k in range(4) for n in [f"sum{k}", f"mean{k}", f"cent{k}"] + ([f"ss{k - 1}"] if k else [])] + ["ss3", "recip"]
NORM_ACT = [f"sq{k}" for k in range(4)] + ["std"]


def token_norm_squares(act, S, dve_s, pre, cent, sq, mean, ss, eps, ready):
    J = NB * T // TM
    for k in range(4):
        j = slice(J // 4 * k, J // 4 * (k + 1))
        act.wait_ge(dve_s.sem, dve_s.at(ready.format(k=k)))
        if k >= 2:
            act.wait_ge(dve_s.sem, dve_s.at(f"{pre}_ss{k - 2}"))
        act.activation(sq[k % 2][:], cent[:, j], ACT.Square).then_inc(S.mark(f"{pre}_sq{k}"), 1)
    act.wait_ge(dve_s.sem, dve_s.at(f"{pre}_ss3"))
    act.activation(mean[:], ss[:], ACT.Sqrt, bias=eps[0:TM], scale=1.0 / C).then_inc(S.mark(f"{pre}_std"), 1)


def joint_in_phase(nc, m, st, ph):
    J = NB * T // TM
    sb = lambda n, s, d=F32: st.enter_context(nc.sbuf_tensor(n, s, d))
    cent = sb("ji_cent", [TM, J, C])
    sq = [sb(f"ji_sq{k}", [TM, J // 4, C]) for k in range(2)]
    mean, ss, eps = sb("ji_mean", [TM, J]), sb("ji_ss", [TM, J]), sb("ji_eps", [128, 1])
    wv, wvT = sb("ji_wv", [C, C]), sb("ji_wvt", [C, C])
    xh = [sb(f"ji_xh{s}", [TM, GJ, C]) for s in range(2)]
    xT = [sb(f"ji_xt{s}", [C, GT]) for s in range(2)]
    vT = [sb(f"ji_vt{s}", [C, GT]) for s in range(2)]
    ps = m.psum
    landed = m.whole.enter_context(nc.semaphore("ji_landed"))
    h_landed = [m.whole.enter_context(nc.semaphore(f"ji_h_landed{k}")) for k in range(4)]
    stored = [Landed(nc, m.whole, f"ji_stored{s}", 2) for s in range(2)]
    dve_n = Steps(nc, m.whole, "ji_dve_norm", ["eps"] + [f"n_{k}" for k in NORM_DVE] + ["wvt"])
    act_n = Steps(nc, m.whole, "ji_act_norm", [f"n_{k}" for k in NORM_ACT])
    pe_n = Steps(nc, m.whole, "ji_pe_w", ["wvt"])
    pe_t, pe_v = Steps(nc, m.whole, "ji_pe_turned", ["turned0", "turned1"]), Steps(nc, m.whole, "ji_pe_v", ["v0", "v1"])
    act_s = Steps(nc, m.whole, "ji_act", ["xt0", "xt1"])
    dve_x, dve_v = Steps(nc, m.whole, "ji_dve_x", ["xh0", "xh1"]), Steps(nc, m.whole, "ji_dve_v", ["vt0", "vt1"])
    P = NG // 2

    def sync(sp):
        for s in range(2):
            stored[s].start(sp)
        sp.dma_start(wv[:], m.dram["attn_Wv"]).then_inc(landed, 16)
        rows = m.dram["h_d"].rearrange("(j p) c -> p j c", p=TM)
        for k in range(4):
            j = slice(J // 4 * k, J // 4 * (k + 1))
            for p0, p1 in ((0, 112), (112, TM)):
                sp.dma_start(m.h[p0:p1, j], rows[p0:p1, j]).then_inc(h_landed[k], 16)
        with sp.Fori(0, P) as i:
            for s in range(2):
                sp.wait_ge(act_s.sem, act_s.at(f"xt{s}", i))
                sp.sem_inc(m.gate, 1)
                sp.dma_start(m.dram["xt_d"][:, bass.ds(i * 2 * GT + s * GT, GT)], xT[s][:]).then_inc(stored[s].sem, 16)
                sp.wait_ge(dve_v.sem, dve_v.at(f"vt{s}", i))
                sp.sem_inc(m.gate, 1)
                sp.dma_start(m.dram["v_d"][bass.ds(i * 2 * GB + s * GB, GB)].rearrange("b (o s) -> o b s", o=C),
                             vT[s][:].rearrange("o (b s) -> o b s", b=GB)).then_inc(stored[s].sem, 16)
        for s in range(2):
            sp.wait_ge(stored[s].sem, stored[s].at(P - 1))
        phase_end(m, sp, ph)

    def tensor(pe):
        for S in (pe_n, pe_t, pe_v):
            S.start(pe)
        pe.wait_ge(landed, 16)
        pe.transpose(ps[0:C, 0, 0:C], wv[:], m.ident[0:C, 0:C]).then_inc(pe_n.mark("wvt"), 1)
        pe.wait_ge(dve_n.sem, dve_n.at("wvt"))

        def turn(s, i):
            pe.wait_ge(dve_x.sem, dve_x.at(f"xh{s}", i))
            pe.wait_ge(act_s.sem, act_s.before(f"xt{s}", i))
            pe.sem_inc(m.gate, 1)
            for j in range(GJ):
                mm = pe.transpose(ps[0:C, 2 * s + j // 4, j % 4 * TM:j % 4 * TM + TM], xh[s][:, j, :], m.ident[0:TM, 0:TM])
            mm.then_inc(pe_t.mark(f"turned{s}"), 1)

        def values(s, i):
            pe.wait_ge(act_s.sem, act_s.at(f"xt{s}", i))
            pe.wait_ge(dve_v.sem, dve_v.before(f"vt{s}", i))
            pe.sem_inc(m.gate, 1)
            for k in range(2):
                mm = pe.matmul(ps[0:C, 4 + 2 * s + k, 0:GT // 2], wvT[:], xT[s][:, GT // 2 * k:GT // 2 * (k + 1)], start=True, stop=True)
            mm.then_inc(pe_v.mark(f"v{s}"), 1)

        skewed(pe, P, turn, values)
        phase_end(m, pe, ph)

    def scalar(act):
        act_n.start(act)
        act_s.start(act)
        token_norm_squares(act, act_n, dve_n, "n", cent, sq, mean, ss, eps, "n_cent{k}")
        with act.Fori(0, P) as i:
            for s in range(2):
                act.wait_ge(pe_t.sem, pe_t.at(f"turned{s}", i))
                act.wait_ge(pe_v.sem, pe_v.before(f"v{s}", i))
                act.wait_ge(stored[s].sem, stored[s].before(i))
                act.activation(xT[s][:, 0:4 * TM], ps[0:C, 2 * s, 0:4 * TM], ACT.Copy)
                act.activation(xT[s][:, 4 * TM:GT], ps[0:C, 2 * s + 1, 0:TM], ACT.Copy).then_inc(act_s.mark(f"xt{s}"), 1)
        phase_end(m, act, ph)

    def vector(dve):
        for S in (dve_n, dve_x, dve_v):
            S.start(dve)
        dve.memset(eps[:], EPS).then_inc(dve_n.mark("eps"), 1)
        token_norm(dve, dve_n, act_n, "n", m.h, cent, sq, mean, ss, h_landed)
        dve.wait_ge(pe_n.sem, pe_n.at("wvt"))
        dve.tensor_copy(wvT[:], ps[0:C, 0, 0:C]).then_inc(dve_n.mark("wvt"), 1)

        def scale(s, i):
            dve.wait_ge(pe_t.sem, pe_t.before(f"turned{s}", i))
            at = bass.ds(i * 2 * GJ + s * GJ, GJ)
            dve.tensor_tensor(xh[s][:], cent[:, at, :], cols(ss[:, at].unsqueeze(2), C), ALU.mult).then_inc(dve_x.mark(f"xh{s}"), 1)

        def copy_values(s, i):
            dve.wait_ge(pe_v.sem, pe_v.at(f"v{s}", i))
            dve.wait_ge(stored[s].sem, stored[s].before(i))
            dve.tensor_copy(vT[s][:].rearrange("o (k n) -> o k n", k=2), ps[0:C, 4 + 2 * s:6 + 2 * s, 0:GT // 2]).then_inc(dve_v.mark(f"vt{s}"), 1)

        skewed(dve, P, scale, copy_values)
        phase_end(m, dve, ph)

    def gpsimd(pool):
        phase_end(m, pool, ph)

    return dict(sync=sync, tensor=tensor, scalar=scalar, vector=vector, gpsimd=gpsimd)


def joint_phase(nc, m, st, ph):
    H, KD, KM = 8, 64, 128
    KT = T - KM
    D1 = KD + 1
    NJ = 8 * T // (2 * TM)
    NBP = 4
    NU = NBP * NJ // 2
    BU = 4
    first = [(b * NJ) // 2 for b in range(NBP)]
    last_unit = [(b * NJ + NJ - 1) // 2 for b in range(NBP)]
    asked = {(first[b] - 3) % NU: (b, int(first[b] < 3)) for b in range(NBP)}
    sb = lambda n, s, d=F32: st.enter_context(nc.sbuf_tensor(n, s, d))
    wq, wk = sb("jo_wq", [KD, 2, 2, 2, C]), sb("jo_wk", [KD, C])
    wqk = sb("jo_wqk", [128, 2, 2 * C])
    xs = [sb(f"jo_x{s}", [128, 2, T]) for s in range(NBP)]
    v = [sb(f"jo_v{s}", [KM, D1]) for s in range(NBP)]
    v_tail = [sb(f"jo_v_tail{s}", [BU * KT, BU * D1]) for s in range(NBP)]
    v_cross = [sb(f"jo_v_cross{k}", [BU * KT, BU * D1]) for k in range(NBP // 2)]
    q = [sb(f"jo_q{s}", [128, T, H // 2]) for s in range(NBP)]
    mx = [sb(f"jo_max{u}", [TM, BU]) for u in range(2)]
    sc = [sb(f"jo_sc{u}", [TM, BU, T]) for u in range(2)]
    pr = [sb(f"jo_pr{u}", [TM, BU, KM]) for u in range(2)]
    pr_tail = [sb(f"jo_pr_tail{u}", [TM, BU * KT]) for u in range(2)]
    pT = [sb(f"jo_pt{u}", [KM, BU, TM]) for u in range(2)]
    pT_tail = [sb(f"jo_pt_tail{u}", [BU * KT, TM]) for u in range(2)]
    rs = [sb(f"jo_rs{u}", [TM, BU]) for u in range(2)]
    ctx = [sb(f"jo_ctx{s}", [TM, 2 * NJ, KD]) for s in range(NBP)]
    ps = m.psum
    NP = NB // NBP
    TURNED, TAIL, CTX, QUERIES = 4, 5, 6, 7
    wl = m.whole.enter_context(nc.semaphore("jo_weights_landed"))
    xl = [Landed(nc, m.whole, f"jo_x_landed{s}", 2) for s in range(NBP)]
    vl = [Landed(nc, m.whole, f"jo_v_landed{s}", 3 + BU) for s in range(NBP)]
    stored = [Landed(nc, m.whole, f"jo_ctx_stored{s}", 2) for s in range(NBP)]
    S1 = lambda n, steps: Steps(nc, m.whole, n, steps)
    pe_w, act_w, dve_w = S1("jo_pe_w", ["wqk"]), S1("jo_act_w", ["wqk"]), S1("jo_dve_w", ["ready"])
    pe_q = S1("jo_queries", [f"q{s}{k}" for s in range(NBP) for k in range(2)])
    act_q = S1("jo_queries_copied", [f"q{s}{k}" for s in range(NBP) for k in range(2)])
    pe_sc = S1("jo_scores", [f"s{n}" for n in range(NU)])
    dve_sc = S1("jo_shifted", [f"{w}{n}" for n in range(NU) for w in ("max", "minus")])
    act_e = S1("jo_exp", [f"e{n}" for n in range(NU)])
    pe_t = S1("jo_turned", [f"t{n}" for n in range(NU)])
    act_t = S1("jo_turned_copied", [f"t{n}" for n in range(NU)])
    pe_v = S1("jo_attended", [f"v{n}" for n in range(NU)])
    dve_v = S1("jo_normed", [f"{w}{n}" for n in range(NU) for w in ("recip", "ctx")])

    def wrapped(n, i):
        return (n, i) if n < NU else (n - NU, i + 1)

    def back(S, fmt, n, i, by):
        return S.at(fmt.format(n - by), i) if n >= by else S.before(fmt.format(n - by + NU), i)

    def tiles(n):
        return [divmod(2 * n + k, NJ) for k in range(2)]

    def sync(sp):
        for s in range(NBP):
            xl[s].start(sp)
            vl[s].start(sp)
            stored[s].start(sp)
        for h in range(H):
            sp.dma_start(wq[:, h // 4, h % 2, h // 2 % 2], m.dram["attn_Wq"][h * KD:(h + 1) * KD]).then_inc(wl, 16)
        sp.dma_start(wk[:], m.dram["attn_Wk"]).then_inc(wl, 16)
        for blocks in v_tail + v_cross:
            sp.dma_start(blocks[:], m.dram["tail_blocks"]).then_inc(wl, 16)
        sp.wait_ge(wl, 16 * 15)
        sp.wait_ge(dve_w.sem, dve_w.at("ready"))

        def load_x(s, i):
            sp.wait_ge(pe_sc.sem, pe_sc.before(f"s{last_unit[s]}", i))
            sp.sem_inc(m.gate, 1)
            for par in range(2):
                sp.dma_start(xs[s][C * par:C * par + C, par], m.dram["xt_d"][:, bass.ds(i * NBP * T + s * T, T)]).then_inc(xl[s].sem, 16)

        def load_v(s, i):
            sp.wait_ge(pe_v.sem, pe_v.before(f"v{last_unit[s]}", i))
            sp.sem_inc(m.gate, 1)
            rows = m.dram["v_d"][bass.ds(i * NBP + s, 1)].rearrange("b (t d) -> t (b d)", d=KD)
            sp.dma_start(v[s][:, 0:KD], rows[0:KM]).then_inc(vl[s].sem, 16)
            half = 2 * (s % 2)
            for dst, js in ((v_tail[s], range(BU)), (v_cross[s // 2], (half, half + 1))):
                for j in js:
                    sp.dma_start(dst[KT * j:KT * (j + 1), D1 * j:D1 * j + KD], rows[KM:T]).then_inc(vl[s].sem, 16)

        def store(s, i, ready):
            sp.wait_ge(dve_v.sem, ready)
            sp.sem_inc(m.gate, 1)
            dst = m.dram["ctx_d"][bass.ds(i * NBP + s, 1)].rearrange("b (p n) -> p (b n)", p=TM)
            src = ctx[s][:].rearrange("p n d -> p (n d)")
            for p0, p1 in ((0, 112), (112, TM)):
                sp.dma_start(dst[p0:p1], src[p0:p1]).then_inc(stored[s].sem, 16)

        for s in range(NBP):
            load_x(s, 0)
            load_v(s, 0)
        with sp.Fori(1, NP) as i:
            for s in range(NBP):
                load_x(s, i)
                load_v(s, i)
                store(s, i - 1, dve_v.before(f"ctx{last_unit[s]}", i))
        for s in range(NBP):
            store(s, NP - 1, dve_v.at(f"ctx{last_unit[s]}", NP - 1))
        for s in range(NBP):
            sp.wait_ge(stored[s].sem, stored[s].at(NP - 1))
        phase_end(m, sp, ph)

    def tensor(pe):
        for S in (pe_w, pe_q, pe_sc, pe_t, pe_v):
            S.start(pe)
        pe.wait_ge(wl, 16 * 15)
        for k in range(2):
            for par in range(2):
                mm = pe.matmul(ps[:, 0, (2 * k + par) * C:(2 * k + par + 1) * C], wq[:, k, par].rearrange("d f c -> d (f c)"), wk[:], start=True, stop=True)
        mm.then_inc(pe_w.mark("wqk"), 1)
        pe.wait_ge(act_w.sem, act_w.at("wqk"))

        def queries(s, i, k):
            if k == 0:
                pe.wait_ge(xl[s].sem, xl[s].at(i))
            before = act_q.at(f"q{s}0", i) if k else (act_q.at(f"q{s - 1}1", i) if s else act_q.before(f"q{NBP - 1}1", i))
            pe.wait_ge(act_q.sem, before)
            pe.sem_inc(m.gate, 1)
            mm = pe.matmul(ps[:, QUERIES, 0:2 * T], wqk[:, k], xs[s][:].rearrange("p f s -> p (f s)"), start=True, stop=True)
            mm.then_inc(pe_q.mark(f"q{s}{k}"), 1)

        def scores(n, i):
            n, i = wrapped(n, i)
            u = n % 2
            if n in first:
                pe.wait_ge(act_q.sem, act_q.at(f"q{first.index(n)}1", i))
            pe.wait_ge(dve_sc.sem, back(dve_sc, "minus{}", n, i, 2))
            pe.sem_inc(m.gate, 1)
            for k, (s, j) in enumerate(tiles(n)):
                mm = pe.matmul(ps[0:TM, 2 * u + k, 0:2 * T], q[s][:].rearrange("c s h -> c (s h)")[:, j::NJ], xs[s][:].rearrange("p f s -> p (f s)"),
                               start=True, stop=True)
            mm.then_inc(pe_sc.mark(f"s{n}"), 1)

        def turn(n, i):
            n, i = wrapped(n, i)
            u = n % 2
            pe.wait_ge(act_e.sem, act_e.at(f"e{n}", i))
            pe.wait_ge(act_t.sem, back(act_t, "t{}", n, i, 1))
            pe.sem_inc(m.gate, 1)
            for b in range(BU):
                pe.transpose(ps[:, TURNED, b * TM:(b + 1) * TM], pr[u][:, b, :], m.ident[0:TM, 0:TM])
            pe.transpose(ps[0:BU * KT, TAIL, 0:TM], pr_tail[u][:, 0:BU * KT], m.ident[0:TM, 0:TM]).then_inc(pe_t.mark(f"t{n}"), 1)

        def attend(n, i):
            u, ((s0, _), (s1, _)) = n % 2, tiles(n)
            if n in first:
                s = first.index(n)
                pe.wait_ge(vl[s].sem, vl[s].at(i))
            pe.wait_ge(act_t.sem, act_t.at(f"t{n}", i))
            pe.wait_ge(dve_v.sem, back(dve_v, "ctx{}", n, i, 1))
            pe.sem_inc(m.gate, 1)
            pe.matmul(ps[0:TM, CTX, 0:BU * D1], pT_tail[u][:], (v_tail[s0] if s0 == s1 else v_cross[s0 // 2])[:], start=True, stop=False)
            for b in range(BU):
                mm = pe.matmul(ps[0:TM, CTX, b * D1:(b + 1) * D1], pT[u][:, b, :], v[(s0, s1)[b // 2]][:], start=False, stop=b == BU - 1)
            mm.then_inc(pe_v.mark(f"v{n}"), 1)

        def one_pass(i, last=False):
            for n in range(NU):
                s, more = asked.get(n, (0, 1))
                ask = n in asked and not (last and more)
                if ask:
                    queries(s, i + more, 0)
                if not (last and n + 2 >= NU):
                    scores(n + 2, i)
                if ask:
                    queries(s, i + more, 1)
                attend(n, i)
                if not (last and n + 1 >= NU):
                    turn(n + 1, i)

        assert first[1] == 2
        for s in range(2):
            for k in range(2):
                queries(s, 0, k)
            scores(s, 0)
        turn(0, 0)
        with pe.Fori(0, NP - 1) as i:
            one_pass(i)
        one_pass(NP - 1, last=True)
        phase_end(m, pe, ph)

    def scalar(act):
        for S in (act_w, act_q, act_e, act_t):
            S.start(act)
        act.wait_ge(pe_w.sem, pe_w.at("wqk"))
        act.activation(wqk[:].rearrange("c k o -> c (k o)"), ps[:, 0, 0:4 * C], ACT.Copy, scale=H ** -0.5).then_inc(act_w.mark("wqk"), 1)
        act.preload_act_table(ACT.Exp)

        def copy_queries(s, i):
            for k in range(2):
                act.wait_ge(pe_q.sem, pe_q.at(f"q{s}{k}", i))
                if k == 0:
                    act.wait_ge(pe_sc.sem, pe_sc.before(f"s{last_unit[s]}", i))
                act.activation(q[s][:, :, 2 * k:2 * k + 2].rearrange("p s h -> p h s"), ps[:, QUERIES, 0:2 * T].rearrange("p (h s) -> p h s", h=2),
                               ACT.Copy).then_inc(act_q.mark(f"q{s}{k}"), 1)

        def exp(n, i):
            n, i = wrapped(n, i)
            u = n % 2
            act.wait_ge(dve_sc.sem, dve_sc.at(f"minus{n}", i))
            act.wait_ge(pe_t.sem, back(pe_t, "t{}", n, i, 2))
            act.activation(pr[u][:], sc[u][:, :, 0:KM], ACT.Exp)
            act.activation(pr_tail[u][:, 0:BU * KT].rearrange("p (b t) -> p b t", b=BU), sc[u][:, :, KM:T], ACT.Exp).then_inc(act_e.mark(f"e{n}"), 1)

        def copy_turned(n, i):
            u = n % 2
            act.wait_ge(pe_t.sem, pe_t.at(f"t{n}", i))
            act.wait_ge(pe_v.sem, back(pe_v, "v{}", n, i, 2))
            act.activation(pT_tail[u][0:BU * KT], ps[0:BU * KT, TAIL, 0:TM], ACT.Copy)
            act.activation(pT[u][:].rearrange("p n m -> p (n m)"), ps[:, TURNED, 0:BU * TM], ACT.Copy).then_inc(act_t.mark(f"t{n}"), 1)

        def one_pass(i, last=False):
            for n in range(NU):
                copy_turned(n, i)
                s, more = asked.get(n, (0, 1))
                if n in asked and not (last and more):
                    copy_queries(s, i + more)
                if not (last and n + 1 >= NU):
                    exp(n + 1, i)

        for s in range(2):
            copy_queries(s, 0)
        exp(0, 0)
        with act.Fori(0, NP - 1) as i:
            one_pass(i)
        one_pass(NP - 1, last=True)
        phase_end(m, act, ph)

    def vector(dve):
        for S in (dve_w, dve_sc, dve_v):
            S.start(dve)
        for s in range(NBP):
            dve.memset(v[s][:, KD:D1], 1.0)
            clear = dve.memset(xs[s][:], 0.0)
        clear.then_inc(dve_w.mark("ready"), 1)

        def shift(n, i):
            n, i = wrapped(n, i)
            u = n % 2
            split = lambda ap: ap.rearrange("p (j r) t -> p j r t", r=2)
            scored = ps[0:TM, 2 * u:2 * u + 2, 0:2 * T].rearrange("p j (r t) -> p j r t", r=2)
            dve.wait_ge(pe_sc.sem, pe_sc.at(f"s{n}", i))
            dve.tensor_reduce(mx[u][:].rearrange("p (j r) -> p j r", r=2), scored, X, ALU.max).then_inc(dve_sc.mark(f"max{n}"), 1)
            dve.wait_ge(dve_sc.sem, dve_sc.at(f"max{n}", i))
            dve.wait_ge(act_e.sem, back(act_e, "e{}", n, i, 2))
            dve.tensor_tensor(split(sc[u][:]), scored, split(cols(mx[u][:].unsqueeze(2), T)), ALU.subtract).then_inc(dve_sc.mark(f"minus{n}"), 1)

        def normalise(n, i):
            u = n % 2
            o = ps[0:TM, CTX, 0:BU * D1].rearrange("p (b d) -> p b d", b=BU)
            dve.wait_ge(pe_v.sem, pe_v.at(f"v{n}", i))
            dve.reciprocal(rs[u][:], o[:, :, KD]).then_inc(dve_v.mark(f"recip{n}"), 1)
            dve.wait_ge(dve_v.sem, dve_v.at(f"recip{n}", i))
            if n in first:
                s = first.index(n)
                dve.wait_ge(stored[s].sem, stored[s].before(i))
            (s0, j0), (s1, j1) = tiles(n)
            parts = [(s0, j0, 0, BU)] if s0 == s1 else [(s0, j0, 0, 2), (s1, j1, 2, BU)]
            for s, j, a, b in parts:
                done = dve.tensor_tensor(ctx[s][:, 2 * j:2 * j + b - a, :], o[:, a:b, 0:KD], cols(rs[u][:, a:b].unsqueeze(2), KD), ALU.mult)
            done.then_inc(dve_v.mark(f"ctx{n}"), 1)

        def one_pass(i, last=False):
            for n in range(NU):
                if not (last and n + 2 >= NU):
                    shift(n + 2, i)
                normalise(n, i)

        for n in range(2):
            shift(n, 0)
        with dve.Fori(0, NP - 1) as i:
            one_pass(i)
        one_pass(NP - 1, last=True)
        phase_end(m, dve, ph)

    def gpsimd(pool):
        phase_end(m, pool, ph)

    return dict(sync=sync, tensor=tensor, scalar=scalar, vector=vector, gpsimd=gpsimd)


def joint_out_phase(nc, m, st, ph):
    J, KT = NB * T // TM, 4
    sb = lambda n, s, d=F32: st.enter_context(nc.sbuf_tensor(n, s, d))
    wo, woT = sb("po_wo", [C, 128, KT]), sb("po_wot", [128, KT, C])
    cx = [sb(f"po_cx{s}", [128, GB, KT, T]) for s in range(2)]
    oT = [sb(f"po_ot{s}", [C, GT]) for s in range(2)]
    sq = [sb(f"po_sq{k}", [TM, J // 4, C]) for k in range(2)]
    mean, ss, eps, eps_rms = sb("po_mean", [TM, J]), sb("po_ss", [TM, J]), sb("po_eps", [128, 1]), sb("po_eps_rms", [128, 1])
    zt = [sb(f"po_z{s}", [TM, GJ, C]) for s in range(2)]
    zT = [sb(f"po_zt{s}", [C, GT]) for s in range(2)]
    ps = m.psum
    P = NG // 2
    S1 = lambda n, steps: Steps(nc, m.whole, n, steps)
    wl = m.whole.enter_context(nc.semaphore("po_weights_landed"))
    cl = [Landed(nc, m.whole, f"po_ctx_landed{s}", GB) for s in range(2)]
    stored = [Landed(nc, m.whole, f"po_z_stored{s}", 1) for s in range(2)]
    pe_w = S1("po_pe_w", ["wot"])
    pe_o, pe_t = S1("po_pe_out", ["out0", "out1"]), S1("po_pe_turned", ["turned0", "turned1"])
    act_s = S1("po_act", ["ot0", "ot1"])
    dve_s = S1("po_dve", ["h0", "h1"])
    dve_n = S1("po_dve_norm", ["eps", "wot"] + [f"n_{k}" for k in NORM_DVE] + [f"y{k}" for k in range(4)] + [f"r_ss{k}" for k in range(4)] + ["r_recip"])
    act_n = S1("po_act_norm", [f"n_{k}" for k in NORM_ACT] + [f"r_{k}" for k in NORM_ACT])
    pe_z, act_z, dve_z = S1("po_pe_z", ["z0", "z1"]), S1("po_act_z", ["z0", "z1"]), S1("po_dve_z", ["z0", "z1"])

    def sync(sp):
        for s in range(2):
            cl[s].start(sp)
            stored[s].start(sp)
        sp.dma_start(wo[:], m.dram["attn_Wo"].rearrange("o (p k) -> o p k", k=KT)).then_inc(wl, 16)
        with sp.Fori(0, P) as i:
            for s in range(2):
                sp.wait_ge(pe_o.sem, pe_o.before(f"out{s}", i))
                sp.sem_inc(m.gate, 1)
                for b in range(GB):
                    sp.dma_start(cx[s][:, b].rearrange("p k t -> p (k t)"),
                                 m.dram["ctx_d"][bass.ds(i * 2 * GB + (s * GB + b), 1)].rearrange("b (p n) -> p (b n)", p=128)).then_inc(cl[s].sem, 16)
        with sp.Fori(0, P) as i:
            for s in range(2):
                sp.wait_ge(act_z.sem, act_z.at(f"z{s}", i))
                sp.sem_inc(m.gate, 1)
                sp.dma_start(m.dram["zt_d"][:, bass.ds(i * 2 * GT + s * GT, GT)], zT[s][:]).then_inc(stored[s].sem, 16)
        for s in range(2):
            sp.wait_ge(stored[s].sem, stored[s].at(P - 1))
        phase_end(m, sp, ph)

    def tensor(pe):
        for S in (pe_w, pe_o, pe_t, pe_z):
            S.start(pe)
        pe.wait_ge(wl, 16)
        for k in range(KT):
            mm = pe.transpose(ps[:, 0, k * C:(k + 1) * C], wo[:, :, k], m.ident[0:C, 0:C])
        mm.then_inc(pe_w.mark("wot"), 1)
        pe.wait_ge(dve_n.sem, dve_n.at("wot"))

        def project(s, i):
            pe.wait_ge(cl[s].sem, cl[s].at(i))
            pe.wait_ge(act_s.sem, act_s.before(f"ot{s}", i))
            pe.sem_inc(m.gate, 1)
            for half in range(2):
                for k in range(KT):
                    mm = pe.matmul(ps[0:C, 2 * s + half, 0:2 * T], woT[:, k, :], cx[s][:, 2 * half:2 * half + 2, k, :], start=k == 0, stop=k == KT - 1)
            mm.then_inc(pe_o.mark(f"out{s}"), 1)

        def turn(s, i):
            pe.wait_ge(act_s.sem, act_s.at(f"ot{s}", i))
            pe.wait_ge(dve_s.sem, dve_s.before(f"h{s}", i))
            pe.sem_inc(m.gate, 1)
            for j in range(GJ):
                mm = pe.transpose(ps[0:TM, 4 + s, j * C:(j + 1) * C], oT[s][:, j * TM:(j + 1) * TM], m.ident[0:C, 0:C])
            mm.then_inc(pe_t.mark(f"turned{s}"), 1)

        skewed(pe, P, project, turn)
        turn_groups(m, pe, P, pe_z, dve_z, act_z, zt, C)
        phase_end(m, pe, ph)

    def scalar(act):
        for S in (act_s, act_n, act_z):
            S.start(act)
        with act.Fori(0, P) as i:
            for s in range(2):
                act.wait_ge(pe_o.sem, pe_o.at(f"out{s}", i))
                act.wait_ge(pe_t.sem, pe_t.before(f"turned{s}", i))
                act.activation(oT[s][:].rearrange("c (h n) -> c h n", h=2), ps[0:C, 2 * s:2 * s + 2, 0:2 * T], ACT.Copy).then_inc(act_s.mark(f"ot{s}"), 1)
        token_norm_squares(act, act_n, dve_n, "n", m.y, sq, mean, ss, eps, "n_cent{k}")
        token_norm_squares(act, act_n, dve_n, "r", m.y, sq, mean, ss, eps_rms, "y{k}")
        with act.Fori(0, P) as i:
            for s in range(2):
                act.wait_ge(pe_z.sem, pe_z.at(f"z{s}", i))
                act.wait_ge(stored[s].sem, stored[s].before(i))
                act.activation(zT[s][:, 0:4 * TM], ps[0:C, 2 * s, 0:4 * TM], ACT.Copy)
                act.activation(zT[s][:, 4 * TM:GT], ps[0:C, 2 * s + 1, 0:TM], ACT.Copy).then_inc(act_z.mark(f"z{s}"), 1)
        phase_end(m, act, ph)

    def vector(dve):
        for S in (dve_s, dve_n, dve_z):
            S.start(dve)
        dve.memset(eps[:], EPS)
        dve.memset(eps_rms[:], 1e-6).then_inc(dve_n.mark("eps"), 1)
        dve.wait_ge(pe_w.sem, pe_w.at("wot"))
        dve.tensor_copy(woT[:], ps[:, 0, 0:KT * C].rearrange("p (k o) -> p k o", k=KT)).then_inc(dve_n.mark("wot"), 1)
        with dve.Fori(0, P) as i:
            for s in range(2):
                at = bass.ds(i * 2 * GJ + s * GJ, GJ)
                dve.wait_ge(pe_t.sem, pe_t.at(f"turned{s}", i))
                dve.tensor_tensor(m.h[:, at, :], ps[0:TM, 4 + s, 0:GJ * C].rearrange("p (j c) -> p j c", c=C), m.h[:, at, :], ALU.add).then_inc(dve_s.mark(f"h{s}"), 1)
        dve.wait_ge(dve_s.sem, dve_s.at("h1", P - 1))
        token_norm(dve, dve_n, act_n, "n", m.h, m.y, sq, mean, ss)
        for k in range(4):
            j = slice(J // 4 * k, J // 4 * (k + 1))
            dve.tensor_tensor(m.y[:, j], m.y[:, j], cols(ss[:, j].unsqueeze(2), C), ALU.mult).then_inc(dve_n.mark(f"y{k}"), 1)
        root_mean_square(dve, dve_n, act_n, sq, mean, ss, "y3")
        scale_groups(dve, P, dve_z, pe_z, zt, m.y, ss)
        phase_end(m, dve, ph)

    def gpsimd(pool):
        phase_end(m, pool, ph)

    return dict(sync=sync, tensor=tensor, scalar=scalar, vector=vector, gpsimd=gpsimd)


def root_mean_square(dve, S, act_s, sq, mean, ss, last_use):
    J = NB * T // TM
    dve.wait_ge(S.sem, S.at(last_use))
    for k in range(4):
        j = slice(J // 4 * k, J // 4 * (k + 1))
        dve.wait_ge(act_s.sem, act_s.at(f"r_sq{k}"))
        dve.tensor_reduce(ss[:, j], sq[k % 2][:], X, ALU.add).then_inc(S.mark(f"r_ss{k}"), 1)
    dve.wait_ge(act_s.sem, act_s.at("r_std"))
    dve.reciprocal(ss[:], mean[:]).then_inc(S.mark("r_recip"), 1)
    dve.wait_ge(S.sem, S.at("r_recip"))


def scale_groups(dve, passes, S, pe_s, dst, src, factor):
    with dve.Fori(0, passes) as i:
        for s in range(2):
            dve.wait_ge(pe_s.sem, pe_s.before(f"z{s}", i))
            at = bass.ds(i * 2 * GJ + s * GJ, GJ)
            dve.tensor_tensor(dst[s][:], src[:, at, :], cols(factor[:, at].unsqueeze(2), C), ALU.mult).then_inc(S.mark(f"z{s}"), 1)


def turn_groups(m, pe, passes, S, dve_s, act_s, src, rows):
    with pe.Fori(0, passes) as i:
        for s in range(2):
            pe.wait_ge(dve_s.sem, dve_s.at(f"z{s}", i))
            pe.wait_ge(act_s.sem, act_s.before(f"z{s}", i))
            pe.sem_inc(m.gate, 1)
            for j in range(GJ):
                mm = pe.transpose(m.psum[0:rows, 2 * s + j // 4, j % 4 * TM:j % 4 * TM + TM], src[s][:, j, :], m.ident[0:TM, 0:TM])
            mm.then_inc(S.mark(f"z{s}"), 1)


def causal_phase(nc, m, st, ph):
    H, HD, KV, R, KM = 4, 16, 2, 32, 128
    KT, NJ, D1 = T - KM, H * T // TM, KV * HD + 1
    sb = lambda n, s, d=F32: st.enter_context(nc.sbuf_tensor(n, s, d))
    w4, wT = sb("ca_w4", [128, 2, 2, C]), sb("ca_wt", [2 * C, 2, 128])
    wv, wvT = sb("ca_wv", [KV * HD, C]), sb("ca_wvt", [C, KV * HD])
    l1 = sb("ca_ln1", [2 * C, 1])
    cos, sin = sb("ca_cos", [128, 2 * T]), sb("ca_sin", [128, 2 * T])
    mask32, mask = sb("ca_mask32", [TM, NJ * T]), sb("ca_mask", [TM, NJ * T], BF16)
    ident = sb("ca_ident", [TM, TM], BF16)
    pick, own = sb("ca_pick", [TM, NJ, KV]), sb("ca_own", [NJ * KT, NJ])
    z = [sb(f"ca_z{k}", [2 * C, 2, T]) for k in range(4)]
    z_tail = [sb(f"ca_z_tail{k}", [C, NJ, KT]) for k in range(4)]
    v = [sb(f"ca_v{k}", [KM, D1]) for k in range(4)]
    v_tail = [sb(f"ca_v_tail{k}", [NJ * KT, NJ, D1]) for k in range(4)]
    y = [sb(f"ca_y{k}", [TM, NJ, HD]) for k in range(4)]
    t1, t2 = ([sb(f"ca_{n}{s}", [128, 2 * T]) for s in range(2)] for n in ("t1", "t2"))
    qz = [sb(f"ca_q{s}", [128, T, H]) for s in range(2)]
    kk = [sb(f"ca_k{s}", [128, T]) for s in range(2)]
    sc = [sb(f"ca_sc{s}", [TM, NJ, T]) for s in range(2)]
    pr = [sb(f"ca_pr{s}", [TM, NJ, KM]) for s in range(2)]
    pr_tail = [sb(f"ca_pr_tail{s}", [TM, NJ, KT]) for s in range(2)]
    mx = [sb(f"ca_mx{s}", [TM, NJ]) for s in range(2)]
    pT = [sb(f"ca_pt{s}", [KM, NJ, TM]) for s in range(2)]
    pT_tail = [sb(f"ca_pt_tail{s}", [NJ * KT, TM]) for s in range(2)]
    rs = [sb(f"ca_rs{s}", [TM, NJ]) for s in range(2)]
    picked = [sb(f"ca_picked{s}", [TM, NJ, KV]) for s in range(2)]
    both = [sb(f"ca_both{s}", [TM, NJ, KV, HD]) for s in range(2)]
    ps = m.psum
    NU = 4
    NP = NB // NU
    HALVES = ((0, 0, 3), (1, 3, NJ))
    TURNED, COS, SIN = (4, 5), 6, 7
    OUT, VC = 2 * TM, 2 * T
    S1 = lambda n, steps: Steps(nc, m.whole, n, steps)
    each = lambda *names: [f"{w}{n}" for n in range(NU) for w in names]
    wl = m.whole.enter_context(nc.semaphore("ca_weights_landed"))
    zl = [Landed(nc, m.whole, f"ca_z_landed{n}", 3) for n in range(NU)]
    stored = [Landed(nc, m.whole, f"ca_y_stored{n}", 2) for n in range(NU)]
    dve_w, pe_w, act_w = S1("ca_dve_w", ["ones", "clear", "mask"]), S1("ca_pe_w", ["turned"]), S1("ca_act_w", ["wt", "wvt"])
    pe_q, pe_sc, pe_t, pe_v = (S1(f"ca_pe_{n}", each(x)) for n, x in (("qkv", "qkv"), ("scores", "s"), ("turned", "t"), ("attended", "o")))
    dve_r = S1("ca_dve_rope", each("cos", "sin", "v", "v_tail"))
    pool_r, pool_y = S1("ca_pool_rope", each(*[f"q{h}_" for h in range(H)], "k")), S1("ca_pool_y", each("y"))
    dve_sc = S1("ca_dve_scores", each("max0_", "max1_", "minus0_", "minus1_"))
    dve_o = S1("ca_dve_out", each("recip", "picked", "both"))
    act_e, act_t = S1("ca_act_exp", each("e")), S1("ca_act_turned", each("t"))

    def wrapped(n, i):
        return (n, i) if n < NU else (n - NU, i + 1)

    def back(S, name, n, i, by):
        return S.at(f"{name}{n - by}", i) if n >= by else S.before(f"{name}{n - by + NU}", i)

    def sync(sp):
        for n in range(NU):
            zl[n].start(sp)
            stored[n].start(sp)
        for dst, src in ((l1[0:C], m.dram["ffn_ln1_w"].rearrange("(c o) -> c o", o=1)), (l1[C:2 * C], m.dram["ffn_ln1_w"].rearrange("(c o) -> c o", o=1)), (wv[:], m.dram["ffn_wv"]), (cos[:], m.dram["rope_cos"]),
                         (sin[:], m.dram["rope_sin"]), (mask32[:], m.dram["causal_mask"]), (own[:], m.dram["own_block"]),
                         (pick[:].rearrange("p j k -> p (j k)"), m.dram["pick_value_head"])):
            sp.dma_start(dst, src).then_inc(wl, 16)
        sp.wait_ge(dve_w.sem, dve_w.at("clear"))
        for h in range(H):
            for k, src, r0 in ((0, m.dram["ffn_wq"], HD * h), (1, m.dram["ffn_wk"], HD * (h // 2))):
                sp.dma_start(w4[R * h:R * h + HD, 0, k], src[r0:r0 + HD]).then_inc(wl, 16)
                sp.dma_start(w4[R * h:R * h + HD // 2, 1, k], src[r0 + HD // 2:r0 + HD]).then_inc(wl, 16)
                sp.dma_start(w4[R * h + HD // 2:R * h + HD, 1, k], src[r0:r0 + HD // 2]).then_inc(wl, 16)

        def load(n, i):
            sp.wait_ge(pe_q.sem, pe_q.before(f"qkv{n}", i))
            sp.sem_inc(m.gate, 1)
            t0 = i * NU * T + n * T
            for k in range(2):
                sp.dma_start(z[n][C * k:C * k + C, k], m.dram["zt_d"][:, bass.ds(t0, T)]).then_inc(zl[n].sem, 16)
            sp.dma_start(z_tail[n][:], m.dram["zt_d"][:, bass.ds(t0 + KM, KT)].unsqueeze(1).broadcast_to([C, NJ, KT])).then_inc(zl[n].sem, 16)

        def store(n, i, ready):
            sp.wait_ge(pool_y.sem, ready)
            sp.sem_inc(m.gate, 1)
            dst = m.dram["y_d"][bass.ds(i * NU + n, 1)].rearrange("b (p n) -> p (b n)", p=TM)
            src = y[n][:].rearrange("p j d -> p (j d)")
            for p0, p1 in ((0, 112), (112, TM)):
                sp.dma_start(dst[p0:p1], src[p0:p1]).then_inc(stored[n].sem, 16)

        for n in range(NU):
            load(n, 0)
        with sp.Fori(1, NP) as i:
            for n in range(NU):
                load(n, i)
                store(n, i - 1, pool_y.before(f"y{n}", i))
        for n in range(NU):
            store(n, NP - 1, pool_y.at(f"y{n}", NP - 1))
        for n in range(NU):
            sp.wait_ge(stored[n].sem, stored[n].at(NP - 1))
        phase_end(m, sp, ph)

    def tensor(pe):
        for S in (pe_w, pe_q, pe_sc, pe_t, pe_v):
            S.start(pe)
        pe.wait_ge(wl, 16 * 32)
        for k in range(2):
            pe.transpose(ps[:, 0, 128 * k:128 * k + 128], w4[:, k].rearrange("p q c -> p (q c)"), m.ident[:])
        pe.transpose(ps[0:C, 1, 0:KV * HD], wv[:], m.ident[0:KV * HD, 0:KV * HD]).then_inc(pe_w.mark("turned"), 1)
        pe.wait_ge(act_w.sem, act_w.at("wvt"))
        pe.wait_ge(dve_w.sem, dve_w.at("mask"))

        def project(n, i):
            n, i = wrapped(n, i)
            pe.wait_ge(zl[n].sem, zl[n].at(i))
            pe.wait_ge(dve_r.sem, back(dve_r, "v_tail", n, i, 1))
            pe.sem_inc(m.gate, 1)
            for k in range(2):
                pe.matmul(ps[:, COS + k, 0:2 * T], wT[:, k, :], z[n][:].rearrange("c q t -> c (q t)"), start=True, stop=True)
            pe.matmul(ps[:, SIN, VC:VC + KV * HD], z[n][0:C, 0, 0:KM], wvT[:], start=True, stop=True)
            pe.matmul(ps[0:NJ * KT, SIN, VC + KV * HD:VC + 2 * KV * HD], z_tail[n][:].rearrange("c j t -> c (j t)"), wvT[:],
                      start=True, stop=True).then_inc(pe_q.mark(f"qkv{n}"), 1)

        def scores(n, i):
            n, i = wrapped(n, i)
            s = n % 2
            pe.wait_ge(pool_r.sem, pool_r.at(f"k{n}", i))
            pe.wait_ge(dve_sc.sem, back(dve_sc, "minus1_", n, i, 2))
            pe.sem_inc(m.gate, 1)
            rows = qz[s][:].rearrange("c t h -> c (t h)")
            for k, a, b in HALVES:
                pe.matmul(ps[0:TM, 2 * s + k, 0:(b - a) * T], ident[:], mask[:, a * T:b * T], start=True, stop=False)
                for j in range(a, b):
                    mm = pe.matmul(ps[0:TM, 2 * s + k, (j - a) * T:(j - a + 1) * T], rows[:, j::NJ], kk[s][:], start=False, stop=j == b - 1)
            mm.then_inc(pe_sc.mark(f"s{n}"), 1)

        def turn(n, i):
            n, i = wrapped(n, i)
            s = n % 2
            pe.wait_ge(act_e.sem, act_e.at(f"e{n}", i))
            pe.wait_ge(act_t.sem, back(act_t, "t", n, i, 1))
            pe.wait_ge(dve_o.sem, back(dve_o, "both", n, i, 1))
            pe.sem_inc(m.gate, 1)
            for j in range(NJ):
                pe.transpose(ps[:, 4 + j // 4, j % 4 * TM:j % 4 * TM + TM], pr[s][:, j, :], m.ident[0:TM, 0:TM])
            pe.transpose(ps[0:NJ * KT, 5, TM:2 * TM], pr_tail[s][:].rearrange("p j t -> p (j t)"), m.ident[0:TM, 0:TM]).then_inc(pe_t.mark(f"t{n}"), 1)

        def attend(n, i):
            s = n % 2
            pe.wait_ge(act_t.sem, act_t.at(f"t{n}", i))
            pe.sem_inc(m.gate, 1)
            o = ps[0:TM, TURNED[1], OUT:OUT + NJ * D1]
            pe.matmul(o, pT_tail[s][:], v_tail[n][:].rearrange("k j d -> k (j d)"), start=True, stop=False)
            for j in range(NJ):
                mm = pe.matmul(o[:, j * D1:(j + 1) * D1], pT[s][:, j, :], v[n][:], start=False, stop=j == NJ - 1)
            mm.then_inc(pe_v.mark(f"o{n}"), 1)

        def one_pass(i, end=False):
            for n in range(NU):
                if not (end and n + 3 >= NU):
                    project(n + 3, i)
                attend(n, i)
                if not (end and n + 2 >= NU):
                    scores(n + 2, i)
                if not (end and n + 1 >= NU):
                    turn(n + 1, i)

        for n in range(3):
            project(n, 0)
        for n in range(2):
            scores(n, 0)
        turn(0, 0)
        with pe.Fori(0, NP - 1) as i:
            one_pass(i)
        one_pass(NP - 1, end=True)
        phase_end(m, pe, ph)

    def scalar(act):
        for S in (act_w, act_e, act_t):
            S.start(act)
        act.wait_ge(wl, 16 * 32)
        act.wait_ge(pe_w.sem, pe_w.at("turned"))
        act.activation(wT[:].rearrange("c k n -> c (k n)"), ps[:, 0, 0:256], ACT.Copy, scale=l1[:]).then_inc(act_w.mark("wt"), 1)
        act.activation(wvT[:], ps[0:C, 1, 0:KV * HD], ACT.Copy, scale=l1[0:C]).then_inc(act_w.mark("wvt"), 1)
        act.preload_act_table(ACT.Exp)

        def exp(n, i):
            n, i = wrapped(n, i)
            s = n % 2
            act.wait_ge(dve_sc.sem, dve_sc.at(f"minus1_{n}", i))
            act.wait_ge(pe_t.sem, back(pe_t, "t", n, i, 2))
            act.activation(pr[s][:], sc[s][:, :, 0:KM], ACT.Exp)
            act.activation(pr_tail[s][:], sc[s][:, :, KM:T], ACT.Exp).then_inc(act_e.mark(f"e{n}"), 1)

        def copy_turned(n, i):
            s = n % 2
            act.wait_ge(pe_t.sem, pe_t.at(f"t{n}", i))
            act.wait_ge(pe_v.sem, back(pe_v, "o", n, i, 2))
            act.activation(pT[s][:, 0:4].rearrange("k j p -> k (j p)"), ps[:, 4, 0:4 * TM], ACT.Copy)
            act.activation(pT[s][:, 4], ps[:, 5, 0:TM], ACT.Copy)
            act.activation(pT_tail[s][:], ps[0:NJ * KT, 5, TM:2 * TM], ACT.Copy).then_inc(act_t.mark(f"t{n}"), 1)

        def one_pass(i, end=False):
            for n in range(NU):
                copy_turned(n, i)
                if not (end and n + 1 >= NU):
                    exp(n + 1, i)

        exp(0, 0)
        with act.Fori(0, NP - 1) as i:
            one_pass(i)
        one_pass(NP - 1, end=True)
        phase_end(m, act, ph)

    def vector(dve):
        for S in (dve_w, dve_r, dve_sc, dve_o):
            S.start(dve)
        for s in range(2):
            dve.memset(qz[s][:], 0.0)
        for n in range(NU):
            dve.memset(v[n][:, D1 - 1:D1], 1.0)
            ins = dve.memset(z[n][:], 0.0)
        ins.then_inc(dve_w.mark("ones"), 1)
        dve.memset(w4[:], 0.0).then_inc(dve_w.mark("clear"), 1)
        dve.wait_ge(wl, 16 * 32)
        for n in range(NU):
            dve.tensor_copy(v_tail[n][:, :, D1 - 1], own[:])
        dve.tensor_copy(ident[:], m.ident[0:TM, 0:TM])
        dve.tensor_copy(mask[:], mask32[:]).then_inc(dve_w.mark("mask"), 1)
        dve.wait_ge(dve_w.sem, dve_w.at("mask"))

        def rotate(n, i):
            n, i = wrapped(n, i)
            s = n % 2
            dve.wait_ge(pe_q.sem, pe_q.at(f"qkv{n}", i))
            dve.wait_ge(pool_r.sem, back(pool_r, "k", n, i, 2))
            dve.tensor_tensor(t1[s][:], ps[:, COS, 0:2 * T], cos[:], ALU.mult).then_inc(dve_r.mark(f"cos{n}"), 1)
            dve.tensor_tensor(t2[s][:], ps[:, SIN, 0:2 * T], sin[:], ALU.mult).then_inc(dve_r.mark(f"sin{n}"), 1)
            dve.wait_ge(pe_v.sem, pe_v.before(f"o{n}", i))
            dve.tensor_copy(v[n][:, 0:KV * HD], ps[:, SIN, VC:VC + KV * HD]).then_inc(dve_r.mark(f"v{n}"), 1)
            dve.tensor_tensor(v_tail[n][:, :, 0:KV * HD], ps[0:NJ * KT, SIN, VC + KV * HD:VC + 2 * KV * HD].unsqueeze(1).broadcast_to([NJ * KT, NJ, KV * HD]),
                              cols(own[:].unsqueeze(2), KV * HD), ALU.mult).then_inc(dve_r.mark(f"v_tail{n}"), 1)

        def shift(n, i):
            n, i = wrapped(n, i)
            s = n % 2
            scored = lambda k, a, b: ps[0:TM, 2 * s + k, 0:(b - a) * T].rearrange("p (j t) -> p j t", t=T)
            dve.wait_ge(pe_sc.sem, pe_sc.at(f"s{n}", i))
            for k, a, b in HALVES:
                dve.tensor_reduce(mx[s][:, a:b], scored(k, a, b), X, ALU.max).then_inc(dve_sc.mark(f"max{k}_{n}"), 1)
            dve.wait_ge(act_e.sem, back(act_e, "e", n, i, 2))
            for k, a, b in HALVES:
                dve.wait_ge(dve_sc.sem, dve_sc.at(f"max{k}_{n}", i))
                dve.tensor_tensor(sc[s][:, a:b], scored(k, a, b), cols(mx[s][:, a:b].unsqueeze(2), T), ALU.subtract).then_inc(dve_sc.mark(f"minus{k}_{n}"), 1)

        def normalise(n, i):
            s = n % 2
            o = ps[0:TM, TURNED[1], OUT:OUT + NJ * D1].rearrange("p (j d) -> p j d", j=NJ)
            dve.wait_ge(pe_v.sem, pe_v.at(f"o{n}", i))
            dve.reciprocal(rs[s][:], o[:, :, D1 - 1]).then_inc(dve_o.mark(f"recip{n}"), 1)
            dve.wait_ge(dve_o.sem, dve_o.at(f"recip{n}", i))
            dve.tensor_tensor(picked[s][:], pick[:], cols(rs[s][:].unsqueeze(2), KV), ALU.mult).then_inc(dve_o.mark(f"picked{n}"), 1)
            dve.wait_ge(dve_o.sem, dve_o.at(f"picked{n}", i))
            dve.wait_ge(pool_y.sem, back(pool_y, "y", n, i, 2))
            dve.tensor_tensor(both[s][:], o[:, :, 0:KV * HD].rearrange("p j (k d) -> p j k d", k=KV), cols(picked[s][:].unsqueeze(3), HD),
                              ALU.mult).then_inc(dve_o.mark(f"both{n}"), 1)

        def one_pass(i, end=False):
            for n in range(NU):
                if not (end and n + 3 >= NU):
                    rotate(n + 3, i)
                normalise(n, i)
                if not (end and n + 2 >= NU):
                    shift(n + 2, i)

        for n in range(3):
            rotate(n, 0)
        for n in range(2):
            shift(n, 0)
        with dve.Fori(0, NP - 1) as i:
            one_pass(i)
        one_pass(NP - 1, end=True)
        phase_end(m, dve, ph)

    def gpsimd(pool):
        pool_r.start(pool)
        pool_y.start(pool)
        pool.wait_ge(dve_w.sem, dve_w.at("ones"))

        def rotate(n, i):
            n, i = wrapped(n, i)
            s = n % 2
            pool.wait_ge(dve_r.sem, dve_r.at(f"sin{n}", i))
            pool.wait_ge(pe_sc.sem, back(pe_sc, "s", n, i, 2))
            pool.wait_ge(pool_r.sem, back(pool_r, "k", n, i, 1))
            pool.wait_ge(pool_y.sem, pool_y.before(f"y{n}", i))
            pool.sem_inc(m.gate, 1)
            for h in range(H):
                r = slice(R * h, R * h + R)
                pool.tensor_tensor(qz[s][r, :, h], t1[s][r, 0:T], t2[s][r, 0:T], ALU.add).then_inc(pool_r.mark(f"q{h}_{n}"), 1)
            pool.wait_ge(pool_r.sem, pool_r.at(f"q{H - 1}_{n}", i))
            pool.tensor_tensor(kk[s][:], t1[s][:, T:2 * T], t2[s][:, T:2 * T], ALU.add).then_inc(pool_r.mark(f"k{n}"), 1)

        def pick_sum(n, i, rotated):
            if rotated:
                n3, i3 = wrapped(n + 3, i)
                pool.wait_ge(pool_r.sem, pool_r.at(f"k{n3}", i3))
            pool.wait_ge(dve_o.sem, dve_o.at(f"both{n}", i))
            pool.wait_ge(stored[n].sem, stored[n].before(i))
            pool.sem_inc(m.gate, 1)
            pool.tensor_tensor(y[n][:], both[n % 2][:, :, 0], both[n % 2][:, :, 1], ALU.add).then_inc(pool_y.mark(f"y{n}"), 1)

        def one_pass(i, end=False):
            for n in range(NU):
                rotated = not (end and n + 3 >= NU)
                if rotated:
                    rotate(n + 3, i)
                pick_sum(n, i, rotated)

        for n in range(3):
            rotate(n, 0)
        with pool.Fori(0, NP - 1) as i:
            one_pass(i)
        one_pass(NP - 1, end=True)
        phase_end(m, pool, ph)

    return dict(sync=sync, tensor=tensor, scalar=scalar, vector=vector, gpsimd=gpsimd)


def causal_out_phase(nc, m, st, ph):
    J, NE = NB * T // TM, 8
    sb = lambda n, s, d=F32: st.enter_context(nc.sbuf_tensor(n, s, d))
    wo, woT = sb("fo_wo", [C, C]), sb("fo_wot", [C, C])
    rw, rT, l2 = sb("fo_router", [NE, C]), sb("fo_router_t", [C, NE]), sb("fo_ln2", [C, 1])
    yr = [sb(f"fo_y{s}", [TM, GJ, C]) for s in range(2)]
    yt = [sb(f"fo_yt{s}", [C, GT]) for s in range(2)]
    sq = [sb(f"fo_sq{k}", [TM, J // 4, C]) for k in range(2)]
    mean, ss, eps_rms = sb("fo_mean", [TM, J]), sb("fo_ss", [TM, J]), sb("fo_eps_rms", [128, 1])
    zt = [sb(f"fo_z{s}", [TM, GJ, C]) for s in range(2)]
    zT = [sb(f"fo_zt{s}", [C, GT]) for s in range(2)]
    lg, pr, eq, one1, one2 = (sb(f"fo_{n}", [TM, J, NE]) for n in ("logits", "probs", "eq", "one1", "one2"))
    desc = sb("fo_desc", [TM, NE])
    mx, rs, p2, ws = (sb(f"fo_{n}", [TM, J]) for n in ("mx", "rs", "p2", "ws"))
    ps = m.psum
    P = NG // 2
    S1 = lambda n, steps: Steps(nc, m.whole, n, steps)
    wl = m.whole.enter_context(nc.semaphore("fo_weights_landed"))
    yl = [Landed(nc, m.whole, f"fo_y_landed{s}", 2) for s in range(2)]
    stored = [Landed(nc, m.whole, f"fo_z_stored{s}", 1) for s in range(2)]
    pe_w, act_w = S1("fo_pe_w", ["wot", "rt"]), S1("fo_act_w", ["wot", "rt"])
    pe_y, act_y = S1("fo_pe_y", ["y0", "y1"]), S1("fo_act_y", ["y0", "y1"])
    pe_s, dve_s = S1("fo_pe", ["o0", "o1"]), S1("fo_dve_y", ["y0", "y1"])
    gate_steps = ["max", "minus", "sum", "recip", "probs", "p1", "eq1", "cand1", "best1", "one1", "rest", "p2",
                  "eq2", "cand2", "best2", "one2", "wsum", "wrecip", "both", "picked", "gates"]
    dve_n = S1("fo_dve", ["eps"] + [f"r_ss{k}" for k in range(4)] + ["r_recip", "h"] + gate_steps)
    act_n = S1("fo_act", [f"r_{k}" for k in NORM_ACT] + ["exp"])
    pe_z, act_z, dve_z = S1("fo_pe_z", ["z0", "z1"]), S1("fo_act_z", ["z0", "z1"]), S1("fo_dve_z", ["z0", "z1"])
    pe_l, dve_l = S1("fo_pe_logits", ["l0", "l1"]), S1("fo_dve_logits", ["l0", "l1"])

    def sync(sp):
        for s in range(2):
            yl[s].start(sp)
            stored[s].start(sp)
        sp.dma_start(wo[:], m.dram["ffn_wo"]).then_inc(wl, 16)
        sp.dma_start(rw[:], m.dram["ffn_router_w"]).then_inc(wl, 16)
        sp.dma_start(l2[:], m.dram["ffn_ln2_w"].rearrange("(c o) -> c o", o=1)).then_inc(wl, 16)
        sp.dma_start(desc[:], m.dram["descending"].partition_broadcast(TM)).then_inc(wl, 16)
        with sp.Fori(0, P) as i:
            for s in range(2):
                sp.wait_ge(pe_y.sem, pe_y.before(f"y{s}", i))
                sp.sem_inc(m.gate, 1)
                rows = m.dram["y_d"].rearrange("b (t c) -> (b t) c", c=C)[bass.ds(i * 2 * GT + s * GT, GT)].rearrange("(j p) c -> p j c", p=TM)
                for p0, p1 in ((0, 112), (112, TM)):
                    sp.dma_start(yr[s][p0:p1], rows[p0:p1]).then_inc(yl[s].sem, 16)
        with sp.Fori(0, P) as i:
            for s in range(2):
                sp.wait_ge(act_z.sem, act_z.at(f"z{s}", i))
                sp.sem_inc(m.gate, 1)
                sp.dma_start(m.dram["zt_d"][:, bass.ds(i * 2 * GT + s * GT, GT)], zT[s][:]).then_inc(stored[s].sem, 16)
        for s in range(2):
            sp.wait_ge(stored[s].sem, stored[s].at(P - 1))
        phase_end(m, sp, ph)

    def tensor(pe):
        for S in (pe_w, pe_y, pe_s, pe_z, pe_l):
            S.start(pe)
        pe.wait_ge(wl, 64)
        pe.transpose(ps[0:C, 0, 0:C], wo[:], m.ident[0:C, 0:C]).then_inc(pe_w.mark("wot"), 1)
        pe.transpose(ps[0:C, 1, 0:NE], rw[:], m.ident[0:NE, 0:NE]).then_inc(pe_w.mark("rt"), 1)
        pe.wait_ge(act_w.sem, act_w.at("rt"))

        def turn_y(s, i):
            pe.wait_ge(yl[s].sem, yl[s].at(i))
            pe.wait_ge(act_y.sem, act_y.before(f"y{s}", i))
            pe.sem_inc(m.gate, 1)
            for j in range(GJ):
                mm = pe.transpose(ps[0:C, 2 + 2 * s + j // 4, j % 4 * TM:j % 4 * TM + TM], yr[s][:, j, :], m.ident[0:TM, 0:TM])
            mm.then_inc(pe_y.mark(f"y{s}"), 1)

        def project(s, i):
            pe.wait_ge(act_y.sem, act_y.at(f"y{s}", i))
            pe.wait_ge(dve_s.sem, dve_s.before(f"y{s}", i))
            pe.sem_inc(m.gate, 1)
            for j in range(GJ):
                mm = pe.matmul(ps[0:TM, s, j * C:(j + 1) * C], yt[s][:, j * TM:(j + 1) * TM], woT[:], start=True, stop=True)
            mm.then_inc(pe_s.mark(f"o{s}"), 1)

        def turn_z(s, i):
            pe.wait_ge(dve_z.sem, dve_z.at(f"z{s}", i))
            pe.wait_ge(act_z.sem, act_z.before(f"z{s}", i))
            pe.sem_inc(m.gate, 1)
            for j in range(GJ):
                mm = pe.transpose(ps[0:C, 2 * s + j // 4, j % 4 * TM:j % 4 * TM + TM], zt[s][:, j, :], m.ident[0:TM, 0:TM])
            mm.then_inc(pe_z.mark(f"z{s}"), 1)

        def logits(s, i):
            pe.wait_ge(act_z.sem, act_z.at(f"z{s}", i))
            pe.wait_ge(dve_l.sem, dve_l.before(f"l{s}", i))
            pe.sem_inc(m.gate, 1)
            for j in range(GJ):
                mm = pe.matmul(ps[0:TM, 4 + s, j * NE:(j + 1) * NE], zT[s][:, j * TM:(j + 1) * TM], rT[:], start=True, stop=True)
            mm.then_inc(pe_l.mark(f"l{s}"), 1)

        skewed(pe, P, turn_y, project)
        skewed(pe, P, turn_z, logits)
        phase_end(m, pe, ph)

    def scalar(act):
        for S in (act_w, act_y, act_n, act_z):
            S.start(act)
        act.wait_ge(wl, 64)
        act.wait_ge(pe_w.sem, pe_w.at("rt"))
        act.activation(woT[:], ps[0:C, 0, 0:C], ACT.Copy).then_inc(act_w.mark("wot"), 1)
        act.activation(rT[:], ps[0:C, 1, 0:NE], ACT.Copy, scale=l2[:]).then_inc(act_w.mark("rt"), 1)
        with act.Fori(0, P) as i:
            for s in range(2):
                act.wait_ge(pe_y.sem, pe_y.at(f"y{s}", i))
                act.wait_ge(pe_s.sem, pe_s.before(f"o{s}", i))
                act.activation(yt[s][:, 0:4 * TM], ps[0:C, 2 + 2 * s, 0:4 * TM], ACT.Copy)
                act.activation(yt[s][:, 4 * TM:GT], ps[0:C, 3 + 2 * s, 0:TM], ACT.Copy).then_inc(act_y.mark(f"y{s}"), 1)
        act.wait_ge(dve_s.sem, dve_s.at("y1", P - 1))
        for k in range(4):
            j = slice(J // 4 * k, J // 4 * (k + 1))
            if k >= 2:
                act.wait_ge(dve_n.sem, dve_n.at(f"r_ss{k - 2}"))
            act.activation(sq[k % 2][:], m.y[:, j], ACT.Square).then_inc(act_n.mark(f"r_sq{k}"), 1)
        act.wait_ge(dve_n.sem, dve_n.at("r_ss3"))
        act.activation(mean[:], ss[:], ACT.Sqrt, bias=eps_rms[0:TM], scale=1.0 / C).then_inc(act_n.mark("r_std"), 1)
        with act.Fori(0, P) as i:
            for s in range(2):
                act.wait_ge(pe_z.sem, pe_z.at(f"z{s}", i))
                act.wait_ge(stored[s].sem, stored[s].before(i))
                act.wait_ge(pe_l.sem, pe_l.before(f"l{s}", i))
                act.activation(zT[s][:, 0:4 * TM], ps[0:C, 2 * s, 0:4 * TM], ACT.Copy)
                act.activation(zT[s][:, 4 * TM:GT], ps[0:C, 2 * s + 1, 0:TM], ACT.Copy).then_inc(act_z.mark(f"z{s}"), 1)
        act.wait_ge(dve_n.sem, dve_n.at("minus"))
        act.activation(pr[:], lg[:], ACT.Exp).then_inc(act_n.mark("exp"), 1)
        phase_end(m, act, ph)

    def vector(dve):
        for S in (dve_s, dve_n, dve_z, dve_l):
            S.start(dve)
        dve.memset(eps_rms[:], 1e-6).then_inc(dve_n.mark("eps"), 1)
        with dve.Fori(0, P) as i:
            for s in range(2):
                at = bass.ds(i * 2 * GJ + s * GJ, GJ)
                dve.wait_ge(pe_s.sem, pe_s.at(f"o{s}", i))
                dve.tensor_tensor(m.y[:, at, :], ps[0:TM, s, 0:GJ * C].rearrange("p (j c) -> p j c", c=C), m.y[:, at, :], ALU.add).then_inc(dve_s.mark(f"y{s}"), 1)
        dve.wait_ge(dve_s.sem, dve_s.at("y1", P - 1))
        for k in range(4):
            j = slice(J // 4 * k, J // 4 * (k + 1))
            dve.wait_ge(act_n.sem, act_n.at(f"r_sq{k}"))
            dve.tensor_reduce(ss[:, j], sq[k % 2][:], X, ALU.add).then_inc(dve_n.mark(f"r_ss{k}"), 1)
        dve.wait_ge(act_n.sem, act_n.at("r_std"))
        dve.reciprocal(ss[:], mean[:]).then_inc(dve_n.mark("r_recip"), 1)
        dve.tensor_tensor(m.h[:], m.h[:], m.y[:], ALU.add).then_inc(dve_n.mark("h"), 1)
        dve.wait_ge(dve_n.sem, dve_n.at("h"))

        def scale(s, i):
            at = bass.ds(i * 2 * GJ + s * GJ, GJ)
            dve.wait_ge(pe_z.sem, pe_z.before(f"z{s}", i))
            dve.tensor_tensor(zt[s][:], m.y[:, at, :], cols(ss[:, at].unsqueeze(2), C), ALU.mult).then_inc(dve_z.mark(f"z{s}"), 1)

        def copy_logits(s, i):
            at = bass.ds(i * 2 * GJ + s * GJ, GJ)
            dve.wait_ge(pe_l.sem, pe_l.at(f"l{s}", i))
            dve.tensor_scalar(lg[:, at, :], ps[0:TM, 4 + s, 0:GJ * NE].rearrange("p (j e) -> p j e", e=NE), 1.0, None, ALU.mult).then_inc(dve_l.mark(f"l{s}"), 1)

        skewed(dve, P, scale, copy_logits)
        S = dve_n
        wide = lambda v: cols(v[:].unsqueeze(2), NE)
        place = desc[:].unsqueeze(1).broadcast_to([TM, J, NE])
        dve.wait_ge(wl, 64)
        dve.wait_ge(dve_l.sem, dve_l.at("l1", P - 1))
        dve.tensor_reduce(mx[:], lg[:], X, ALU.max).then_inc(S.mark("max"), 1)
        dve.wait_ge(S.sem, S.at("max"))
        dve.tensor_tensor(lg[:], lg[:], wide(mx), ALU.subtract).then_inc(S.mark("minus"), 1)
        dve.wait_ge(act_n.sem, act_n.at("exp"))
        dve.tensor_reduce(rs[:], pr[:], X, ALU.add).then_inc(S.mark("sum"), 1)
        dve.wait_ge(S.sem, S.at("sum"))
        dve.reciprocal(mx[:], rs[:]).then_inc(S.mark("recip"), 1)
        dve.wait_ge(S.sem, S.at("recip"))
        dve.tensor_tensor(pr[:], pr[:], wide(mx), ALU.mult).then_inc(S.mark("probs"), 1)
        dve.wait_ge(S.sem, S.at("probs"))
        dve.tensor_reduce(mx[:], pr[:], X, ALU.max).then_inc(S.mark("p1"), 1)
        dve.wait_ge(S.sem, S.at("p1"))
        dve.tensor_tensor(eq[:], pr[:], wide(mx), ALU.is_equal).then_inc(S.mark("eq1"), 1)
        dve.wait_ge(S.sem, S.at("eq1"))
        dve.tensor_tensor(eq[:], eq[:], place, ALU.mult).then_inc(S.mark("cand1"), 1)
        dve.wait_ge(S.sem, S.at("cand1"))
        dve.tensor_reduce(rs[:], eq[:], X, ALU.max).then_inc(S.mark("best1"), 1)
        dve.wait_ge(S.sem, S.at("best1"))
        dve.tensor_tensor(one1[:], place, wide(rs), ALU.is_equal).then_inc(S.mark("one1"), 1)
        dve.wait_ge(S.sem, S.at("one1"))
        dve.scalar_tensor_tensor(out=lg[:], in0=one1[:], scalar=-2.0, in1=pr[:], op0=ALU.mult, op1=ALU.add).then_inc(S.mark("rest"), 1)
        dve.wait_ge(S.sem, S.at("rest"))
        dve.tensor_reduce(p2[:], lg[:], X, ALU.max).then_inc(S.mark("p2"), 1)
        dve.wait_ge(S.sem, S.at("p2"))
        dve.tensor_tensor(eq[:], lg[:], wide(p2), ALU.is_equal).then_inc(S.mark("eq2"), 1)
        dve.wait_ge(S.sem, S.at("eq2"))
        dve.tensor_tensor(eq[:], eq[:], place, ALU.mult).then_inc(S.mark("cand2"), 1)
        dve.wait_ge(S.sem, S.at("cand2"))
        dve.tensor_reduce(rs[:], eq[:], X, ALU.max).then_inc(S.mark("best2"), 1)
        dve.wait_ge(S.sem, S.at("best2"))
        dve.tensor_tensor(one2[:], place, wide(rs), ALU.is_equal).then_inc(S.mark("one2"), 1)
        dve.scalar_tensor_tensor(out=ws[:], in0=mx[:], scalar=1e-9, in1=p2[:], op0=ALU.add, op1=ALU.add).then_inc(S.mark("wsum"), 1)
        dve.wait_ge(S.sem, S.at("wsum"))
        dve.reciprocal(rs[:], ws[:]).then_inc(S.mark("wrecip"), 1)
        dve.wait_ge(S.sem, S.at("wrecip"))
        dve.tensor_tensor(one1[:], one1[:], one2[:], ALU.add).then_inc(S.mark("both"), 1)
        dve.wait_ge(S.sem, S.at("both"))
        dve.tensor_tensor(one1[:], one1[:], pr[:], ALU.mult).then_inc(S.mark("picked"), 1)
        dve.wait_ge(S.sem, S.at("picked"))
        dve.tensor_tensor(m.gates[:], one1[:], wide(rs), ALU.mult).then_inc(S.mark("gates"), 1)
        phase_end(m, dve, ph)

    def gpsimd(pool):
        phase_end(m, pool, ph)

    return dict(sync=sync, tensor=tensor, scalar=scalar, vector=vector, gpsimd=gpsimd)


def experts_phase(nc, m, st, ph):
    NE, HID, KH, N = 8, 170, 85, 2 * TM
    J = NB * T // TM
    R = 3
    P = J // 2 // R
    assert J // 2 == R * P + 1
    NU = R * NE
    GT5 = J * NE // 128
    sb = lambda n, s, d=F32: st.enter_context(nc.sbuf_tensor(n, s, d))
    w13, w2 = sb("ex_w13", [KH, NE, 2, 2, 2, C]), sb("ex_w2", [C, NE, HID])
    rest = sb("ex_w_rest", [2 * C, NE, 4, KH])
    w_hi, w_mid, w_low = (sb(f"ex_w_{n}", [2 * C, NE, 4, KH], BF16) for n in ("hi", "mid", "low_hi"))
    w2T = sb("ex_w2t", [KH, NE, 2, C])
    l2 = sb("ex_ln2", [2 * C, 1])
    gT = sb("ex_gates_turned", [128, GT5, TM])
    z = [sb(f"ex_z{s}", [2 * C, N]) for s in range(R)]
    z_hi, z_rest = sb("ex_z_hi", [2 * C, N], BF16), sb("ex_z_rest", [2 * C, N])
    z_him, z_hil = ([sb(f"ex_z_{n}{s}", [2 * C, N], BF16) for s in range(R)] for n in ("hi_mid", "hi_low"))
    gate_rows = [sb(f"ex_gate_rows{s}", [KH, 2, NE, TM]) for s in range(R)]
    silu = [sb(f"ex_silu{k}", [KH, 2 * N]) for k in range(3)]
    gated = [sb(f"ex_gated{k}", [KH, 2, N]) for k in range(3)]
    hid = [sb(f"ex_hid{k}", [KH, 2, N]) for k in range(3)]
    outT = [sb(f"ex_out_t{s}", [C, N]) for s in range(R)]
    turned = [sb(f"ex_turned{s}", [TM, 2, C]) for s in range(R)]
    res = [sb(f"ex_out{s}", [TM, 2, C]) for s in range(R)]
    ps = m.psum
    OUT, TURNED = 6, 7
    S1 = lambda n, steps: Steps(nc, m.whole, n, steps)
    wl = m.whole.enter_context(nc.semaphore("ex_weights_landed"))
    gates_stored = m.whole.enter_context(nc.semaphore("ex_gates_stored"))
    zl = [Landed(nc, m.whole, f"ex_z_landed{s}", 3) for s in range(R)]
    stored = [Landed(nc, m.whole, f"ex_stored{s}", 2) for s in range(R)]
    pe_w, act_w = S1("ex_pe_w", ["gates"] + [f"w{e}" for e in range(NE)]), S1("ex_act_w", ["gates"] + [f"w{e}" for e in range(NE)])
    pe_u = S1("ex_pe_up", [f"{g}{n}" for n in range(NU) for g in ("silu", "up")])
    pe_d = S1("ex_pe_down", [f"d{n}" for n in range(NU)])
    pe_t = S1("ex_pe_turned", [f"t{s}" for s in range(R)])
    act_s = S1("ex_act_silu", [f"s{n}" for n in range(NU)])
    act_o = S1("ex_act_out", [f"{k}{s}" for s in range(R) for k in ("o", "t")])
    dve_w = S1("ex_dve_w", ["hi", "rest", "mid", "rest2", "low", "low_hi"])
    dve_g = S1("ex_dve_gated", [f"g{n}" for n in range(NU)])
    parts = ["hi", "rest", "mid", "rest2", "low", "hi_mid", "hi_low"]
    pool_z = S1("ex_pool_parts", [f"{n}{s}" for s in range(R) for n in parts])
    dve_h = S1("ex_dve_hidden", [f"h{n}" for n in range(NU)])
    pool_o = S1("ex_pool_out", [f"o{s}" for s in range(R)])

    def wrapped(n, i):
        return (n, i) if n < NU else (n - NU, i + 1)

    def back(S, k, n, i, by):
        return S.at(f"{k}{n - by}", i) if n >= by else S.before(f"{k}{n - by + NU}", i)

    def sync(sp):
        for s in range(R):
            zl[s].start(sp)
            stored[s].start(sp)
        for k, w in enumerate(("ffn_w1", "ffn_w3")):
            for t in range(2):
                for twice in range(2):
                    sp.dma_start(w13[:, :, k, t, twice], m.dram[w][:, t * KH:(t + 1) * KH].rearrange("e k c -> k e c")).then_inc(wl, 16)
        sp.dma_start(w2[:], m.dram["ffn_w2"].rearrange("e c k -> c e k")).then_inc(wl, 16)
        for k in range(2):
            sp.dma_start(l2[C * k:C * k + C], m.dram["ffn_ln2_w"].rearrange("(c o) -> c o", o=1)).then_inc(wl, 16)
        sp.wait_ge(act_w.sem, act_w.at("gates"))
        sp.dma_start(m.dram["gates_d"].rearrange("(b q) p -> q b p", q=128), gT[:]).then_inc(gates_stored, 16)
        sp.wait_ge(gates_stored, 16)

        def load(s, i):
            sp.wait_ge(pool_z.sem, pool_z.before(f"hi_low{s}", i))
            sp.sem_inc(m.gate, 1)
            sp.wait_ge(dve_g.sem, dve_g.before(f"g{s * NE + NE - 1}", i))
            sp.sem_inc(m.gate, 1)
            for k in range(2):
                sp.dma_start(z[s][C * k:C * k + C], m.dram["zt_d"][:, bass.ds(i * R * N + s * N, N)]).then_inc(zl[s].sem, 16)
            rows = m.dram["gates_d"][bass.ds(i * R * 2 * NE + s * 2 * NE, 2 * NE)].rearrange("(o r) p -> o (r p)", o=1)
            sp.dma_start(gate_rows[s][:].rearrange("c j e p -> c (j e p)"), rows.broadcast_to([KH, 2 * NE * TM])).then_inc(zl[s].sem, 16)

        def store(s, i, ready):
            sp.wait_ge(pool_o.sem, ready)
            sp.sem_inc(m.gate, 1)
            dst = m.out.rearrange("b t c -> (b t) c")[bass.ds(i * R * N + s * N, N)].rearrange("(j p) c -> p j c", p=TM)
            for p0, p1 in ((0, 112), (112, TM)):
                sp.dma_start(dst[p0:p1], res[s][p0:p1]).then_inc(stored[s].sem, 16)

        for s in range(R):
            load(s, 0)
        with sp.Fori(1, P) as i:
            for s in range(R):
                load(s, i)
                store(s, i - 1, pool_o.before(f"o{s}", i))
        load(0, P)
        for s in range(R):
            store(s, P - 1, pool_o.at(f"o{s}", P - 1))
        store(0, P, pool_o.at("o0", P))
        sp.wait_ge(stored[0].sem, stored[0].at(P))
        for s in range(1, R):
            sp.wait_ge(stored[s].sem, stored[s].at(P - 1))
        phase_end(m, sp, ph)

    def tensor(pe):
        for S in (pe_w, pe_u, pe_d, pe_t):
            S.start(pe)
        for b in range(GT5):
            mm = pe.transpose(ps[:, 4 + b // 4, b % 4 * TM:b % 4 * TM + TM], m.gates[:, 16 * b:16 * b + 16, :].rearrange("p j e -> p (j e)"), m.ident[0:TM, 0:TM])
        mm.then_inc(pe_w.mark("gates"), 1)
        pe.wait_ge(wl, 16 * 11)
        for e in range(NE):
            if e >= 2:
                pe.wait_ge(act_w.sem, act_w.at(f"w{e - 2}"))
            b = 2 * (e % 2)
            for t in range(2):
                for k in range(2):
                    pe.transpose(ps[:, b, (2 * k + t) * KH:(2 * k + t + 1) * KH], w13[:, e, k, t].rearrange("k w c -> k (w c)"), m.ident[0:KH, 0:KH])
                mm = pe.transpose(ps[0:KH, b + 1, t * C:(t + 1) * C], w2[:, e, t * KH:(t + 1) * KH], m.ident[0:C, 0:C])
            mm.then_inc(pe_w.mark(f"w{e}"), 1)
        pe.wait_ge(act_w.sem, act_w.at(f"w{NE - 1}"))
        pe.wait_ge(dve_w.sem, dve_w.at("low_hi"))

        def up(n, i):
            n, i = wrapped(n, i)
            s, e = divmod(n, NE)
            if e == 0:
                pe.wait_ge(pool_z.sem, pool_z.at(f"hi_low{s}", i))
            pe.wait_ge(dve_h.sem, back(dve_h, "h", n, i, 3))
            pe.sem_inc(m.gate, 1)
            b = 2 * (n % 3)
            for k, name in enumerate(("silu", "up")):
                for t in range(2):
                    for w, x in ((w_hi, z_him), (w_mid, z_him), (w_low, z_hil)):
                        mm = pe.matmul(ps[0:KH, b + k, t * N:(t + 1) * N], w[:, e, 2 * k + t, :], x[s][:], start=w is w_hi, stop=w is w_low)
                mm.then_inc(pe_u.mark(f"{name}{n}"), 1)

        def down(n, i):
            s, e = divmod(n, NE)
            pe.wait_ge(dve_h.sem, dve_h.at(f"h{n}", i))
            if e == 0:
                pe.wait_ge(act_o.sem, act_o.at(f"o{s - 1}", i) if s else act_o.before(f"o{R - 1}", i))
            pe.sem_inc(m.gate, 1)
            for t in range(2):
                mm = pe.matmul(ps[0:C, OUT, 0:N], w2T[:, e, t, :], hid[n % 3][:, t], start=e == 0 and t == 0, stop=e == NE - 1 and t == 1)
            mm.then_inc(pe_d.mark(f"d{n}"), 1)

        def turn(s, i):
            pe.wait_ge(act_o.sem, act_o.at(f"o{s}", i))
            pe.wait_ge(act_o.sem, act_o.at(f"t{s - 1}", i) if s else act_o.before(f"t{R - 1}", i))
            pe.sem_inc(m.gate, 1)
            for j in range(2):
                mm = pe.transpose(ps[0:TM, TURNED, j * C:(j + 1) * C], outT[s][:, j * TM:(j + 1) * TM], m.ident[0:C, 0:C])
            mm.then_inc(pe_t.mark(f"t{s}"), 1)

        def one_pass(i, units=NU, end=False):
            for n in range(units):
                if n % NE and not (end and n + 2 >= units):
                    up(n + 2, i)
                down(n, i)
                if n % NE == NE - 1:
                    if not end:
                        up(n + 3, i)
                    turn(n // NE, i)

        for n in range(3):
            up(n, 0)
        with pe.Fori(0, P) as i:
            one_pass(i)
        one_pass(P, NE, end=True)
        phase_end(m, pe, ph)

    def scalar(act):
        for S in (act_w, act_s, act_o):
            S.start(act)
        act.wait_ge(pe_w.sem, pe_w.at("gates"))
        act.activation(gT[:, 0:4], ps[:, 4, 0:4 * TM].rearrange("q (b p) -> q b p", b=4), ACT.Copy)
        act.activation(gT[:, 4], ps[:, 5, 0:TM], ACT.Copy).then_inc(act_w.mark("gates"), 1)
        act.wait_ge(wl, 16 * 11)
        for e in range(NE):
            b = 2 * (e % 2)
            act.wait_ge(pe_w.sem, pe_w.at(f"w{e}"))
            act.activation(rest[:, e], ps[:, b, 0:4 * KH].rearrange("c (t k) -> c t k", t=4), ACT.Copy, scale=l2[:])
            act.activation(w2T[:, e], ps[0:KH, b + 1, 0:2 * C].rearrange("c (t k) -> c t k", t=2), ACT.Copy).then_inc(act_w.mark(f"w{e}"), 1)
        act.preload_act_table(ACT.Silu)

        def silu_of(n, i):
            n, i = wrapped(n, i)
            act.wait_ge(pe_u.sem, pe_u.at(f"silu{n}", i))
            act.wait_ge(dve_h.sem, back(dve_h, "h", n, i, 3))
            act.activation(silu[n % 3][:], ps[0:KH, 2 * (n % 3), 0:2 * N], ACT.Silu).then_inc(act_s.mark(f"s{n}"), 1)

        def one_pass(i, units=NU, end=False):
            for n in range(units):
                if n % NE and not (end and n + 2 >= units):
                    silu_of(n + 2, i)
                if n % NE == NE - 1:
                    s = n // NE
                    act.wait_ge(pe_d.sem, pe_d.at(f"d{n}", i))
                    act.wait_ge(pe_t.sem, pe_t.before(f"t{s}", i))
                    act.activation(outT[s][:], ps[0:C, OUT, 0:N], ACT.Copy).then_inc(act_o.mark(f"o{s}"), 1)
                    if not end:
                        silu_of(n + 3, i)
                    act.wait_ge(pe_t.sem, pe_t.at(f"t{s}", i))
                    act.wait_ge(pool_o.sem, pool_o.before(f"o{s}", i))
                    act.activation(turned[s][:], ps[0:TM, TURNED, 0:2 * C].rearrange("p (j c) -> p j c", j=2), ACT.Copy).then_inc(act_o.mark(f"t{s}"), 1)

        for n in range(3):
            silu_of(n, 0)
        with act.Fori(0, P) as i:
            one_pass(i)
        one_pass(P, NE, end=True)
        phase_end(m, act, ph)

    def vector(dve):
        for S in (dve_w, dve_g, dve_h):
            S.start(dve)
        dve.wait_ge(act_w.sem, act_w.at(f"w{NE - 1}"))
        dve.tensor_copy(w_hi[:], rest[:]).then_inc(dve_w.mark("hi"), 1)
        dve.wait_ge(dve_w.sem, dve_w.at("hi"))
        dve.tensor_tensor(rest[:], rest[:], w_hi[:], ALU.subtract).then_inc(dve_w.mark("rest"), 1)
        dve.wait_ge(dve_w.sem, dve_w.at("rest"))
        dve.tensor_copy(w_mid[:], rest[:]).then_inc(dve_w.mark("mid"), 1)
        dve.wait_ge(dve_w.sem, dve_w.at("mid"))
        dve.tensor_tensor(rest[:], rest[:], w_mid[:], ALU.subtract).then_inc(dve_w.mark("rest2"), 1)
        dve.wait_ge(dve_w.sem, dve_w.at("rest2"))
        dve.tensor_copy(w_low[0:C], rest[0:C]).then_inc(dve_w.mark("low"), 1)
        dve.tensor_copy(w_low[C:2 * C], w_hi[C:2 * C]).then_inc(dve_w.mark("low_hi"), 1)

        def hidden(n, i):
            s, e = divmod(n, NE)
            if e == 0:
                dve.wait_ge(zl[s].sem, zl[s].at(i))
            dve.wait_ge(act_s.sem, act_s.at(f"s{n}", i))
            dve.tensor_tensor(gated[n % 3][:].rearrange("k t (j p) -> k t j p", j=2), silu[n % 3][:].rearrange("k (t j p) -> k t j p", t=2, j=2),
                              gate_rows[s][:, :, e].unsqueeze(1).broadcast_to([KH, 2, 2, TM]), ALU.mult).then_inc(dve_g.mark(f"g{n}"), 1)
            dve.wait_ge(dve_g.sem, dve_g.at(f"g{n}", i))
            dve.wait_ge(pe_u.sem, pe_u.at(f"up{n}", i))
            dve.wait_ge(pe_d.sem, back(pe_d, "d", n, i, 3))
            dve.tensor_tensor(hid[n % 3][:].rearrange("k t n -> k (t n)"), ps[0:KH, 2 * (n % 3) + 1, 0:2 * N], gated[n % 3][:].rearrange("k t n -> k (t n)"), ALU.mult).then_inc(dve_h.mark(f"h{n}"), 1)

        def one_pass(i, units=NU, end=False):
            for n in range(units):
                hidden(n, i)

        with dve.Fori(0, P) as i:
            one_pass(i)
        one_pass(P, NE, end=True)
        phase_end(m, dve, ph)

    def gpsimd(pool):
        pool_o.start(pool)
        pool_z.start(pool)

        def split(s, i):
            top, low = slice(0, C), slice(C, 2 * C)
            step = lambda n: pool_z.at(f"{n}{s}", i)
            pool.wait_ge(zl[s].sem, zl[s].at(i))
            pool.wait_ge(pe_u.sem, pe_u.before(f"up{s * NE + NE - 1}", i))
            pool.sem_inc(m.gate, 1)
            pool.tensor_copy(z_hi[:], z[s][:]).then_inc(pool_z.mark(f"hi{s}"), 1)
            pool.wait_ge(pool_z.sem, step("hi"))
            pool.sem_inc(m.gate, 1)
            pool.tensor_tensor(z_rest[:], z[s][:], z_hi[:], ALU.subtract).then_inc(pool_z.mark(f"rest{s}"), 1)
            pool.wait_ge(pool_z.sem, step("rest"))
            pool.sem_inc(m.gate, 1)
            pool.tensor_copy(z_him[s][low], z_rest[low]).then_inc(pool_z.mark(f"mid{s}"), 1)
            pool.wait_ge(pool_z.sem, step("mid"))
            pool.sem_inc(m.gate, 1)
            pool.tensor_tensor(z_rest[low], z_rest[low], z_him[s][low], ALU.subtract).then_inc(pool_z.mark(f"rest2{s}"), 1)
            pool.wait_ge(pool_z.sem, step("rest2"))
            pool.sem_inc(m.gate, 1)
            pool.tensor_copy(z_hil[s][low], z_rest[low]).then_inc(pool_z.mark(f"low{s}"), 1)
            pool.tensor_copy(z_him[s][top], z_hi[top]).then_inc(pool_z.mark(f"hi_mid{s}"), 1)
            pool.tensor_copy(z_hil[s][top], z_hi[top]).then_inc(pool_z.mark(f"hi_low{s}"), 1)
            pool.wait_ge(pool_z.sem, step("hi_low"))
            pool.sem_inc(m.gate, 1)

        def finish(s, i):
            pool.wait_ge(act_o.sem, act_o.at(f"t{s}", i))
            pool.wait_ge(stored[s].sem, stored[s].before(i))
            pool.sem_inc(m.gate, 1)
            pool.tensor_tensor(res[s][:], turned[s][:], m.h[:, bass.ds(i * 2 * R + 2 * s, 2), :], ALU.add).then_inc(pool_o.mark(f"o{s}"), 1)

        for s in range(R):
            split(s, 0)
        with pool.Fori(0, P - 1) as i:
            for s in range(R):
                finish(s, i)
                split(s, i + 1)
        for s in range(R):
            finish(s, P - 1)
            if s == 0:
                split(0, P)
        finish(0, P)
        phase_end(m, pool, ph)

    return dict(sync=sync, tensor=tensor, scalar=scalar, vector=vector, gpsimd=gpsimd)


PHASES = [patch_phase, vit_phase, text_phase, joint_in_phase, joint_phase, joint_out_phase, causal_phase, causal_out_phase, experts_phase]
DEBUG = False





def program(nc, dram, scratch, out):
    with ExitStack() as whole:
        m = Shared({**dram, **scratch})
        m.out = out
        m.whole = whole
        m.psum = whole.enter_context(nc.psum_tensor("banks", [128, 8, BANK], F32))
        m.ident = whole.enter_context(nc.sbuf_tensor("ident", [128, 128], F32))
        m.phase_done = whole.enter_context(nc.semaphore("phase_done"))
        m.gate = whole.enter_context(nc.semaphore("gate"))
        m.ident_landed = whole.enter_context(nc.semaphore("ident_landed"))
        m.vit_x = whole.enter_context(nc.sbuf_tensor("vit_x", [128, 16, C], F32))
        m.pos_tile = whole.enter_context(nc.sbuf_tensor("pos_tile", [128, C], F32))
        m.h = whole.enter_context(nc.sbuf_tensor("h", [TM, NB * T // TM, C], F32))
        m.y = whole.enter_context(nc.sbuf_tensor("y", [TM, NB * T // TM, C], F32))
        m.gates = whole.enter_context(nc.sbuf_tensor("gates", [TM, NB * T // TM, 8], F32))
        phases = []
        for ph, build in enumerate(PHASES):
            with ExitStack() as st:
                phases.append(build(nc, m, st, ph))
        block = whole.enter_context(nc.Block())

        @block.sync
        def _(sp):
            sp.dma_start(m.ident[:], m.dram["identity"]).then_inc(m.ident_landed, 16)
            for p in phases:
                p["sync"](sp)

        @block.tensor
        def _(pe):
            pe.wait_ge(m.ident_landed, 16)
            for p in phases:
                p["tensor"](pe)

        @block.scalar
        def _(act):
            for p in phases:
                p["scalar"](act)

        @block.vector
        def _(dve):
            for p in phases:
                p["vector"](dve)

        @block.gpsimd
        def _(pool):
            for p in phases:
                p["gpsimd"](pool)


def _constants(np):
    f = np.float32
    freqs = np.outer(np.arange(T, dtype=f), 1.0 / 10000.0 ** (np.arange(0, 16, 2, dtype=f) / 16)).astype(f)
    sign = np.repeat(np.array([-1, 1], f), 8)[:, None]
    cos, sin = np.cos(np.tile(freqs, 2)).T, sign * np.sin(np.tile(freqs, 2)).T
    table = lambda t: np.tile(np.concatenate([np.concatenate([0.25 * t, t], 1), np.zeros((16, 2 * T), f)]), (4, 1)).astype(f)
    row = 5 * np.arange(TM)[:, None] + np.arange(5)
    mask = np.where(np.arange(T) <= (row // 4)[:, :, None], 0, MASKED).astype(f).reshape(TM, 5 * T)
    pick = (row[:, :, None] % 4 // 2 == np.arange(2)).astype(f).reshape(TM, 10)
    tail = np.kron(np.eye(4, dtype=f), np.concatenate([np.zeros((17, 64), f), np.ones((17, 1), f)], 1))
    return {
        "tail_blocks": tail,
        "rope_cos": table(cos),
        "rope_sin": table(sin),
        "causal_mask": mask,
        "pick_value_head": pick,
        "own_block": np.kron(np.eye(5, dtype=f), np.ones((17, 1), f)),
        "descending": np.arange(8, 0, -1).astype(f),
        "identity": np.eye(128, dtype=f),
        "inv_count": (1 / np.minimum(np.arange(16) + 1, 5)).astype(f),
        "id_col": (np.arange(128) % 64).astype(f)[:, None],
        "id_row": np.arange(64).astype(f),
    }


_SCRATCH = {"h_d": (NB * T, C), "xt_d": (C, NB * T), "v_d": (NB, T * C), "ctx_d": (NB, T * 8 * C),
            "zt_d": (C, NB * T), "y_d": (NB, T * C), "gates_d": (NB * T // TM * 8, TM)}


def kernel(**inputs):
    import numpy as _np
    import concourse.bacc as _bacc
    from concourse import mybir as _mybir
    from concourse.bass_utils import run_bass_kernel_spmd as _run

    nc = _bacc.Bacc("TRN2", target_bir_lowering=False, num_devices=1)
    arrays, dram = {}, {}
    for name, a in {**inputs, **_constants(_np)}.items():
        a = _np.ascontiguousarray(a)
        arrays[f"in_{name}"] = a
        dram[name.removeprefix("L0_")] = nc.dram_tensor(f"in_{name}", a.shape, _mybir.dt.from_np(a.dtype), kind="ExternalInput").ap()
    scratch = {n: nc.dram_tensor(n, s, _mybir.dt.float32, kind="ExternalOutput" if DEBUG else "Internal").ap() for n, s in _SCRATCH.items()}
    out = nc.dram_tensor("fused_out", (NB, T, C), _mybir.dt.float32, kind="ExternalOutput").ap()
    program(nc, dram, scratch, out)
    r = _run(nc, [arrays], core_ids=[0])
    return r.results[0]["fused_out"]
```
